# Optimizing a Trainium2 kernel written in Bass

```python
import numpy as np
import jax
import jax.numpy as jnp

def _softmax(x, axis=-1):
    return jax.nn.softmax(x, axis=axis)

def _gelu(x):
    return jax.nn.gelu(x, approximate=True)

def _silu(x):
    return jax.nn.silu(x)

def _sigmoid(x):
    return jax.nn.sigmoid(x)

def _layernorm(x, axis=-1, eps=1e-05):
    m = jnp.mean(x, axis=axis, keepdims=True)
    v = jnp.var(x, axis=axis, keepdims=True)
    return (x - m) / jnp.sqrt(v + eps)

def _scatter_add(tgt, idx, src, axis=0):
    return tgt.at[idx].add(src)

def _segment_sum(src, seg, n):
    return jax.ops.segment_sum(src, seg, n)
kernel_name = 'mk_decoder_postln_d4_seqx_r8_adec67'

def setup_inputs(seed: int=0):
    np.random.seed(seed)
    _w = jnp.asarray

    def _rec_inputs():
        import jax
        import jax.numpy as jnp
        _rk = jax.random.key(seed)
        x = -0.0002928 + 1 * jax.random.normal(jax.random.fold_in(_rk, 1), (8, 256, 128), jnp.float32)
        _lenS = 256 - jax.random.randint(jax.random.fold_in(_rk, 7), (8,), 0, max(1, 256 // 4) + 1, jnp.int32)
        _lenS2 = 256 - jax.random.randint(jax.random.fold_in(_rk, 8), (8,), 0, max(1, 256 // 4) + 1, jnp.int32)
        _ctx_1024P = jax.random.normal(jax.random.fold_in(_rk, 11), (8, 16, 128), jnp.float32)
        _ctx_1024c = jax.random.dirichlet(jax.random.fold_in(_rk, 511), 0.3 * jnp.ones((16,), jnp.float32), (8, 256))
        _ctx_1024t = jnp.einsum('bsk,bkd->bsd', _ctx_1024c, _ctx_1024P)
        _ctx_1024t = _ctx_1024t * jax.lax.rsqrt(jnp.mean(jnp.square(_ctx_1024t)) + 1e-12) * 0.953939
        ctx_1024 = -1.39393e-06 + 0.999914 * (_ctx_1024t + 0.3 * jax.random.normal(jax.random.fold_in(_rk, 611), (8, 256, 128), jnp.float32))
        pos_BxS2 = jnp.broadcast_to(jnp.arange(256, dtype=jnp.int32), (8, 256))
        _validS = jnp.arange(256)[None, :] < _lenS[:, None]
        _validS2 = jnp.arange(256)[None, :] < _lenS2[:, None]
        _causal = jnp.tril(jnp.ones((256, 256), dtype=bool))
        mask_Bx1xSxS2_ik1 = jnp.where(jnp.broadcast_to(_validS2[:, None, None, :], (8, 1, 256, 256)), 1, 0).astype(jnp.int32)
        mask_Bx1x1xS2_ff1 = jnp.where(jnp.ones((8, 1, 1, 256), dtype=bool), 1.0, 0.0).astype(jnp.float32)
        return (x, ctx_1024, pos_BxS2, mask_Bx1xSxS2_ik1, mask_Bx1x1xS2_ff1)
    x, ctx_1024, pos_BxS2, mask_Bx1xSxS2_ik1, mask_Bx1x1xS2_ff1 = _rec_inputs()

    def _L0_attn_setup():
        import jax, jax.numpy as jnp
        import numpy as np
        HEAD_DIM = 128
        HIDDEN_DIM = 128
        B, S = (4, 512)
        key = jax.random.key(seed)
        k_x, k_q, k_k, k_v, k_o = jax.random.split(key, 5)
        scale = 1.0 / np.sqrt(HIDDEN_DIM)
        return {'x': jax.random.normal(k_x, (B, S, HIDDEN_DIM), dtype=jnp.float32), 'head_dim_mask': jnp.ones((HEAD_DIM,), dtype=jnp.int32), 'w_q': jax.random.normal(k_q, (HIDDEN_DIM, HEAD_DIM), dtype=jnp.float32) * scale, 'w_k': jax.random.normal(k_k, (HIDDEN_DIM, HEAD_DIM), dtype=jnp.float32) * scale, 'w_v': jax.random.normal(k_v, (HIDDEN_DIM, HEAD_DIM), dtype=jnp.float32) * scale, 'w_o': jax.random.normal(k_o, (HEAD_DIM, HIDDEN_DIM), dtype=jnp.float32) * (1.0 / np.sqrt(HEAD_DIM))}
    _L0_attn_all = _L0_attn_setup()
    _L0_attn_in = {k: v for k, v in _L0_attn_all.items() if k in ('head_dim_mask', 'w_q', 'w_k', 'w_v', 'w_o')}
    del _L0_attn_all

    def _L0_xattn_setup():
        import jax, jax.numpy as jnp
        import numpy as np
        DIM = 128
        HEADS = 16
        HEAD_DIM = DIM // HEADS
        key = jax.random.key(seed)
        ks = jax.random.split(key, 12)
        B, Tq, Tk = (2, 256, 256)
        inp = {'query': jax.random.normal(ks[0], (B, Tq, DIM), jnp.float32), 'key': jax.random.normal(ks[1], (B, Tk, DIM), jnp.float32), 'value': jax.random.normal(ks[2], (B, Tk, DIM), jnp.float32), 'mask': jax.random.randint(ks[3], (B, 1, Tq, Tk), 0, 2, jnp.int32), 'wq': jax.random.uniform(ks[4], (DIM, DIM), jnp.float32, -1.0, 1.0) * np.sqrt(6.0 / (2 * DIM)), 'wk': jax.random.uniform(ks[5], (DIM, DIM), jnp.float32, -1.0, 1.0) * np.sqrt(6.0 / (2 * DIM)), 'wv': jax.random.uniform(ks[6], (DIM, DIM), jnp.float32, -1.0, 1.0) * np.sqrt(6.0 / (2 * DIM)), 'wo': jax.random.uniform(ks[7], (DIM, DIM), jnp.float32, -1.0, 1.0) * np.sqrt(6.0 / (2 * DIM)), 'bq': jnp.zeros((DIM,), jnp.float32), 'bk': jnp.zeros((DIM,), jnp.float32), 'bv': jnp.zeros((DIM,), jnp.float32), 'bo': jnp.zeros((DIM,), jnp.float32)}
        return inp
    _L0_xattn_all = _L0_xattn_setup()
    _L0_xattn_in = {k: v for k, v in _L0_xattn_all.items() if k in ('wq', 'wk', 'wv', 'wo', 'bq', 'bk', 'bv', 'bo')}
    del _L0_xattn_all

    def _L0_ffn_setup():
        import jax, jax.numpy as jnp
        import numpy as np
        E = 8
        TOP_K = 2
        B, S, D = (2, 512, 128)
        H = 512
        CAPACITY = 256

        def _moe(x, Wg, W1, b1, W2, b2):
            b, s, d = x.shape
            xf = x.reshape(b * s, d)
            logits = xf.astype(jnp.float32) @ Wg.astype(jnp.float32)
            probs = jax.nn.softmax(logits, axis=-1)
            vals, idx = jax.lax.top_k(probs, TOP_K)
            w = vals / (jnp.sum(vals, axis=-1, keepdims=True) + 1e-09)
            counts = jnp.zeros((E,), dtype=jnp.int32)
            combine = jnp.zeros((b * s, E), dtype=jnp.float32)
            for k in range(TOP_K):
                oh = jax.nn.one_hot(idx[:, k], E, dtype=jnp.int32)
                pos = jnp.cumsum(oh, axis=0) - 1 + counts[None, :]
                keep = (oh == 1) & (pos < CAPACITY)
                counts = counts + jnp.sum(keep.astype(jnp.int32), axis=0)
                combine = combine + w[:, k][:, None] * keep.astype(jnp.float32)
            out = jnp.zeros_like(xf)
            for e in range(E):
                h = jax.nn.gelu(xf @ W1[e] + b1[e])
                ye = h @ W2[e] + b2[e]
                out = out + combine[:, e][:, None].astype(xf.dtype) * ye
            return out.reshape(b, s, d)
        key = jax.random.key(seed)
        k0, k1, k2, k3 = jax.random.split(key, 4)
        return {'x': jax.random.normal(k0, (B, S, D), dtype=jnp.float32), 'Wg': jax.random.normal(k1, (D, E), dtype=jnp.float32) * 0.02, 'W1': jax.random.normal(k2, (E, D, H), dtype=jnp.float32) * 0.02, 'b1': jnp.zeros((E, H), dtype=jnp.float32), 'W2': jax.random.normal(k3, (E, H, D), dtype=jnp.float32) * 0.02, 'b2': jnp.zeros((E, D), dtype=jnp.float32)}
    _L0_ffn_all = _L0_ffn_setup()
    _L0_ffn_in = {k: v for k, v in _L0_ffn_all.items() if k in ('Wg', 'W1', 'b1', 'W2', 'b2')}
    del _L0_ffn_all

    def _L1_attn_setup():
        import jax, jax.numpy as jnp
        import numpy as np
        INF_APPROX = 1e+30
        ROTARY_BASE = 10000.0
        D_HEAD = 128

        def _rope(x, base=ROTARY_BASE):
            _, length, _, width = x.shape
            half = width // 2
            positions = jnp.arange(length, dtype=x.dtype)
            dims = jnp.arange(half, dtype=x.dtype)
            ang_freqs = jnp.power(base, -dims / half)
            radians = positions[:, None] * ang_freqs[None, :]
            cos = jnp.cos(radians)[None, :, None, :]
            sin = jnp.sin(radians)[None, :, None, :]
            even, odd = jnp.split(x, 2, axis=-1)
            return jnp.concatenate([even * cos - odd * sin, even * sin + odd * cos], axis=-1)
        key = jax.random.key(seed)
        k1, k2, k3, k4, k5 = jax.random.split(key, 5)
        B, T, M, H, D = (2, 512, 128, 8, 128)
        n_layer = 24
        x = jax.random.normal(k1, (B, T, M), dtype=jnp.float32)
        std_qkv = M ** (-0.5)
        std_o = (M * 2 * n_layer) ** (-0.5)
        w_aq = jnp.zeros((M, H, D), dtype=jnp.float32)
        w_ak = std_qkv * jax.random.normal(k3, (M, H, D), dtype=jnp.float32)
        w_av = std_qkv * jax.random.normal(k4, (M, H, D), dtype=jnp.float32)
        w_ao = std_o * jax.random.normal(k5, (H, D, M), dtype=jnp.float32)
        return {'x': x, 'w_aq': w_aq, 'w_ak': w_ak, 'w_av': w_av, 'w_ao': w_ao}
    _L1_attn_all = _L1_attn_setup()
    _L1_attn_in = {k: v for k, v in _L1_attn_all.items() if k in ('w_aq', 'w_ak', 'w_av', 'w_ao')}
    del _L1_attn_all

    def _L1_xattn_setup():
        import jax, jax.numpy as jnp
        import numpy as np
        D_MODEL = 128
        N_HEADS = 16
        D_K = D_MODEL // N_HEADS
        key = jax.random.key(seed)
        ks = jax.random.split(key, 11)
        B, L, S = (2, 256, 256)
        scale = 1.0 / np.sqrt(D_MODEL)
        return {'x_q': jax.random.normal(ks[0], (B, L, D_MODEL), jnp.float32), 'x_k': jax.random.normal(ks[1], (B, S, D_MODEL), jnp.float32), 'x_v': jax.random.normal(ks[2], (B, S, D_MODEL), jnp.float32), 'W_Q': jax.random.normal(ks[3], (D_MODEL, D_MODEL), jnp.float32) * scale, 'b_Q': jax.random.normal(ks[4], (D_MODEL,), jnp.float32) * 0.01, 'W_K': jax.random.normal(ks[5], (D_MODEL, D_MODEL), jnp.float32) * scale, 'b_K': jax.random.normal(ks[6], (D_MODEL,), jnp.float32) * 0.01, 'W_V': jax.random.normal(ks[7], (D_MODEL, D_MODEL), jnp.float32) * scale, 'b_V': jax.random.normal(ks[8], (D_MODEL,), jnp.float32) * 0.01, 'W_O': jax.random.normal(ks[9], (D_MODEL, D_MODEL), jnp.float32) * scale, 'b_O': jax.random.normal(ks[10], (D_MODEL,), jnp.float32) * 0.01}
    _L1_xattn_all = _L1_xattn_setup()
    _L1_xattn_in = {k: v for k, v in _L1_xattn_all.items() if k in ('W_Q', 'b_Q', 'W_K', 'b_K', 'W_V', 'b_V', 'W_O', 'b_O')}
    del _L1_xattn_all

    def _L1_ffn_setup():
        import jax, jax.numpy as jnp
        import numpy as np
        DIM = 128
        HIDDEN = 384
        SCALE = 1.0 / 127.0

        def _dequant(w_int, dtype):
            return w_int.astype(dtype) * jnp.asarray(SCALE, dtype)
        key = jax.random.key(seed)
        k_x, k_g, k_u, k_d = jax.random.split(key, 4)
        x = jax.random.normal(k_x, (4, 256, DIM), dtype=jnp.float32)
        w_gate = jax.random.randint(k_g, (HIDDEN, DIM), -127, 128, dtype=jnp.int32)
        w_up = jax.random.randint(k_u, (HIDDEN, DIM), -127, 128, dtype=jnp.int32)
        w_down = jax.random.randint(k_d, (DIM, HIDDEN), -127, 128, dtype=jnp.int32)
        return {'x': x, 'w_gate': w_gate, 'w_up': w_up, 'w_down': w_down}
    _L1_ffn_all = _L1_ffn_setup()
    _L1_ffn_in = {k: v for k, v in _L1_ffn_all.items() if k in ('w_gate', 'w_up', 'w_down')}
    del _L1_ffn_all

    def _L2_attn_setup():
        import jax, jax.numpy as jnp
        import numpy as np
        BATCH, L, DM, N, R = (2, 256, 128, 16, 64)
        DT_MIN, DT_MAX = (0.001, 0.1)
        key = jax.random.key(seed)
        ks = jax.random.split(key, 6)
        x = jax.random.normal(ks[0], (BATCH, L, DM), jnp.float32)
        W_in = jax.random.normal(ks[1], (DM, 2 * N), jnp.float32) / np.sqrt(DM)
        b_in = jnp.zeros((2 * N,), jnp.float32)
        W_dt1 = jax.random.normal(ks[2], (DM, R), jnp.float32) / np.sqrt(DM)
        b_dt1 = jnp.zeros((R,), jnp.float32)
        dt_std = R ** (-0.5)
        W_dt2 = jax.random.uniform(ks[3], (R, DM), jnp.float32, minval=-dt_std, maxval=dt_std)
        u = jax.random.uniform(ks[4], (DM,), jnp.float32)
        dt0 = jnp.exp(u * (np.log(DT_MAX) - np.log(DT_MIN)) + np.log(DT_MIN))
        b_dt2 = dt0 + jnp.log(-jnp.expm1(-dt0))
        A_row = -(1.0 + jnp.arange(N, dtype=jnp.float32))
        A = jnp.tile(A_row[None, None, None, :], (1, 1, DM, 1))
        D = jnp.ones((DM,), jnp.float32)
        return {'x': x, 'W_in': W_in, 'b_in': b_in, 'W_dt1': W_dt1, 'b_dt1': b_dt1, 'W_dt2': W_dt2, 'b_dt2': b_dt2, 'A': A, 'D': D}
    _L2_attn_all = _L2_attn_setup()
    _L2_attn_in = {k: v for k, v in _L2_attn_all.items() if k in ('W_in', 'b_in', 'W_dt1', 'b_dt1', 'W_dt2', 'b_dt2', 'A', 'D')}
    del _L2_attn_all

    def _L2_xattn_setup():
        import jax, jax.numpy as jnp
        import numpy as np
        D_MODEL = 128
        NUM_HEADS = 16
        HEAD_DIM = D_MODEL // NUM_HEADS
        THETA = 10000.0
        B, S = (4, 256)

        def _rope(x, pos):
            half = HEAD_DIM // 2
            inv_freq = THETA ** (-(jnp.arange(half, dtype=jnp.float32) * 2.0) / HEAD_DIM)
            ang = pos.astype(jnp.float32)[:, None, :, None] * inv_freq
            cos, sin = (jnp.cos(ang), jnp.sin(ang))
            x1, x2 = (x[..., 0::2], x[..., 1::2])
            r1 = x1 * cos - x2 * sin
            r2 = x1 * sin + x2 * cos
            return jnp.stack([r1, r2], axis=-1).reshape(x.shape)
        key = jax.random.key(seed)
        ks = jax.random.split(key, 12)
        scale = 1.0 / np.sqrt(D_MODEL)
        inp = {'query': jax.random.normal(ks[0], (B, S, D_MODEL), dtype=jnp.float32), 'key': jax.random.normal(ks[1], (B, S, D_MODEL), dtype=jnp.float32), 'value': jax.random.normal(ks[2], (B, S, D_MODEL), dtype=jnp.float32), 'token_positions': jnp.broadcast_to(jnp.arange(S, dtype=jnp.int32), (B, S)), 'w_q': jax.random.normal(ks[3], (D_MODEL, D_MODEL), dtype=jnp.float32) * scale, 'b_q': jnp.zeros((D_MODEL,), dtype=jnp.float32), 'w_k': jax.random.normal(ks[4], (D_MODEL, D_MODEL), dtype=jnp.float32) * scale, 'b_k': jnp.zeros((D_MODEL,), dtype=jnp.float32), 'w_v': jax.random.normal(ks[5], (D_MODEL, D_MODEL), dtype=jnp.float32) * scale, 'b_v': jnp.zeros((D_MODEL,), dtype=jnp.float32), 'w_o': jax.random.normal(ks[6], (D_MODEL, D_MODEL), dtype=jnp.float32) * scale, 'b_o': jnp.zeros((D_MODEL,), dtype=jnp.float32)}
        return inp
    _L2_xattn_all = _L2_xattn_setup()
    _L2_xattn_in = {k: v for k, v in _L2_xattn_all.items() if k in ('w_q', 'b_q', 'w_k', 'b_k', 'w_v', 'b_v', 'w_o', 'b_o')}
    del _L2_xattn_all

    def _L2_ffn_setup():
        import jax, jax.numpy as jnp
        import numpy as np
        import math
        D = 128
        H = 16
        E = 8
        TOPK = 2
        LAT = D // 2
        KPH = LAT // H
        HD = D // H

        def _forward(hs, q_w, q_b, k_w, k_b, v_w, v_b, o_w, o_b, router_w, router_b, w1, b1, w2, b2):
            B, S, _ = hs.shape
            Q = (hs @ q_w + q_b).reshape(B, S, H, HD).transpose(0, 2, 1, 3)
            K = (hs @ k_w + k_b).reshape(B, S, H, KPH).transpose(0, 2, 1, 3)
            V = (hs @ v_w + v_b).reshape(B, S, H, KPH).transpose(0, 2, 1, 3)
            scores = jnp.einsum('bhsk,bhtk->bhst', Q[..., :KPH], K) / math.sqrt(KPH)
            attn = jax.nn.softmax(scores, axis=-1)
            ao = jnp.einsum('bhst,bhtv->bhsv', attn, V)
            ao = ao.transpose(0, 2, 1, 3).reshape(B, S, H * KPH)
            ao = jnp.concatenate([ao, jnp.zeros((B, S, D - LAT), ao.dtype)], axis=-1)
            mla_out = ao @ o_w + o_b
            probs = jax.nn.softmax(mla_out @ router_w + router_b, axis=-1)
            topw, topi = jax.lax.top_k(probs, TOPK)
            topw = topw / (topw.sum(-1, keepdims=True) + 1e-08)
            combine = jnp.sum(jax.nn.one_hot(topi, E, dtype=probs.dtype) * topw[..., None], axis=-2)
            h1 = jnp.einsum('bsd,edf->ebsf', mla_out, w1) + b1[:, None, None, :]
            h1 = jax.nn.gelu(h1, approximate=False)
            h2 = jnp.einsum('ebsf,efd->ebsd', h1, w2) + b2[:, None, None, :]
            moe_out = jnp.einsum('bse,ebsd->bsd', combine, h2)
            return hs + 0.3 * moe_out
        key = jax.random.key(seed)
        ks = jax.random.split(key, 16)
        s = 0.02
        inp = {'hidden_states': jax.random.normal(ks[0], (2, 256, D), jnp.float32), 'q_w': jax.random.normal(ks[1], (D, D), jnp.float32) * s, 'q_b': jnp.zeros((D,), jnp.float32), 'k_w': jax.random.normal(ks[2], (D, LAT), jnp.float32) * s, 'k_b': jnp.zeros((LAT,), jnp.float32), 'v_w': jax.random.normal(ks[3], (D, LAT), jnp.float32) * s, 'v_b': jnp.zeros((LAT,), jnp.float32), 'o_w': jax.random.normal(ks[4], (D, D), jnp.float32) * s, 'o_b': jnp.zeros((D,), jnp.float32), 'router_w': jax.random.normal(ks[5], (D, E), jnp.float32) * s, 'router_b': jnp.zeros((E,), jnp.float32), 'w1': jax.random.normal(ks[6], (E, D, 2 * D), jnp.float32) * s, 'b1': jnp.zeros((E, 2 * D), jnp.float32), 'w2': jax.random.normal(ks[7], (E, 2 * D, D), jnp.float32) * s, 'b2': jnp.zeros((E, D), jnp.float32)}
        return inp
    _L2_ffn_all = _L2_ffn_setup()
    _L2_ffn_in = {k: v for k, v in _L2_ffn_all.items() if k in ('q_w', 'q_b', 'k_w', 'k_b', 'v_w', 'v_b', 'o_w', 'o_b', 'router_w', 'router_b', 'w1', 'b1', 'w2', 'b2')}
    del _L2_ffn_all

    def _L3_attn_setup():
        import jax, jax.numpy as jnp
        import numpy as np
        import math
        E, H, T, B = (128, 16, 256, 2)
        HD = E // H
        NUM_BUCKETS, MAX_DIST = (32, 128)

        def _rel_bucket(rp):
            nb = NUM_BUCKETS // 2
            buckets = (rp > 0).astype(jnp.int32) * nb
            rpa = jnp.abs(rp)
            max_exact = nb // 2
            large = max_exact + (jnp.log(jnp.maximum(rpa, 1).astype(jnp.float32) / max_exact) / math.log(MAX_DIST / max_exact) * (nb - max_exact)).astype(jnp.int32)
            large = jnp.minimum(large, nb - 1)
            return buckets + jnp.where(rpa < max_exact, rpa, large)
        key = jax.random.key(seed)
        ks = jax.random.split(key, 8)
        s = 0.02
        return {'query': jax.random.normal(ks[0], (T, B, E), jnp.float32), 'q_w': jax.random.normal(ks[1], (E, E), jnp.float32) * s, 'q_b': jnp.zeros((E,), jnp.float32), 'k_w': jax.random.normal(ks[2], (E, E), jnp.float32) * s, 'k_b': jnp.zeros((E,), jnp.float32), 'v_w': jax.random.normal(ks[3], (E, E), jnp.float32) * s, 'v_b': jnp.zeros((E,), jnp.float32), 'out_w': jax.random.normal(ks[4], (E, E), jnp.float32) * s, 'out_b': jnp.zeros((E,), jnp.float32), 'rel_emb': jax.random.normal(ks[5], (NUM_BUCKETS, H), jnp.float32) * s, 'grep_w': jax.random.normal(ks[6], (8, HD), jnp.float32) * s, 'grep_b': jnp.zeros((8,), jnp.float32), 'grep_a': jnp.ones((1, H, 1, 1), jnp.float32)}
    _L3_attn_all = _L3_attn_setup()
    _L3_attn_in = {k: v for k, v in _L3_attn_all.items() if k in ('q_w', 'q_b', 'k_w', 'k_b', 'v_w', 'v_b', 'out_w', 'out_b', 'rel_emb', 'grep_w', 'grep_b', 'grep_a')}
    del _L3_attn_all

    def _L3_xattn_setup():
        import jax, jax.numpy as jnp
        import numpy as np
        D_MODEL = 128
        NUM_HEADS = 16
        DEPTH = D_MODEL // NUM_HEADS

        def _split_heads(x, B):
            return x.reshape(B, -1, NUM_HEADS, DEPTH).transpose(0, 2, 1, 3)
        key = jax.random.key(seed)
        ks = jax.random.split(key, 12)
        B, S = (2, 512)
        s = 1.0 / np.sqrt(D_MODEL)
        return {'Q': jax.random.normal(ks[0], (B, S, D_MODEL), jnp.float32), 'K': jax.random.normal(ks[1], (B, S, D_MODEL), jnp.float32), 'V': jax.random.normal(ks[2], (B, S, D_MODEL), jnp.float32), 'mask': jnp.ones((B, 1, 1, S), jnp.float32), 'Wq': jax.random.normal(ks[3], (D_MODEL, D_MODEL), jnp.float32) * s, 'bq': jax.random.normal(ks[4], (D_MODEL,), jnp.float32) * s, 'Wk': jax.random.normal(ks[5], (D_MODEL, D_MODEL), jnp.float32) * s, 'bk': jax.random.normal(ks[6], (D_MODEL,), jnp.float32) * s, 'Wv': jax.random.normal(ks[7], (D_MODEL, D_MODEL), jnp.float32) * s, 'bv': jax.random.normal(ks[8], (D_MODEL,), jnp.float32) * s, 'Wo': jax.random.normal(ks[9], (D_MODEL, D_MODEL), jnp.float32) * s, 'bo': jax.random.normal(ks[10], (D_MODEL,), jnp.float32) * s}
    _L3_xattn_all = _L3_xattn_setup()
    _L3_xattn_in = {k: v for k, v in _L3_xattn_all.items() if k in ('Wq', 'bq', 'Wk', 'bk', 'Wv', 'bv', 'Wo', 'bo')}
    del _L3_xattn_all

    def _L3_ffn_setup():
        import jax, jax.numpy as jnp
        import numpy as np
        HIDDEN = 128
        INNER = 512

        def _weight_quant(w):
            scale = 1.0 / jnp.clip(jnp.mean(jnp.abs(w)), 1e-05)
            wq = jnp.clip(jnp.round(w * scale), -1.0, 1.0) / scale
            return w + jax.lax.stop_gradient(wq - w)

        def _act_quant(x):
            scale = 127.0 / jnp.clip(jnp.max(jnp.abs(x), axis=-1, keepdims=True), 1e-05)
            xq = jnp.clip(jnp.round(x * scale), -128.0, 127.0) / scale
            return x + jax.lax.stop_gradient(xq - x)

        def _bitlinear(x, w):
            return jnp.einsum('bsi,oi->bso', _act_quant(x), _weight_quant(w))
        key = jax.random.key(seed)
        k0, k1, k2, k3 = jax.random.split(key, 4)
        x = jax.random.normal(k0, (4, 256, HIDDEN), dtype=jnp.float32)
        w_gate = jax.random.normal(k1, (INNER, HIDDEN), dtype=jnp.float32) / np.sqrt(HIDDEN)
        w_up = jax.random.normal(k2, (INNER, HIDDEN), dtype=jnp.float32) / np.sqrt(HIDDEN)
        w_down = jax.random.normal(k3, (HIDDEN, INNER), dtype=jnp.float32) / np.sqrt(INNER)
        return {'x': x, 'w_gate': w_gate, 'w_up': w_up, 'w_down': w_down}
    _L3_ffn_all = _L3_ffn_setup()
    _L3_ffn_in = {k: v for k, v in _L3_ffn_all.items() if k in ('w_gate', 'w_up', 'w_down')}
    del _L3_ffn_all
    return {'x': x, 'ctx_1024': ctx_1024, 'pos_BxS2': pos_BxS2, 'mask_Bx1xSxS2_ik1': mask_Bx1xSxS2_ik1, 'mask_Bx1x1xS2_ff1': mask_Bx1x1xS2_ff1, 'L0_attn_head_dim_mask': _L0_attn_in['head_dim_mask'], 'L0_attn_w_q': _L0_attn_in['w_q'], 'L0_attn_w_k': _L0_attn_in['w_k'], 'L0_attn_w_v': _L0_attn_in['w_v'], 'L0_attn_w_o': _L0_attn_in['w_o'], 'L0_xattn_wq': _L0_xattn_in['wq'], 'L0_xattn_wk': _L0_xattn_in['wk'], 'L0_xattn_wv': _L0_xattn_in['wv'], 'L0_xattn_wo': _L0_xattn_in['wo'], 'L0_xattn_bq': _L0_xattn_in['bq'], 'L0_xattn_bk': _L0_xattn_in['bk'], 'L0_xattn_bv': _L0_xattn_in['bv'], 'L0_xattn_bo': _L0_xattn_in['bo'], 'L0_ffn_Wg': _L0_ffn_in['Wg'], 'L0_ffn_W1': _L0_ffn_in['W1'], 'L0_ffn_b1': _L0_ffn_in['b1'], 'L0_ffn_W2': _L0_ffn_in['W2'], 'L0_ffn_b2': _L0_ffn_in['b2'], 'L1_attn_w_aq': _L1_attn_in['w_aq'], 'L1_attn_w_ak': _L1_attn_in['w_ak'], 'L1_attn_w_av': _L1_attn_in['w_av'], 'L1_attn_w_ao': _L1_attn_in['w_ao'], 'L1_xattn_W_Q': _L1_xattn_in['W_Q'], 'L1_xattn_b_Q': _L1_xattn_in['b_Q'], 'L1_xattn_W_K': _L1_xattn_in['W_K'], 'L1_xattn_b_K': _L1_xattn_in['b_K'], 'L1_xattn_W_V': _L1_xattn_in['W_V'], 'L1_xattn_b_V': _L1_xattn_in['b_V'], 'L1_xattn_W_O': _L1_xattn_in['W_O'], 'L1_xattn_b_O': _L1_xattn_in['b_O'], 'L1_ffn_w_gate': _L1_ffn_in['w_gate'], 'L1_ffn_w_up': _L1_ffn_in['w_up'], 'L1_ffn_w_down': _L1_ffn_in['w_down'], 'L2_attn_W_in': _L2_attn_in['W_in'], 'L2_attn_b_in': _L2_attn_in['b_in'], 'L2_attn_W_dt1': _L2_attn_in['W_dt1'], 'L2_attn_b_dt1': _L2_attn_in['b_dt1'], 'L2_attn_W_dt2': _L2_attn_in['W_dt2'], 'L2_attn_b_dt2': _L2_attn_in['b_dt2'], 'L2_attn_A': _L2_attn_in['A'], 'L2_attn_D': _L2_attn_in['D'], 'L2_xattn_w_q': _L2_xattn_in['w_q'], 'L2_xattn_b_q': _L2_xattn_in['b_q'], 'L2_xattn_w_k': _L2_xattn_in['w_k'], 'L2_xattn_b_k': _L2_xattn_in['b_k'], 'L2_xattn_w_v': _L2_xattn_in['w_v'], 'L2_xattn_b_v': _L2_xattn_in['b_v'], 'L2_xattn_w_o': _L2_xattn_in['w_o'], 'L2_xattn_b_o': _L2_xattn_in['b_o'], 'L2_ffn_q_w': _L2_ffn_in['q_w'], 'L2_ffn_q_b': _L2_ffn_in['q_b'], 'L2_ffn_k_w': _L2_ffn_in['k_w'], 'L2_ffn_k_b': _L2_ffn_in['k_b'], 'L2_ffn_v_w': _L2_ffn_in['v_w'], 'L2_ffn_v_b': _L2_ffn_in['v_b'], 'L2_ffn_o_w': _L2_ffn_in['o_w'], 'L2_ffn_o_b': _L2_ffn_in['o_b'], 'L2_ffn_router_w': _L2_ffn_in['router_w'], 'L2_ffn_router_b': _L2_ffn_in['router_b'], 'L2_ffn_w1': _L2_ffn_in['w1'], 'L2_ffn_b1': _L2_ffn_in['b1'], 'L2_ffn_w2': _L2_ffn_in['w2'], 'L2_ffn_b2': _L2_ffn_in['b2'], 'L3_attn_q_w': _L3_attn_in['q_w'], 'L3_attn_q_b': _L3_attn_in['q_b'], 'L3_attn_k_w': _L3_attn_in['k_w'], 'L3_attn_k_b': _L3_attn_in['k_b'], 'L3_attn_v_w': _L3_attn_in['v_w'], 'L3_attn_v_b': _L3_attn_in['v_b'], 'L3_attn_out_w': _L3_attn_in['out_w'], 'L3_attn_out_b': _L3_attn_in['out_b'], 'L3_attn_rel_emb': _L3_attn_in['rel_emb'], 'L3_attn_grep_w': _L3_attn_in['grep_w'], 'L3_attn_grep_b': _L3_attn_in['grep_b'], 'L3_attn_grep_a': _L3_attn_in['grep_a'], 'L3_xattn_Wq': _L3_xattn_in['Wq'], 'L3_xattn_bq': _L3_xattn_in['bq'], 'L3_xattn_Wk': _L3_xattn_in['Wk'], 'L3_xattn_bk': _L3_xattn_in['bk'], 'L3_xattn_Wv': _L3_xattn_in['Wv'], 'L3_xattn_bv': _L3_xattn_in['bv'], 'L3_xattn_Wo': _L3_xattn_in['Wo'], 'L3_xattn_bo': _L3_xattn_in['bo'], 'L3_ffn_w_gate': _L3_ffn_in['w_gate'], 'L3_ffn_w_up': _L3_ffn_in['w_up'], 'L3_ffn_w_down': _L3_ffn_in['w_down']}

def reference(x, ctx_1024, pos_BxS2, mask_Bx1xSxS2_ik1, mask_Bx1x1xS2_ff1, L0_attn_head_dim_mask, L0_attn_w_q, L0_attn_w_k, L0_attn_w_v, L0_attn_w_o, L0_xattn_wq, L0_xattn_wk, L0_xattn_wv, L0_xattn_wo, L0_xattn_bq, L0_xattn_bk, L0_xattn_bv, L0_xattn_bo, L0_ffn_Wg, L0_ffn_W1, L0_ffn_b1, L0_ffn_W2, L0_ffn_b2, L1_attn_w_aq, L1_attn_w_ak, L1_attn_w_av, L1_attn_w_ao, L1_xattn_W_Q, L1_xattn_b_Q, L1_xattn_W_K, L1_xattn_b_K, L1_xattn_W_V, L1_xattn_b_V, L1_xattn_W_O, L1_xattn_b_O, L1_ffn_w_gate, L1_ffn_w_up, L1_ffn_w_down, L2_attn_W_in, L2_attn_b_in, L2_attn_W_dt1, L2_attn_b_dt1, L2_attn_W_dt2, L2_attn_b_dt2, L2_attn_A, L2_attn_D, L2_xattn_w_q, L2_xattn_b_q, L2_xattn_w_k, L2_xattn_b_k, L2_xattn_w_v, L2_xattn_b_v, L2_xattn_w_o, L2_xattn_b_o, L2_ffn_q_w, L2_ffn_q_b, L2_ffn_k_w, L2_ffn_k_b, L2_ffn_v_w, L2_ffn_v_b, L2_ffn_o_w, L2_ffn_o_b, L2_ffn_router_w, L2_ffn_router_b, L2_ffn_w1, L2_ffn_b1, L2_ffn_w2, L2_ffn_b2, L3_attn_q_w, L3_attn_q_b, L3_attn_k_w, L3_attn_k_b, L3_attn_v_w, L3_attn_v_b, L3_attn_out_w, L3_attn_out_b, L3_attn_rel_emb, L3_attn_grep_w, L3_attn_grep_b, L3_attn_grep_a, L3_xattn_Wq, L3_xattn_bq, L3_xattn_Wk, L3_xattn_bk, L3_xattn_Wv, L3_xattn_bv, L3_xattn_Wo, L3_xattn_bo, L3_ffn_w_gate, L3_ffn_w_up, L3_ffn_w_down):
    import jax
    import jax.numpy as jnp

    def _L0_attn_ref(x, head_dim_mask, w_q, w_k, w_v, w_o):
        import jax, jax.numpy as jnp
        import numpy as np
        HEAD_DIM = 128
        HIDDEN_DIM = 128
        B, S = (4, 512)
        q = jnp.einsum('bsh,hd->bsd', x, w_q)
        k = jnp.einsum('bsh,hd->bsd', x, w_k)
        v = jnp.einsum('bsh,hd->bsd', x, w_v)
        scale = 1.0 / jnp.sqrt(jnp.asarray(HEAD_DIM, dtype=x.dtype))
        scores = jnp.einsum('bqd,bkd->bqk', q, k) * scale
        A = jax.nn.softmax(scores, axis=-1)
        h = jnp.einsum('bqk,bkd->bqd', A, v)
        h = h * head_dim_mask.astype(h.dtype)
        y = jnp.einsum('bsd,dh->bsh', h, w_o)
        return y

    def _L0_xattn_ref(query, key, value, mask, wq, wk, wv, wo, bq, bk, bv, bo):
        import jax, jax.numpy as jnp
        import numpy as np
        DIM = 128
        HEADS = 16
        HEAD_DIM = DIM // HEADS
        B, Tq, C = query.shape
        Tk = key.shape[1]
        scale = 1.0 / np.sqrt(HEAD_DIM)
        q = (query @ wq.T + bq).reshape(B, Tq, HEADS, HEAD_DIM).transpose(0, 2, 1, 3)
        k = (key @ wk.T + bk).reshape(B, Tk, HEADS, HEAD_DIM).transpose(0, 2, 1, 3)
        v = (value @ wv.T + bv).reshape(B, Tk, HEADS, HEAD_DIM).transpose(0, 2, 1, 3)
        scores = jnp.einsum('bhqd,bhkd->bhqk', q, k) * scale
        scores = jnp.clip(scores, -100.0, 100.0)
        scores = jnp.where(mask == 0, -jnp.inf, scores)
        attn = jax.nn.softmax(scores, axis=-1)
        out = jnp.einsum('bhqk,bhkd->bhqd', attn, v)
        out = out.transpose(0, 2, 1, 3).reshape(B, Tq, HEADS * HEAD_DIM)
        return out @ wo.T + bo

    def _L0_ffn_ref(x, Wg, W1, b1, W2, b2):
        import jax, jax.numpy as jnp
        import numpy as np
        E = 8
        TOP_K = 2
        B, S, D = (2, 512, 128)
        H = 512
        CAPACITY = 256

        def _moe(x, Wg, W1, b1, W2, b2):
            b, s, d = x.shape
            xf = x.reshape(b * s, d)
            logits = xf.astype(jnp.float32) @ Wg.astype(jnp.float32)
            probs = jax.nn.softmax(logits, axis=-1)
            vals, idx = jax.lax.top_k(probs, TOP_K)
            w = vals / (jnp.sum(vals, axis=-1, keepdims=True) + 1e-09)
            counts = jnp.zeros((E,), dtype=jnp.int32)
            combine = jnp.zeros((b * s, E), dtype=jnp.float32)
            for k in range(TOP_K):
                oh = jax.nn.one_hot(idx[:, k], E, dtype=jnp.int32)
                pos = jnp.cumsum(oh, axis=0) - 1 + counts[None, :]
                keep = (oh == 1) & (pos < CAPACITY)
                counts = counts + jnp.sum(keep.astype(jnp.int32), axis=0)
                combine = combine + w[:, k][:, None] * keep.astype(jnp.float32)
            out = jnp.zeros_like(xf)
            for e in range(E):
                h = jax.nn.gelu(xf @ W1[e] + b1[e])
                ye = h @ W2[e] + b2[e]
                out = out + combine[:, e][:, None].astype(xf.dtype) * ye
            return out.reshape(b, s, d)
        return _moe(x, Wg, W1, b1, W2, b2)

    def _L1_attn_ref(x, w_aq, w_ak, w_av, w_ao):
        import jax, jax.numpy as jnp
        import numpy as np
        INF_APPROX = 1e+30
        ROTARY_BASE = 10000.0
        D_HEAD = 128

        def _rope(x, base=ROTARY_BASE):
            _, length, _, width = x.shape
            half = width // 2
            positions = jnp.arange(length, dtype=x.dtype)
            dims = jnp.arange(half, dtype=x.dtype)
            ang_freqs = jnp.power(base, -dims / half)
            radians = positions[:, None] * ang_freqs[None, :]
            cos = jnp.cos(radians)[None, :, None, :]
            sin = jnp.sin(radians)[None, :, None, :]
            even, odd = jnp.split(x, 2, axis=-1)
            return jnp.concatenate([even * cos - odd * sin, even * sin + odd * cos], axis=-1)
        B, T, M = x.shape
        q = jnp.einsum('btm,mhd->bthd', x, w_aq)
        k = jnp.einsum('btm,mhd->bthd', x, w_ak)
        v = jnp.einsum('btm,mhd->bthd', x, w_av)
        q = _rope(q)
        k = _rope(k)
        s = jnp.einsum('bihd,bjhd->bhij', q, k) / D_HEAD
        i = jnp.arange(T)[:, None]
        j = jnp.arange(T)[None, :]
        mask = (i < j).astype(x.dtype)[None, None, :, :]
        s = s - jnp.asarray(INF_APPROX, x.dtype) * mask
        p = jax.nn.softmax(s, axis=-1)
        o = jnp.einsum('bhij,bjhd->bihd', p, v)
        r = jnp.einsum('bihd,hdm->bim', o, w_ao)
        return r

    def _L1_xattn_ref(x_q, x_k, x_v, W_Q, b_Q, W_K, b_K, W_V, b_V, W_O, b_O):
        import jax, jax.numpy as jnp
        import numpy as np
        D_MODEL = 128
        N_HEADS = 16
        D_K = D_MODEL // N_HEADS
        B, L, _ = x_q.shape
        S = x_k.shape[1]
        H, dk = (N_HEADS, D_K)
        Q = (x_q @ W_Q + b_Q).reshape(B, L, H, dk).transpose(0, 2, 1, 3)
        K = (x_k @ W_K + b_K).reshape(B, S, H, dk).transpose(0, 2, 1, 3)
        V = (x_v @ W_V + b_V).reshape(B, S, H, dk).transpose(0, 2, 1, 3)
        scores = jnp.einsum('bhld,bhsd->bhls', Q, K) / jnp.sqrt(jnp.float32(dk))
        attn = jax.nn.softmax(scores, axis=-1)
        ctx = jnp.einsum('bhls,bhsd->bhld', attn, V)
        ctx = ctx.transpose(0, 2, 1, 3).reshape(B, L, H * dk)
        out = ctx @ W_O + b_O
        return out

    def _L1_ffn_ref(x, w_gate, w_up, w_down):
        import jax, jax.numpy as jnp
        import numpy as np
        DIM = 128
        HIDDEN = 384
        SCALE = 1.0 / 127.0

        def _dequant(w_int, dtype):
            return w_int.astype(dtype) * jnp.asarray(SCALE, dtype)
        wg = _dequant(w_gate, x.dtype)
        wu = _dequant(w_up, x.dtype)
        wd = _dequant(w_down, x.dtype)
        gate = jnp.einsum('bsd,hd->bsh', x, wg)
        up = jnp.einsum('bsd,hd->bsh', x, wu)
        h = jax.nn.silu(gate) * up
        return jnp.einsum('bsh,dh->bsd', h, wd)

    def _L2_attn_ref(x, W_in, b_in, W_dt1, b_dt1, W_dt2, b_dt2, A, D):
        import jax, jax.numpy as jnp
        import numpy as np
        BATCH, L, DM, N, R = (2, 256, 128, 16, 64)
        DT_MIN, DT_MAX = (0.001, 0.1)
        BC = x @ W_in + b_in
        Bm, Cm = (BC[..., :N], BC[..., N:])
        dt = jax.nn.softplus((x @ W_dt1 + b_dt1) @ W_dt2 + b_dt2)
        dt = jnp.clip(dt, 1e-07, 1000000.0)
        tmp = A * dt[..., None]
        A_bar = jnp.exp(tmp)
        B_barX = jnp.expm1(tmp) / tmp * dt[..., None] * Bm[:, :, None, :] * x[..., None]

        def combine(e1, e2):
            a1, b1 = e1
            a2, b2 = e2
            return (a1 * a2, a2 * b1 + b2)
        _, h = jax.lax.associative_scan(combine, (A_bar, B_barX), axis=1)
        return jnp.sum(h * Cm[:, :, None, :], axis=-1) + D * x

    def _L2_xattn_ref(query, key, value, token_positions, w_q, b_q, w_k, b_k, w_v, b_v, w_o, b_o):
        import jax, jax.numpy as jnp
        import numpy as np
        D_MODEL = 128
        NUM_HEADS = 16
        HEAD_DIM = D_MODEL // NUM_HEADS
        THETA = 10000.0
        B, S = (4, 256)

        def _rope(x, pos):
            half = HEAD_DIM // 2
            inv_freq = THETA ** (-(jnp.arange(half, dtype=jnp.float32) * 2.0) / HEAD_DIM)
            ang = pos.astype(jnp.float32)[:, None, :, None] * inv_freq
            cos, sin = (jnp.cos(ang), jnp.sin(ang))
            x1, x2 = (x[..., 0::2], x[..., 1::2])
            r1 = x1 * cos - x2 * sin
            r2 = x1 * sin + x2 * cos
            return jnp.stack([r1, r2], axis=-1).reshape(x.shape)
        b, s, _ = query.shape
        Q = query @ w_q + b_q
        K = key @ w_k + b_k
        V = value @ w_v + b_v
        Q = Q.reshape(b, s, NUM_HEADS, HEAD_DIM).transpose(0, 2, 1, 3)
        K = K.reshape(b, s, NUM_HEADS, HEAD_DIM).transpose(0, 2, 1, 3)
        V = V.reshape(b, s, NUM_HEADS, HEAD_DIM).transpose(0, 2, 1, 3)
        Q = _rope(Q, token_positions)
        K = _rope(K, token_positions)
        scores = jnp.einsum('bhqd,bhkd->bhqk', Q, K) / jnp.sqrt(jnp.float32(HEAD_DIM))
        causal = jnp.tril(jnp.ones((s, s), dtype=bool))
        scores = jnp.where(causal, scores, -jnp.inf)
        attn = jax.nn.softmax(scores, axis=-1)
        out = jnp.einsum('bhqk,bhkd->bhqd', attn, V)
        out = out.transpose(0, 2, 1, 3).reshape(b, s, D_MODEL)
        return out @ w_o + b_o

    def _L2_ffn_ref(hidden_states, q_w, q_b, k_w, k_b, v_w, v_b, o_w, o_b, router_w, router_b, w1, b1, w2, b2):
        import jax, jax.numpy as jnp
        import numpy as np
        import math
        D = 128
        H = 16
        E = 8
        TOPK = 2
        LAT = D // 2
        KPH = LAT // H
        HD = D // H

        def _forward(hs, q_w, q_b, k_w, k_b, v_w, v_b, o_w, o_b, router_w, router_b, w1, b1, w2, b2):
            B, S, _ = hs.shape
            Q = (hs @ q_w + q_b).reshape(B, S, H, HD).transpose(0, 2, 1, 3)
            K = (hs @ k_w + k_b).reshape(B, S, H, KPH).transpose(0, 2, 1, 3)
            V = (hs @ v_w + v_b).reshape(B, S, H, KPH).transpose(0, 2, 1, 3)
            scores = jnp.einsum('bhsk,bhtk->bhst', Q[..., :KPH], K) / math.sqrt(KPH)
            attn = jax.nn.softmax(scores, axis=-1)
            ao = jnp.einsum('bhst,bhtv->bhsv', attn, V)
            ao = ao.transpose(0, 2, 1, 3).reshape(B, S, H * KPH)
            ao = jnp.concatenate([ao, jnp.zeros((B, S, D - LAT), ao.dtype)], axis=-1)
            mla_out = ao @ o_w + o_b
            probs = jax.nn.softmax(mla_out @ router_w + router_b, axis=-1)
            topw, topi = jax.lax.top_k(probs, TOPK)
            topw = topw / (topw.sum(-1, keepdims=True) + 1e-08)
            combine = jnp.sum(jax.nn.one_hot(topi, E, dtype=probs.dtype) * topw[..., None], axis=-2)
            h1 = jnp.einsum('bsd,edf->ebsf', mla_out, w1) + b1[:, None, None, :]
            h1 = jax.nn.gelu(h1, approximate=False)
            h2 = jnp.einsum('ebsf,efd->ebsd', h1, w2) + b2[:, None, None, :]
            moe_out = jnp.einsum('bse,ebsd->bsd', combine, h2)
            return hs + 0.3 * moe_out
        return _forward(hidden_states, q_w, q_b, k_w, k_b, v_w, v_b, o_w, o_b, router_w, router_b, w1, b1, w2, b2)

    def _L3_attn_ref(query, q_w, q_b, k_w, k_b, v_w, v_b, out_w, out_b, rel_emb, grep_w, grep_b, grep_a):
        import jax, jax.numpy as jnp
        import numpy as np
        import math
        E, H, T, B = (128, 16, 256, 2)
        HD = E // H
        NUM_BUCKETS, MAX_DIST = (32, 128)

        def _rel_bucket(rp):
            nb = NUM_BUCKETS // 2
            buckets = (rp > 0).astype(jnp.int32) * nb
            rpa = jnp.abs(rp)
            max_exact = nb // 2
            large = max_exact + (jnp.log(jnp.maximum(rpa, 1).astype(jnp.float32) / max_exact) / math.log(MAX_DIST / max_exact) * (nb - max_exact)).astype(jnp.int32)
            large = jnp.minimum(large, nb - 1)
            return buckets + jnp.where(rpa < max_exact, rpa, large)
        t, b, e = query.shape
        scaling = HD ** (-0.5)
        rp = jnp.arange(t)[None, :] - jnp.arange(t)[:, None]
        pos_bias = jnp.transpose(rel_emb[_rel_bucket(rp)], (2, 0, 1))
        ql = jnp.transpose(query, (1, 0, 2)).reshape(b, t, H, HD).transpose(0, 2, 1, 3)
        gate_in = (ql @ grep_w.T + grep_b).reshape(b, H, t, 2, 4).sum(-1)
        gate = jax.nn.sigmoid(gate_in)
        gate_a, gate_b = (gate[..., 0:1], gate[..., 1:2])
        gate_a_1 = gate_a * (gate_b * grep_a - 1.0) + 2.0
        bias = gate_a_1 * pos_bias[None]
        q = (query @ q_w.T + q_b) * scaling
        k = query @ k_w.T + k_b
        v = query @ v_w.T + v_b
        qh = q.reshape(t, b, H, HD)
        kh = k.reshape(t, b, H, HD)
        vh = v.reshape(t, b, H, HD)
        scores = jnp.einsum('tbhd,sbhd->bhts', qh, kh) + bias
        attn = jax.nn.softmax(scores, axis=-1)
        out = jnp.einsum('bhts,sbhd->tbhd', attn, vh).reshape(t, b, e)
        return out @ out_w.T + out_b

    def _L3_xattn_ref(Q, K, V, mask, Wq, bq, Wk, bk, Wv, bv, Wo, bo):
        import jax, jax.numpy as jnp
        import numpy as np
        D_MODEL = 128
        NUM_HEADS = 16
        DEPTH = D_MODEL // NUM_HEADS

        def _split_heads(x, B):
            return x.reshape(B, -1, NUM_HEADS, DEPTH).transpose(0, 2, 1, 3)
        B = Q.shape[0]
        q = _split_heads(Q @ Wq.T + bq, B)
        k = _split_heads(K @ Wk.T + bk, B)
        v = _split_heads(V @ Wv.T + bv, B)
        scale = 1.0 / jnp.sqrt(jnp.asarray(DEPTH, q.dtype))
        scores = jnp.einsum('bhqd,bhkd->bhqk', q, k) * scale
        scores = jnp.where(mask == 0, jnp.asarray(-1000000000.0, scores.dtype), scores)
        attn = jax.nn.softmax(scores, axis=-1)
        out = jnp.einsum('bhqk,bhkd->bhqd', attn, v)
        out = out.transpose(0, 2, 1, 3).reshape(B, -1, D_MODEL)
        return out @ Wo.T + bo

    def _L3_ffn_ref(x, w_gate, w_up, w_down):
        import jax, jax.numpy as jnp
        import numpy as np
        HIDDEN = 128
        INNER = 512

        def _weight_quant(w):
            scale = 1.0 / jnp.clip(jnp.mean(jnp.abs(w)), 1e-05)
            wq = jnp.clip(jnp.round(w * scale), -1.0, 1.0) / scale
            return w + jax.lax.stop_gradient(wq - w)

        def _act_quant(x):
            scale = 127.0 / jnp.clip(jnp.max(jnp.abs(x), axis=-1, keepdims=True), 1e-05)
            xq = jnp.clip(jnp.round(x * scale), -128.0, 127.0) / scale
            return x + jax.lax.stop_gradient(xq - x)

        def _bitlinear(x, w):
            return jnp.einsum('bsi,oi->bso', _act_quant(x), _weight_quant(w))
        gate = jax.nn.silu(_bitlinear(x, w_gate))
        up = _bitlinear(x, w_up)
        return _bitlinear(gate * up, w_down)
    x = _layernorm(x + _L0_attn_ref(x, L0_attn_head_dim_mask, L0_attn_w_q, L0_attn_w_k, L0_attn_w_v, L0_attn_w_o), axis=-1)
    x = _layernorm(x + _L0_xattn_ref(x, ctx_1024, ctx_1024, mask_Bx1xSxS2_ik1, L0_xattn_wq, L0_xattn_wk, L0_xattn_wv, L0_xattn_wo, L0_xattn_bq, L0_xattn_bk, L0_xattn_bv, L0_xattn_bo), axis=-1)
    x = _layernorm(x + _L0_ffn_ref(x, L0_ffn_Wg, L0_ffn_W1, L0_ffn_b1, L0_ffn_W2, L0_ffn_b2), axis=-1)
    x = _layernorm(x + _L1_attn_ref(x, L1_attn_w_aq, L1_attn_w_ak, L1_attn_w_av, L1_attn_w_ao), axis=-1)
    x = _layernorm(x + _L1_xattn_ref(x, ctx_1024, ctx_1024, L1_xattn_W_Q, L1_xattn_b_Q, L1_xattn_W_K, L1_xattn_b_K, L1_xattn_W_V, L1_xattn_b_V, L1_xattn_W_O, L1_xattn_b_O), axis=-1)
    x = _layernorm(x + _L1_ffn_ref(x, L1_ffn_w_gate, L1_ffn_w_up, L1_ffn_w_down), axis=-1)
    x = _layernorm(x + _L2_attn_ref(x, L2_attn_W_in, L2_attn_b_in, L2_attn_W_dt1, L2_attn_b_dt1, L2_attn_W_dt2, L2_attn_b_dt2, L2_attn_A, L2_attn_D), axis=-1)
    x = _layernorm(x + _L2_xattn_ref(x, ctx_1024, ctx_1024, pos_BxS2, L2_xattn_w_q, L2_xattn_b_q, L2_xattn_w_k, L2_xattn_b_k, L2_xattn_w_v, L2_xattn_b_v, L2_xattn_w_o, L2_xattn_b_o), axis=-1)
    x = _layernorm(x + _L2_ffn_ref(x, L2_ffn_q_w, L2_ffn_q_b, L2_ffn_k_w, L2_ffn_k_b, L2_ffn_v_w, L2_ffn_v_b, L2_ffn_o_w, L2_ffn_o_b, L2_ffn_router_w, L2_ffn_router_b, L2_ffn_w1, L2_ffn_b1, L2_ffn_w2, L2_ffn_b2), axis=-1)
    x = _layernorm(x + _L3_attn_ref(x, L3_attn_q_w, L3_attn_q_b, L3_attn_k_w, L3_attn_k_b, L3_attn_v_w, L3_attn_v_b, L3_attn_out_w, L3_attn_out_b, L3_attn_rel_emb, L3_attn_grep_w, L3_attn_grep_b, L3_attn_grep_a), axis=-1)
    x = _layernorm(x + _L3_xattn_ref(x, ctx_1024, ctx_1024, mask_Bx1x1xS2_ff1, L3_xattn_Wq, L3_xattn_bq, L3_xattn_Wk, L3_xattn_bk, L3_xattn_Wv, L3_xattn_bv, L3_xattn_Wo, L3_xattn_bo), axis=-1)
    x = _layernorm(x + _L3_ffn_ref(x, L3_ffn_w_gate, L3_ffn_w_up, L3_ffn_w_down), axis=-1)
    return x

_drawn_inputs = setup_inputs


def setup_inputs(seed=0):
    import zlib

    import numpy as np

    out = dict(_drawn_inputs(seed))
    spreads = {'L0_xattn_bq': (0.0, 0.1),
     'L0_xattn_bk': (0.0, 2.0),
     'L0_xattn_bv': (0.0, 0.1),
     'L0_xattn_bo': (0.0, 0.1),
     'L0_ffn_b1': (0.0, 0.564),
     'L0_ffn_b2': (0.0, 0.1),
     'L1_attn_w_aq': (0.0, 0.8),
     'L2_attn_b_in': (0.0, 0.3),
     'L2_attn_b_dt1': (0.0, 0.8),
     'L2_attn_D': (1.0, 0.2),
     'L2_xattn_b_q': (0.0, 0.478),
     'L2_xattn_b_k': (0.0, 0.673),
     'L2_xattn_b_v': (0.0, 0.1),
     'L2_xattn_b_o': (0.0, 0.1),
     'L2_ffn_q_b': (0.0, 0.8),
     'L2_ffn_k_b': (0.0, 2.0),
     'L2_ffn_v_b': (0.0, 0.8),
     'L2_ffn_o_b': (0.0, 0.8),
     'L2_ffn_router_b': (0.0, 0.755),
     'L2_ffn_b1': (0.0, 0.8),
     'L2_ffn_b2': (0.0, 0.769),
     'L3_attn_q_b': (0.0, 0.8),
     'L3_attn_k_b': (0.0, 2.0),
     'L3_attn_v_b': (0.0, 0.317),
     'L3_attn_out_b': (0.0, 0.1),
     'L3_attn_grep_b': (0.0, 2.0),
     'L3_attn_grep_a': (1.0, 0.6)}
    factors = {'L1_attn_w_ak': 8.0,
     'L1_xattn_b_Q': 8.0,
     'L1_xattn_b_K': 64.0,
     'L1_xattn_b_V': 4.469,
     'L1_xattn_b_O': 4.441,
     'L2_ffn_q_w': 8.0,
     'L2_ffn_k_w': 8.0,
     'L2_ffn_v_w': 8.0,
     'L2_ffn_o_w': 8.0,
     'L2_ffn_router_w': 7.725,
     'L2_ffn_w1': 8.0,
     'L2_ffn_w2': 8.0,
     'L3_attn_q_w': 8.0,
     'L3_attn_k_w': 8.0,
     'L3_attn_v_w': 3.183,
     'L3_attn_rel_emb': 31.565,
     'L3_attn_grep_w': 64.0,
     'L3_xattn_bq': 3.203,
     'L3_xattn_bk': 64.0}
    for name, (base, spread) in spreads.items():
        noise = np.random.default_rng([zlib.crc32(name.encode()), seed]).standard_normal(out[name].shape)
        drawn = base * np.exp(spread * noise) if base else spread * noise
        out[name] = jnp.asarray(drawn.astype(out[name].dtype))
    for name, factor in factors.items():
        out[name] = (out[name] * factor).astype(out[name].dtype)
    return out
```

```python
from contextlib import ExitStack

import concourse.bass as bass
from concourse import mybir

F32 = mybir.dt.float32
BF16 = mybir.dt.bfloat16
F32R = mybir.dt.float32r
I32 = mybir.dt.int32
U32 = mybir.dt.uint32
ALU = mybir.AluOpType
ACT = mybir.ActivationFunctionType
AX = mybir.AxisListType

P = 128
B = 8
S = 256
D = 128
NT = B * S // P
BIG = 1.0e30
E = 8
CAPACITY = 256
CONSTS = 13
TERM = 8
SHIFT_ROW = 24
MASK_ROW = 26
MAGIC = 12582912.0


class Attn:

    def __init__(self, name, heads, dim, small, scale, bias=True, rope=None, causal=False, clip=False,
                 keymask=False, vcols=128, self_attn=False, tail=True):
        self.name, self.heads, self.dim, self.small, self.scale = name, heads, dim, small, scale
        self.bias, self.rope, self.causal, self.clip, self.keymask = bias, rope, causal, clip, keymask
        self.vcols, self.self_attn, self.tail = vcols, self_attn, tail
        self.turned_scores = small and not clip
        self.tiles = 4 if small else heads
        self.group = min(4, self.tiles)

    def items(self):
        out = []
        for t in range(0, self.tiles, self.group):
            for w in "qk":
                out.append((w, t))
                if self.rope:
                    out.append((w + "r", t))
        return out

    def rows(self, h):
        return (32 * (h % 4), 32) if self.small else (0, P)

    def tile(self, h):
        return h // 4 if self.small else h


R8 = 1.0 / 8 ** 0.5
ATTNS = {
    "L0a": Attn("L0a", 1, 128, False, 1.0 / 128 ** 0.5, bias=False, self_attn=True),
    "L0x": Attn("L0x", 16, 8, True, R8, clip=True),
    "L1a": Attn("L1a", 8, 128, False, 1.0, bias=False, rope="half", causal=True, self_attn=True, vcols=1024),
    "L1x": Attn("L1x", 16, 8, True, R8),
    "L2x": Attn("L2x", 16, 8, True, R8, rope="pair", causal=True),
    "L2f": Attn("L2f", 16, 4, True, 0.5, self_attn=True, vcols=64, tail=False),
    "L3x": Attn("L3x", 16, 8, True, R8, keymask=True),
}


def weight_columns():
    cols, at = {}, [0]

    def add(group, name, n):
        cols[name] = (at[0], n, group)
        at[0] += n

    def attn(a):
        n = a.name
        for w in "qk":
            add(n, f"{n}_w{w}", a.tiles * 128)
            if a.bias:
                add(n, f"{n}_b{w}", a.tiles)
            if a.rope:
                add(n, f"{n}_w{w}r", a.tiles * 128)
                if a.bias:
                    add(n, f"{n}_b{w}r", a.tiles)
        add(n, f"{n}_wv", a.vcols)
        if a.bias:
            add(n, f"{n}_bv", a.vcols)
            add(n, f"{n}_bo", 128)
        add(n, f"{n}_wo", a.heads * 128 if n == "L1a" else 128)

    add("const", "ident", 128)
    add("const", "w8", E)
    add("const", "lo_q", 1)
    add("const", "sign_q", 1)
    add("const", "lo_k", 1)
    add("const", "sign_k", 1)
    add("const", "row_mask", 1)
    add("const", "row_one", 1)
    attn(ATTNS["L0a"])
    attn(ATTNS["L0x"])
    add("L0f", "L0f_wg", E)
    add("L0f", "L0f_w1", E * 512)
    add("L0f", "L0f_b1", E * 4)
    add("L0f", "L0f_w2", E * 4 * 128)
    add("L0f", "L0f_b2", 128)
    attn(ATTNS["L1a"])
    add("L1a", "L1a_cos", 256)
    add("L1a", "L1a_sin", 256)
    attn(ATTNS["L1x"])
    attn(ATTNS["L2x"])
    add("L2x", "L2x_freq", 1)
    add("L2x", "L2x_sign", 1)
    add("L2a", "L2a_win", 32)
    add("L2a", "L2a_bin", 1)
    add("L2a", "L2a_wdt1", 64)
    add("L2a", "L2a_bdt1", 1)
    add("L2a", "L2a_wdt2", 128)
    add("L2a", "L2a_bdt2", 1)
    add("L2a", "L2a_A", 16)
    add("L2a", "L2a_D", 1)
    attn(ATTNS["L2f"])
    add("L2f", "L2f_ob", 1)
    add("L2f", "L2f_wr", E)
    add("L2f", "L2f_br", E)
    add("L2f", "L2f_w1", E * 256)
    add("L2f", "L2f_b1", E * 2)
    add("L2f", "L2f_w2", E * 2 * 128)
    add("L2f", "L2f_b2", 128)
    add("L3a", "L3a_w", 512)
    add("L3a", "L3a_b", 512)
    add("L3a", "L3a_wo", 128)
    add("L3a", "L3a_bo", 128)
    add("L3a", "L3a_ga", 16)
    add("L3a", "L3a_rel", 15 * 16)
    attn(ATTNS["L3x"])
    add("L3f", "L3f_wg", 512)
    add("L3f", "L3f_wu", 512)
    add("L3f", "L3f_wd", 512)
    return cols, at[0]


COLS, NCOL = weight_columns()
ORDER = ["L0a", "L0x", "L0f", "L1a", "L1x", "L1f", "L2a", "L2x", "L2f", "L3a", "L3x", "L3f"]


def weight_places():
    span = {}
    for at, n, g in COLS.values():
        a, b = span.get(g, (at, at))
        span[g] = (min(a, at), max(b, at + n))
    size = {g: b - a for g, (a, b) in span.items()}
    width = [max(size.get(s, 0) for s in ORDER[k::2]) for k in range(2)]
    place = {"const": 0}
    for k, s in enumerate(ORDER):
        if s in size:
            place[s] = size["const"] + (k % 2) * width[0]
    return span, place, size["const"] + sum(width)


SPAN, PLACE, WIDTH = weight_places()


class Chain:

    def __init__(self, eng, sem, per, first=0):
        self.eng, self.sem, self.per, self.first, self.n = eng, sem, per, first, 0

    def turn(self, i):
        self.base, self.n = self.first + i * self.per, 0

    def end(self):
        assert self.n == self.per, (self.sem, self.n)

    def did(self, ins):
        ins.then_inc(self.sem, 1)
        self.n += 1

    def wait(self):
        self.eng.wait_ge(self.sem, self.base + self.n)

    def step(self, ins):
        self.did(ins)
        self.wait()



STAGES = ORDER

PER = {"L0a": 7, "L0x": 10, "L1a": 18, "L1x": 13, "L2x": 33, "L3x": 16, "L0r": 43, "L0f": 6, "L1f": 6, "L2a": 36, "L2f": 37,
       "L3a": 7, "L3m": 111, "L3f": 40, "L3q": 10}


def counts(n):
    each = {"staged": 1}
    if n not in ("L3a", "L3f"):
        each.update(xT_psum=1, xT=1)
    if n[-1] != "r":
        each.update(var=1, rstd=1, dve_step=PER[n])
        if n not in ("L0f", "L2f"):
            each.update(y=1)
    if n == "L3a":
        each.update(oT_psum=1, oT=1)
    if n in ATTNS:
        a = ATTNS[n]
        H, NI, NO = a.heads, len(a.items()), max(1, a.vcols // P)
        each.update(V_psum=1, V=1, item_psum=NI, item_a=(NI + 1) // 2, item_b=NI // 2, scores=H, max=H, probs=H,
                    turned=H, pt_a=(H + 1) // 2, pt_v=H // 2, values=H, on=H if a.vcols > 512 else 1,
                    oT_psum=NO, oT=NO)
        if a.clip:
            each.update(clipped=H)
        if a.small:
            each.update(rounded=2, stack=2)
        if a.keymask:
            each.update(masked=1)
        if a.turned_scores:
            for role in ("turned", "pt_a", "pt_v"):
                del each[role]
            each.update(shift=a.tiles, shift_psum=a.tiles, shifted=a.tiles, probs=H // 2, values=H // 2,
                        turned_scores=H // 2, outputs=a.tiles, outputs_psum=1)
    return {role: B * c for role, c in each.items()}


def before(n, role):
    total = 0
    for s in STAGES:
        for part in (s + "r", s) if s in ("L0f", "L3a") else (s,):
            if part == n:
                return total
            total += counts(part).get(role, 0)
    raise KeyError(n)



def decoder(nc, wpack, x_in, ctx_in, mask_in, kmask_in, pos_in, hdm_in, wint_in, out):
    ctx = ExitStack()
    with ctx:
        def sb(name, shape, dt=F32):
            return ctx.enter_context(nc.sbuf_tensor(name, shape, dt))

        sems = {}

        def sem(name):
            if name not in sems:
                sems[name] = ctx.enter_context(nc.semaphore(name))
            return sems[name]

        W = sb("W", [P, WIDTH])
        x_tok = sb("x_tok", [P, NT, D])
        ctxT = sb("ctxT", [P, B * S])
        xs = sb("xs", [P, 2, D])
        cs = sb("cs", [P, S])
        xT = sb("xT", [P, S])
        QT = sb("QT", [P, 8, S])
        KT = sb("KT", [P, 8, S])
        QS = sb("QS", [P, 4, S], F32R)
        KS = sb("KS", [P, 4, S], F32R)
        V = sb("V", [P, 2, 1024])
        negmax = sb("negmax", [P, 16, 2])
        sums = sb("sums", [P, 16, 2])
        rsum = sb("rsum", [P, 16, 2])
        On = sb("On", [P, 2, 1024])
        OT = sb("OT", [P, 8, S])
        res = sb("res", [P, 2, D])
        stats = sb("stats", [P, 2, 6])
        mv = sb("mv", [P, 2, 2])
        veps = sb("veps", [P, 2])
        rstd = sb("rstd", [P, 2])
        mhalf = sb("mhalf", [P, 2])
        identb = sb("identb", [P, P], BF16)
        causal = sb("causal", [P, 2, S], BF16)
        onesb = sb("onesb", [P, P], BF16)
        onesf = sb("onesf", [P, P])
        tri = sb("tri", [P, P], BF16)
        SEL = sb("SEL", [96, 32, P], BF16)
        kmask = sb("kmask", [P, S])
        keep = sb("keep", [P, S])
        kbias = sb("kbias", [P, S])
        causalT = sb("causalT", [P, P], BF16)
        big = sb("big", [P, 8192])
        RT = big[:, 0:1024].rearrange("p (a b) -> p a b", a=4)
        PR = big[:, 1024:2560].rearrange("p (r a b) -> p r a b", r=3, a=2)
        SC = big[:, 2560:3584].rearrange("p (r a b) -> p r a b", r=2, a=2)
        PT = big[:, 3584:4608].rearrange("p (r a b) -> p r a b", r=2, a=2)
        PX = big[:, 1024:3072].rearrange("p (r a b) -> p r a b", r=2, a=2)
        SH = big[:, 4608:5632].rearrange("p (t j r c) -> p t j r c", t=4, j=2, r=4)
        wint = sb("wint", [P, 1152], I32)
        wdeq = big[:, 4096:5248]
        tern = sb("tern", [P, 3, 512], BF16)
        comb = sb("comb", [P, NT, E])
        combs = sb("combs", [P, 2, E])
        combT = sb("combT", [E, S])
        rt = sb("rt", [P, 6, NT, E])
        rts = sb("rts", [P, 6, NT])
        ohb = sb("ohb", [P, 2, NT, E], BF16)
        hdm_i = sb("hdm_i", [P, 1], I32)
        hdm = sb("hdm", [P, 1])
        mask_i = sb("mask_i", [P, 2, S], I32)
        cap = sb("cap", [P, 2, S])
        pos_i = sb("pos_i", [P, S], I32)
        rot = sb("rot", [P, 6, S])
        PS = ctx.enter_context(nc.psum_tensor("PS", [P, 8, 512], F32))
        SCB, PTB, OB, PB = (0, 1, 2), (3, 4), 5, (6, 7)
        MAXB, SHB, EXPB = (0, 1), 2, (3, 6)
        GA, GB = 0, 3

        x_done = sem("x_done")
        w_in = {g: sem(f"w_in_{g}") for g in SPAN}
        x_loaded, ctx_loaded, small_loaded = sem("x_loaded"), sem("ctx_loaded"), sem("small_loaded")
        consts, dve_consts = sem("consts"), sem("dve_consts")
        out_sent = sem("out_sent")

        def w(name, a=0, b=None, rows=P):
            at, n, g = COLS[name]
            at += PLACE[g] - SPAN[g][0]
            b = n if b is None else b
            return W[0:rows, at + a:at + b]

        ident = w("ident")

        def tile2(i, b=None):
            return x_tok[:, bass.ds(2 * i, 2), :]

        base = {s: 8 * k + 1 for k, s in enumerate(STAGES)}
        last_x = 8 * len(STAGES) + 1

        block = ctx.enter_context(nc.Block())

        @block.sync
        def _(sp):
            sp.dma_start(x_tok[:, :, :], x_in).then_inc(x_loaded, 16)
            def load(g):
                if g in SPAN:
                    a, b = SPAN[g]
                    sp.dma_start(W[:, PLACE[g]:PLACE[g] + b - a], wpack[:, a:b]).then_inc(w_in[g], 16)

            load("const")
            load(STAGES[0])
            sp.dma_start(hdm_i[:, :], hdm_in).then_inc(small_loaded, 16)
            sp.dma_start(wint[:, :], wint_in).then_inc(small_loaded, 16)
            sp.dma_start(ctxT[:, :], ctx_in).then_inc(ctx_loaded, 16)
            for k, s in enumerate(STAGES):
                if k + 1 < len(STAGES):
                    sp.wait_ge(x_done, base[s])
                    load(STAGES[k + 1])
                if s == "L0x":
                    with sp.Fori(0, B) as i:
                        sp.wait_ge(x_done, i + base[s])
                        sp.dma_start(mask_i[:, :, :], mask_in[:, bass.ds(2 * i, 2), :]).then_inc(sem("mask_in"), 16)
                if s == "L2x":
                    with sp.Fori(0, B) as i:
                        sp.wait_ge(x_done, i + base[s])
                        sp.dma_start(pos_i[:, :], pos_in[:, bass.ds(i * S, S)].broadcast_to([P, S]))\
                          .then_inc(sem("pos_in"), 16)
                if s == "L3x":
                    with sp.Fori(0, B) as i:
                        sp.wait_ge(x_done, i + base[s])
                        sp.dma_start(kmask[:, :], kmask_in[:, bass.ds(i * S, S)].broadcast_to([P, S]))\
                          .then_inc(sem("kmask_in"), 16)
            sp.wait_ge(x_done, last_x)
            sp.dma_start(out, x_tok[:, :, :]).then_inc(out_sent, 16)
            sp.wait_ge(out_sent, 16)

        @block.gpsimd
        def _(pool):
            nc.gpsimd.memset(mhalf[:, :], -0.5).then_inc(consts, 1)
            nc.gpsimd.memset(onesb[:, :], 1.0).then_inc(consts, 1)
            nc.gpsimd.memset(causal[:, :, :], 0.0).then_inc(consts, 1)
            nc.gpsimd.memset(onesf[:, :], 1.0).then_inc(consts, 1)
            nc.gpsimd.memset(tri[:, :], 1.0).then_inc(consts, 1)
            nc.gpsimd.memset(SEL[:, :, :], 0.0).then_inc(consts, 1)
            pool.wait_ge(consts, 6)
            nc.gpsimd.affine_select(out=tri[:, :], in_=tri[:, :], compare_op=ALU.is_ge, fill=0.0,
                                    base=0, pattern=[[1, P]], channel_multiplier=-1).then_inc(consts, 1)
            for q in range(3):
                pool.wait_ge(consts, 7 + q)
                rows = SEL[32 * q:32 * q + 32, :, :]
                nc.gpsimd.affine_select(out=rows, in_=rows, compare_op=ALU.not_equal, fill=1.0,
                                        base=0, pattern=[[-1, 32], [0, P]], channel_multiplier=1).then_inc(consts, 1)
            pool.wait_ge(consts, 10)
            nc.gpsimd.affine_select(out=causal[:, :, :], in_=causal[:, :, :], compare_op=ALU.is_ge, fill=-BIG,
                                    base=0, pattern=[[128, 2], [-1, S]], channel_multiplier=1).then_inc(consts, 1)
            pool.wait_ge(consts, 11)
            nc.gpsimd.memset(causalT[:, :], 0.0).then_inc(consts, 1)
            pool.wait_ge(consts, 12)
            nc.gpsimd.affine_select(out=causalT[:, :], in_=causalT[:, :], compare_op=ALU.is_ge, fill=-BIG,
                                    base=0, pattern=[[1, P]], channel_multiplier=-1).then_inc(consts, 1)
            pool.wait_ge(consts, CONSTS)

            def inverse_roots(s):
                with pool.Fori(0, B) as i:
                    if s == "L3x":
                        pool.wait_ge(sem("item_b"), before(s, "item_b") + i + 1)
                        nc.gpsimd.tensor_tensor(KT[:, 0:4, :], KT[:, 0:4, :],
                                                kbias[:, :].unsqueeze(1).broadcast_to([P, 4, S]), ALU.add)\
                          .then_inc(sem("masked"), 1)
                    pool.wait_ge(sem("var"), before(s, "var") + i + 1)
                    nc.gpsimd.tensor_tensor(rstd[:, :], veps[:, :], mhalf[:, :], ALU.pow)\
                      .then_inc(sem("rstd"), 1)

            for s in STAGES:
                inverse_roots(s)

        @block.tensor
        def _(pe):
            pe.wait_ge(w_in["const"], 16)
            pe.wait_ge(consts, CONSTS)
            pe.wait_ge(dve_consts, 1)

            def attention(a, i):
                n, H = a.name, a.heads
                items = a.items()
                NI = len(items)
                LAG = 2
                pe.wait_ge(w_in[n], 16)
                pe.wait_ge(sem("staged"), before(n, "staged") + i + 1)
                for j in range(2):
                    mm = nc.tensor.transpose(PS[:, PB[0], j * P:(j + 1) * P], xs[:, j, :], ident)
                mm.then_inc(sem("xT_psum"), 1)
                pe.wait_ge(sem("xT"), before(n, "xT") + i + 1)
                src = xT if a.self_attn else cs
                for j in range(2):
                    for c in range(0, a.vcols, 512):
                        c1 = min(c + 512, a.vcols)
                        bank, at = (PB[1], j * a.vcols) if a.vcols <= 256 else ((5, 6, 7, 2)[2 * j + c // 512], 0)
                        mm = nc.tensor.matmul(PS[:, bank, at:at + c1 - c], src[:, j * P:(j + 1) * P],
                                              w(f"{n}_wv", c, c1), start=True, stop=True)
                mm.then_inc(sem("V_psum"), 1)
                for k, (what, t0) in enumerate(items):
                    if k >= 2:
                        role = "item_a" if k % 2 == 0 else "item_b"
                        pe.wait_ge(sem(role), before(n, role) + i * ((NI + 1 - k % 2) // 2) + k // 2)
                    rhs = src if what[0] == "k" else xT
                    for t in range(a.group):
                        g = (GA, GB)[k % 2]
                        mm = nc.tensor.matmul(PS[:, g + t // 2, (t % 2) * S:(t % 2 + 1) * S],
                                              w(f"{n}_w{what}", (t0 + t) * P, (t0 + t + 1) * P), rhs[:, :],
                                              start=True, stop=True)
                    mm.then_inc(sem("item_psum"), 1)

                def pt(h):
                    return "pt_v" if h % 2 else "pt_a"

                def half(h):
                    return H // 2 if h % 2 else (H + 1) // 2

                def scores(h):
                    if h >= len(SCB):
                        role = "clipped" if a.clip else "probs"
                        pe.wait_ge(sem(role), before(n, role) + i * H + h - len(SCB) + 1)
                    r0, rn = a.rows(h)
                    bank = SCB[h % len(SCB)]
                    q, k = (QS, KS) if a.small else (QT, KT)
                    for j in range(2):
                        o = PS[:, bank, j * S:(j + 1) * S]
                        mm = nc.tensor.matmul(o, q[r0:r0 + rn, a.tile(h), j * P:(j + 1) * P],
                                              k[r0:r0 + rn, a.tile(h), :], start=True, stop=not a.causal)
                        if a.causal:
                            mm = nc.tensor.matmul(o, identb[:, :], causal[:, j, :], start=False, stop=True)
                    mm.then_inc(sem("scores"), 1)

                def turn(h):
                    pe.wait_ge(sem("probs"), before(n, "probs") + i * H + h + 1)
                    if h >= 2:
                        pe.wait_ge(sem(pt(h)), before(n, pt(h)) + i * half(h) + h // 2)
                    for kb in range(2):
                        for j in range(2):
                            mm = nc.tensor.transpose(PS[:, PTB[h % 2], kb * S + j * P:kb * S + (j + 1) * P],
                                                     PR[:, h % 3, j, kb * P:(kb + 1) * P], ident)
                    mm.then_inc(sem("turned"), 1)

                def values(h):
                    pe.wait_ge(sem(pt(h)), before(n, pt(h)) + i * half(h) + h // 2 + 1)
                    dv = a.vcols // H
                    for j in range(2):
                        if a.vcols > 512:
                            o = PS[:, (5, 6, 7, 5, 6, 7, 5, 6)[h], j * dv:(j + 1) * dv]
                            if h >= 3 and j == 0:
                                pe.wait_ge(sem("on"), before(n, "on") + i * H + h - 2)
                        else:
                            o = PS[:, OB, j * a.vcols + h * dv:j * a.vcols + (h + 1) * dv]
                        for kb in range(2):
                            mm = nc.tensor.matmul(o, PT[:, h % 2, kb, j * P:(j + 1) * P],
                                                  V[:, kb, h * dv:(h + 1) * dv], start=kb == 0, stop=kb == 1)
                    mm.then_inc(sem("values"), 1)

                if a.small:
                    pe.wait_ge(sem("stack"), before(n, "stack") + 2 * i + 2)
                else:
                    pe.wait_ge(sem("item_a"), before(n, "item_a") + (i + 1) * ((NI + 1) // 2))
                    pe.wait_ge(sem("item_b"), before(n, "item_b") + (i + 1) * (NI // 2))
                pe.wait_ge(sem("V"), before(n, "V") + i + 1)
                if a.turned_scores:
                    small_heads(a, i)
                else:
                    for h in range(H + LAG + 1):
                        if h < H:
                            scores(h)
                        if LAG <= h < H + LAG:
                            turn(h - LAG)
                        if h > LAG:
                            values(h - LAG - 1)
                NO = max(1, a.vcols // P)
                rows = min(P, a.vcols)
                if a.vcols > 512:
                    for k in range(NO):
                        pe.wait_ge(sem("on"), before(n, "on") + i * H + k + 1)
                        if k >= 2:
                            pe.wait_ge(sem("oT"), before(n, "oT") + i * NO + k - 1)
                        for j in range(2):
                            mm = nc.tensor.transpose(PS[:, PTB[k % 2], j * P:(j + 1) * P],
                                                     On[:, j, k * P:(k + 1) * P], ident)
                        mm.then_inc(sem("oT_psum"), 1)
                else:
                    pe.wait_ge(sem("on"), before(n, "on") + i + 1)
                    if rows < P:
                        pe.sem_inc(sem("on_passed"), 1)
                    for j in range(2):
                        mm = nc.tensor.transpose(PS[0:rows, PTB[0], j * P:(j + 1) * P], On[:, j, 0:rows], ident)
                    mm.then_inc(sem("oT_psum"), 1)
                pe.wait_ge(sem("oT"), before(n, "oT") + (i + 1) * NO)
                if a.tail:
                    for j in range(2):
                        for k in range(NO):
                            mm = nc.tensor.matmul(PS[:, PB[0], j * P:(j + 1) * P], OT[0:rows, k, j * P:(j + 1) * P],
                                                  w(f"{n}_wo", k * P, (k + 1) * P, rows=rows),
                                                  start=k == 0, stop=k == NO - 1)
                    mm.then_inc(sem("y"), 1)

            def small_heads(a, i):
                n, H, T = a.name, a.heads, a.tiles
                def scores(h):
                    if h >= 2:
                        pe.wait_ge(sem("max"), before(n, "max") + i * H + h - 1)
                    r, t = slice(32 * (h % 4), 32 * (h % 4) + 32), h // 4
                    for j in range(2):
                        o = PS[:, MAXB[h % 2], j * S:(j + 1) * S]
                        mm = nc.tensor.matmul(o, QS[r, t, j * P:(j + 1) * P], KS[r, t, :],
                                              start=True, stop=not a.causal)
                        if a.causal:
                            mm = nc.tensor.matmul(o, identb[:, :], causal[:, j, :], start=False, stop=True)
                    mm.then_inc(sem("scores"), 1)

                def shift(t):
                    pe.wait_ge(sem("shift"), before(n, "shift") + i * T + t + 1)
                    if t >= 1:
                        pe.wait_ge(sem("shifted"), before(n, "shifted") + i * T + t)
                    for j in range(2):
                        mm = nc.tensor.transpose(PS[:, SHB, j * P:(j + 1) * P],
                                                 SH[:, t, j, :, :].rearrange("p r c -> p (r c)"), ident)
                    mm.then_inc(sem("shift_psum"), 1)

                def turned_scores(p):
                    t = p // 2
                    if p % 2 == 0:
                        pe.wait_ge(sem("shifted"), before(n, "shifted") + i * T + t + 1)
                    if p >= 2:
                        pe.wait_ge(sem("probs"), before(n, "probs") + i * (H // 2) + p - 1)
                    for half in range(2):
                        h = 2 * p + half
                        r, bank = slice(32 * (h % 4), 32 * (h % 4) + 32), EXPB[p % 2] + half
                        if a.causal:
                            nc.tensor.matmul(PS[:, bank, P:S], KS[r, t, 0:P], QS[r, t, P:S], start=True, stop=True)
                            for kb in range(2):
                                o = PS[:, bank, 2 * kb * P:(2 * kb + 1) * P]
                                nc.tensor.matmul(o, KS[r, t, kb * P:(kb + 1) * P], QS[r, t, kb * P:(kb + 1) * P],
                                                 start=True, stop=False)
                                mm = nc.tensor.matmul(o, identb[:, :], causalT[:, :], start=False, stop=True)
                        else:
                            for kb in range(2):
                                mm = nc.tensor.matmul(PS[:, bank, kb * S:(kb + 1) * S], KS[r, t, kb * P:(kb + 1) * P],
                                                      QS[r, t, :], start=True, stop=True)
                    mm.then_inc(sem("turned_scores"), 1)

                def values(p):
                    pe.wait_ge(sem("probs"), before(n, "probs") + i * (H // 2) + p + 1)
                    t = p // 2
                    if p % 2 == 0 and t >= 1:
                        pe.wait_ge(sem("outputs"), before(n, "outputs") + i * T + t)
                    for half in range(2):
                        h = 2 * p + half
                        r, at = slice(32 * (h % 4), 32 * (h % 4) + 32), (t % 2) * S
                        for kb in range(2):
                            v = V[:, kb, 32 * h:32 * h + 32]
                            px = PX[:, p % 2, half, :]
                            if not a.causal:
                                mm = nc.tensor.matmul(PS[r, OB, at:at + S], v, px[:, kb * S:(kb + 1) * S],
                                                      start=kb == 0, stop=kb == 1)
                            elif kb == 0:
                                nc.tensor.matmul(PS[r, OB, at:at + P], v, px[:, 0:P], start=True, stop=True)
                                nc.tensor.matmul(PS[r, OB, at + P:at + S], v, px[:, P:S], start=True, stop=False)
                            else:
                                mm = nc.tensor.matmul(PS[r, OB, at + P:at + S], v, px[:, S:S + P],
                                                      start=False, stop=True)
                    mm.then_inc(sem("values"), 1)

                for t in range(T + 1):
                    for r in range(4):
                        if t < T:
                            scores(4 * t + r)
                        if t >= 1:
                            if r == 0:
                                shift(t - 1)
                            if r in (1, 3):
                                p = 2 * (t - 1) + r // 2
                                turned_scores(p)
                                if p >= 1:
                                    values(p - 1)
                values(H // 2 - 1)
                for t in range(T):
                    pe.wait_ge(sem("outputs"), before(n, "outputs") + i * T + t + 1)
                    for j in range(2):
                        mm = nc.tensor.transpose(PS[:, EXPB[0] + j, t * P:(t + 1) * P],
                                                 OT[:, 4 + t, j * P:(j + 1) * P], ident)
                mm.then_inc(sem("outputs_psum"), 1)

            def turn_x(n, i):
                pe.wait_ge(sem("staged"), before(n, "staged") + i + 1)
                for j in range(2):
                    mm = nc.tensor.transpose(PS[:, PB[0], j * P:(j + 1) * P], xs[:, j, :], ident)
                mm.then_inc(sem("xT_psum"), 1)
                pe.wait_ge(sem("xT"), before(n, "xT") + i + 1)

            def experts(n, i, src, chunks):
                HB, YB = (GA, GB), (5, 7)
                for e in range(E + 1):
                    if e < E:
                        if e >= 2:
                            pe.wait_ge(sem(f"{n}_h"), i * E + e - 1)
                        for c in range(chunks):
                            mm = nc.tensor.matmul(PS[:, HB[e % 2] + c // 2, (c % 2) * S:(c % 2 + 1) * S],
                                                  w(f"{n}_w1", (e * chunks + c) * P, (e * chunks + c + 1) * P),
                                                  src[:, :], start=True, stop=True)
                        mm.then_inc(sem(f"{n}_h_psum"), 1)
                    if e >= 1:
                        g = e - 1
                        pe.wait_ge(sem(f"{n}_h"), i * E + g + 1)
                        if g >= 2:
                            pe.wait_ge(sem(f"{n}_acc"), i * E + g - 1)
                        for j in range(2):
                            for c in range(chunks):
                                mm = nc.tensor.matmul(PS[:, YB[g % 2], j * P:(j + 1) * P],
                                                      QT[:, 4 * (g % 2) + c, j * P:(j + 1) * P],
                                                      w(f"{n}_w2", (g * chunks + c) * P, (g * chunks + c + 1) * P),
                                                      start=c == 0, stop=c == chunks - 1)
                        mm.then_inc(sem(f"{n}_ye"), 1)
                pe.wait_ge(sem(f"{n}_combs"), i + 1)
                for j in range(2):
                    mm = nc.tensor.transpose(PS[0:E, 2, j * P:(j + 1) * P], combs[:, j, :], ident)
                mm.then_inc(sem(f"{n}_combT_psum"), 1)
                pe.wait_ge(sem(f"{n}_combT"), i + 1)
                for j in range(2):
                    mm = nc.tensor.matmul(PS[:, PB[0], j * P:(j + 1) * P], combT[:, j * P:(j + 1) * P],
                                          w(f"{n}_b2", rows=E), start=True, stop=True)
                mm.then_inc(sem(f"{n}_yb"), 1)

            def L0f():
                n = "L0f"
                pe.wait_ge(w_in[n], 16)
                with pe.Fori(0, B) as i:
                    turn_x(n + "r", i)
                    for j in range(2):
                        mm = nc.tensor.matmul(PS[:, PB[1], j * E:(j + 1) * E], xT[:, j * P:(j + 1) * P],
                                              w(f"{n}_wg"), start=True, stop=True)
                    mm.then_inc(sem(f"{n}_lg_psum"), 1)
                pe.wait_ge(sem(f"{n}_onehots"), 1)
                for k in range(2):
                    nc.tensor.matmul(PS[:, 0, k * P:(k + 1) * P], tri[:, :],
                                     ohb[:, k, :, :].rearrange("p t e -> p (t e)"), start=True, stop=True)
                    mm = nc.tensor.matmul(PS[:, 1, k * P:(k + 1) * P], onesb[:, :],
                                          ohb[:, k, :, :].rearrange("p t e -> p (t e)"), start=True, stop=True)
                mm.then_inc(sem(f"{n}_counts"), 1)
                pe.wait_ge(sem(f"{n}_routed"), 1)
                with pe.Fori(0, B) as i:
                    turn_x(n, i)
                    experts(n, i, xT, 4)

            def L2f():
                n = "L2f"
                with pe.Fori(0, B) as i:
                    attention(ATTNS[n], i)
                    nc.tensor.matmul(PS[:, PB[1], 0:S], w(f"{n}_wo", rows=64), OT[0:64, 0, :],
                                     start=True, stop=True).then_inc(sem(f"{n}_mla_psum"), 1)
                    pe.wait_ge(sem(f"{n}_mla"), i + 1)
                    for j in range(2):
                        mm = nc.tensor.matmul(PS[:, PB[1], j * E:(j + 1) * E], OT[:, 1, j * P:(j + 1) * P],
                                              w(f"{n}_wr"), start=True, stop=True)
                    mm.then_inc(sem(f"{n}_lg_psum"), 1)
                    pe.wait_ge(sem(f"{n}_lg"), i + 1)
                    experts(n, i, OT[:, 1, :], 2)

            def L1f():
                n = "L1f"
                pe.wait_ge(sem("wdeq_ready"), 1)
                with pe.Fori(0, B) as i:
                    turn_x(n, i)
                    for k, bank in enumerate((GA, GB)):
                        for c in range(3):
                            at = k * 384 + c * P
                            mm = nc.tensor.matmul(PS[:, bank + c // 2, (c % 2) * S:(c % 2 + 1) * S],
                                                  wdeq[:, at:at + P], xT[:, :], start=True, stop=True)
                        mm.then_inc(sem(f"{n}_h_psum"), 1)
                    pe.wait_ge(sem(f"{n}_h"), i + 1)
                    for j in range(2):
                        for c in range(3):
                            mm = nc.tensor.matmul(PS[:, PB[0], j * P:(j + 1) * P], QT[:, 3 + c, j * P:(j + 1) * P],
                                                  wdeq[:, 768 + c * P:896 + c * P], start=c == 0, stop=c == 2)
                    mm.then_inc(sem("y"), 1)

            def L2a():
                n = "L2a"
                stk = OT[0:96, 2, 0:P].bitcast(BF16)
                pe.wait_ge(w_in[n], 16)
                with pe.Fori(0, B) as i:
                    turn_x(n, i)
                    nc.tensor.matmul(PS[0:32, 0, 0:S], w(f"{n}_win"), xT[:, :], start=True, stop=True)\
                      .then_inc(sem(f"{n}_bc_psum"), 1)
                    nc.tensor.matmul(PS[0:64, 1, 0:S], w(f"{n}_wdt1"), xT[:, :], start=True, stop=True)\
                      .then_inc(sem(f"{n}_dt_psum"), 1)
                    pe.wait_ge(sem(f"{n}_dt1"), i + 1)
                    nc.tensor.matmul(PS[:, 2, 0:S], w(f"{n}_wdt2", rows=64), OT[0:64, 0, :], start=True, stop=True)\
                      .then_inc(sem(f"{n}_dt_psum"), 1)
                    pe.wait_ge(sem(f"{n}_stack"), i + 1)
                    for half in range(2):
                        if half:
                            pe.wait_ge(sem(f"{n}_g"), i * 2 + 1)
                        else:
                            pe.wait_ge(sem(f"{n}_z"), i + 1)
                        for k in range(8):
                            mm = nc.tensor.matmul(PS[:, k // 2, (k % 2) * S:(k % 2 + 1) * S],
                                                  SEL[:, half * 8 + k, :], stk, start=True, stop=True)
                        mm.then_inc(sem(f"{n}_B"), 1)
                        if half:
                            pe.wait_ge(sem(f"{n}_hc"), i * 2 + 1)
                        for k in range(8):
                            mm = nc.tensor.matmul(PS[:, 4 + k // 2, (k % 2) * S:(k % 2 + 1) * S],
                                                  SEL[:, 16 + half * 8 + k, :], stk, start=True, stop=True)
                        mm.then_inc(sem(f"{n}_C"), 1)
                    pe.wait_ge(sem(f"{n}_ysum"), i + 1)
                    for j in range(2):
                        mm = nc.tensor.transpose(PS[:, PB[0], j * P:(j + 1) * P], OT[:, 5, j * P:(j + 1) * P], ident)
                    mm.then_inc(sem("y"), 1)

            def L3a():
                n = "L3a"
                pe.wait_ge(w_in[n], 16)
                with pe.Fori(0, B) as i:
                    turn_x(n + "r", i)
                    for j in range(2):
                        mm = nc.tensor.matmul(PS[:, j, :], xT[:, j * P:(j + 1) * P], w(f"{n}_w"), start=True, stop=True)
                    mm.then_inc(sem(f"{n}_qkvg_psum"), 1)
                    pe.wait_ge(sem(f"{n}_qkvg"), i + 1)
                with pe.Fori(0, B) as i:
                    pe.wait_ge(sem("staged"), before(n, "staged") + i + 1)
                    for j in range(2):
                        mm = nc.tensor.transpose(PS[:, PTB[0], j * P:(j + 1) * P], On[:, j, 0:P], ident)
                    mm.then_inc(sem("oT_psum"), 1)
                    pe.wait_ge(sem("oT"), before(n, "oT") + i + 1)
                    for j in range(2):
                        mm = nc.tensor.matmul(PS[:, PB[0], j * P:(j + 1) * P], OT[:, 0, j * P:(j + 1) * P],
                                              w(f"{n}_wo"), start=True, stop=True)
                    mm.then_inc(sem("y"), 1)

            def L3f():
                n = "L3f"
                pe.wait_ge(sem(f"{n}_wsum"), 1)
                nc.tensor.matmul(PS[:, 0, 0:3], onesf[:, :], mv[:, :, :].rearrange("p a b -> p (a b)")[:, 0:3],
                                 start=True, stop=True).then_inc(sem(f"{n}_wmean_psum"), 1)
                pe.wait_ge(sem(f"{n}_tern"), 1)
                nT = OT[:, 0, :].bitcast(BF16)
                mT = OT[:, 4:8, :].rearrange("p a b -> p (a b)").bitcast(BF16)
                nq = On[:, :, 0:64].bitcast(BF16)
                hq = On[:, :, 128:384].bitcast(BF16)
                idb = identb[:, :]
                with pe.Fori(0, B) as i:
                    pe.wait_ge(sem(f"{n}_nq"), i + 1)
                    for j in range(2):
                        mm = nc.tensor.transpose(PS[:, PB[0], :].bitcast(BF16)[:, j * P:(j + 1) * P], nq[:, j, :], idb)
                    mm.then_inc(sem(f"{n}_nT_psum"), 1)
                    pe.wait_ge(sem(f"{n}_nT"), i + 1)
                    for j in range(2):
                        for k in range(2):
                            mm = nc.tensor.matmul(PS[:, 2 * j + k, :], nT[:, j * P:(j + 1) * P], tern[:, k, :],
                                                  start=True, stop=True)
                    mm.then_inc(sem(f"{n}_h_psum"), 1)
                    pe.wait_ge(sem(f"{n}_hq"), i + 1)
                    for j in range(2):
                        for c in range(4):
                            mm = nc.tensor.transpose(PS[:, 4 + j, :].bitcast(BF16)[:, c * P:(c + 1) * P],
                                                     hq[:, j, c * P:(c + 1) * P], idb)
                    mm.then_inc(sem(f"{n}_mT_psum"), 1)
                    pe.wait_ge(sem(f"{n}_mT"), i + 1)
                    for j in range(2):
                        for c in range(4):
                            mm = nc.tensor.matmul(PS[:, PB[1], j * P:(j + 1) * P],
                                                  mT[:, (4 * j + c) * P:(4 * j + c + 1) * P],
                                                  tern[:, 2, c * P:(c + 1) * P], start=c == 0, stop=c == 3)
                    mm.then_inc(sem("y"), 1)

            own = {"L0f": L0f, "L1f": L1f, "L2a": L2a, "L2f": L2f, "L3a": L3a, "L3f": L3f}
            for s in STAGES:
                if s in own:
                    own[s]()
                else:
                    with pe.Fori(0, B) as i:
                        attention(ATTNS[s], i)

        @block.scalar
        def _(act):
            def attention(a, i):
                n, H = a.name, a.heads
                items = a.items()
                NI = len(items)
                act.wait_ge(w_in[n], 16)
                if not a.self_attn:
                    act.wait_ge(ctx_loaded, 16)
                if n == "L0a":
                    act.wait_ge(sem("hdm_ready"), 1)
                act.wait_ge(x_done, i + base[n])
                st = nc.scalar.copy(xs[:, :, :], tile2(i))
                if not a.self_attn:
                    st = nc.scalar.copy(cs[:, :], ctxT[:, bass.ds(i * S, S)])
                st.then_inc(sem("staged"), 1)
                act.wait_ge(sem("xT_psum"), before(n, "xT_psum") + i + 1)
                nc.scalar.copy(xT[:, :], PS[:, PB[0], 0:S]).then_inc(sem("xT"), 1)
                if n == "L2x":
                    act.wait_ge(sem("angles"), i + 1)
                    nc.scalar.activation(rot[:, 4, :], rot[:, 4, :], ACT.Sin).then_inc(sem("sines"), 1)
                    nc.scalar.activation(rot[:, 0, :], rot[:, 5, :], ACT.Sin).then_inc(sem("sines"), 1)
                for k, (what, t0) in enumerate(items):
                    if k % 2 and not a.rope and not a.keymask:
                        act.wait_ge(sem("item_psum"), before(n, "item_psum") + i * NI + k + 1)
                        for t in range(a.group):
                            src = PS[:, GB + t // 2, (t % 2) * S:(t % 2 + 1) * S]
                            if a.bias:
                                ins = nc.scalar.activation(KT[:, t0 + t, :], src, ACT.Identity,
                                                           bias=w(f"{n}_bk", t0 + t, t0 + t + 1))
                            else:
                                ins = nc.scalar.copy(KT[:, t0 + t, :], src)
                        ins.then_inc(sem("item_b"), 1)
                if a.small:
                    na, nb = (NI + 1) // 2, NI // 2
                    act.wait_ge(sem("item_b"), before(n, "item_b") + (i + 1) * nb)
                    if a.keymask:
                        act.wait_ge(sem("masked"), before(n, "masked") + i + 1)
                    nc.scalar.activation(KS[:, :, :], KT[:, 0:4, :], ACT.Copy, scale=w("sign_k"))\
                      .then_inc(sem("rounded"), 1)
                    act.wait_ge(sem("item_a"), before(n, "item_a") + (i + 1) * na)
                    nc.scalar.activation(QS[:, :, :], QT[:, 0:4, :], ACT.Copy, scale=w("sign_q"))\
                      .then_inc(sem("rounded"), 1)
                if a.turned_scores:
                    for p in range(H // 2):
                        act.wait_ge(sem("turned_scores"), before(n, "turned_scores") + i * (H // 2) + p + 1)
                        if p >= 2:
                            act.wait_ge(sem("values"), before(n, "values") + i * (H // 2) + p - 1)
                        cols = 3 * P if a.causal else 4 * P
                        nc.scalar.activation(PX[:, p % 2, :, 0:cols], PS[:, EXPB[p % 2]:EXPB[p % 2] + 2, 0:cols],
                                             ACT.Exp).then_inc(sem("probs"), 1)
                        for t in ([p // 2 - 1] if p % 2 == 0 and p >= 2 else [p // 2] if p == H // 2 - 1 else []):
                            act.wait_ge(sem("values"), before(n, "values") + i * (H // 2) + 2 * t + 2)
                            nc.scalar.copy(OT[:, 4 + t, :], PS[:, OB, (t % 2) * S:(t % 2 + 1) * S])\
                              .then_inc(sem("outputs"), 1)
                for h in range(0 if a.turned_scores else H + 3):
                    if h < H:
                        act.wait_ge(sem("max"), before(n, "max") + i * H + h + 1)
                        if h >= 3:
                            act.wait_ge(sem("turned"), before(n, "turned") + i * H + h - 2)
                        for j in range(2):
                            src = SC[:, h % 2, j, :] if a.clip else PS[:, SCB[h % 3], j * S:(j + 1) * S]
                            ins = nc.scalar.activation(PR[:, h % 3, j, :], src, ACT.Exp,
                                                       bias=negmax[:, h, j:j + 1], accum_out=sums[:, h, j:j + 1])
                        ins.then_inc(sem("probs"), 1)
                    g = h - 2
                    if g >= 0 and g < H and g % 2 == 0:
                        act.wait_ge(sem("turned"), before(n, "turned") + i * H + g + 1)
                        if g >= 2:
                            act.wait_ge(sem("values"), before(n, "values") + i * H + g - 1)
                        nc.scalar.copy(PT[:, 0, :, :], PS[:, PTB[0], :].rearrange("p (a b) -> p a b", a=2))\
                          .then_inc(sem("pt_a"), 1)
                NO = max(1, a.vcols // P)
                rows = min(P, a.vcols)
                for k in range(NO):
                    act.wait_ge(sem("oT_psum"), before(n, "oT_psum") + i * NO + k + 1)
                    src = PS[0:rows, PTB[k % 2], 0:S]
                    if n == "L0a":
                        ins = nc.scalar.activation(OT[:, 0, :], src, ACT.Copy, scale=hdm[:, 0:1])
                    else:
                        ins = nc.scalar.copy(OT[0:rows, k, :], src)
                    ins.then_inc(sem("oT"), 1)

            def stage_x(n, i, first=None):
                act.wait_ge(x_done, i + (base[n] if first is None else first))
                nc.scalar.copy(xs[:, :, :], tile2(i)).then_inc(sem("staged"), 1)

            def copy_xT(n, i):
                act.wait_ge(sem("xT_psum"), before(n, "xT_psum") + i + 1)
                nc.scalar.copy(xT[:, :], PS[:, PB[0], 0:S]).then_inc(sem("xT"), 1)

            def experts(n, i, chunks, func):
                for e in range(E):
                    act.wait_ge(sem(f"{n}_h_psum"), i * E + e + 1)
                    if e >= 2:
                        act.wait_ge(sem(f"{n}_ye"), i * E + e - 1)
                    for c in range(chunks):
                        ins = nc.scalar.activation(QT[:, 4 * (e % 2) + c, :],
                                                   PS[:, (GA, GB)[e % 2] + c // 2, (c % 2) * S:(c % 2 + 1) * S],
                                                   func, bias=w(f"{n}_b1", e * chunks + c, e * chunks + c + 1))
                    ins.then_inc(sem(f"{n}_h"), 1)
                act.wait_ge(sem(f"{n}_combT_psum"), i + 1)
                nc.scalar.copy(combT[:, :], PS[0:E, 2, 0:S]).then_inc(sem(f"{n}_combT"), 1)

            def L0f():
                n = "L0f"
                act.wait_ge(w_in[n], 16)
                with act.Fori(0, B) as i:
                    act.wait_ge(x_done, base[n])
                    nc.scalar.copy(xs[:, :, :], tile2(i)).then_inc(sem("staged"), 1)
                    copy_xT(n + "r", i)
                    act.wait_ge(sem(f"{n}_lg"), i + 1)
                act.wait_ge(sem(f"{n}_shifted"), 1)
                nc.scalar.activation(rt[:, 1, :, :], rt[:, 0, :, :], ACT.Exp).then_inc(sem(f"{n}_exp"), 1)
                with act.Fori(0, B) as i:
                    stage_x(n, i)
                    copy_xT(n, i)
                    experts(n, i, 4, ACT.Gelu_apprx_tanh)

            def L2f():
                n = "L2f"
                with act.Fori(0, B) as i:
                    attention(ATTNS[n], i)
                    act.wait_ge(sem(f"{n}_mla_psum"), i + 1)
                    nc.scalar.activation(OT[:, 1, :], PS[:, PB[1], 0:S], ACT.Identity, bias=w(f"{n}_ob"))\
                      .then_inc(sem(f"{n}_mla"), 1)
                    act.wait_ge(sem(f"{n}_shifted"), i + 1)
                    nc.scalar.activation(rt[:, 1, 0:2, :], rt[:, 0, 0:2, :], ACT.Exp).then_inc(sem(f"{n}_exp"), 1)
                    experts(n, i, 2, ACT.Gelu)

            def L1f():
                n = "L1f"
                with act.Fori(0, B) as i:
                    stage_x(n, i)
                    copy_xT(n, i)
                    act.wait_ge(sem(f"{n}_h_psum"), i * 2 + 1)
                    nc.scalar.activation(QT[:, 0:3, :], PS[:, GA:GA + 2, :].rearrange("p a b -> p (a b)")[:, 0:768]
                                         .rearrange("p (a b) -> p a b", a=3), ACT.Silu).then_inc(sem(f"{n}_silu"), 1)

            def L2a():
                n = "L2a"
                ab = big[:, 0:2048].rearrange("p (a b) -> p a b", a=8)
                th = big[:, 2048:4096].rearrange("p (a b) -> p a b", a=8)
                xa = big[:, 4096:6144].rearrange("p (a b) -> p a b", a=8)
                act.wait_ge(w_in[n], 16)
                act.wait_ge(sem(f"{n}_Aready"), 1)
                with act.Fori(0, B) as i:
                    stage_x(n, i)
                    copy_xT(n, i)
                    act.wait_ge(sem(f"{n}_bc_psum"), i + 1)
                    nc.scalar.activation(OT[0:32, 1, :], PS[0:32, 0, 0:S], ACT.Identity, bias=w(f"{n}_bin", rows=32))\
                      .then_inc(sem(f"{n}_bc"), 1)
                    act.wait_ge(sem(f"{n}_dt_psum"), 2 * i + 1)
                    nc.scalar.activation(OT[0:64, 0, :], PS[0:64, 1, 0:S], ACT.Identity, bias=w(f"{n}_bdt1", rows=64))\
                      .then_inc(sem(f"{n}_dt1"), 1)
                    act.wait_ge(sem(f"{n}_zdt"), i + 1)
                    nc.scalar.activation(OT[:, 4, :], OT[:, 6, :], ACT.Abs).then_inc(sem(f"{n}_absz"), 1)
                    act.wait_ge(sem(f"{n}_absz"), i + 1)
                    nc.scalar.activation(OT[:, 4, :], OT[:, 4, :], ACT.Exp, scale=-1.0).then_inc(sem(f"{n}_u"), 1)
                    act.wait_ge(sem(f"{n}_dt"), i + 1)
                    for half in range(2):
                        if half:
                            act.wait_ge(sem(f"{n}_scan"), 2 * i + 1)
                        for k in range(8):
                            s = half * 8 + k
                            nc.scalar.activation(ab[:, k, :], OT[:, 3, :], ACT.Exp, scale=w(f"{n}_A", s, s + 1))
                            nc.scalar.activation(th[:, k, :], OT[:, 3, :], ACT.Tanh, scale=negmax[:, s, 0:1])
                            ins = nc.scalar.activation(xa[:, k, :], xT[:, :], ACT.Copy, scale=negmax[:, s, 1:2])
                        ins.then_inc(sem(f"{n}_abar"), 1)

            def L3a():
                n = "L3a"
                act.wait_ge(w_in[n], 16)
                with act.Fori(0, B) as i:
                    act.wait_ge(x_done, base[n])
                    nc.scalar.copy(xs[:, :, :], tile2(i)).then_inc(sem("staged"), 1)
                    copy_xT(n + "r", i)
                    act.wait_ge(sem(f"{n}_qkvg"), i + 1)
                act.wait_ge(sem(f"{n}_gin"), 1)
                nc.scalar.activation(rt[:, 0:4, :, :], rt[:, 0:4, :, :], ACT.Exp, scale=-1.0).then_inc(sem(f"{n}_gexp"), 1)
                for j in range(2):
                    act.wait_ge(sem(f"{n}_s"), j + 1)
                    nc.scalar.activation(QT[:, 0:4, :], QT[:, 0:4, :], ACT.Exp).then_inc(sem(f"{n}_p"), 1)
                with act.Fori(0, B) as i:
                    act.wait_ge(sem(f"{n}_O"), 1)
                    act.wait_ge(x_done, i + base[n])
                    nc.scalar.copy(On[:, :, 0:P], KT[:, :, :].rearrange("p a b -> p (a b)")
                                   .rearrange("p (t d) -> p t d", t=NT)[:, bass.ds(2 * i, 2), :])
                    nc.scalar.copy(xs[:, :, :], tile2(i)).then_inc(sem("staged"), 1)
                    act.wait_ge(sem("oT_psum"), before(n, "oT_psum") + i + 1)
                    nc.scalar.copy(OT[:, 0, :], PS[:, PTB[0], 0:S]).then_inc(sem("oT"), 1)

            def L3f():
                n = "L3f"
                nT = OT[:, 0, :].bitcast(BF16)
                mT = OT[:, 4:8, :].rearrange("p a b -> p (a b)").bitcast(BF16)
                with act.Fori(0, B) as i:
                    stage_x(n, i)
                    act.wait_ge(sem(f"{n}_nT_psum"), i + 1)
                    nc.scalar.copy(nT[:, 0:S], PS[:, PB[0], :].bitcast(BF16)[:, 0:S]).then_inc(sem(f"{n}_nT"), 1)
                    act.wait_ge(sem(f"{n}_h_psum"), i + 1)
                    for j in range(2):
                        nc.scalar.activation(QT[:, 2 * j:2 * j + 2, :].rearrange("p a b -> p (a b)"), PS[:, 2 * j, :],
                                             ACT.Silu, scale=rsum[:, 0, j:j + 1]).then_inc(sem(f"{n}_silu"), 1)
                    act.wait_ge(sem(f"{n}_mT_psum"), i + 1)
                    for j in range(2):
                        ins = nc.scalar.copy(mT[:, 512 * j:512 * (j + 1)], PS[:, 4 + j, :].bitcast(BF16)[:, 0:512])
                    ins.then_inc(sem(f"{n}_mT"), 1)

            own = {"L0f": L0f, "L1f": L1f, "L2a": L2a, "L2f": L2f, "L3a": L3a, "L3f": L3f}
            for s in STAGES:
                if s in own:
                    own[s]()
                else:
                    with act.Fori(0, B) as i:
                        attention(ATTNS[s], i)

        @block.vector
        def _(dve):
            dve.wait_ge(small_loaded, 32)
            dve.wait_ge(w_in["const"], 16)
            nc.vector.tensor_copy(identb[:, :], ident).then_inc(dve_consts, 1)
            nc.vector.tensor_copy(hdm[:, :], hdm_i[:, :]).then_inc(sem("hdm_ready"), 1)
            dve.wait_ge(x_loaded, 16)
            nc.vector.memset(veps[:, :], 0.0).then_inc(x_done, 1)

            def prepare(s):
                a = ATTNS[s]
                dve.wait_ge(x_done, base[s])
                if not a.turned_scores:
                    return
                H, dv = a.heads, a.vcols // a.heads
                nc.vector.memset(SH[:, :, :, :, :], 0.0).then_inc(sem(f"{s}_cleared"), 1)
                nc.vector.memset(V[:, :, 0:32 * H], 0.0).then_inc(sem(f"{s}_cleared"), 1)
                dve.wait_ge(sem(f"{s}_cleared"), 2)
                for j in range(2):
                    ones = V[:, j, 0:32 * H].rearrange("p (h d) -> p h d", h=H)[:, :, dv]
                    nc.vector.memset(ones, 1.0).then_inc(sem(f"{s}_cleared"), 1)
                dve.wait_ge(sem(f"{s}_cleared"), 4)

            def layernorm(s, i, ch, bo):
                if bo is not None:
                    ch.step(nc.vector.tensor_tensor(res[:, :, :], res[:, :, :],
                                                    bo.unsqueeze(1).broadcast_to([P, 2, D]), ALU.add))
                for j in range(2):
                    ch.did(nc.vector.bn_stats(stats[:, j, :], res[:, j, :]))
                ch.wait()
                dve.sem_inc(sem("stats_passed"), 1)
                for j in range(2):
                    ch.did(nc.vector.bn_aggr(mv[:, j, :], stats[:, j, :]))
                ch.wait()
                nc.vector.tensor_scalar(veps[:, :], mv[:, :, 1], 1e-5, None, ALU.add).then_inc(sem("var"), 1)
                dve.wait_ge(sem("rstd"), before(s, "rstd") + i + 1)
                for j in range(2):
                    ins = nc.vector.tensor_scalar(x_tok[:, bass.ds(2 * i + j, 1), :].rearrange("p a d -> p (a d)"),
                                                  res[:, j, :], mv[:, j, 0:1], rstd[:, j:j + 1],
                                                  ALU.subtract, ALU.mult)
                    if j == 0:
                        ch.did(ins)
                    else:
                        ch.wait()
                        ins.then_inc(x_done, 1)

            def attention(a, i, ch):
                n, H = a.name, a.heads
                items = a.items()
                NI = len(items)
                dve.wait_ge(w_in[n], 16)
                if a.clip:
                    dve.wait_ge(sem("mask_in"), i * 16 + 16)
                    ch.step(nc.vector.tensor_scalar(cap[:, :, :], mask_i[:, :, :], 0.0, -BIG,
                                                    ALU.is_equal, ALU.mult))
                    ch.step(nc.vector.tensor_scalar(cap[:, :, :], cap[:, :, :], 100.0, None, ALU.add))
                if a.keymask:
                    dve.wait_ge(sem("kmask_in"), i * 16 + 16)
                    ch.did(nc.vector.tensor_scalar(kbias[:, :], kmask[:, :], 0.0, -1.0e9,
                                                   ALU.is_equal, ALU.mult))
                    ch.step(nc.vector.tensor_scalar(keep[:, :], kmask[:, :], 0.0, w("row_one"),
                                                    ALU.not_equal, ALU.max))
                    ch.step(nc.vector.tensor_scalar(kbias[:, :], kbias[:, :], w("row_mask"), None, ALU.mult))
                if n == "L2x":
                    rotations(i, ch)
                dve.wait_ge(sem("V_psum"), before(n, "V_psum") + i + 1)
                if a.vcols > 512:
                    for k in range(4):
                        ins = nc.vector.tensor_copy(V[:, k // 2, (k % 2) * 512:(k % 2 + 1) * 512],
                                                    PS[:, (5, 6, 7, 2)[k], :])
                elif a.turned_scores:
                    dv = a.vcols // H
                    for j in range(2):
                        ins = nc.vector.tensor_tensor(
                            V[:, j, 0:32 * H].rearrange("p (h d) -> p h d", h=H)[:, :, 0:dv],
                            PS[:, PB[1], j * a.vcols:(j + 1) * a.vcols].rearrange("p (h d) -> p h d", h=H),
                            w(f"{n}_bv").rearrange("p (h d) -> p h d", h=H), ALU.add)
                else:
                    src = PS[:, PB[1], 0:2 * a.vcols].rearrange("p (a b) -> p a b", a=2)
                    if a.bias:
                        ins = nc.vector.tensor_tensor(V[:, :, 0:a.vcols], src,
                                                      w(f"{n}_bv").unsqueeze(1).broadcast_to([P, 2, a.vcols]), ALU.add)
                    else:
                        ins = nc.vector.tensor_copy(V[:, :, 0:a.vcols], src)
                ins.then_inc(sem("V"), 1)
                for k, (what, t0) in enumerate(items):
                    if k % 2 and not a.rope and not a.keymask:
                        continue
                    dve.wait_ge(sem("item_psum"), before(n, "item_psum") + i * NI + k + 1)
                    g = (GA, GB)[k % 2]
                    dst = QT if what[0] == "q" else KT
                    if a.rope:
                        tab = (1 if what[1:] else 0) + (2 if what[0] == "q" and n == "L2x" else 0)
                        to = RT[:, :, :] if what[1:] else dst[:, t0:t0 + 4, :]
                        if n == "L1a":
                            t = w("L1a_sin") if what[1:] else w("L1a_cos")
                            if what == "q" or what == "qr":
                                ins = nc.vector.scalar_tensor_tensor(
                                    to.rearrange("p (a b) s -> p a b s", a=2)[:, :, :, :].rearrange("p a b s -> p (a b) s"),
                                    PS[:, g:g + 2, :].rearrange("p a (b s) -> p (a b) s", b=2), 1.0 / 128,
                                    t.unsqueeze(1).broadcast_to([P, 4, S]), ALU.mult, ALU.mult)
                            else:
                                ins = nc.vector.tensor_tensor(
                                    to, PS[:, g:g + 2, :].rearrange("p a (b s) -> p (a b) s", b=2),
                                    t.unsqueeze(1).broadcast_to([P, 4, S]), ALU.mult)
                        else:
                            for t in range(4):
                                ins = nc.vector.scalar_tensor_tensor(
                                    to[:, t, :], PS[:, g + t // 2, (t % 2) * S:(t % 2 + 1) * S],
                                    w(f"{n}_b{what}", t, t + 1), rot[:, tab, :], ALU.add, ALU.mult)
                        if what[1:]:
                            ch.step(ins)
                            ins = nc.vector.tensor_tensor(dst[:, t0:t0 + 4, :], dst[:, t0:t0 + 4, :], RT[:, :, :], ALU.add)
                            ins.then_inc(sem("item_b" if k % 2 else "item_a"), 1)
                            dve.wait_ge(sem("item_b"), before(n, "item_b") + i * (NI // 2) + k // 2 + 1)
                        else:
                            ins.then_inc(sem("item_b" if k % 2 else "item_a"), 1)
                            dve.wait_ge(sem("item_a"), before(n, "item_a") + i * (NI // 2) + k // 2 + 1)
                    elif what == "k":
                        for t in range(4):
                            ins = nc.vector.scalar_tensor_tensor(
                                KT[:, t, :], PS[:, g + t // 2, (t % 2) * S:(t % 2 + 1) * S],
                                w(f"{n}_bk", t, t + 1), keep[:, :], ALU.add, ALU.mult)
                        ins.then_inc(sem("item_b"), 1)
                    else:
                        for t in range(a.group):
                            src = PS[:, g + t // 2, (t % 2) * S:(t % 2 + 1) * S]
                            if a.bias:
                                ins = nc.vector.tensor_scalar(QT[:, t0 + t, :], src, w(f"{n}_bq", t0 + t, t0 + t + 1),
                                                              a.scale, ALU.add, ALU.mult)
                            else:
                                ins = nc.vector.tensor_scalar(QT[:, t0 + t, :], src, a.scale, None, ALU.mult)
                        ins.then_inc(sem("item_a"), 1)
                if a.small:
                    for k, (dst, src, x) in enumerate(((KS, KT, "k"), (QS, QT, "q"))):
                        dve.wait_ge(sem("rounded"), before(n, "rounded") + 2 * i + k + 1)
                        nc.vector.scalar_tensor_tensor(dst[:, :, :], src[:, 0:4, :], w(f"lo_{x}"),
                                                       dst[:, :, :].bitcast(F32), ALU.mult, ALU.add)\
                          .then_inc(sem("stack"), 1)
                if a.turned_scores:
                    T = a.tiles
                    for h in range(H + 1):
                        if h < H:
                            dve.wait_ge(sem("scores"), before(n, "scores") + i * H + h + 1)
                            nc.vector.tensor_reduce(negmax[:, h, :], PS[:, MAXB[h % 2], :]
                                                    .rearrange("p (a b) -> p a b", a=2), AX.X, ALU.max, negate=True)\
                              .then_inc(sem("max"), 1)
                        if h % 4 == 3:
                            t = h // 4
                            dve.wait_ge(sem("max"), before(n, "max") + i * H + h + 1)
                            m = negmax[:, 4 * t:4 * t + 4, :].rearrange("p r j -> p j r")
                            hi, lo = SH[:, t, :, :, SHIFT_ROW], SH[:, t, :, :, SHIFT_ROW + 1]
                            ch.step(nc.vector.tensor_copy(hi.bitcast(F32R), m))
                            nc.vector.tensor_tensor(lo, m, hi, ALU.subtract).then_inc(sem("shift"), 1)
                        if h % 4 == 0 and h >= 4:
                            t = h // 4 - 1
                            dve.wait_ge(sem("shift_psum"), before(n, "shift_psum") + i * T + t + 1)
                            dve.wait_ge(sem("stack"), before(n, "stack") + 2 * i + 2)
                            nc.vector.tensor_tensor(QS[:, t, :], QS[:, t, :].bitcast(F32), PS[:, SHB, 0:S], ALU.add)\
                              .then_inc(sem("shifted"), 1)
                    dv = a.vcols // H
                    dve.wait_ge(sem("outputs_psum"), before(n, "outputs_psum") + i + 1)
                    o = [PS[:, EXPB[0] + j, :].rearrange("p (h d) -> p h d", h=H) for j in range(2)]
                    for j in range(2):
                        ch.did(nc.vector.reciprocal(rsum[:, 0:H, j], o[j][:, :, dv]))
                    ch.wait()
                    for j in range(2):
                        ins = nc.vector.tensor_tensor(
                            On[:, j, 0:a.vcols].rearrange("p (h d) -> p h d", h=H), o[j][:, :, 0:dv],
                            rsum[:, 0:H, j].unsqueeze(2).broadcast_to([P, H, dv]), ALU.mult)
                    ins.then_inc(sem("on"), 1)
                for h in range(0 if a.turned_scores else H + 3):
                    if h < H:
                        dve.wait_ge(sem("scores"), before(n, "scores") + i * H + h + 1)
                        src = PS[:, SCB[h % 3], :].rearrange("p (a b) -> p a b", a=2)
                        if a.clip:
                            if h >= 2:
                                dve.wait_ge(sem("probs"), before(n, "probs") + i * H + h - 1)
                            nc.vector.scalar_tensor_tensor(SC[:, h % 2, :, :], src, -100.0, cap[:, :, :],
                                                           ALU.max, ALU.min).then_inc(sem("clipped"), 1)
                            dve.wait_ge(sem("clipped"), before(n, "clipped") + i * H + h + 1)
                            src = SC[:, h % 2, :, :]
                        nc.vector.tensor_reduce(negmax[:, h, :], src, AX.X, ALU.max, negate=True)\
                          .then_inc(sem("max"), 1)
                    g = h - 2
                    if g >= 0 and g < H and g % 2 == 1:
                        dve.wait_ge(sem("turned"), before(n, "turned") + i * H + g + 1)
                        if g >= 2:
                            dve.wait_ge(sem("values"), before(n, "values") + i * H + g - 1)
                        nc.vector.tensor_copy(PT[:, 1, :, :], PS[:, PTB[1], :].rearrange("p (a b) -> p a b", a=2))\
                          .then_inc(sem("pt_v"), 1)
                    if a.vcols > 512 and h >= 3:
                        g = h - 3
                        dve.wait_ge(sem("values"), before(n, "values") + i * H + g + 1)
                        ch.step(nc.vector.reciprocal(rsum[:, g, :], sums[:, g, :]))
                        ins = nc.vector.tensor_tensor(
                            On[:, :, g * P:(g + 1) * P],
                            PS[:, (5, 6, 7, 5, 6, 7, 5, 6)[g], 0:2 * P].rearrange("p (a b) -> p a b", a=2),
                            rsum[:, g, :].unsqueeze(2).broadcast_to([P, 2, P]), ALU.mult)
                        ins.then_inc(sem("on"), 1)
                if a.vcols <= 512 and not a.turned_scores:
                    dv = a.vcols // H
                    dve.wait_ge(sem("values"), before(n, "values") + i * H + H)
                    ch.step(nc.vector.reciprocal(rsum[:, 0:H, :], sums[:, 0:H, :]))
                    for j in range(2):
                        ins = nc.vector.tensor_tensor(
                            On[:, j, 0:a.vcols].rearrange("p (h d) -> p h d", h=H),
                            PS[:, OB, j * a.vcols:(j + 1) * a.vcols].rearrange("p (h d) -> p h d", h=H),
                            rsum[:, 0:H, j].unsqueeze(2).broadcast_to([P, H, dv]), ALU.mult)
                    ins.then_inc(sem("on"), 1)
                if a.tail:
                    dve.wait_ge(sem("y"), before(n, "y") + i + 1)
                    ch.step(nc.vector.tensor_tensor(res[:, :, :], PS[:, PB[0], 0:S].rearrange("p (a b) -> p a b", a=2),
                                                    xs[:, :, :], ALU.add))
                    layernorm(n, i, ch, w(f"{n}_bo") if a.bias else None)

            def rotations(i, ch):
                dve.wait_ge(sem("pos_in"), i * 16 + 16)
                two_pi = 6.283185307179586
                hi = 6.28125
                mid = 0.0019350051879882812
                lo = two_pi - hi - mid
                ch.step(nc.vector.tensor_copy(rot[:, 1, :], pos_i[:, :]))
                ch.step(nc.vector.tensor_scalar(rot[:, 1, :], rot[:, 1, :], w("L2x_freq"), None, ALU.mult))
                for c, shift in ((4, 0.0), (5, two_pi / 4)):
                    ch.step(nc.vector.tensor_scalar(rot[:, 2, :], rot[:, 1, :], 1.0 / two_pi, shift / two_pi, ALU.mult, ALU.add))
                    ch.step(nc.vector.tensor_scalar(rot[:, 2, :], rot[:, 2, :], MAGIC, MAGIC, ALU.add, ALU.subtract))
                    ch.step(nc.vector.scalar_tensor_tensor(rot[:, 3, :], rot[:, 2, :], -hi, rot[:, 1, :], ALU.mult, ALU.add))
                    ch.step(nc.vector.scalar_tensor_tensor(rot[:, 3, :], rot[:, 2, :], -mid, rot[:, 3, :], ALU.mult, ALU.add))
                    ch.step(nc.vector.scalar_tensor_tensor(rot[:, 3, :], rot[:, 2, :], -lo, rot[:, 3, :], ALU.mult, ALU.add))
                    ch.step(nc.vector.tensor_scalar(rot[:, 3, :], rot[:, 3, :], shift, 3.1415925, ALU.add, ALU.min))
                    ins = nc.vector.tensor_scalar(rot[:, c, :], rot[:, 3, :], -3.1415925, None, ALU.max)
                    if c == 4:
                        ch.step(ins)
                    else:
                        ins.then_inc(sem("angles"), 1)
                dve.wait_ge(sem("sines"), i * 2 + 2)
                ch.did(nc.vector.tensor_scalar(rot[:, 1, :], rot[:, 4, :], w("L2x_sign"), None, ALU.mult))
                ch.did(nc.vector.tensor_scalar(rot[:, 2, :], rot[:, 0, :], ATTNS["L2x"].scale, None, ALU.mult))
                ch.did(nc.vector.tensor_scalar(rot[:, 3, :], rot[:, 4, :], w("L2x_sign"), ATTNS["L2x"].scale,
                                               ALU.mult, ALU.mult))
                ch.wait()

            def flat(t):
                return t.rearrange("p a b -> p (a b)")

            def both(t):
                return t.rearrange("p (a b) -> p a b", a=2)

            def top2(T, ch, count=None):
                def r(k):
                    return rt[:, k, 0:T, :]

                def c(k):
                    return rts[:, k, 0:T]

                def wide(k):
                    return c(k).unsqueeze(2).broadcast_to([P, T, E])

                ch.step(nc.vector.tensor_reduce(c(0), r(1), AX.X, ALU.add))
                ch.step(nc.vector.reciprocal(c(1), c(0)))
                ch.step(nc.vector.tensor_tensor(r(1), r(1), wide(1), ALU.mult))
                for k in range(2):
                    ch.step(nc.vector.tensor_reduce(c(2 + k), r(1), AX.X, ALU.max))
                    ch.step(nc.vector.tensor_tensor(r(4), r(1), wide(2 + k), ALU.is_equal))
                    ch.step(nc.vector.tensor_tensor(r(4), r(4), w("w8").unsqueeze(1).broadcast_to([P, T, E]), ALU.mult))
                    ch.step(nc.vector.tensor_reduce(c(4), r(4), AX.X, ALU.max))
                    ch.step(nc.vector.tensor_tensor(r(2 + k), r(4), wide(4), ALU.is_equal))
                    if k == 0:
                        ch.step(nc.vector.scalar_tensor_tensor(r(1), r(2), -2.0, r(1), ALU.mult, ALU.add))

            def weigh(T, ch, eps, dst, sig):
                def c(k):
                    return rts[:, k, 0:T]

                ch.step(nc.vector.tensor_tensor(c(4), c(2), c(3), ALU.add))
                ch.step(nc.vector.tensor_scalar(c(4), c(4), eps, None, ALU.add))
                ch.step(nc.vector.reciprocal(c(5), c(4)))
                for k in (2, 3):
                    ch.did(nc.vector.tensor_tensor(c(k), c(k), c(5), ALU.mult))
                ch.wait()
                for k in (2, 3):
                    ch.did(nc.vector.tensor_tensor(rt[:, k, 0:T, :], rt[:, k, 0:T, :],
                                                   c(k).unsqueeze(2).broadcast_to([P, T, E]), ALU.mult))
                ch.wait()
                nc.vector.tensor_tensor(dst, rt[:, 2, 0:T, :], rt[:, 3, 0:T, :], ALU.add).then_inc(sig, 1)

            def experts(n, i, ch, factor, start):
                for e in range(E):
                    dve.wait_ge(sem(f"{n}_ye"), i * E + e + 1)
                    if e == 0:
                        dve.wait_ge(sem(f"{n}_combs"), i + 1)
                    else:
                        dve.wait_ge(sem(f"{n}_acc"), i * E + e)
                    for j in range(2):
                        ins = nc.vector.scalar_tensor_tensor(res[:, j, :], PS[:, (5, 7)[e % 2], j * P:(j + 1) * P],
                                                             combs[:, j, e:e + 1], (start if e == 0 else res)[:, j, :],
                                                             ALU.mult, ALU.add)
                    ins.then_inc(sem(f"{n}_acc"), 1)
                dve.wait_ge(sem(f"{n}_yb"), i + 1)
                dve.wait_ge(sem(f"{n}_acc"), i * E + E)
                ch.step(nc.vector.tensor_tensor(res[:, :, :], res[:, :, :], both(PS[:, PB[0], 0:S]), ALU.add))

            def L0f():
                n = "L0f"
                dve.wait_ge(x_done, base[n])
                dve.wait_ge(w_in[n], 16)
                with dve.Fori(0, B) as i:
                    dve.wait_ge(sem(f"{n}_lg_psum"), i + 1)
                    nc.vector.tensor_copy(rt[:, 0, bass.ds(2 * i, 2), :], PS[:, PB[1], 0:2 * E].rearrange(
                        "p (a b) -> p a b", a=2)).then_inc(sem(f"{n}_lg"), 1)
                ch = Chain(dve, sem(f"{n}_route"), PER["L0r"])
                ch.turn(0)
                dve.wait_ge(sem(f"{n}_lg"), B)
                ch.step(nc.vector.tensor_reduce(rts[:, 0, :], rt[:, 0, :, :], AX.X, ALU.max))
                nc.vector.tensor_tensor(rt[:, 0, :, :], rt[:, 0, :, :], rts[:, 0, :].unsqueeze(2).broadcast_to([P, NT, E]),
                                        ALU.subtract).then_inc(sem(f"{n}_shifted"), 1)
                dve.wait_ge(sem(f"{n}_exp"), 1)
                top2(NT, ch)
                nc.vector.tensor_copy(ohb[:, :, :, :], rt[:, 2:4, :, :]).then_inc(sem(f"{n}_onehots"), 1)
                dve.wait_ge(sem(f"{n}_counts"), 1)
                cnt = big[:, 0:256].rearrange("p (k t e) -> p k t e", k=2, t=NT)
                pre = big[:, 256:512].rearrange("p (k t e) -> p k t e", k=2, t=NT)
                ch.step(nc.vector.tensor_copy(big[:, 0:256], PS[:, 1, 0:256]))
                a, b = cnt, pre
                for d in (1, 2, 4, 8):
                    ch.did(nc.vector.tensor_copy(b[:, :, 0:d, :], a[:, :, 0:d, :]))
                    for k in range(2):
                        ch.did(nc.vector.tensor_tensor(b[:, k, d:NT, :], a[:, k, d:NT, :], a[:, k, 0:NT - d, :], ALU.add))
                    ch.wait()
                    a, b = b, a
                ch.step(nc.vector.tensor_scalar(big[:, 512:520], a[:, 0, NT - 1, :], float(CAPACITY), None, ALU.min))
                pos = big[:, 768:1024].rearrange("p (k t e) -> p k t e", k=2, t=NT)
                ch.did(nc.vector.tensor_copy(big[:, 768:1024], PS[:, 0, 0:256]))
                ch.wait()
                for k in range(2):
                    ch.did(nc.vector.tensor_tensor(pos[:, k, 1:NT, :], pos[:, k, 1:NT, :], a[:, k, 0:NT - 1, :], ALU.add))
                ch.wait()
                ch.step(nc.vector.tensor_tensor(pos[:, 1, :, :], pos[:, 1, :, :],
                                                big[:, 512:520].unsqueeze(1).broadcast_to([P, NT, E]), ALU.add))
                ch.step(nc.vector.tensor_scalar(big[:, 768:1024], big[:, 768:1024], float(CAPACITY), None, ALU.is_le))
                for k in range(2):
                    ch.did(nc.vector.tensor_tensor(rt[:, 2 + k, :, :], rt[:, 2 + k, :, :], pos[:, k, :, :], ALU.mult))
                ch.wait()
                weigh(NT, ch, 1e-9, comb[:, :, :], sem(f"{n}_routed"))
                ch.end()
                dve.wait_ge(sem(f"{n}_routed"), 1)
                ch = Chain(dve, sem("dve_step"), PER[n], before(n, "dve_step"))
                with dve.Fori(0, B) as i:
                    ch.turn(i)
                    dve.wait_ge(sem("staged"), before(n, "staged") + i + 1)
                    nc.vector.tensor_copy(combs[:, :, :], comb[:, bass.ds(2 * i, 2), :]).then_inc(sem(f"{n}_combs"), 1)
                    experts(n, i, ch, 1.0, xs)
                    layernorm(n, i, ch, None)
                    ch.end()

            def L2f():
                n = "L2f"
                prepare(n)
                ch = Chain(dve, sem("dve_step"), PER[n], before(n, "dve_step"))
                with dve.Fori(0, B) as i:
                    ch.turn(i)
                    attention(ATTNS[n], i, ch)
                    dve.wait_ge(sem(f"{n}_lg_psum"), i + 1)
                    nc.vector.tensor_tensor(rt[:, 0, 0:2, :], PS[:, PB[1], 0:2 * E].rearrange("p (a b) -> p a b", a=2),
                                            w(f"{n}_br").unsqueeze(1).broadcast_to([P, 2, E]), ALU.add)\
                      .then_inc(sem(f"{n}_lg"), 1)
                    dve.wait_ge(sem(f"{n}_lg"), i + 1)
                    ch.step(nc.vector.tensor_reduce(rts[:, 0, 0:2], rt[:, 0, 0:2, :], AX.X, ALU.max))
                    nc.vector.tensor_tensor(rt[:, 0, 0:2, :], rt[:, 0, 0:2, :],
                                            rts[:, 0, 0:2].unsqueeze(2).broadcast_to([P, 2, E]),
                                            ALU.subtract).then_inc(sem(f"{n}_shifted"), 1)
                    dve.wait_ge(sem(f"{n}_exp"), i + 1)
                    top2(2, ch)
                    weigh(2, ch, 1e-8, combs[:, :, :], sem(f"{n}_combs"))
                    ch.step(nc.vector.memset(OT[:, 7, :], 0.0))
                    experts(n, i, ch, 1.0, OT[:, 7, :].rearrange("p (a b) -> p a b", a=2))
                    ch.step(nc.vector.tensor_scalar(res[:, :, :], res[:, :, :], 0.3, None, ALU.mult))
                    ch.step(nc.vector.scalar_tensor_tensor(flat(res[:, :, :]), flat(xs[:, :, :]), 2.0, flat(res[:, :, :]),
                                                           ALU.mult, ALU.add))
                    layernorm(n, i, ch, None)
                    ch.end()

            def L1f():
                n = "L1f"
                dve.wait_ge(x_done, base[n])
                nc.vector.tensor_scalar(wdeq[:, :], wint[:, :], 1.0 / 127.0, None, ALU.mult).then_inc(sem("wdeq_ready"), 1)
                ch = Chain(dve, sem("dve_step"), PER[n], before(n, "dve_step"))
                with dve.Fori(0, B) as i:
                    ch.turn(i)
                    dve.wait_ge(sem(f"{n}_h_psum"), i * 2 + 2)
                    dve.wait_ge(sem(f"{n}_silu"), i + 1)
                    nc.vector.tensor_tensor(QT[:, 3:6, :], QT[:, 0:3, :],
                                            PS[:, GB:GB + 2, :].rearrange("p a b -> p (a b)")[:, 0:768]
                                            .rearrange("p (a b) -> p a b", a=3), ALU.mult).then_inc(sem(f"{n}_h"), 1)
                    dve.wait_ge(sem("y"), before(n, "y") + i + 1)
                    ch.step(nc.vector.tensor_tensor(res[:, :, :], both(PS[:, PB[0], 0:S]), xs[:, :, :], ALU.add))
                    layernorm(n, i, ch, None)
                    ch.end()

            def L2a():
                n = "L2a"
                dve.wait_ge(x_done, base[n])
                ab, th, xa, hh = (big[:, 2048 * k:2048 * (k + 1)] for k in range(4))
                z, dt, u, y = OT[:, 6, :], OT[:, 3, :], OT[:, 4, :], OT[:, 5, :]
                bc = OT[0:32, 1, :]
                stk = OT[0:96, 2, 0:P].bitcast(BF16)
                s1, s2, s3 = KT[:, 0, :], KT[:, 1, :], KT[:, 2, :]
                dve.wait_ge(w_in[n], 16)
                nc.vector.tensor_scalar(negmax[:, :, 0], w(f"{n}_A"), 0.5, None, ALU.mult)
                nc.vector.reciprocal(negmax[:, :, 1], w(f"{n}_A")).then_inc(sem(f"{n}_Aready"), 1)
                ch = Chain(dve, sem("dve_step"), PER[n], before(n, "dve_step"))
                with dve.Fori(0, B) as i:
                    ch.turn(i)
                    dve.wait_ge(sem(f"{n}_bc"), i + 1)
                    ch.step(nc.vector.tensor_copy(stk[0:32, :], bc))
                    ch.step(nc.vector.tensor_tensor(bc, bc, stk[0:32, :], ALU.subtract))
                    ch.step(nc.vector.tensor_copy(stk[32:64, :], bc))
                    ch.step(nc.vector.tensor_copy(KT[0:32, 3, :], stk[32:64, :]))
                    ch.step(nc.vector.tensor_tensor(bc, bc, KT[0:32, 3, :], ALU.subtract))
                    nc.vector.tensor_copy(stk[64:96, :], bc).then_inc(sem(f"{n}_stack"), 1)
                    dve.wait_ge(sem(f"{n}_dt_psum"), 2 * i + 2)
                    nc.vector.tensor_scalar(z, PS[:, 2, 0:S], w(f"{n}_bdt2"), None, ALU.add)\
                      .then_inc(sem(f"{n}_zdt"), 1)
                    dve.wait_ge(sem(f"{n}_u"), i + 1)
                    ch.step(nc.vector.tensor_scalar(s1, u, 2.0, None, ALU.add))
                    ch.step(nc.vector.reciprocal(s2, s1))
                    ch.step(nc.vector.tensor_tensor(s1, u, s2, ALU.mult))
                    ch.step(nc.vector.tensor_tensor(s2, s1, s1, ALU.mult))
                    ch.step(nc.vector.tensor_scalar(s3, s2, 2.0 / 17, None, ALU.mult))
                    for k in (15, 13, 11, 9, 7, 5, 3):
                        ch.step(nc.vector.scalar_tensor_tensor(s3, s3, 2.0 / k, s2, ALU.add, ALU.mult))
                    ch.step(nc.vector.scalar_tensor_tensor(s3, s3, 2.0, s1, ALU.add, ALU.mult))
                    ch.step(nc.vector.scalar_tensor_tensor(z, z, 0.0, s3, ALU.max, ALU.add))
                    nc.vector.tensor_scalar(dt, z, 1e-7, 1e6, ALU.max, ALU.min).then_inc(sem(f"{n}_dt"), 1)
                    ch.did(nc.vector.memset(y, 0.0))
                    nc.vector.memset(s1, 0.0).then_inc(sem(f"{n}_z"), 1)
                    ch.wait()
                    for half in range(2):
                        dve.wait_ge(sem(f"{n}_abar"), 2 * i + half + 1)
                        ch.step(nc.vector.scalar_tensor_tensor(th, ab, 1.0, th, ALU.add, ALU.mult))
                        dve.wait_ge(sem(f"{n}_B"), 2 * i + half + 1)
                        nc.vector.tensor_tensor(xa, xa, PS[:, 0:4, :].rearrange("p a b -> p (a b)"), ALU.mult)\
                          .then_inc(sem(f"{n}_g"), 1)
                        dve.wait_ge(sem(f"{n}_g"), 2 * i + half + 1)
                        ch.did(nc.vector.tensor_tensor(th, th, xa, ALU.mult))
                        ch.did(nc.vector.memset(ab.rearrange("p (a b) -> p a b", a=8)[:, :, 0:1], 0.0))
                        ch.wait()
                        nc.vector.tensor_tensor_scan(hh, ab, th, 0.0, ALU.mult, ALU.add).then_inc(sem(f"{n}_scan"), 1)
                        dve.wait_ge(sem(f"{n}_scan"), 2 * i + half + 1)
                        dve.wait_ge(sem(f"{n}_C"), 2 * i + half + 1)
                        nc.vector.tensor_tensor(hh, hh, PS[:, 4:8, :].rearrange("p a b -> p (a b)"), ALU.mult)\
                          .then_inc(sem(f"{n}_hc"), 1)
                        dve.wait_ge(sem(f"{n}_hc"), 2 * i + half + 1)
                        ch.step(nc.vector.tensor_reduce(s2, hh.rearrange("p (n l) -> p l n", n=8), AX.X, ALU.add))
                        ch.step(nc.vector.tensor_tensor(y, y, s2, ALU.add))
                    nc.vector.scalar_tensor_tensor(y, xT[:, :], w(f"{n}_D"), y, ALU.mult, ALU.add)\
                      .then_inc(sem(f"{n}_ysum"), 1)
                    dve.wait_ge(sem("y"), before(n, "y") + i + 1)
                    ch.step(nc.vector.tensor_tensor(res[:, :, :], both(PS[:, PB[0], 0:S]), xs[:, :, :], ALU.add))
                    layernorm(n, i, ch, None)
                    ch.end()

            def L3a():
                n = "L3a"
                dve.wait_ge(x_done, base[n])
                qkvg = big[:, :].rearrange("p (t j c) -> p t j c", t=B, j=2)
                dve.wait_ge(w_in[n], 16)
                with dve.Fori(0, B) as i:
                    dve.wait_ge(sem(f"{n}_qkvg_psum"), i + 1)
                    nc.vector.tensor_tensor(qkvg[:, bass.ds(i, 1), :, :].rearrange("p t j c -> p (t j) c"), PS[:, 0:2, :],
                                            w(f"{n}_b").unsqueeze(1).broadcast_to([P, 2, 512]), ALU.add)\
                      .then_inc(sem(f"{n}_qkvg"), 1)
                ch = Chain(dve, sem(f"{n}_mid"), PER["L3m"])
                ch.turn(0)
                dve.wait_ge(sem(f"{n}_qkvg"), B)
                allt = big[:, :].rearrange("p (t c) -> p t c", t=NT)
                gin = rt[:, 0:4, :, :].rearrange("p k t e -> p (k t e)")
                ch.did(nc.vector.tensor_reduce(gin.rearrange("p (t g) -> p t g", t=NT),
                                               allt[:, :, 384:512].rearrange("p t (g k) -> p t g k", k=4), AX.X, ALU.add))
                ch.step(nc.vector.tensor_scalar(allt[:, :, 0:128], allt[:, :, 0:128], R8, None, ALU.mult))
                dve.sem_inc(sem(f"{n}_gin"), 1)
                dve.wait_ge(sem(f"{n}_gexp"), 1)
                ch.step(nc.vector.tensor_scalar(gin, gin, 1.0, None, ALU.add))
                ch.step(nc.vector.reciprocal(gin, gin))
                ab = gin.rearrange("p (t h k) -> p t h k", t=NT, k=2)
                g1 = comb[:, :, :].rearrange("p t e -> p (t e)")
                ga = OT[:, 0, 0:256].rearrange("p (t h) -> p t h", t=NT)
                ch.step(nc.vector.tensor_tensor(ga, ab[:, :, :, 1], w(f"{n}_ga").unsqueeze(1).broadcast_to([P, NT, 16]),
                                                ALU.mult))
                ch.step(nc.vector.scalar_tensor_tensor(ga, ga, -1.0, ab[:, :, :, 0], ALU.add, ALU.mult))
                ch.step(nc.vector.tensor_scalar(ga, ga, 2.0, None, ALU.add))
                rel = w(f"{n}_rel").rearrange("p (a h) -> p a h", a=15)
                sc = QT[:, 0:4, :].rearrange("p a b -> p (a b)").rearrange("p (t u h) -> p t u h", t=B, u=B)
                pr = V[:, :, :].rearrange("p a b -> p (a b)")
                Oall = KT[:, :, :].rearrange("p a b -> p (a b)").rearrange("p (t j c) -> p t j c", t=B, j=2)
                for j in range(2):
                    for t in range(B):
                        q = qkvg[:, t, j, 0:128].unsqueeze(1).broadcast_to([P, B, 128])
                        k = qkvg[:, :, j, 128:256]
                        at = 1024 * (t % 2)
                        prod = pr[:, at:at + 1024].rearrange("p (u c) -> p u c", u=B)
                        ch.did(nc.vector.tensor_tensor(prod, q, k, ALU.mult))
                        ch.did(nc.vector.tensor_tensor(On[:, 0, t * P:(t + 1) * P].rearrange("p (u h) -> p u h", u=B),
                                                       rel[:, 7 - t:15 - t, :],
                                                       ga[:, 2 * t + j, :].unsqueeze(1).broadcast_to([P, B, 16]), ALU.mult))
                        ch.wait()
                        ch.did(nc.vector.tensor_reduce(sc[:, t, :, :], pr[:, at:at + 1024].rearrange(
                            "p (u h d) -> p u h d", u=B, h=16), AX.X, ALU.add))
                    ch.wait()
                    scf = QT[:, 0:4, :].rearrange("p a b -> p (a b)")
                    ch.step(nc.vector.tensor_tensor(scf, scf, On[:, 0, :], ALU.add))
                    scu = scf.rearrange("p (t u h) -> p t h u", t=B, u=B)
                    mx = OT[:, 1, 0:128].rearrange("p (t h) -> p t h", t=B)
                    ch.step(nc.vector.tensor_reduce(mx, scu, AX.X, ALU.max))
                    nc.vector.tensor_tensor(sc, sc, mx.unsqueeze(2).broadcast_to([P, B, B, 16]), ALU.subtract)\
                      .then_inc(sem(f"{n}_s"), 1)
                    dve.wait_ge(sem(f"{n}_p"), j + 1)
                    sm = OT[:, 1, 128:256].rearrange("p (t h) -> p t h", t=B)
                    ch.step(nc.vector.tensor_reduce(sm, scu, AX.X, ALU.add))
                    ch.step(nc.vector.reciprocal(sm, sm))
                    for t in range(B):
                        at = 1024 * (t % 2)
                        ch.step(nc.vector.tensor_tensor(
                            pr[:, at:at + 1024].rearrange("p (u h d) -> p u h d", u=B, h=16),
                            sc[:, t, :, :].unsqueeze(3).broadcast_to([P, B, 16, 8]),
                            qkvg[:, :, j, 256:384].rearrange("p u (h d) -> p u h d", h=16), ALU.mult))
                        ch.step(nc.vector.tensor_reduce(Oall[:, t, j, :], pr[:, at:at + 1024].rearrange(
                            "p (u c) -> p c u", u=B), AX.X, ALU.add))
                        ch.did(nc.vector.tensor_tensor(
                            Oall[:, t, j, :].rearrange("p (h d) -> p h d", h=16),
                            Oall[:, t, j, :].rearrange("p (h d) -> p h d", h=16),
                            sm[:, t, :].unsqueeze(2).broadcast_to([P, 16, 8]), ALU.mult))
                ch.wait()
                dve.sem_inc(sem(f"{n}_O"), 1)
                ch.end()
                ch = Chain(dve, sem("dve_step"), PER[n], before(n, "dve_step"))
                with dve.Fori(0, B) as i:
                    ch.turn(i)
                    dve.wait_ge(sem("y"), before(n, "y") + i + 1)
                    ch.step(nc.vector.tensor_tensor(res[:, :, :], both(PS[:, PB[0], 0:S]), xs[:, :, :], ALU.add))
                    layernorm(n, i, ch, w(f"{n}_bo"))
                    ch.end()

            def L3f():
                n = "L3f"
                dve.wait_ge(x_done, base[n])
                nq = On[:, :, 0:64].bitcast(BF16)
                hq = On[:, :, 128:384].bitcast(BF16)
                dve.wait_ge(w_in[n], 16)
                means = mv[:, :, :].rearrange("p a b -> p (a b)")
                ch = Chain(dve, sem(f"{n}_quant"), PER["L3q"])
                ch.turn(0)
                for k, name in enumerate(("wg", "wu", "wd")):
                    ins = nc.vector.tensor_reduce(means[:, k:k + 1], w(f"{n}_{name}"), AX.X, ALU.add,
                                                  apply_absolute_value=True)
                ins.then_inc(sem(f"{n}_wsum"), 1)
                dve.wait_ge(sem(f"{n}_wmean_psum"), 1)
                wm, ws = sums[:, 0:3, 0], sums[:, 0:3, 1]
                ch.step(nc.vector.tensor_scalar(wm, PS[:, 0, 0:3], 1.0 / (512 * 128), 1e-5, ALU.mult, ALU.max))
                ch.step(nc.vector.reciprocal(ws, wm))
                for k, name in enumerate(("wg", "wu", "wd")):
                    tmp = KT[:, 2 * k:2 * k + 2, :].rearrange("p a b -> p (a b)")
                    ch.step(nc.vector.tensor_scalar(tmp, w(f"{n}_{name}"), sums[:, k, 1:2], 1.0, ALU.mult, ALU.min))
                    ch.step(nc.vector.tensor_scalar(tmp, tmp, -1.0, MAGIC, ALU.max, ALU.add))
                    ins = nc.vector.tensor_scalar(tern[:, k, :], tmp, MAGIC, None, ALU.subtract)
                    if k < 2:
                        ch.did(ins)
                    else:
                        ch.wait()
                        ins.then_inc(sem(f"{n}_tern"), 1)
                ch.end()

                def quantise(ch, src, dst, tmp, j, slot, sig):
                    amax, inv = rts[:, 0, j:j + 1], rts[:, 1, j:j + 1]
                    ch.step(nc.vector.tensor_reduce(amax, src, AX.X, ALU.max, apply_absolute_value=True))
                    ch.step(nc.vector.tensor_scalar(amax, amax, 1e-5, None, ALU.max))
                    ch.step(nc.vector.reciprocal(inv, amax))
                    ch.did(nc.vector.tensor_scalar(rsum[:, slot, j:j + 1], amax, 1.0 / 127, None, ALU.mult))
                    ch.step(nc.vector.tensor_scalar(inv, inv, 127.0, None, ALU.mult))
                    ch.step(nc.vector.tensor_scalar(tmp, src, inv, MAGIC, ALU.mult, ALU.add))
                    ch.step(nc.vector.tensor_scalar(tmp, tmp, MAGIC, 127.0, ALU.subtract, ALU.min))
                    nc.vector.tensor_scalar(dst, tmp, -128.0, None, ALU.max).then_inc(sig, 1)

                ch = Chain(dve, sem("dve_step"), PER[n], before(n, "dve_step"))
                with dve.Fori(0, B) as i:
                    ch.turn(i)
                    dve.wait_ge(sem("staged"), before(n, "staged") + i + 1)
                    for j in range(2):
                        quantise(ch, xs[:, j, :], nq[:, j, :], KT[:, 2 * j, 0:P], j, 1, sem(f"{n}_dve2"))
                    ch.did(nc.vector.tensor_scalar(rsum[:, 0, :], rsum[:, 1, :], sums[:, 0, 0:1], None, ALU.mult))
                    ch.step(nc.vector.tensor_scalar(rsum[:, 2, :], rsum[:, 1, :], sums[:, 1, 0:1], None, ALU.mult))
                    dve.wait_ge(sem(f"{n}_dve2"), i * 4 + 2)
                    dve.sem_inc(sem(f"{n}_nq"), 1)
                    dve.wait_ge(sem(f"{n}_h_psum"), i + 1)
                    for j in range(2):
                        dve.wait_ge(sem(f"{n}_silu"), 2 * i + j + 1)
                        g = QT[:, 2 * j:2 * j + 2, :].rearrange("p a b -> p (a b)")
                        ch.step(nc.vector.scalar_tensor_tensor(g, PS[:, 2 * j + 1, :], rsum[:, 2, j:j + 1], g,
                                                               ALU.mult, ALU.mult))
                        quantise(ch, g, hq[:, j, :], KT[:, 2 * j:2 * j + 2, :].rearrange("p a b -> p (a b)"), j, 3,
                                 sem(f"{n}_dve2"))
                    ch.step(nc.vector.tensor_scalar(rsum[:, 4, :], rsum[:, 3, :], sums[:, 2, 0:1], None, ALU.mult))
                    dve.wait_ge(sem(f"{n}_dve2"), i * 4 + 4)
                    dve.sem_inc(sem(f"{n}_hq"), 1)
                    dve.wait_ge(sem("y"), before(n, "y") + i + 1)
                    for j in range(2):
                        ch.did(nc.vector.scalar_tensor_tensor(res[:, j, :], PS[:, PB[1], j * P:(j + 1) * P],
                                                              rsum[:, 4, j:j + 1], xs[:, j, :], ALU.mult, ALU.add))
                    ch.wait()
                    layernorm(n, i, ch, None)
                    ch.end()

            own = {"L0f": L0f, "L1f": L1f, "L2a": L2a, "L2f": L2f, "L3a": L3a, "L3f": L3f}
            for s in STAGES:
                if s in own:
                    own[s]()
                else:
                    prepare(s)
                    ch = Chain(dve, sem("dve_step"), PER[s], before(s, "dve_step"))
                    with dve.Fori(0, B) as i:
                        ch.turn(i)
                        attention(ATTNS[s], i, ch)
                        ch.end()


def pack(inputs):
    import numpy as np
    f = {k: np.asarray(v) for k, v in inputs.items()}
    out = np.zeros((P, NCOL), np.float32)

    def put(name, a, rows=P):
        at, n, _ = COLS[name]
        out[0:rows, at:at + n] = a.reshape(rows, n)

    def rep(name, a):
        at, n, _ = COLS[name]
        out[:, at:at + n] = a.reshape(1, n)

    def spread(name, m, dim, rows=P):
        at, n, _ = COLS[name]
        view = out[0:rows, at:at + n].reshape(rows, 4, 4, 32)
        for term in range(3):
            view[:, :, :, TERM * term:TERM * term + dim] = m.reshape(rows, 4, 4, dim)
        out[0:rows, at:at + n] = view.reshape(rows, n)

    def spread_bias(name, v, dim):
        at, n, _ = COLS[name]
        t = np.zeros((4, 4, 32), np.float32)
        for term in range(3):
            t[:, :, TERM * term:TERM * term + dim] = v.reshape(4, 4, dim)
        if name.endswith("bk"):
            t[:, :, SHIFT_ROW:SHIFT_ROW + 2] = 1.0
        if name == "L3x_bq":
            t[:, :, MASK_ROW] = 1.0 / ATTNS["L3x"].scale
        out[:, at:at + n] = t.reshape(4, P).T

    put("ident", np.eye(P, dtype=np.float32))
    rep("w8", 8.0 - np.arange(E, dtype=np.float32))
    put("L0a_wq", f["L0_attn_w_q"])
    put("L0a_wk", f["L0_attn_w_k"])
    put("L0a_wv", f["L0_attn_w_v"])
    put("L0a_wo", f["L0_attn_w_o"])

    def xattn(n, wq, bq, wk, bk, wv, bv, wo, bo):
        spread(f"{n}_wq", wq, 8)
        spread(f"{n}_wk", wk, 8)
        spread_bias(f"{n}_bq", bq, 8)
        spread_bias(f"{n}_bk", bk, 8)
        put(f"{n}_wv", wv)
        rep(f"{n}_bv", bv)
        put(f"{n}_wo", wo)
        rep(f"{n}_bo", bo)
        if ATTNS[n].rope:
            def swap(m):
                return m.reshape(m.shape[:-1] + (64, 2))[..., ::-1].reshape(m.shape)
            spread(f"{n}_wqr", swap(wq), 8)
            spread(f"{n}_wkr", swap(wk), 8)
            spread_bias(f"{n}_bqr", swap(bq), 8)
            spread_bias(f"{n}_bkr", swap(bk), 8)

    xattn("L0x", f["L0_xattn_wq"].T, f["L0_xattn_bq"], f["L0_xattn_wk"].T, f["L0_xattn_bk"],
          f["L0_xattn_wv"].T, f["L0_xattn_bv"], f["L0_xattn_wo"].T, f["L0_xattn_bo"])
    xattn("L1x", f["L1_xattn_W_Q"], f["L1_xattn_b_Q"], f["L1_xattn_W_K"], f["L1_xattn_b_K"],
          f["L1_xattn_W_V"], f["L1_xattn_b_V"], f["L1_xattn_W_O"], f["L1_xattn_b_O"])
    xattn("L2x", f["L2_xattn_w_q"], f["L2_xattn_b_q"], f["L2_xattn_w_k"], f["L2_xattn_b_k"],
          f["L2_xattn_w_v"], f["L2_xattn_b_v"], f["L2_xattn_w_o"], f["L2_xattn_b_o"])
    xattn("L3x", f["L3_xattn_Wq"].T, f["L3_xattn_bq"], f["L3_xattn_Wk"].T, f["L3_xattn_bk"],
          f["L3_xattn_Wv"].T, f["L3_xattn_bv"], f["L3_xattn_Wo"].T, f["L3_xattn_bo"])
    d = np.arange(P) % 32
    put("lo_q", (d // TERM == 2).astype(np.float32))
    put("sign_q", np.where(d // TERM == 2, -1.0, 1.0).astype(np.float32))
    put("lo_k", (d // TERM == 1).astype(np.float32))
    put("sign_k", np.where(d // TERM == 1, -1.0, 1.0).astype(np.float32))
    put("row_mask", (d == MASK_ROW).astype(np.float32))
    put("row_one", (d >= SHIFT_ROW).astype(np.float32))
    fr = (10000.0 ** (-(np.arange(4, dtype=np.float32) * 2.0) / 8)).astype(np.float32)
    put("L2x_freq", np.where(d < SHIFT_ROW, fr[(d // 2) % 4], 0).astype(np.float32))
    put("L2x_sign", np.where(d % 2 == 0, -1.0, 1.0).astype(np.float32))

    for what, src in (("q", "L1_attn_w_aq"), ("k", "L1_attn_w_ak")):
        m = f[src]
        put(f"L1a_w{what}", m)
        put(f"L1a_w{what}r", np.concatenate([m[:, :, 64:], m[:, :, :64]], axis=2))
    put("L1a_wv", f["L1_attn_w_av"])
    put("L1a_wo", f["L1_attn_w_ao"].transpose(1, 0, 2))
    ang = (np.arange(S, dtype=np.float32)[None, :] *
           np.power(np.float32(10000.0), -np.arange(64, dtype=np.float32) / 64)[:, None])
    put("L1a_cos", np.concatenate([np.cos(ang)] * 2).astype(np.float32))
    put("L1a_sin", np.concatenate([-np.sin(ang), np.sin(ang)]).astype(np.float32))

    put("L0f_wg", f["L0_ffn_Wg"])
    put("L0f_w1", f["L0_ffn_W1"].transpose(1, 0, 2))
    put("L0f_b1", f["L0_ffn_b1"].reshape(E, 4, P).transpose(2, 0, 1))
    put("L0f_w2", f["L0_ffn_W2"].reshape(E, 4, P, D).transpose(2, 0, 1, 3))
    put("L0f_b2", f["L0_ffn_b2"], rows=E)

    put("L2a_win", f["L2_attn_W_in"])
    put("L2a_bin", f["L2_attn_b_in"], rows=32)
    put("L2a_wdt1", f["L2_attn_W_dt1"])
    put("L2a_bdt1", f["L2_attn_b_dt1"], rows=64)
    put("L2a_wdt2", f["L2_attn_W_dt2"], rows=64)
    put("L2a_bdt2", f["L2_attn_b_dt2"])
    put("L2a_A", f["L2_attn_A"])
    put("L2a_D", f["L2_attn_D"])

    spread("L2f_wq", f["L2_ffn_q_w"].reshape(D, 16, 8)[:, :, :4], 4)
    spread_bias("L2f_bq", f["L2_ffn_q_b"].reshape(16, 8)[:, :4], 4)
    spread("L2f_wk", f["L2_ffn_k_w"], 4)
    spread_bias("L2f_bk", f["L2_ffn_k_b"], 4)
    put("L2f_wv", f["L2_ffn_v_w"])
    rep("L2f_bv", f["L2_ffn_v_b"])
    put("L2f_wo", f["L2_ffn_o_w"])
    put("L2f_ob", f["L2_ffn_o_b"])
    put("L2f_wr", f["L2_ffn_router_w"])
    rep("L2f_br", f["L2_ffn_router_b"])
    put("L2f_w1", f["L2_ffn_w1"].transpose(1, 0, 2))
    put("L2f_b1", f["L2_ffn_b1"].reshape(E, 2, P).transpose(2, 0, 1))
    put("L2f_w2", f["L2_ffn_w2"].reshape(E, 2, P, D).transpose(2, 0, 1, 3))
    put("L2f_b2", f["L2_ffn_b2"], rows=E)

    gates = np.zeros((16, 8, 16, 8), np.float32)
    for h in range(16):
        gates[h, :, h, :] = f["L3_attn_grep_w"].T
    put("L3a_w", np.concatenate([f["L3_attn_q_w"].T, f["L3_attn_k_w"].T, f["L3_attn_v_w"].T,
                                 gates.reshape(P, P)], axis=1))
    rep("L3a_b", np.concatenate([f["L3_attn_q_b"], f["L3_attn_k_b"], f["L3_attn_v_b"]] + [f["L3_attn_grep_b"]] * 16))
    put("L3a_wo", f["L3_attn_out_w"].T)
    rep("L3a_bo", f["L3_attn_out_b"])
    rep("L3a_ga", f["L3_attn_grep_a"])
    delta = np.arange(-7, 8)
    rep("L3a_rel", f["L3_attn_rel_emb"][np.abs(delta) + 16 * (delta > 0)])

    put("L3f_wg", f["L3_ffn_w_gate"].T)
    put("L3f_wu", f["L3_ffn_w_up"].T)
    put("L3f_wd", f["L3_ffn_w_down"].T.reshape(4, P, D).transpose(1, 0, 2))
    return out


def kernel(**inputs):
    import numpy as np
    import concourse.bacc as bacc
    from concourse.bass_utils import run_bass_kernel_spmd

    f = {k: np.asarray(v) for k, v in inputs.items()}
    arrays = {
        "wpack": pack(inputs),
        "x": np.ascontiguousarray(f["x"].reshape(NT, P, D).transpose(1, 0, 2)),
        "ctx": np.ascontiguousarray(f["ctx_1024"].reshape(B * S, D).T),
        "mask": np.ascontiguousarray(f["mask_Bx1xSxS2_ik1"].reshape(NT, P, S).transpose(1, 0, 2)),
        "kmask": np.ascontiguousarray(f["mask_Bx1x1xS2_ff1"].reshape(1, B * S)),
        "pos": np.ascontiguousarray(f["pos_BxS2"].reshape(1, B * S)),
        "hdm": np.ascontiguousarray(f["L0_attn_head_dim_mask"].reshape(P, 1)),
        "wint": np.concatenate([f["L1_ffn_w_gate"].T, f["L1_ffn_w_up"].T,
                                f["L1_ffn_w_down"].T.reshape(3, P, P).transpose(1, 0, 2).reshape(P, 384)], axis=1),
    }
    nc = bacc.Bacc("TRN2", target_bir_lowering=False, num_devices=1)
    aps = [nc.dram_tensor(f"in_{k}", a.shape, mybir.dt.from_np(a.dtype), kind="ExternalInput").ap() for k, a in arrays.items()]
    out = nc.dram_tensor("y", (P, NT, D), F32, kind="ExternalOutput").ap()
    decoder(nc, *aps, out)
    r = run_bass_kernel_spmd(nc, [{f"in_{k}": a for k, a in arrays.items()}], core_ids=[0])
    y = r.results[0]["y"]
    return np.ascontiguousarray(y.transpose(1, 0, 2).reshape(B, S, D))
```

```python
from contextlib import ExitStack

import concourse.bass as bass
from concourse import mybir

F32 = mybir.dt.float32
BF16 = mybir.dt.bfloat16
F32R = mybir.dt.float32r
I32 = mybir.dt.int32
U32 = mybir.dt.uint32
ALU = mybir.AluOpType
ACT = mybir.ActivationFunctionType
AX = mybir.AxisListType

P = 128
B = 8
S = 256
D = 128
NT = B * S // P
BIG = 1.0e30
E = 8
CAPACITY = 256
CONSTS = 13
TERM = 8
SHIFT_ROW = 24
MASK_ROW = 26
MAGIC = 12582912.0


class Attn:

    def __init__(self, name, heads, dim, small, scale, bias=True, rope=None, causal=False, clip=False,
                 keymask=False, vcols=128, self_attn=False, tail=True):
        self.name, self.heads, self.dim, self.small, self.scale = name, heads, dim, small, scale
        self.bias, self.rope, self.causal, self.clip, self.keymask = bias, rope, causal, clip, keymask
        self.vcols, self.self_attn, self.tail = vcols, self_attn, tail
        self.turned_scores = small and not clip
        self.tiles = 4 if small else heads
        self.group = 2 if small else min(4, self.tiles)
        self.small = small

    def items(self):
        out = []
        for t in range(0, self.tiles, self.group):
            for w in "qk":
                out.append((w, t))
                if self.rope:
                    out.append((w + "r", t))
        return out

    def item_step(self, k):
        return 8 + (k if self.rope else 2 * k)


R8 = 1.0 / 8 ** 0.5
ATTNS = {
    "L0a": Attn("L0a", 1, 128, False, 1.0 / 128 ** 0.5, bias=False, self_attn=True),
    "L0x": Attn("L0x", 16, 8, True, R8, clip=True),
    "L1a": Attn("L1a", 8, 128, False, 1.0, bias=False, rope="half", causal=True, self_attn=True, vcols=1024),
    "L1x": Attn("L1x", 16, 8, True, R8),
    "L2x": Attn("L2x", 16, 8, True, R8, rope="pair", causal=True),
    "L2f": Attn("L2f", 16, 4, True, 0.5, self_attn=True, vcols=64, tail=False),
    "L3x": Attn("L3x", 16, 8, True, R8, keymask=True),
}


def weight_columns():
    cols, at = {}, [0]

    def add(group, name, n):
        cols[name] = (at[0], n, group)
        at[0] += n

    def attn(a):
        n = a.name
        for w in "qk":
            add(n, f"{n}_w{w}", a.tiles * 128)
            if a.bias:
                add(n, f"{n}_b{w}", a.tiles)
            if a.rope:
                add(n, f"{n}_w{w}r", a.tiles * 128)
                if a.bias:
                    add(n, f"{n}_b{w}r", a.tiles)
        add(n, f"{n}_wv", a.vcols)
        if a.bias:
            add(n, f"{n}_bv", a.vcols)
            add(n, f"{n}_bo", 128)
        add(n, f"{n}_wo", a.heads * 128 if n == "L1a" else 128)

    add("const", "ident", 128)
    add("const", "w8", E)
    add("const", "lo_q", 1)
    add("const", "sign_q", 1)
    add("const", "lo_k", 1)
    add("const", "sign_k", 1)
    add("const", "row_mask", 1)
    add("const", "row_one", 1)
    attn(ATTNS["L0a"])
    attn(ATTNS["L0x"])
    add("L0f", "L0f_wg", E)
    add("L0f", "L0f_w1", E * 512)
    add("L0f", "L0f_b1", E * 4)
    add("L0f", "L0f_w2", E * 4 * 128)
    add("L0f", "L0f_b2", 128)
    attn(ATTNS["L1a"])
    add("L1a", "L1a_cos", 256)
    add("L1a", "L1a_sin", 256)
    attn(ATTNS["L1x"])
    attn(ATTNS["L2x"])
    add("L2x", "L2x_freq", 1)
    add("L2x", "L2x_sign", 1)
    add("L2a", "L2a_win", 32)
    add("L2a", "L2a_bin", 1)
    add("L2a", "L2a_wdt1", 64)
    add("L2a", "L2a_bdt1", 1)
    add("L2a", "L2a_wdt2", 128)
    add("L2a", "L2a_bdt2", 1)
    add("L2a", "L2a_A", 16)
    add("L2a", "L2a_D", 1)
    attn(ATTNS["L2f"])
    add("L2f", "L2f_ob", 1)
    add("L2f", "L2f_wr", E)
    add("L2f", "L2f_br", E)
    add("L2f", "L2f_w1", E * 256)
    add("L2f", "L2f_b1", E * 2)
    add("L2f", "L2f_w2", E * 2 * 128)
    add("L2f", "L2f_b2", 128)
    add("L3a", "L3a_w", 512)
    add("L3a", "L3a_b", 512)
    add("L3a", "L3a_wo", 128)
    add("L3a", "L3a_bo", 128)
    add("L3a", "L3a_ga", 16)
    add("L3a", "L3a_rel", 15 * 16)
    attn(ATTNS["L3x"])
    add("L3f", "L3f_wg", 512)
    add("L3f", "L3f_wu", 512)
    add("L3f", "L3f_wd", 512)
    return cols, at[0]


COLS, NCOL = weight_columns()
ORDER = ["L0a", "L0x", "L0f", "L1a", "L1x", "L1f", "L2a", "L2x", "L2f", "L3a", "L3x", "L3f"]


def weight_places():
    span = {}
    for at, n, g in COLS.values():
        a, b = span.get(g, (at, at))
        span[g] = (min(a, at), max(b, at + n))
    size = {g: b - a for g, (a, b) in span.items()}
    width = [max(size.get(s, 0) for s in ORDER[k::2]) for k in range(2)]
    place = {"const": 0}
    for k, s in enumerate(ORDER):
        if s in size:
            place[s] = size["const"] + (k % 2) * width[0]
    return span, place, size["const"] + sum(width)


SPAN, PLACE, WIDTH = weight_places()


class Chain:

    def __init__(self, eng, sem, key, first=0):
        self.eng, self.sem, self.key, self.per, self.first, self.n = eng, sem, key, PER[key], first, 0

    def turn(self, i):
        self.base, self.n = self.first + i * self.per, 0

    def end(self):
        assert self.n == self.per, f"{self.key}: {self.n} steps, {self.per} stated"

    def did(self, ins):
        ins.then_inc(self.sem, 1)
        self.n += 1

    def wait(self):
        self.eng.wait_ge(self.sem, self.base + self.n)

    def step(self, ins):
        self.did(ins)
        self.wait()


STEPS = 20
TURN_X_STEP, V_STEP, OT_STEP, Y_STEP = 6, 7, 2, 3
STAGES = ORDER

PER = {"L0a": 7, "L1a": 18, "L0r": 43, "L0f": 6, "L1f": 6, "L2a": 36, "L3a": 7, "L3m": 111, "L3f": 40, "L3q": 10}
PER.update({"L0x_heads": 2, "L0x_front": 0, "L0x_tail": 8, "L1x_heads": 4, "L1x_front": 0, "L1x_tail": 8, "L2x_heads": 4, "L2x_front": 22, "L2x_tail": 8, "L2f_heads": 4, "L2f_front": 0, "L2f_tail": 33, "L3x_heads": 4, "L3x_front": 3, "L3x_tail": 8})


def counts(n):
    each = {"staged": 1}
    if n not in ("L3a", "L3f"):
        each.update(xT_psum=1, xT=1)
    if n[-1] != "r":
        each.update(var=1, rstd=1)
        if n in ATTNS and ATTNS[n].small:
            each.update({f"{part}_step": PER[f"{n}_{part}"] for part in ("heads", "front", "tail")})
        else:
            each.update(dve_step=PER[n])
        if n not in ("L0f", "L2f"):
            each.update(y=1)
    if n == "L3a":
        each.update(oT_psum=1, oT=1)
    if n in ATTNS:
        a = ATTNS[n]
        H, NI, NO = a.heads, len(a.items()), max(1, a.vcols // P)
        each.update(V_psum=1, V=1, item_psum=NI, item_a=(NI + 1) // 2, item_b=NI // 2, scores=H, max=H,
                    probs=H, values=H, on=H if a.vcols > 512 else 1, oT_psum=NO, oT=NO)
        if not a.turned_scores:
            each.update(turned=H, pt_a=(H + 1) // 2, pt_v=H // 2)
        if a.clip:
            each.update(clipped=H)
        if a.small:
            each.update(V_held=1, rounded=2, stack=2, outputs=a.tiles, outputs_psum=1)
            if a.tail:
                each.update(y_read=1)
        if a.keymask:
            each.update(masked=1)
        if a.turned_scores:
            each.update(shift=a.tiles, shift_psum=a.tiles, shifted=a.tiles, probs=H // 2, values=H // 2,
                        turned_scores=H // 2)
    return {role: B * c for role, c in each.items()}


def before(n, role):
    total = 0
    for s in STAGES:
        for part in (s + "r", s) if s in ("L0f", "L3a") else (s,):
            if part == n:
                return total
            total += counts(part).get(role, 0)
    raise KeyError(n)



def decoder(nc, wpack, x_in, ctx_in, mask_in, kmask_in, pos_in, hdm_in, wint_in, out):
    ctx = ExitStack()
    with ctx:
        def sb(name, shape, dt=F32):
            return ctx.enter_context(nc.sbuf_tensor(name, shape, dt))

        sems = {}

        def sem(name):
            if name not in sems:
                sems[name] = ctx.enter_context(nc.semaphore(name))
            return sems[name]

        W = sb("W", [P, WIDTH])
        x_tok = sb("x_tok", [P, NT, D])
        ctxT = sb("ctxT", [P, B * S])
        xs = sb("xs", [P, 2, D])
        cs = sb("cs", [P, S])
        xT = sb("xT", [P, S])
        QT = sb("QT", [P, 8, S])
        KT = sb("KT", [P, 8, S])
        QS = sb("QS", [P, 4, S], F32R)
        KS = sb("KS", [P, 4, S], F32R)
        V = sb("V", [P, 2, 1024])
        negmax = sb("negmax", [P, 16, 2])
        sums = sb("sums", [P, 16, 2])
        rsum = sb("rsum", [P, 16, 2])
        On = sb("On", [P, 2, 1024])
        OT = sb("OT", [P, 8, S])
        res = sb("res", [P, 2, D])
        stats = sb("stats", [P, 2, 6])
        mv = sb("mv", [P, 2, 2])
        veps = sb("veps", [P, 2])
        rstd = sb("rstd", [P, 2])
        mhalf = sb("mhalf", [P, 2])
        identb = sb("identb", [P, P], BF16)
        causal = sb("causal", [P, 2, S], BF16)
        onesb = sb("onesb", [P, P], BF16)
        onesf = sb("onesf", [P, P])
        tri = sb("tri", [P, P], BF16)
        SEL = sb("SEL", [96, 32, P], BF16)
        kmask = sb("kmask", [P, S])
        keep = sb("keep", [P, S])
        kbias = sb("kbias", [P, S])
        causalT = sb("causalT", [P, P], BF16)
        big = sb("big", [P, 8192])
        RT = big[:, 0:1024].rearrange("p (a b) -> p a b", a=4)
        PR = big[:, 1024:2560].rearrange("p (r a b) -> p r a b", r=3, a=2)
        SC = big[:, 2560:3584].rearrange("p (r a b) -> p r a b", r=2, a=2)
        PT = big[:, 3584:4608].rearrange("p (r a b) -> p r a b", r=2, a=2)
        PX = big[:, 1024:3072].rearrange("p (r a b) -> p r a b", r=2, a=2)
        VT = big[:, 5632:5888].rearrange("p (a b) -> p a b", a=2)
        SH = big[:, 4608:5632].rearrange("p (t j r c) -> p t j r c", t=4, j=2, r=4)
        wint = sb("wint", [P, 1152], I32)
        wdeq = big[:, 4096:5248]
        tern = sb("tern", [P, 3, 512], BF16)
        comb = sb("comb", [P, NT, E])
        combs = sb("combs", [P, 2, E])
        combT = sb("combT", [E, S])
        rt = sb("rt", [P, 6, NT, E])
        rts = sb("rts", [P, 6, NT])
        ohb = sb("ohb", [P, 2, NT, E], BF16)
        hdm_i = sb("hdm_i", [P, 1], I32)
        hdm = sb("hdm", [P, 1])
        mask_i = sb("mask_i", [P, 2, S], I32)
        cap = sb("cap", [P, 2, S])
        pos_i = sb("pos_i", [P, S], I32)
        rot = sb("rot", [P, 6, S])
        PS = ctx.enter_context(nc.psum_tensor("PS", [P, 8, 512], F32))
        SCB, PTB, OB, PB = (0, 1, 2), (3, 4), 5, (6, 7)
        MAXB, SHB, EXPB = (0, 1), 2, (3, 4)
        GA, GB = 0, 3

        x_done = sem("x_done")
        w_in = {g: sem(f"w_in_{g}") for g in SPAN}
        x_loaded, ctx_loaded, small_loaded = sem("x_loaded"), sem("ctx_loaded"), sem("small_loaded")
        consts, dve_consts = sem("consts"), sem("dve_consts")
        out_sent = sem("out_sent")

        def w(name, a=0, b=None, rows=P):
            at, n, g = COLS[name]
            at += PLACE[g] - SPAN[g][0]
            b = n if b is None else b
            return W[0:rows, at + a:at + b]

        ident = w("ident")

        def tile2(i, b=None):
            return x_tok[:, bass.ds(2 * i, 2), :]

        base = {s: 8 * k + 1 for k, s in enumerate(STAGES)}
        last_x = 8 * len(STAGES) + 1

        def hidden(e, c, chunks):
            return 4 * (e % 2) + c if chunks == 4 else 4 + 2 * (e % 2) + c

        block = ctx.enter_context(nc.Block())

        @block.sync
        def _(sp):
            sp.dma_start(x_tok[:, :, :], x_in).then_inc(x_loaded, 16)
            def load(g):
                if g in SPAN:
                    a, b = SPAN[g]
                    sp.dma_start(W[:, PLACE[g]:PLACE[g] + b - a], wpack[:, a:b]).then_inc(w_in[g], 16)

            load("const")
            load(STAGES[0])
            sp.dma_start(hdm_i[:, :], hdm_in).then_inc(small_loaded, 16)
            sp.dma_start(wint[:, :], wint_in).then_inc(small_loaded, 16)
            sp.dma_start(ctxT[:, :], ctx_in).then_inc(ctx_loaded, 16)
            for k, s in enumerate(STAGES):
                if k + 1 < len(STAGES):
                    sp.wait_ge(x_done, base[s])
                    load(STAGES[k + 1])
                tile = {"L0x": lambda i: (mask_i[:, :, :], mask_in[:, bass.ds(2 * i, 2), :], "mask_in"),
                        "L2x": lambda i: (pos_i[:, :], pos_in[:, bass.ds(i * S, S)].broadcast_to([P, S]), "pos_in"),
                        "L3x": lambda i: (kmask[:, :], kmask_in[:, bass.ds(i * S, S)].broadcast_to([P, S]), "kmask_in")}
                if s in tile:
                    dst, src, signal = tile[s](0)
                    sp.dma_start(dst, src).then_inc(sem(signal), 16)
                    with sp.Fori(1, B) as i:
                        dst, src, signal = tile[s](i)
                        sp.wait_ge(sem(f"{s}_tile_read"), i)
                        sp.dma_start(dst, src).then_inc(sem(signal), 16)
            sp.wait_ge(x_done, last_x)
            sp.dma_start(out, x_tok[:, :, :]).then_inc(out_sent, 16)
            sp.wait_ge(out_sent, 16)

        @block.gpsimd
        def _(pool):
            nc.gpsimd.memset(mhalf[:, :], -0.5).then_inc(consts, 1)
            nc.gpsimd.memset(onesb[:, :], 1.0).then_inc(consts, 1)
            nc.gpsimd.memset(causal[:, :, :], 0.0).then_inc(consts, 1)
            nc.gpsimd.memset(onesf[:, :], 1.0).then_inc(consts, 1)
            nc.gpsimd.memset(tri[:, :], 1.0).then_inc(consts, 1)
            nc.gpsimd.memset(SEL[:, :, :], 0.0).then_inc(consts, 1)
            pool.wait_ge(consts, 6)
            nc.gpsimd.affine_select(out=tri[:, :], in_=tri[:, :], compare_op=ALU.is_ge, fill=0.0,
                                    base=0, pattern=[[1, P]], channel_multiplier=-1).then_inc(consts, 1)
            for q in range(3):
                pool.wait_ge(consts, 7 + q)
                rows = SEL[32 * q:32 * q + 32, :, :]
                nc.gpsimd.affine_select(out=rows, in_=rows, compare_op=ALU.not_equal, fill=1.0,
                                        base=0, pattern=[[-1, 32], [0, P]], channel_multiplier=1).then_inc(consts, 1)
            pool.wait_ge(consts, 10)
            nc.gpsimd.affine_select(out=causal[:, :, :], in_=causal[:, :, :], compare_op=ALU.is_ge, fill=-BIG,
                                    base=0, pattern=[[128, 2], [-1, S]], channel_multiplier=1).then_inc(consts, 1)
            pool.wait_ge(consts, 11)
            nc.gpsimd.memset(causalT[:, :], 0.0).then_inc(consts, 1)
            pool.wait_ge(consts, 12)
            nc.gpsimd.affine_select(out=causalT[:, :], in_=causalT[:, :], compare_op=ALU.is_ge, fill=-BIG,
                                    base=0, pattern=[[1, P]], channel_multiplier=-1).then_inc(consts, 1)
            pool.wait_ge(consts, CONSTS)

            def inverse_root(s, i):
                pool.wait_ge(sem("var"), before(s, "var") + i + 1)
                nc.gpsimd.tensor_tensor(rstd[:, :], veps[:, :], mhalf[:, :], ALU.pow).then_inc(sem("rstd"), 1)

            def add_mask(s, i):
                nb = len(ATTNS[s].items()) // 2
                pool.wait_ge(sem("item_b"), before(s, "item_b") + (i + 1) * nb)
                nc.gpsimd.tensor_tensor(KT[:, 0:4, :], KT[:, 0:4, :], kbias[:, :].unsqueeze(1).broadcast_to([P, 4, S]),
                                        ALU.add).then_inc(sem("masked"), 1)

            for s in STAGES:
                if s == "L3x":
                    add_mask(s, 0)
                    add_mask(s, 1)
                    with pool.Fori(1, B - 1) as i:
                        inverse_root(s, i - 1)
                        add_mask(s, i + 1)
                    inverse_root(s, B - 2)
                    inverse_root(s, B - 1)
                else:
                    with pool.Fori(0, B) as i:
                        inverse_root(s, i)

        @block.tensor
        def _(pe):
            pe.wait_ge(w_in["const"], 16)
            pe.wait_ge(consts, CONSTS)
            pe.wait_ge(dve_consts, 1)

            def attention(a, i):
                n, H = a.name, a.heads
                items = a.items()
                NI = len(items)
                LAG = 2
                pe.wait_ge(w_in[n], 16)
                pe.wait_ge(sem("staged"), before(n, "staged") + i + 1)
                for j in range(2):
                    mm = nc.tensor.transpose(PS[:, PB[0], j * P:(j + 1) * P], xs[:, j, :], ident)
                mm.then_inc(sem("xT_psum"), 1)
                pe.wait_ge(sem("xT"), before(n, "xT") + i + 1)
                src = xT if a.self_attn else cs
                for j in range(2):
                    for c in range(0, a.vcols, 512):
                        c1 = min(c + 512, a.vcols)
                        bank, at = (PB[1], j * a.vcols) if a.vcols <= 256 else ((5, 6, 7, 2)[2 * j + c // 512], 0)
                        mm = nc.tensor.matmul(PS[:, bank, at:at + c1 - c], src[:, j * P:(j + 1) * P],
                                              w(f"{n}_wv", c, c1), start=True, stop=True)
                mm.then_inc(sem("V_psum"), 1)
                for k, (what, t0) in enumerate(items):
                    if k >= 2:
                        role = "item_a" if k % 2 == 0 else "item_b"
                        pe.wait_ge(sem(role), before(n, role) + i * ((NI + 1 - k % 2) // 2) + k // 2)
                    rhs = src if what[0] == "k" else xT
                    for t in range(a.group):
                        g = (GA, GB)[k % 2]
                        mm = nc.tensor.matmul(PS[:, g + t // 2, (t % 2) * S:(t % 2 + 1) * S],
                                              w(f"{n}_w{what}", (t0 + t) * P, (t0 + t + 1) * P), rhs[:, :],
                                              start=True, stop=True)
                    mm.then_inc(sem("item_psum"), 1)

                def pt(h):
                    return "pt_v" if h % 2 else "pt_a"

                def half(h):
                    return H // 2 if h % 2 else (H + 1) // 2

                def scores(h):
                    if h >= len(SCB):
                        pe.wait_ge(sem("probs"), before(n, "probs") + i * H + h - len(SCB) + 1)
                    bank = SCB[h % len(SCB)]
                    for j in range(2):
                        o = PS[:, bank, j * S:(j + 1) * S]
                        mm = nc.tensor.matmul(o, QT[:, h, j * P:(j + 1) * P], KT[:, h, :],
                                              start=True, stop=not a.causal)
                        if a.causal:
                            mm = nc.tensor.matmul(o, identb[:, :], causal[:, j, :], start=False, stop=True)
                    mm.then_inc(sem("scores"), 1)

                def turn(h):
                    pe.wait_ge(sem("probs"), before(n, "probs") + i * H + h + 1)
                    if h >= 2:
                        pe.wait_ge(sem(pt(h)), before(n, pt(h)) + i * half(h) + h // 2)
                    for kb in range(2):
                        for j in range(2):
                            mm = nc.tensor.transpose(PS[:, PTB[h % 2], kb * S + j * P:kb * S + (j + 1) * P],
                                                     PR[:, h % 3, j, kb * P:(kb + 1) * P], ident)
                    mm.then_inc(sem("turned"), 1)

                def values(h):
                    pe.wait_ge(sem(pt(h)), before(n, pt(h)) + i * half(h) + h // 2 + 1)
                    dv = a.vcols // H
                    for j in range(2):
                        if a.vcols > 512:
                            o = PS[:, (5, 6, 7, 5, 6, 7, 5, 6)[h], j * dv:(j + 1) * dv]
                            if h >= 3 and j == 0:
                                pe.wait_ge(sem("on"), before(n, "on") + i * H + h - 2)
                        else:
                            o = PS[:, OB, j * a.vcols + h * dv:j * a.vcols + (h + 1) * dv]
                        for kb in range(2):
                            mm = nc.tensor.matmul(o, PT[:, h % 2, kb, j * P:(j + 1) * P],
                                                  V[:, kb, h * dv:(h + 1) * dv], start=kb == 0, stop=kb == 1)
                    mm.then_inc(sem("values"), 1)

                pe.wait_ge(sem("item_a"), before(n, "item_a") + (i + 1) * ((NI + 1) // 2))
                pe.wait_ge(sem("item_b"), before(n, "item_b") + (i + 1) * (NI // 2))
                pe.wait_ge(sem("V"), before(n, "V") + i + 1)
                for h in range(H + LAG + 1):
                    if h < H:
                        scores(h)
                    if LAG <= h < H + LAG:
                        turn(h - LAG)
                    if h > LAG:
                        values(h - LAG - 1)
                NO = max(1, a.vcols // P)
                if a.vcols > 512:
                    for k in range(NO):
                        pe.wait_ge(sem("on"), before(n, "on") + i * H + k + 1)
                        if k >= 2:
                            pe.wait_ge(sem("oT"), before(n, "oT") + i * NO + k - 1)
                        for j in range(2):
                            mm = nc.tensor.transpose(PS[:, PTB[k % 2], j * P:(j + 1) * P],
                                                     On[:, j, k * P:(k + 1) * P], ident)
                        mm.then_inc(sem("oT_psum"), 1)
                else:
                    pe.wait_ge(sem("on"), before(n, "on") + i + 1)
                    for j in range(2):
                        mm = nc.tensor.transpose(PS[:, PTB[0], j * P:(j + 1) * P], On[:, j, 0:P], ident)
                    mm.then_inc(sem("oT_psum"), 1)
                pe.wait_ge(sem("oT"), before(n, "oT") + (i + 1) * NO)
                for j in range(2):
                    for k in range(NO):
                        mm = nc.tensor.matmul(PS[:, PB[0], j * P:(j + 1) * P], OT[:, k, j * P:(j + 1) * P],
                                              w(f"{n}_wo", k * P, (k + 1) * P), start=k == 0, stop=k == NO - 1)
                mm.then_inc(sem("y"), 1)

            def small_front(a, b, s, tails):
                n, items = a.name, a.items()
                NI = len(items)
                src = xT if a.self_attn else cs
                if s == TURN_X_STEP:
                    if not tails:
                        pe.wait_ge(w_in[n], 16)
                    if tails and not a.tail:
                        pe.wait_ge(x_done, base[n] + b - 1)
                    pe.wait_ge(sem("staged"), before(n, "staged") + b + 1)
                    for j in range(2):
                        mm = nc.tensor.transpose(PS[:, PB[0], j * P:(j + 1) * P], xs[:, j, :], ident)
                    mm.then_inc(sem("xT_psum"), 1)
                if s == V_STEP:
                    pe.wait_ge(sem("xT"), before(n, "xT") + b + 1)
                    if tails and a.tail:
                        pe.wait_ge(sem("y_read"), before(n, "y_read") + b - 1)
                    for j in range(2):
                        mm = nc.tensor.matmul(PS[:, PB[1], j * a.vcols:(j + 1) * a.vcols], src[:, j * P:(j + 1) * P],
                                              w(f"{n}_wv"), start=True, stop=True)
                    mm.then_inc(sem("V_psum"), 1)
                for k, (what, t0) in enumerate(items):
                    if s != a.item_step(k):
                        continue
                    if k == 1:
                        pe.wait_ge(sem("V_held"), before(n, "V_held") + b + 1)
                    if k >= 2:
                        role = "item_b" if k % 2 else "item_a"
                        pe.wait_ge(sem(role), before(n, role) + b * (NI // 2) + k // 2)
                    rhs = src if what[0] == "k" else xT
                    for t in range(2):
                        mm = nc.tensor.matmul(PS[:, PB[k % 2], t * S:(t + 1) * S],
                                              w(f"{n}_w{what}", (t0 + t) * P, (t0 + t + 1) * P), rhs[:, :],
                                              start=True, stop=True)
                    mm.then_inc(sem("item_psum"), 1)

            def small_tail(a, i, s):
                n, rows = a.name, min(P, a.vcols)
                if s == OT_STEP:
                    pe.wait_ge(sem("on"), before(n, "on") + i + 1)
                    if rows < P:
                        pe.sem_inc(sem("on_passed"), 1)
                    for j in range(2):
                        mm = nc.tensor.transpose(PS[0:rows, PB[0], j * P:(j + 1) * P], On[:, j, 0:rows], ident)
                    mm.then_inc(sem("oT_psum"), 1)
                if s == Y_STEP:
                    pe.wait_ge(sem("oT"), before(n, "oT") + i + 1)
                    for j in range(2):
                        mm = nc.tensor.matmul(PS[:, PB[1], j * P:(j + 1) * P], OT[:, 0, j * P:(j + 1) * P],
                                              w(f"{n}_wo"), start=True, stop=True)
                    mm.then_inc(sem("y"), 1)

            def small_batch(a, i, first, last):
                n, H, T = a.name, a.heads, a.tiles
                NV = H // 2 if a.turned_scores else H

                def scores(h):
                    r, t = slice(32 * (h % 4), 32 * (h % 4) + 32), h // 4
                    ring = SCB if a.clip else MAXB
                    if h >= len(ring):
                        role = "clipped" if a.clip else "max"
                        pe.wait_ge(sem(role), before(n, role) + i * H + h - len(ring) + 1)
                    for j in range(2):
                        o = PS[:, ring[h % len(ring)], j * S:(j + 1) * S]
                        mm = nc.tensor.matmul(o, QS[r, t, j * P:(j + 1) * P], KS[r, t, :],
                                              start=True, stop=not a.causal)
                        if a.causal:
                            mm = nc.tensor.matmul(o, identb[:, :], causal[:, j, :], start=False, stop=True)
                    mm.then_inc(sem("scores"), 1)

                def turn(h):
                    pt = "pt_v" if h % 2 else "pt_a"
                    pe.wait_ge(sem("probs"), before(n, "probs") + i * H + h + 1)
                    if h >= 2:
                        pe.wait_ge(sem(pt), before(n, pt) + i * (H // 2) + h // 2)
                    for kb in range(2):
                        for j in range(2):
                            mm = nc.tensor.transpose(PS[:, PTB[h % 2], kb * S + j * P:kb * S + (j + 1) * P],
                                                     PR[:, h % 3, j, kb * P:(kb + 1) * P], ident)
                    mm.then_inc(sem("turned"), 1)

                def shift(t):
                    pe.wait_ge(sem("shift"), before(n, "shift") + i * T + t + 1)
                    if t >= 1:
                        pe.wait_ge(sem("shifted"), before(n, "shifted") + i * T + t)
                    for j in range(2):
                        mm = nc.tensor.transpose(PS[:, SHB, j * P:(j + 1) * P],
                                                 SH[:, t, j, :, :].rearrange("p r c -> p (r c)"), ident)
                    mm.then_inc(sem("shift_psum"), 1)

                def turned_scores(p):
                    t = p // 2
                    if p % 2 == 0:
                        pe.wait_ge(sem("shifted"), before(n, "shifted") + i * T + t + 1)
                    if p >= 1:
                        pe.wait_ge(sem("probs"), before(n, "probs") + i * (H // 2) + p)
                    for half in range(2):
                        h = 2 * p + half
                        r, bank = slice(32 * (h % 4), 32 * (h % 4) + 32), EXPB[half]
                        if a.causal:
                            nc.tensor.matmul(PS[:, bank, P:S], KS[r, t, 0:P], QS[r, t, P:S], start=True, stop=True)
                            for kb in range(2):
                                o = PS[:, bank, 2 * kb * P:(2 * kb + 1) * P]
                                nc.tensor.matmul(o, KS[r, t, kb * P:(kb + 1) * P], QS[r, t, kb * P:(kb + 1) * P],
                                                 start=True, stop=False)
                                mm = nc.tensor.matmul(o, identb[:, :], causalT[:, :], start=False, stop=True)
                        else:
                            for kb in range(2):
                                mm = nc.tensor.matmul(PS[:, bank, kb * S:(kb + 1) * S], KS[r, t, kb * P:(kb + 1) * P],
                                                      QS[r, t, :], start=True, stop=True)
                    mm.then_inc(sem("turned_scores"), 1)

                def head_values(h, px):
                    r, v = slice(32 * (h % 4), 32 * (h % 4) + 32), slice(32 * h, 32 * h + 32)
                    if h == 0:
                        pe.wait_ge(sem("V"), before(n, "V") + i + 1)
                        if not a.tail and not first:
                            pe.wait_ge(x_done, base[n] + i)
                    if h % 4 == 0 and h >= 4:
                        pe.wait_ge(sem("outputs"), before(n, "outputs") + i * T + h // 4)
                    if a.causal:
                        nc.tensor.matmul(PS[r, OB, 0:P], V[:, 0, v], px[:, 0:P], start=True, stop=True)
                        nc.tensor.matmul(PS[r, OB, P:S], V[:, 0, v], px[:, P:S], start=True, stop=False)
                        return nc.tensor.matmul(PS[r, OB, P:S], V[:, 1, v], px[:, S:S + P], start=False, stop=True)
                    nc.tensor.matmul(PS[r, OB, 0:S], V[:, 0, v], px[:, 0:S], start=True, stop=False)
                    return nc.tensor.matmul(PS[r, OB, 0:S], V[:, 1, v], px[:, S:2 * S], start=False, stop=True)

                def values(p):
                    if a.turned_scores:
                        pe.wait_ge(sem("probs"), before(n, "probs") + i * NV + p + 1)
                        head_values(2 * p, PX[:, p % 2, 0, :])
                        mm = head_values(2 * p + 1, PX[:, p % 2, 1, :])
                    else:
                        pt = "pt_v" if p % 2 else "pt_a"
                        pe.wait_ge(sem(pt), before(n, pt) + i * (H // 2) + p // 2 + 1)
                        mm = head_values(p, PT[:, p % 2, :, :].rearrange("p a b -> p (a b)"))
                    mm.then_inc(sem("values"), 1)

                pe.wait_ge(sem("stack"), before(n, "stack") + 2 * i + 2)
                for s in range(STEPS):
                    if s < H:
                        scores(s)
                    if a.turned_scores:
                        t, r = s // 4 - 1, s % 4
                        if t >= 0 and r == 0:
                            shift(t)
                        if t >= 0 and r % 2:
                            p = 2 * t + r // 2
                            turned_scores(p)
                            if p >= 1:
                                values(p - 1)
                    else:
                        if 2 <= s < H + 2:
                            turn(s - 2)
                        if 3 <= s < H + 3:
                            values(s - 3)
                    if not first and a.tail:
                        small_tail(a, i - 1, s)
                    if not last:
                        small_front(a, i + 1, s, not first)
                if a.turned_scores:
                    values(H // 2 - 1)
                for t in range(T):
                    pe.wait_ge(sem("outputs"), before(n, "outputs") + i * T + t + 1)
                    for j in range(2):
                        mm = nc.tensor.transpose(PS[:, EXPB[0] + j, t * P:(t + 1) * P],
                                                 OT[:, 4 + t, j * P:(j + 1) * P], ident)
                mm.then_inc(sem("outputs_psum"), 1)

            def small_stage(a):
                for s in range(STEPS):
                    small_front(a, 0, s, False)
                small_batch(a, 0, True, False)
                with pe.Fori(1, B - 1) as i:
                    small_batch(a, i, False, False)
                small_batch(a, B - 1, False, True)
                for s in (OT_STEP, Y_STEP):
                    small_tail(a, B - 1, s)

            def turn_x(n, i):
                pe.wait_ge(sem("staged"), before(n, "staged") + i + 1)
                for j in range(2):
                    mm = nc.tensor.transpose(PS[:, PB[0], j * P:(j + 1) * P], xs[:, j, :], ident)
                mm.then_inc(sem("xT_psum"), 1)
                pe.wait_ge(sem("xT"), before(n, "xT") + i + 1)

            def experts(n, i, src, chunks):
                HB, YB = (GA, GB), (5, 7)
                for e in range(E + 1):
                    if e < E:
                        if e >= 2:
                            pe.wait_ge(sem(f"{n}_h"), i * E + e - 1)
                        for c in range(chunks):
                            mm = nc.tensor.matmul(PS[:, HB[e % 2] + c // 2, (c % 2) * S:(c % 2 + 1) * S],
                                                  w(f"{n}_w1", (e * chunks + c) * P, (e * chunks + c + 1) * P),
                                                  src[:, :], start=True, stop=True)
                        mm.then_inc(sem(f"{n}_h_psum"), 1)
                    if e >= 1:
                        g = e - 1
                        pe.wait_ge(sem(f"{n}_h"), i * E + g + 1)
                        if g >= 2:
                            pe.wait_ge(sem(f"{n}_acc"), i * E + g - 1)
                        for j in range(2):
                            for c in range(chunks):
                                mm = nc.tensor.matmul(PS[:, YB[g % 2], j * P:(j + 1) * P],
                                                      QT[:, hidden(g, c, chunks), j * P:(j + 1) * P],
                                                      w(f"{n}_w2", (g * chunks + c) * P, (g * chunks + c + 1) * P),
                                                      start=c == 0, stop=c == chunks - 1)
                        mm.then_inc(sem(f"{n}_ye"), 1)
                pe.wait_ge(sem(f"{n}_combs"), i + 1)
                for j in range(2):
                    mm = nc.tensor.transpose(PS[0:E, 2, j * P:(j + 1) * P], combs[:, j, :], ident)
                mm.then_inc(sem(f"{n}_combT_psum"), 1)
                pe.wait_ge(sem(f"{n}_combT"), i + 1)
                for j in range(2):
                    mm = nc.tensor.matmul(PS[:, PB[0], j * P:(j + 1) * P], combT[:, j * P:(j + 1) * P],
                                          w(f"{n}_b2", rows=E), start=True, stop=True)
                mm.then_inc(sem(f"{n}_yb"), 1)

            def L0f():
                n = "L0f"
                pe.wait_ge(w_in[n], 16)
                with pe.Fori(0, B) as i:
                    turn_x(n + "r", i)
                    for j in range(2):
                        mm = nc.tensor.matmul(PS[:, PB[1], j * E:(j + 1) * E], xT[:, j * P:(j + 1) * P],
                                              w(f"{n}_wg"), start=True, stop=True)
                    mm.then_inc(sem(f"{n}_lg_psum"), 1)
                pe.wait_ge(sem(f"{n}_onehots"), 1)
                for k in range(2):
                    nc.tensor.matmul(PS[:, 0, k * P:(k + 1) * P], tri[:, :],
                                     ohb[:, k, :, :].rearrange("p t e -> p (t e)"), start=True, stop=True)
                    mm = nc.tensor.matmul(PS[:, 1, k * P:(k + 1) * P], onesb[:, :],
                                          ohb[:, k, :, :].rearrange("p t e -> p (t e)"), start=True, stop=True)
                mm.then_inc(sem(f"{n}_counts"), 1)
                pe.wait_ge(sem(f"{n}_routed"), 1)
                with pe.Fori(0, B) as i:
                    turn_x(n, i)
                    experts(n, i, xT, 4)

            def L2f():
                n = "L2f"
                a = ATTNS[n]

                def batch(i, first, last):
                    small_batch(a, i, first, last)
                    if not last:
                        for role in ("item_a", "item_b"):
                            pe.wait_ge(sem(role), before(n, role) + (i + 2) * (len(a.items()) // 2))
                    small_tail(a, i, OT_STEP)
                    pe.wait_ge(sem("oT"), before(n, "oT") + i + 1)
                    nc.tensor.matmul(PS[:, PB[1], 0:S], w(f"{n}_wo", rows=64), OT[0:64, 0, :],
                                     start=True, stop=True).then_inc(sem(f"{n}_mla_psum"), 1)
                    pe.wait_ge(sem(f"{n}_mla"), i + 1)
                    for j in range(2):
                        mm = nc.tensor.matmul(PS[:, PB[1], j * E:(j + 1) * E], OT[:, 1, j * P:(j + 1) * P],
                                              w(f"{n}_wr"), start=True, stop=True)
                    mm.then_inc(sem(f"{n}_lg_psum"), 1)
                    pe.wait_ge(sem(f"{n}_lg"), i + 1)
                    experts(n, i, OT[:, 1, :], 2)

                for s in range(STEPS):
                    small_front(a, 0, s, False)
                batch(0, True, False)
                with pe.Fori(1, B - 1) as i:
                    batch(i, False, False)
                batch(B - 1, False, True)

            def L1f():
                n = "L1f"
                pe.wait_ge(sem("wdeq_ready"), 1)
                with pe.Fori(0, B) as i:
                    turn_x(n, i)
                    for k, bank in enumerate((GA, GB)):
                        for c in range(3):
                            at = k * 384 + c * P
                            mm = nc.tensor.matmul(PS[:, bank + c // 2, (c % 2) * S:(c % 2 + 1) * S],
                                                  wdeq[:, at:at + P], xT[:, :], start=True, stop=True)
                        mm.then_inc(sem(f"{n}_h_psum"), 1)
                    pe.wait_ge(sem(f"{n}_h"), i + 1)
                    for j in range(2):
                        for c in range(3):
                            mm = nc.tensor.matmul(PS[:, PB[0], j * P:(j + 1) * P], QT[:, 3 + c, j * P:(j + 1) * P],
                                                  wdeq[:, 768 + c * P:896 + c * P], start=c == 0, stop=c == 2)
                    mm.then_inc(sem("y"), 1)

            def L2a():
                n = "L2a"
                stk = OT[0:96, 2, 0:P].bitcast(BF16)
                pe.wait_ge(w_in[n], 16)
                with pe.Fori(0, B) as i:
                    turn_x(n, i)
                    nc.tensor.matmul(PS[0:32, 0, 0:S], w(f"{n}_win"), xT[:, :], start=True, stop=True)\
                      .then_inc(sem(f"{n}_bc_psum"), 1)
                    nc.tensor.matmul(PS[0:64, 1, 0:S], w(f"{n}_wdt1"), xT[:, :], start=True, stop=True)\
                      .then_inc(sem(f"{n}_dt_psum"), 1)
                    pe.wait_ge(sem(f"{n}_dt1"), i + 1)
                    nc.tensor.matmul(PS[:, 2, 0:S], w(f"{n}_wdt2", rows=64), OT[0:64, 0, :], start=True, stop=True)\
                      .then_inc(sem(f"{n}_dt_psum"), 1)
                    pe.wait_ge(sem(f"{n}_stack"), i + 1)
                    for half in range(2):
                        if half:
                            pe.wait_ge(sem(f"{n}_g"), i * 2 + 1)
                        else:
                            pe.wait_ge(sem(f"{n}_z"), i + 1)
                        for k in range(8):
                            mm = nc.tensor.matmul(PS[:, k // 2, (k % 2) * S:(k % 2 + 1) * S],
                                                  SEL[:, half * 8 + k, :], stk, start=True, stop=True)
                        mm.then_inc(sem(f"{n}_B"), 1)
                        if half:
                            pe.wait_ge(sem(f"{n}_hc"), i * 2 + 1)
                        for k in range(8):
                            mm = nc.tensor.matmul(PS[:, 4 + k // 2, (k % 2) * S:(k % 2 + 1) * S],
                                                  SEL[:, 16 + half * 8 + k, :], stk, start=True, stop=True)
                        mm.then_inc(sem(f"{n}_C"), 1)
                    pe.wait_ge(sem(f"{n}_ysum"), i + 1)
                    for j in range(2):
                        mm = nc.tensor.transpose(PS[:, PB[0], j * P:(j + 1) * P], OT[:, 5, j * P:(j + 1) * P], ident)
                    mm.then_inc(sem("y"), 1)

            def L3a():
                n = "L3a"
                pe.wait_ge(w_in[n], 16)
                with pe.Fori(0, B) as i:
                    turn_x(n + "r", i)
                    for j in range(2):
                        mm = nc.tensor.matmul(PS[:, j, :], xT[:, j * P:(j + 1) * P], w(f"{n}_w"), start=True, stop=True)
                    mm.then_inc(sem(f"{n}_qkvg_psum"), 1)
                    pe.wait_ge(sem(f"{n}_qkvg"), i + 1)
                with pe.Fori(0, B) as i:
                    pe.wait_ge(sem("staged"), before(n, "staged") + i + 1)
                    for j in range(2):
                        mm = nc.tensor.transpose(PS[:, PTB[0], j * P:(j + 1) * P], On[:, j, 0:P], ident)
                    mm.then_inc(sem("oT_psum"), 1)
                    pe.wait_ge(sem("oT"), before(n, "oT") + i + 1)
                    for j in range(2):
                        mm = nc.tensor.matmul(PS[:, PB[0], j * P:(j + 1) * P], OT[:, 0, j * P:(j + 1) * P],
                                              w(f"{n}_wo"), start=True, stop=True)
                    mm.then_inc(sem("y"), 1)

            def L3f():
                n = "L3f"
                pe.wait_ge(sem(f"{n}_wsum"), 1)
                nc.tensor.matmul(PS[:, 0, 0:3], onesf[:, :], mv[:, :, :].rearrange("p a b -> p (a b)")[:, 0:3],
                                 start=True, stop=True).then_inc(sem(f"{n}_wmean_psum"), 1)
                pe.wait_ge(sem(f"{n}_tern"), 1)
                nT = OT[:, 0, :].bitcast(BF16)
                mT = OT[:, 4:8, :].rearrange("p a b -> p (a b)").bitcast(BF16)
                nq = On[:, :, 0:64].bitcast(BF16)
                hq = On[:, :, 128:384].bitcast(BF16)
                idb = identb[:, :]
                with pe.Fori(0, B) as i:
                    pe.wait_ge(sem(f"{n}_nq"), i + 1)
                    for j in range(2):
                        mm = nc.tensor.transpose(PS[:, PB[0], :].bitcast(BF16)[:, j * P:(j + 1) * P], nq[:, j, :], idb)
                    mm.then_inc(sem(f"{n}_nT_psum"), 1)
                    pe.wait_ge(sem(f"{n}_nT"), i + 1)
                    for j in range(2):
                        for k in range(2):
                            mm = nc.tensor.matmul(PS[:, 2 * j + k, :], nT[:, j * P:(j + 1) * P], tern[:, k, :],
                                                  start=True, stop=True)
                    mm.then_inc(sem(f"{n}_h_psum"), 1)
                    pe.wait_ge(sem(f"{n}_hq"), i + 1)
                    for j in range(2):
                        for c in range(4):
                            mm = nc.tensor.transpose(PS[:, 4 + j, :].bitcast(BF16)[:, c * P:(c + 1) * P],
                                                     hq[:, j, c * P:(c + 1) * P], idb)
                    mm.then_inc(sem(f"{n}_mT_psum"), 1)
                    pe.wait_ge(sem(f"{n}_mT"), i + 1)
                    for j in range(2):
                        for c in range(4):
                            mm = nc.tensor.matmul(PS[:, PB[1], j * P:(j + 1) * P],
                                                  mT[:, (4 * j + c) * P:(4 * j + c + 1) * P],
                                                  tern[:, 2, c * P:(c + 1) * P], start=c == 0, stop=c == 3)
                    mm.then_inc(sem("y"), 1)

            own = {"L0f": L0f, "L1f": L1f, "L2a": L2a, "L2f": L2f, "L3a": L3a, "L3f": L3f}
            for s in STAGES:
                if s in own:
                    own[s]()
                elif ATTNS[s].small:
                    small_stage(ATTNS[s])
                else:
                    with pe.Fori(0, B) as i:
                        attention(ATTNS[s], i)

        @block.scalar
        def _(act):
            def attention(a, i):
                n, H = a.name, a.heads
                items = a.items()
                NI = len(items)
                act.wait_ge(w_in[n], 16)
                if n == "L0a":
                    act.wait_ge(sem("hdm_ready"), 1)
                act.wait_ge(x_done, i + base[n])
                nc.scalar.copy(xs[:, :, :], tile2(i)).then_inc(sem("staged"), 1)
                act.wait_ge(sem("xT_psum"), before(n, "xT_psum") + i + 1)
                nc.scalar.copy(xT[:, :], PS[:, PB[0], 0:S]).then_inc(sem("xT"), 1)
                for k, (what, t0) in enumerate(items):
                    if k % 2 and not a.rope:
                        act.wait_ge(sem("item_psum"), before(n, "item_psum") + i * NI + k + 1)
                        for t in range(a.group):
                            src = PS[:, GB + t // 2, (t % 2) * S:(t % 2 + 1) * S]
                            ins = nc.scalar.copy(KT[:, t0 + t, :], src)
                        ins.then_inc(sem("item_b"), 1)
                for h in range(H + 3):
                    if h < H:
                        act.wait_ge(sem("max"), before(n, "max") + i * H + h + 1)
                        if h >= 3:
                            act.wait_ge(sem("turned"), before(n, "turned") + i * H + h - 2)
                        for j in range(2):
                            ins = nc.scalar.activation(PR[:, h % 3, j, :], PS[:, SCB[h % 3], j * S:(j + 1) * S], ACT.Exp,
                                                       bias=negmax[:, h, j:j + 1], accum_out=sums[:, h, j:j + 1])
                        ins.then_inc(sem("probs"), 1)
                    g = h - 2
                    if g >= 0 and g < H and g % 2 == 0:
                        act.wait_ge(sem("turned"), before(n, "turned") + i * H + g + 1)
                        if g >= 2:
                            act.wait_ge(sem("values"), before(n, "values") + i * H + g - 1)
                        nc.scalar.copy(PT[:, 0, :, :], PS[:, PTB[0], :].rearrange("p (a b) -> p a b", a=2))\
                          .then_inc(sem("pt_a"), 1)
                NO = max(1, a.vcols // P)
                for k in range(NO):
                    act.wait_ge(sem("oT_psum"), before(n, "oT_psum") + i * NO + k + 1)
                    src = PS[:, PTB[k % 2], 0:S]
                    if n == "L0a":
                        ins = nc.scalar.activation(OT[:, 0, :], src, ACT.Copy, scale=hdm[:, 0:1])
                    else:
                        ins = nc.scalar.copy(OT[:, k, :], src)
                    ins.then_inc(sem("oT"), 1)

            def small_front(a, b, s, first=False):
                n, NI = a.name, len(a.items())
                if s == 1:
                    if first:
                        act.wait_ge(w_in[n], 16)
                        act.wait_ge(x_done, base[n])
                        act.wait_ge(ctx_loaded, 16)
                    else:
                        act.wait_ge(sem("item_psum"), before(n, "item_psum") + b * NI)
                    st = nc.scalar.copy(xs[:, :, :], tile2(b))
                    if not a.self_attn:
                        st = nc.scalar.copy(cs[:, :], ctxT[:, bass.ds(b * S, S)])
                    st.then_inc(sem("staged"), 1)
                if s == TURN_X_STEP:
                    act.wait_ge(sem("xT_psum"), before(n, "xT_psum") + b + 1)
                    nc.scalar.copy(xT[:, :], PS[:, PB[0], 0:S]).then_inc(sem("xT"), 1)
                if n == "L2x" and s == TURN_X_STEP + 1:
                    act.wait_ge(sem("angles"), b + 1)
                    nc.scalar.activation(rot[:, 4, :], rot[:, 4, :], ACT.Sin).then_inc(sem("sines"), 1)
                    nc.scalar.activation(rot[:, 0, :], rot[:, 5, :], ACT.Sin).then_inc(sem("sines"), 1)
                for k, (what, t0) in enumerate(a.items()):
                    if s == a.item_step(k) + 1 and k % 2 and not a.rope and not a.keymask:
                        act.wait_ge(sem("item_psum"), before(n, "item_psum") + b * NI + k + 1)
                        for t in range(2):
                            ins = nc.scalar.activation(KT[:, t0 + t, :], PS[:, PB[1], t * S:(t + 1) * S], ACT.Identity,
                                                       bias=w(f"{n}_bk", t0 + t, t0 + t + 1))
                        ins.then_inc(sem("item_b"), 1)

            def small_rounding(a, b, first):
                n, NI = a.name, len(a.items())
                if not first:
                    if a.turned_scores:
                        act.wait_ge(sem("turned_scores"), before(n, "turned_scores") + b * (a.heads // 2))
                    else:
                        act.wait_ge(sem("scores"), before(n, "scores") + b * a.heads)
                act.wait_ge(sem("item_b"), before(n, "item_b") + (b + 1) * (NI // 2))
                if a.keymask:
                    act.wait_ge(sem("masked"), before(n, "masked") + b + 1)
                nc.scalar.activation(KS[:, :, :], KT[:, 0:4, :], ACT.Copy, scale=w("sign_k")).then_inc(sem("rounded"), 1)
                act.wait_ge(sem("item_a"), before(n, "item_a") + (b + 1) * (NI // 2))
                nc.scalar.activation(QS[:, :, :], QT[:, 0:4, :], ACT.Copy, scale=w("sign_q")).then_inc(sem("rounded"), 1)

            def small_tail(a, i, s):
                n, rows = a.name, min(P, a.vcols)
                if s == OT_STEP:
                    act.wait_ge(sem("oT_psum"), before(n, "oT_psum") + i + 1)
                    nc.scalar.copy(OT[0:rows, 0, :], PS[0:rows, PB[0], 0:S]).then_inc(sem("oT"), 1)

            def small_batch(a, i, first, last):
                n, H, T = a.name, a.heads, a.tiles
                NV = H // 2 if a.turned_scores else H

                def exponentials(p):
                    act.wait_ge(sem("turned_scores"), before(n, "turned_scores") + i * NV + p + 1)
                    if p >= 2:
                        act.wait_ge(sem("values"), before(n, "values") + i * NV + p - 1)
                    cols = 3 * P if a.causal else 4 * P
                    nc.scalar.activation(PX[:, p % 2, :, 0:cols], PS[:, EXPB[0]:EXPB[0] + 2, 0:cols], ACT.Exp)\
                      .then_inc(sem("probs"), 1)

                def clipped_exponentials(h):
                    act.wait_ge(sem("max"), before(n, "max") + i * H + h + 1)
                    if h >= 3:
                        act.wait_ge(sem("turned"), before(n, "turned") + i * H + h - 2)
                    for j in range(2):
                        ins = nc.scalar.activation(PR[:, h % 3, j, :], SC[:, h % 2, j, :], ACT.Exp,
                                                   bias=negmax[:, h, j:j + 1])
                    ins.then_inc(sem("probs"), 1)

                def turned(h):
                    act.wait_ge(sem("turned"), before(n, "turned") + i * H + h + 1)
                    if h >= 2:
                        act.wait_ge(sem("values"), before(n, "values") + i * H + h - 1)
                    nc.scalar.copy(PT[:, 0, :, :], PS[:, PTB[0], :].rearrange("p (a b) -> p a b", a=2))\
                      .then_inc(sem("pt_a"), 1)

                def outputs(t):
                    act.wait_ge(sem("values"), before(n, "values") + i * NV + (t + 1) * (NV // T))
                    nc.scalar.copy(OT[:, 4 + t, :], PS[:, OB, 0:S]).then_inc(sem("outputs"), 1)

                for s in range(STEPS):
                    if a.turned_scores:
                        if s >= 5 and s % 2:
                            exponentials((s - 5) // 2)
                        if s in (9, 13, 17):
                            outputs((s - 9) // 4)
                    else:
                        if s < H:
                            clipped_exponentials(s)
                        if 2 <= s < H + 2 and s % 2 == 0:
                            turned(s - 2)
                        if s >= 7 and s % 4 == 3:
                            outputs((s - 7) // 4)
                    if not first and a.tail:
                        small_tail(a, i - 1, s)
                    if not last:
                        small_front(a, i + 1, s)
                if not last:
                    small_rounding(a, i + 1, False)
                if a.turned_scores:
                    outputs(T - 1)

            def small_stage(a):
                for s in range(STEPS):
                    small_front(a, 0, s, True)
                small_rounding(a, 0, True)
                small_batch(a, 0, True, False)
                with act.Fori(1, B - 1) as i:
                    small_batch(a, i, False, False)
                small_batch(a, B - 1, False, True)
                small_tail(a, B - 1, OT_STEP)

            def stage_x(n, i, first=None):
                act.wait_ge(x_done, i + (base[n] if first is None else first))
                nc.scalar.copy(xs[:, :, :], tile2(i)).then_inc(sem("staged"), 1)

            def copy_xT(n, i):
                act.wait_ge(sem("xT_psum"), before(n, "xT_psum") + i + 1)
                nc.scalar.copy(xT[:, :], PS[:, PB[0], 0:S]).then_inc(sem("xT"), 1)

            def experts(n, i, chunks, func):
                for e in range(E):
                    act.wait_ge(sem(f"{n}_h_psum"), i * E + e + 1)
                    if e >= 2:
                        act.wait_ge(sem(f"{n}_ye"), i * E + e - 1)
                    for c in range(chunks):
                        ins = nc.scalar.activation(QT[:, hidden(e, c, chunks), :],
                                                   PS[:, (GA, GB)[e % 2] + c // 2, (c % 2) * S:(c % 2 + 1) * S],
                                                   func, bias=w(f"{n}_b1", e * chunks + c, e * chunks + c + 1))
                    ins.then_inc(sem(f"{n}_h"), 1)
                act.wait_ge(sem(f"{n}_combT_psum"), i + 1)
                nc.scalar.copy(combT[:, :], PS[0:E, 2, 0:S]).then_inc(sem(f"{n}_combT"), 1)

            def L0f():
                n = "L0f"
                act.wait_ge(w_in[n], 16)
                with act.Fori(0, B) as i:
                    act.wait_ge(x_done, base[n])
                    nc.scalar.copy(xs[:, :, :], tile2(i)).then_inc(sem("staged"), 1)
                    copy_xT(n + "r", i)
                    act.wait_ge(sem(f"{n}_lg"), i + 1)
                act.wait_ge(sem(f"{n}_shifted"), 1)
                nc.scalar.activation(rt[:, 1, :, :], rt[:, 0, :, :], ACT.Exp).then_inc(sem(f"{n}_exp"), 1)
                with act.Fori(0, B) as i:
                    stage_x(n, i)
                    copy_xT(n, i)
                    experts(n, i, 4, ACT.Gelu_apprx_tanh)

            def L2f():
                n = "L2f"
                a = ATTNS[n]

                def batch(i, first, last):
                    small_batch(a, i, first, last)
                    small_tail(a, i, OT_STEP)
                    act.wait_ge(sem(f"{n}_mla_psum"), i + 1)
                    nc.scalar.activation(OT[:, 1, :], PS[:, PB[1], 0:S], ACT.Identity, bias=w(f"{n}_ob"))\
                      .then_inc(sem(f"{n}_mla"), 1)
                    act.wait_ge(sem(f"{n}_shifted"), i + 1)
                    nc.scalar.activation(rt[:, 1, 0:2, :], rt[:, 0, 0:2, :], ACT.Exp).then_inc(sem(f"{n}_exp"), 1)
                    experts(n, i, 2, ACT.Gelu)

                for s in range(STEPS):
                    small_front(a, 0, s, True)
                small_rounding(a, 0, True)
                batch(0, True, False)
                with act.Fori(1, B - 1) as i:
                    batch(i, False, False)
                batch(B - 1, False, True)

            def L1f():
                n = "L1f"
                with act.Fori(0, B) as i:
                    stage_x(n, i)
                    copy_xT(n, i)
                    act.wait_ge(sem(f"{n}_h_psum"), i * 2 + 1)
                    nc.scalar.activation(QT[:, 0:3, :], PS[:, GA:GA + 2, :].rearrange("p a b -> p (a b)")[:, 0:768]
                                         .rearrange("p (a b) -> p a b", a=3), ACT.Silu).then_inc(sem(f"{n}_silu"), 1)

            def L2a():
                n = "L2a"
                ab = big[:, 0:2048].rearrange("p (a b) -> p a b", a=8)
                th = big[:, 2048:4096].rearrange("p (a b) -> p a b", a=8)
                xa = big[:, 4096:6144].rearrange("p (a b) -> p a b", a=8)
                act.wait_ge(w_in[n], 16)
                act.wait_ge(sem(f"{n}_Aready"), 1)
                with act.Fori(0, B) as i:
                    stage_x(n, i)
                    copy_xT(n, i)
                    act.wait_ge(sem(f"{n}_bc_psum"), i + 1)
                    nc.scalar.activation(OT[0:32, 1, :], PS[0:32, 0, 0:S], ACT.Identity, bias=w(f"{n}_bin", rows=32))\
                      .then_inc(sem(f"{n}_bc"), 1)
                    act.wait_ge(sem(f"{n}_dt_psum"), 2 * i + 1)
                    nc.scalar.activation(OT[0:64, 0, :], PS[0:64, 1, 0:S], ACT.Identity, bias=w(f"{n}_bdt1", rows=64))\
                      .then_inc(sem(f"{n}_dt1"), 1)
                    act.wait_ge(sem(f"{n}_zdt"), i + 1)
                    nc.scalar.activation(OT[:, 4, :], OT[:, 6, :], ACT.Abs).then_inc(sem(f"{n}_absz"), 1)
                    act.wait_ge(sem(f"{n}_absz"), i + 1)
                    nc.scalar.activation(OT[:, 4, :], OT[:, 4, :], ACT.Exp, scale=-1.0).then_inc(sem(f"{n}_u"), 1)
                    act.wait_ge(sem(f"{n}_dt"), i + 1)
                    for half in range(2):
                        if half:
                            act.wait_ge(sem(f"{n}_scan"), 2 * i + 1)
                        for k in range(8):
                            s = half * 8 + k
                            nc.scalar.activation(ab[:, k, :], OT[:, 3, :], ACT.Exp, scale=w(f"{n}_A", s, s + 1))
                            nc.scalar.activation(th[:, k, :], OT[:, 3, :], ACT.Tanh, scale=negmax[:, s, 0:1])
                            ins = nc.scalar.activation(xa[:, k, :], xT[:, :], ACT.Copy, scale=negmax[:, s, 1:2])
                        ins.then_inc(sem(f"{n}_abar"), 1)

            def L3a():
                n = "L3a"
                act.wait_ge(w_in[n], 16)
                with act.Fori(0, B) as i:
                    act.wait_ge(x_done, base[n])
                    nc.scalar.copy(xs[:, :, :], tile2(i)).then_inc(sem("staged"), 1)
                    copy_xT(n + "r", i)
                    act.wait_ge(sem(f"{n}_qkvg"), i + 1)
                act.wait_ge(sem(f"{n}_gin"), 1)
                nc.scalar.activation(rt[:, 0:4, :, :], rt[:, 0:4, :, :], ACT.Exp, scale=-1.0).then_inc(sem(f"{n}_gexp"), 1)
                for j in range(2):
                    act.wait_ge(sem(f"{n}_s"), j + 1)
                    nc.scalar.activation(QT[:, 0:4, :], QT[:, 0:4, :], ACT.Exp).then_inc(sem(f"{n}_p"), 1)
                with act.Fori(0, B) as i:
                    act.wait_ge(sem(f"{n}_O"), 1)
                    act.wait_ge(x_done, i + base[n])
                    nc.scalar.copy(On[:, :, 0:P], KT[:, :, :].rearrange("p a b -> p (a b)")
                                   .rearrange("p (t d) -> p t d", t=NT)[:, bass.ds(2 * i, 2), :])
                    nc.scalar.copy(xs[:, :, :], tile2(i)).then_inc(sem("staged"), 1)
                    act.wait_ge(sem("oT_psum"), before(n, "oT_psum") + i + 1)
                    nc.scalar.copy(OT[:, 0, :], PS[:, PTB[0], 0:S]).then_inc(sem("oT"), 1)

            def L3f():
                n = "L3f"
                nT = OT[:, 0, :].bitcast(BF16)
                mT = OT[:, 4:8, :].rearrange("p a b -> p (a b)").bitcast(BF16)
                with act.Fori(0, B) as i:
                    stage_x(n, i)
                    act.wait_ge(sem(f"{n}_nT_psum"), i + 1)
                    nc.scalar.copy(nT[:, 0:S], PS[:, PB[0], :].bitcast(BF16)[:, 0:S]).then_inc(sem(f"{n}_nT"), 1)
                    act.wait_ge(sem(f"{n}_h_psum"), i + 1)
                    for j in range(2):
                        nc.scalar.activation(QT[:, 2 * j:2 * j + 2, :].rearrange("p a b -> p (a b)"), PS[:, 2 * j, :],
                                             ACT.Silu, scale=rsum[:, 0, j:j + 1]).then_inc(sem(f"{n}_silu"), 1)
                    act.wait_ge(sem(f"{n}_mT_psum"), i + 1)
                    for j in range(2):
                        ins = nc.scalar.copy(mT[:, 512 * j:512 * (j + 1)], PS[:, 4 + j, :].bitcast(BF16)[:, 0:512])
                    ins.then_inc(sem(f"{n}_mT"), 1)

            own = {"L0f": L0f, "L1f": L1f, "L2a": L2a, "L2f": L2f, "L3a": L3a, "L3f": L3f}
            for s in STAGES:
                if s in own:
                    own[s]()
                elif ATTNS[s].small:
                    small_stage(ATTNS[s])
                else:
                    with act.Fori(0, B) as i:
                        attention(ATTNS[s], i)

        @block.vector
        def _(dve):
            dve.wait_ge(small_loaded, 32)
            dve.wait_ge(w_in["const"], 16)
            nc.vector.tensor_copy(identb[:, :], ident).then_inc(dve_consts, 1)
            nc.vector.tensor_copy(hdm[:, :], hdm_i[:, :]).then_inc(sem("hdm_ready"), 1)
            dve.wait_ge(x_loaded, 16)
            nc.vector.memset(veps[:, :], 0.0).then_inc(x_done, 1)

            def prepare(s):
                a = ATTNS[s]
                dve.wait_ge(x_done, base[s])
                H, dv = a.heads, a.vcols // a.heads
                nc.vector.memset(SH[:, :, :, :, :], 0.0).then_inc(sem(f"{s}_cleared"), 1)
                nc.vector.memset(V[:, :, 0:32 * H], 0.0).then_inc(sem(f"{s}_cleared"), 1)
                dve.wait_ge(sem(f"{s}_cleared"), 2)
                for j in range(2):
                    ones = V[:, j, 0:32 * H].rearrange("p (h d) -> p h d", h=H)[:, :, dv]
                    nc.vector.memset(ones, 1.0).then_inc(sem(f"{s}_cleared"), 1)
                dve.wait_ge(sem(f"{s}_cleared"), 4)

            def layernorm(s, i, ch, bo):
                moments(ch, bo)
                normalise(s, i, ch)

            def moments(ch, bo):
                if bo is not None:
                    ch.step(nc.vector.tensor_tensor(res[:, :, :], res[:, :, :],
                                                    bo.unsqueeze(1).broadcast_to([P, 2, D]), ALU.add))
                for j in range(2):
                    ch.did(nc.vector.bn_stats(stats[:, j, :], res[:, j, :]))
                ch.wait()
                dve.sem_inc(sem("stats_passed"), 1)
                for j in range(2):
                    ch.did(nc.vector.bn_aggr(mv[:, j, :], stats[:, j, :]))
                ch.wait()
                nc.vector.tensor_scalar(veps[:, :], mv[:, :, 1], 1e-5, None, ALU.add).then_inc(sem("var"), 1)

            def normalise(s, i, ch):
                dve.wait_ge(sem("rstd"), before(s, "rstd") + i + 1)
                for j in range(2):
                    ins = nc.vector.tensor_scalar(x_tok[:, bass.ds(2 * i + j, 1), :].rearrange("p a d -> p (a d)"),
                                                  res[:, j, :], mv[:, j, 0:1], rstd[:, j:j + 1],
                                                  ALU.subtract, ALU.mult)
                    if j == 0:
                        ch.did(ins)
                    else:
                        ch.wait()
                        ins.then_inc(x_done, 1)

            def attention(a, i, ch):
                n, H = a.name, a.heads
                items = a.items()
                NI = len(items)
                dve.wait_ge(w_in[n], 16)
                dve.wait_ge(sem("V_psum"), before(n, "V_psum") + i + 1)
                if a.vcols > 512:
                    for k in range(4):
                        ins = nc.vector.tensor_copy(V[:, k // 2, (k % 2) * 512:(k % 2 + 1) * 512],
                                                    PS[:, (5, 6, 7, 2)[k], :])
                else:
                    ins = nc.vector.tensor_copy(V[:, :, 0:a.vcols],
                                                PS[:, PB[1], 0:2 * a.vcols].rearrange("p (a b) -> p a b", a=2))
                ins.then_inc(sem("V"), 1)
                for k, (what, t0) in enumerate(items):
                    if k % 2 and not a.rope:
                        continue
                    dve.wait_ge(sem("item_psum"), before(n, "item_psum") + i * NI + k + 1)
                    g = (GA, GB)[k % 2]
                    dst = QT if what[0] == "q" else KT
                    if a.rope:
                        to = RT[:, :, :] if what[1:] else dst[:, t0:t0 + 4, :]
                        src = PS[:, g:g + 2, :].rearrange("p a (b s) -> p (a b) s", b=2)
                        t = (w("L1a_sin") if what[1:] else w("L1a_cos")).unsqueeze(1).broadcast_to([P, 4, S])
                        if what[0] == "q":
                            ins = nc.vector.scalar_tensor_tensor(to, src, 1.0 / 128, t, ALU.mult, ALU.mult)
                        else:
                            ins = nc.vector.tensor_tensor(to, src, t, ALU.mult)
                        if what[1:]:
                            ch.step(ins)
                            ins = nc.vector.tensor_tensor(dst[:, t0:t0 + 4, :], dst[:, t0:t0 + 4, :], RT[:, :, :], ALU.add)
                            ins.then_inc(sem("item_b" if k % 2 else "item_a"), 1)
                            dve.wait_ge(sem("item_b"), before(n, "item_b") + i * (NI // 2) + k // 2 + 1)
                        else:
                            ins.then_inc(sem("item_b" if k % 2 else "item_a"), 1)
                            dve.wait_ge(sem("item_a"), before(n, "item_a") + i * (NI // 2) + k // 2 + 1)
                    else:
                        for t in range(a.group):
                            ins = nc.vector.tensor_scalar(QT[:, t0 + t, :], PS[:, g + t // 2, (t % 2) * S:(t % 2 + 1) * S],
                                                          a.scale, None, ALU.mult)
                        ins.then_inc(sem("item_a"), 1)
                for h in range(H + 3):
                    if h < H:
                        dve.wait_ge(sem("scores"), before(n, "scores") + i * H + h + 1)
                        src = PS[:, SCB[h % 3], :].rearrange("p (a b) -> p a b", a=2)
                        nc.vector.tensor_reduce(negmax[:, h, :], src, AX.X, ALU.max, negate=True)\
                          .then_inc(sem("max"), 1)
                    g = h - 2
                    if g >= 0 and g < H and g % 2 == 1:
                        dve.wait_ge(sem("turned"), before(n, "turned") + i * H + g + 1)
                        if g >= 2:
                            dve.wait_ge(sem("values"), before(n, "values") + i * H + g - 1)
                        nc.vector.tensor_copy(PT[:, 1, :, :], PS[:, PTB[1], :].rearrange("p (a b) -> p a b", a=2))\
                          .then_inc(sem("pt_v"), 1)
                    if a.vcols > 512 and h >= 3:
                        g = h - 3
                        dve.wait_ge(sem("values"), before(n, "values") + i * H + g + 1)
                        ch.step(nc.vector.reciprocal(rsum[:, g, :], sums[:, g, :]))
                        ins = nc.vector.tensor_tensor(
                            On[:, :, g * P:(g + 1) * P],
                            PS[:, (5, 6, 7, 5, 6, 7, 5, 6)[g], 0:2 * P].rearrange("p (a b) -> p a b", a=2),
                            rsum[:, g, :].unsqueeze(2).broadcast_to([P, 2, P]), ALU.mult)
                        ins.then_inc(sem("on"), 1)
                if a.vcols <= 512:
                    dv = a.vcols // H
                    dve.wait_ge(sem("values"), before(n, "values") + i * H + H)
                    ch.step(nc.vector.reciprocal(rsum[:, 0:H, :], sums[:, 0:H, :]))
                    for j in range(2):
                        ins = nc.vector.tensor_tensor(
                            On[:, j, 0:a.vcols].rearrange("p (h d) -> p h d", h=H),
                            PS[:, OB, j * a.vcols:(j + 1) * a.vcols].rearrange("p (h d) -> p h d", h=H),
                            rsum[:, 0:H, j].unsqueeze(2).broadcast_to([P, H, dv]), ALU.mult)
                    ins.then_inc(sem("on"), 1)
                dve.wait_ge(sem("y"), before(n, "y") + i + 1)
                ch.step(nc.vector.tensor_tensor(res[:, :, :], PS[:, PB[0], 0:S].rearrange("p (a b) -> p a b", a=2),
                                                xs[:, :, :], ALU.add))
                layernorm(n, i, ch, None)

            def small_chains(a):
                return [Chain(dve, sem(f"{part}_step"), f"{a.name}_{part}", before(a.name, f"{part}_step"))
                        for part in ("heads", "front", "tail")]

            def small_front(a, b, ch, s):
                n, items = a.name, a.items()
                NI = len(items)
                if s == 0:
                    ch.turn(b)
                    dve.wait_ge(w_in[n], 16)
                if a.keymask and s == 5:
                    dve.wait_ge(sem("kmask_in"), b * 16 + 16)
                    ch.did(nc.vector.tensor_scalar(kbias[:, :], kmask[:, :], 0.0, -1.0e9,
                                                   ALU.is_equal, ALU.mult))
                    ch.step(nc.vector.tensor_scalar(keep[:, :], kmask[:, :], 0.0, w("row_one"),
                                                    ALU.not_equal, ALU.max))
                    dve.sem_inc(sem(f"{n}_tile_read"), 1)
                    ch.step(nc.vector.tensor_scalar(kbias[:, :], kbias[:, :], w("row_mask"), None, ALU.mult))
                if n == "L2x" and s == 5:
                    angles(b, ch)
                if n == "L2x" and s == 8:
                    rotations(b, ch)
                if s == V_STEP + 1:
                    dve.wait_ge(sem("V_psum"), before(n, "V_psum") + b + 1)
                    nc.vector.tensor_tensor(VT[:, :, 0:a.vcols],
                                            PS[:, PB[1], 0:2 * a.vcols].rearrange("p (a b) -> p a b", a=2),
                                            w(f"{n}_bv").unsqueeze(1).broadcast_to([P, 2, a.vcols]), ALU.add)\
                      .then_inc(sem("V_held"), 1)
                for k, (what, t0) in enumerate(items):
                    if s != a.item_step(k) + 1 or (what == "k" and not a.rope and not a.keymask):
                        continue
                    dve.wait_ge(sem("item_psum"), before(n, "item_psum") + b * NI + k + 1)
                    dst = (QT if what[0] == "q" else KT)[:, t0:t0 + 2, :]
                    for t in range(2):
                        src, bias = PS[:, PB[k % 2], t * S:(t + 1) * S], w(f"{n}_b{what}", t0 + t, t0 + t + 1)
                        if a.rope:
                            tab = (1 if what[1:] else 0) + (2 if what[0] == "q" else 0)
                            ins = nc.vector.scalar_tensor_tensor((RT if what[1:] else dst)[:, t, :], src, bias,
                                                                 rot[:, tab, :], ALU.add, ALU.mult)
                        elif what == "k":
                            ins = nc.vector.scalar_tensor_tensor(dst[:, t, :], src, bias, keep[:, :],
                                                                 ALU.add, ALU.mult)
                        else:
                            ins = nc.vector.tensor_scalar(dst[:, t, :], src, bias, a.scale, ALU.add, ALU.mult)
                    if what[1:]:
                        ch.step(ins)
                        dve.wait_ge(sem("item_a"), before(n, "item_a") + b * (NI // 2) + k // 2 + 1)
                        ins = nc.vector.tensor_tensor(dst, dst, RT[:, 0:2, :], ALU.add)
                    ins.then_inc(sem("item_b" if k % 2 else "item_a"), 1)
                    if what[1:]:
                        dve.wait_ge(sem("item_b"), before(n, "item_b") + b * (NI // 2) + k // 2 + 1)
                if s == STEPS - 1:
                    ch.end()

            def small_rounding(a, b):
                n = a.name
                for k, (dst, src, x) in enumerate(((KS, KT, "k"), (QS, QT, "q"))):
                    dve.wait_ge(sem("rounded"), before(n, "rounded") + 2 * b + k + 1)
                    nc.vector.scalar_tensor_tensor(dst[:, :, :], src[:, 0:4, :], w(f"lo_{x}"),
                                                   dst[:, :, :].bitcast(F32), ALU.mult, ALU.add)\
                      .then_inc(sem("stack"), 1)

            def small_outputs(a, i, ch):
                n, H, dv = a.name, a.heads, a.vcols // a.heads
                ch.turn(i)
                dve.wait_ge(sem("outputs_psum"), before(n, "outputs_psum") + i + 1)
                o = [PS[:, EXPB[0] + j, :].rearrange("p (h d) -> p h d", h=H) for j in range(2)]
                for j in range(2):
                    ch.did(nc.vector.reciprocal(rsum[:, 0:H, j], o[j][:, :, dv]))
                ch.wait()
                for j in range(2):
                    ins = nc.vector.tensor_tensor(
                        On[:, j, 0:a.vcols].rearrange("p (h d) -> p h d", h=H), o[j][:, :, 0:dv],
                        rsum[:, 0:H, j].unsqueeze(2).broadcast_to([P, H, dv]), ALU.mult)
                ins.then_inc(sem("on"), 1)

            def small_tail(a, i, ch, s):
                n = a.name
                if s == Y_STEP + 1:
                    dve.wait_ge(sem("y"), before(n, "y") + i + 1)
                    nc.vector.tensor_tensor(res[:, :, :], PS[:, PB[1], 0:S].rearrange("p (a b) -> p a b", a=2),
                                            tile2(i), ALU.add).then_inc(sem("y_read"), 1)
                    dve.wait_ge(sem("y_read"), before(n, "y_read") + i + 1)
                if s == Y_STEP + 2:
                    moments(ch, w(f"{n}_bo"))
                if s == Y_STEP + 3:
                    normalise(n, i, ch)
                    ch.end()

            def small_batch(a, i, chains, first, last):
                n, H, T, dv = a.name, a.heads, a.tiles, a.vcols // a.heads
                ch, front, tail = chains

                def maximum(h):
                    dve.wait_ge(sem("scores"), before(n, "scores") + i * H + h + 1)
                    if a.clip:
                        if h >= 2:
                            dve.wait_ge(sem("probs"), before(n, "probs") + i * H + h - 1)
                        nc.vector.scalar_tensor_tensor(
                            SC[:, h % 2, :, :], PS[:, SCB[h % 3], :].rearrange("p (a b) -> p a b", a=2), -100.0,
                            cap[:, :, :], ALU.max, ALU.min).then_inc(sem("clipped"), 1)
                        dve.wait_ge(sem("clipped"), before(n, "clipped") + i * H + h + 1)
                        src = SC[:, h % 2, :, :]
                    else:
                        src = PS[:, MAXB[h % 2], :].rearrange("p (a b) -> p a b", a=2)
                    nc.vector.tensor_reduce(negmax[:, h, :], src, AX.X, ALU.max, negate=True)\
                      .then_inc(sem("max"), 1)

                def shift(t):
                    dve.wait_ge(sem("max"), before(n, "max") + i * H + 4 * t + 4)
                    m = negmax[:, 4 * t:4 * t + 4, :].rearrange("p r j -> p j r")
                    hi, lo = SH[:, t, :, :, SHIFT_ROW], SH[:, t, :, :, SHIFT_ROW + 1]
                    ch.step(nc.vector.tensor_copy(hi.bitcast(F32R), m))
                    nc.vector.tensor_tensor(lo, m, hi, ALU.subtract).then_inc(sem("shift"), 1)

                def shifted(t):
                    dve.wait_ge(sem("shift_psum"), before(n, "shift_psum") + i * T + t + 1)
                    dve.wait_ge(sem("stack"), before(n, "stack") + 2 * i + 2)
                    nc.vector.tensor_tensor(QS[:, t, :], QS[:, t, :].bitcast(F32), PS[:, SHB, 0:S], ALU.add)\
                      .then_inc(sem("shifted"), 1)

                def turned(h):
                    dve.wait_ge(sem("turned"), before(n, "turned") + i * H + h + 1)
                    if h >= 2:
                        dve.wait_ge(sem("values"), before(n, "values") + i * H + h - 1)
                    nc.vector.tensor_copy(PT[:, 1, :, :], PS[:, PTB[1], :].rearrange("p (a b) -> p a b", a=2))\
                      .then_inc(sem("pt_v"), 1)

                ch.turn(i)
                if not first and a.tail:
                    small_outputs(a, i - 1, tail)
                dve.wait_ge(sem("V_held"), before(n, "V_held") + i + 1)
                for j in range(2):
                    ins = nc.vector.tensor_copy(V[:, j, 0:32 * H].rearrange("p (h d) -> p h d", h=H)[:, :, 0:dv],
                                                VT[:, j, 0:a.vcols].rearrange("p (h d) -> p h d", h=H))
                ins.then_inc(sem("V"), 1)
                if a.clip:
                    dve.wait_ge(sem("mask_in"), i * 16 + 16)
                    ch.step(nc.vector.tensor_scalar(cap[:, :, :], mask_i[:, :, :], 0.0, -BIG,
                                                    ALU.is_equal, ALU.mult))
                    dve.sem_inc(sem(f"{n}_tile_read"), 1)
                    ch.step(nc.vector.tensor_scalar(cap[:, :, :], cap[:, :, :], 100.0, None, ALU.add))
                for s in range(STEPS):
                    if s < H:
                        maximum(s)
                    if a.turned_scores:
                        if s < H and s % 4 == 3:
                            shift(s // 4)
                        if s % 4 == 0 and 4 <= s <= H:
                            shifted(s // 4 - 1)
                    elif 2 <= s < H + 2 and s % 2:
                        turned(s - 2)
                    if not first and a.tail:
                        small_tail(a, i - 1, tail, s)
                    if not last:
                        small_front(a, i + 1, front, s)
                ch.end()
                if not last:
                    small_rounding(a, i + 1)

            def small_stage(a, batch):
                prepare(a.name)
                chains = small_chains(a)
                for s in range(STEPS):
                    small_front(a, 0, chains[1], s)
                small_rounding(a, 0)
                batch(a, 0, chains, True, False)
                with dve.Fori(1, B - 1) as i:
                    batch(a, i, chains, False, False)
                batch(a, B - 1, chains, False, True)
                if a.tail:
                    small_outputs(a, B - 1, chains[2])
                    for s in range(STEPS):
                        small_tail(a, B - 1, chains[2], s)

            def angles(i, ch):
                dve.wait_ge(sem("pos_in"), i * 16 + 16)
                two_pi = 6.283185307179586
                hi = 6.28125
                mid = 0.0019350051879882812
                lo = two_pi - hi - mid
                ch.step(nc.vector.tensor_copy(rot[:, 1, :], pos_i[:, :]))
                dve.sem_inc(sem("L2x_tile_read"), 1)
                ch.step(nc.vector.tensor_scalar(rot[:, 1, :], rot[:, 1, :], w("L2x_freq"), None, ALU.mult))
                for c, shift in ((4, 0.0), (5, two_pi / 4)):
                    ch.step(nc.vector.tensor_scalar(rot[:, 2, :], rot[:, 1, :], 1.0 / two_pi, shift / two_pi, ALU.mult, ALU.add))
                    ch.step(nc.vector.tensor_scalar(rot[:, 2, :], rot[:, 2, :], MAGIC, MAGIC, ALU.add, ALU.subtract))
                    ch.step(nc.vector.scalar_tensor_tensor(rot[:, 3, :], rot[:, 2, :], -hi, rot[:, 1, :], ALU.mult, ALU.add))
                    ch.step(nc.vector.scalar_tensor_tensor(rot[:, 3, :], rot[:, 2, :], -mid, rot[:, 3, :], ALU.mult, ALU.add))
                    ch.step(nc.vector.scalar_tensor_tensor(rot[:, 3, :], rot[:, 2, :], -lo, rot[:, 3, :], ALU.mult, ALU.add))
                    ch.step(nc.vector.tensor_scalar(rot[:, 3, :], rot[:, 3, :], shift, 3.1415925, ALU.add, ALU.min))
                    ins = nc.vector.tensor_scalar(rot[:, c, :], rot[:, 3, :], -3.1415925, None, ALU.max)
                    if c == 4:
                        ch.step(ins)
                    else:
                        ins.then_inc(sem("angles"), 1)

            def rotations(i, ch):
                dve.wait_ge(sem("sines"), i * 2 + 2)
                ch.did(nc.vector.tensor_scalar(rot[:, 1, :], rot[:, 4, :], w("L2x_sign"), None, ALU.mult))
                ch.did(nc.vector.tensor_scalar(rot[:, 2, :], rot[:, 0, :], ATTNS["L2x"].scale, None, ALU.mult))
                ch.did(nc.vector.tensor_scalar(rot[:, 3, :], rot[:, 4, :], w("L2x_sign"), ATTNS["L2x"].scale,
                                               ALU.mult, ALU.mult))
                ch.wait()

            def flat(t):
                return t.rearrange("p a b -> p (a b)")

            def both(t):
                return t.rearrange("p (a b) -> p a b", a=2)

            def top2(T, ch, count=None):
                def r(k):
                    return rt[:, k, 0:T, :]

                def c(k):
                    return rts[:, k, 0:T]

                def wide(k):
                    return c(k).unsqueeze(2).broadcast_to([P, T, E])

                ch.step(nc.vector.tensor_reduce(c(0), r(1), AX.X, ALU.add))
                ch.step(nc.vector.reciprocal(c(1), c(0)))
                ch.step(nc.vector.tensor_tensor(r(1), r(1), wide(1), ALU.mult))
                for k in range(2):
                    ch.step(nc.vector.tensor_reduce(c(2 + k), r(1), AX.X, ALU.max))
                    ch.step(nc.vector.tensor_tensor(r(4), r(1), wide(2 + k), ALU.is_equal))
                    ch.step(nc.vector.tensor_tensor(r(4), r(4), w("w8").unsqueeze(1).broadcast_to([P, T, E]), ALU.mult))
                    ch.step(nc.vector.tensor_reduce(c(4), r(4), AX.X, ALU.max))
                    ch.step(nc.vector.tensor_tensor(r(2 + k), r(4), wide(4), ALU.is_equal))
                    if k == 0:
                        ch.step(nc.vector.scalar_tensor_tensor(r(1), r(2), -2.0, r(1), ALU.mult, ALU.add))

            def weigh(T, ch, eps, dst, sig):
                def c(k):
                    return rts[:, k, 0:T]

                ch.step(nc.vector.tensor_tensor(c(4), c(2), c(3), ALU.add))
                ch.step(nc.vector.tensor_scalar(c(4), c(4), eps, None, ALU.add))
                ch.step(nc.vector.reciprocal(c(5), c(4)))
                for k in (2, 3):
                    ch.did(nc.vector.tensor_tensor(c(k), c(k), c(5), ALU.mult))
                ch.wait()
                for k in (2, 3):
                    ch.did(nc.vector.tensor_tensor(rt[:, k, 0:T, :], rt[:, k, 0:T, :],
                                                   c(k).unsqueeze(2).broadcast_to([P, T, E]), ALU.mult))
                ch.wait()
                nc.vector.tensor_tensor(dst, rt[:, 2, 0:T, :], rt[:, 3, 0:T, :], ALU.add).then_inc(sig, 1)

            def experts(n, i, ch, factor, start):
                for e in range(E):
                    dve.wait_ge(sem(f"{n}_ye"), i * E + e + 1)
                    if e == 0:
                        dve.wait_ge(sem(f"{n}_combs"), i + 1)
                    else:
                        dve.wait_ge(sem(f"{n}_acc"), i * E + e)
                    for j in range(2):
                        ins = nc.vector.scalar_tensor_tensor(res[:, j, :], PS[:, (5, 7)[e % 2], j * P:(j + 1) * P],
                                                             combs[:, j, e:e + 1], (start if e == 0 else res)[:, j, :],
                                                             ALU.mult, ALU.add)
                    ins.then_inc(sem(f"{n}_acc"), 1)
                dve.wait_ge(sem(f"{n}_yb"), i + 1)
                dve.wait_ge(sem(f"{n}_acc"), i * E + E)
                ch.step(nc.vector.tensor_tensor(res[:, :, :], res[:, :, :], both(PS[:, PB[0], 0:S]), ALU.add))

            def L0f():
                n = "L0f"
                dve.wait_ge(x_done, base[n])
                dve.wait_ge(w_in[n], 16)
                with dve.Fori(0, B) as i:
                    dve.wait_ge(sem(f"{n}_lg_psum"), i + 1)
                    nc.vector.tensor_copy(rt[:, 0, bass.ds(2 * i, 2), :], PS[:, PB[1], 0:2 * E].rearrange(
                        "p (a b) -> p a b", a=2)).then_inc(sem(f"{n}_lg"), 1)
                ch = Chain(dve, sem(f"{n}_route"), "L0r")
                ch.turn(0)
                dve.wait_ge(sem(f"{n}_lg"), B)
                ch.step(nc.vector.tensor_reduce(rts[:, 0, :], rt[:, 0, :, :], AX.X, ALU.max))
                nc.vector.tensor_tensor(rt[:, 0, :, :], rt[:, 0, :, :], rts[:, 0, :].unsqueeze(2).broadcast_to([P, NT, E]),
                                        ALU.subtract).then_inc(sem(f"{n}_shifted"), 1)
                dve.wait_ge(sem(f"{n}_exp"), 1)
                top2(NT, ch)
                nc.vector.tensor_copy(ohb[:, :, :, :], rt[:, 2:4, :, :]).then_inc(sem(f"{n}_onehots"), 1)
                dve.wait_ge(sem(f"{n}_counts"), 1)
                cnt = big[:, 0:256].rearrange("p (k t e) -> p k t e", k=2, t=NT)
                pre = big[:, 256:512].rearrange("p (k t e) -> p k t e", k=2, t=NT)
                ch.step(nc.vector.tensor_copy(big[:, 0:256], PS[:, 1, 0:256]))
                a, b = cnt, pre
                for d in (1, 2, 4, 8):
                    ch.did(nc.vector.tensor_copy(b[:, :, 0:d, :], a[:, :, 0:d, :]))
                    for k in range(2):
                        ch.did(nc.vector.tensor_tensor(b[:, k, d:NT, :], a[:, k, d:NT, :], a[:, k, 0:NT - d, :], ALU.add))
                    ch.wait()
                    a, b = b, a
                ch.step(nc.vector.tensor_scalar(big[:, 512:520], a[:, 0, NT - 1, :], float(CAPACITY), None, ALU.min))
                pos = big[:, 768:1024].rearrange("p (k t e) -> p k t e", k=2, t=NT)
                ch.did(nc.vector.tensor_copy(big[:, 768:1024], PS[:, 0, 0:256]))
                ch.wait()
                for k in range(2):
                    ch.did(nc.vector.tensor_tensor(pos[:, k, 1:NT, :], pos[:, k, 1:NT, :], a[:, k, 0:NT - 1, :], ALU.add))
                ch.wait()
                ch.step(nc.vector.tensor_tensor(pos[:, 1, :, :], pos[:, 1, :, :],
                                                big[:, 512:520].unsqueeze(1).broadcast_to([P, NT, E]), ALU.add))
                ch.step(nc.vector.tensor_scalar(big[:, 768:1024], big[:, 768:1024], float(CAPACITY), None, ALU.is_le))
                for k in range(2):
                    ch.did(nc.vector.tensor_tensor(rt[:, 2 + k, :, :], rt[:, 2 + k, :, :], pos[:, k, :, :], ALU.mult))
                ch.wait()
                weigh(NT, ch, 1e-9, comb[:, :, :], sem(f"{n}_routed"))
                ch.end()
                dve.wait_ge(sem(f"{n}_routed"), 1)
                ch = Chain(dve, sem("dve_step"), n, before(n, "dve_step"))
                with dve.Fori(0, B) as i:
                    ch.turn(i)
                    dve.wait_ge(sem("staged"), before(n, "staged") + i + 1)
                    nc.vector.tensor_copy(combs[:, :, :], comb[:, bass.ds(2 * i, 2), :]).then_inc(sem(f"{n}_combs"), 1)
                    experts(n, i, ch, 1.0, xs)
                    layernorm(n, i, ch, None)
                    ch.end()

            def L2f():
                n = "L2f"

                def batch(a, i, chains, first, last):
                    small_batch(a, i, chains, first, last)
                    ch = chains[2]
                    small_outputs(a, i, ch)
                    dve.wait_ge(sem(f"{n}_lg_psum"), i + 1)
                    nc.vector.tensor_tensor(rt[:, 0, 0:2, :], PS[:, PB[1], 0:2 * E].rearrange("p (a b) -> p a b", a=2),
                                            w(f"{n}_br").unsqueeze(1).broadcast_to([P, 2, E]), ALU.add)\
                      .then_inc(sem(f"{n}_lg"), 1)
                    dve.wait_ge(sem(f"{n}_lg"), i + 1)
                    ch.step(nc.vector.tensor_reduce(rts[:, 0, 0:2], rt[:, 0, 0:2, :], AX.X, ALU.max))
                    nc.vector.tensor_tensor(rt[:, 0, 0:2, :], rt[:, 0, 0:2, :],
                                            rts[:, 0, 0:2].unsqueeze(2).broadcast_to([P, 2, E]),
                                            ALU.subtract).then_inc(sem(f"{n}_shifted"), 1)
                    dve.wait_ge(sem(f"{n}_exp"), i + 1)
                    top2(2, ch)
                    weigh(2, ch, 1e-8, combs[:, :, :], sem(f"{n}_combs"))
                    ch.step(nc.vector.memset(OT[:, 7, :], 0.0))
                    experts(n, i, ch, 1.0, OT[:, 7, :].rearrange("p (a b) -> p a b", a=2))
                    ch.step(nc.vector.tensor_scalar(res[:, :, :], res[:, :, :], 0.3, None, ALU.mult))
                    ch.step(nc.vector.scalar_tensor_tensor(flat(res[:, :, :]), flat(tile2(i)), 2.0, flat(res[:, :, :]),
                                                           ALU.mult, ALU.add))
                    layernorm(n, i, ch, None)
                    ch.end()

                small_stage(ATTNS[n], batch)

            def L1f():
                n = "L1f"
                dve.wait_ge(x_done, base[n])
                nc.vector.tensor_scalar(wdeq[:, :], wint[:, :], 1.0 / 127.0, None, ALU.mult).then_inc(sem("wdeq_ready"), 1)
                ch = Chain(dve, sem("dve_step"), n, before(n, "dve_step"))
                with dve.Fori(0, B) as i:
                    ch.turn(i)
                    dve.wait_ge(sem(f"{n}_h_psum"), i * 2 + 2)
                    dve.wait_ge(sem(f"{n}_silu"), i + 1)
                    nc.vector.tensor_tensor(QT[:, 3:6, :], QT[:, 0:3, :],
                                            PS[:, GB:GB + 2, :].rearrange("p a b -> p (a b)")[:, 0:768]
                                            .rearrange("p (a b) -> p a b", a=3), ALU.mult).then_inc(sem(f"{n}_h"), 1)
                    dve.wait_ge(sem("y"), before(n, "y") + i + 1)
                    ch.step(nc.vector.tensor_tensor(res[:, :, :], both(PS[:, PB[0], 0:S]), xs[:, :, :], ALU.add))
                    layernorm(n, i, ch, None)
                    ch.end()

            def L2a():
                n = "L2a"
                dve.wait_ge(x_done, base[n])
                ab, th, xa, hh = (big[:, 2048 * k:2048 * (k + 1)] for k in range(4))
                z, dt, u, y = OT[:, 6, :], OT[:, 3, :], OT[:, 4, :], OT[:, 5, :]
                bc = OT[0:32, 1, :]
                stk = OT[0:96, 2, 0:P].bitcast(BF16)
                s1, s2, s3 = KT[:, 0, :], KT[:, 1, :], KT[:, 2, :]
                dve.wait_ge(w_in[n], 16)
                nc.vector.tensor_scalar(negmax[:, :, 0], w(f"{n}_A"), 0.5, None, ALU.mult)
                nc.vector.reciprocal(negmax[:, :, 1], w(f"{n}_A")).then_inc(sem(f"{n}_Aready"), 1)
                ch = Chain(dve, sem("dve_step"), n, before(n, "dve_step"))
                with dve.Fori(0, B) as i:
                    ch.turn(i)
                    dve.wait_ge(sem(f"{n}_bc"), i + 1)
                    ch.step(nc.vector.tensor_copy(stk[0:32, :], bc))
                    ch.step(nc.vector.tensor_tensor(bc, bc, stk[0:32, :], ALU.subtract))
                    ch.step(nc.vector.tensor_copy(stk[32:64, :], bc))
                    ch.step(nc.vector.tensor_copy(KT[0:32, 3, :], stk[32:64, :]))
                    ch.step(nc.vector.tensor_tensor(bc, bc, KT[0:32, 3, :], ALU.subtract))
                    nc.vector.tensor_copy(stk[64:96, :], bc).then_inc(sem(f"{n}_stack"), 1)
                    dve.wait_ge(sem(f"{n}_dt_psum"), 2 * i + 2)
                    nc.vector.tensor_scalar(z, PS[:, 2, 0:S], w(f"{n}_bdt2"), None, ALU.add)\
                      .then_inc(sem(f"{n}_zdt"), 1)
                    dve.wait_ge(sem(f"{n}_u"), i + 1)
                    ch.step(nc.vector.tensor_scalar(s1, u, 2.0, None, ALU.add))
                    ch.step(nc.vector.reciprocal(s2, s1))
                    ch.step(nc.vector.tensor_tensor(s1, u, s2, ALU.mult))
                    ch.step(nc.vector.tensor_tensor(s2, s1, s1, ALU.mult))
                    ch.step(nc.vector.tensor_scalar(s3, s2, 2.0 / 17, None, ALU.mult))
                    for k in (15, 13, 11, 9, 7, 5, 3):
                        ch.step(nc.vector.scalar_tensor_tensor(s3, s3, 2.0 / k, s2, ALU.add, ALU.mult))
                    ch.step(nc.vector.scalar_tensor_tensor(s3, s3, 2.0, s1, ALU.add, ALU.mult))
                    ch.step(nc.vector.scalar_tensor_tensor(z, z, 0.0, s3, ALU.max, ALU.add))
                    nc.vector.tensor_scalar(dt, z, 1e-7, 1e6, ALU.max, ALU.min).then_inc(sem(f"{n}_dt"), 1)
                    ch.did(nc.vector.memset(y, 0.0))
                    nc.vector.memset(s1, 0.0).then_inc(sem(f"{n}_z"), 1)
                    ch.wait()
                    for half in range(2):
                        dve.wait_ge(sem(f"{n}_abar"), 2 * i + half + 1)
                        ch.step(nc.vector.scalar_tensor_tensor(th, ab, 1.0, th, ALU.add, ALU.mult))
                        dve.wait_ge(sem(f"{n}_B"), 2 * i + half + 1)
                        nc.vector.tensor_tensor(xa, xa, PS[:, 0:4, :].rearrange("p a b -> p (a b)"), ALU.mult)\
                          .then_inc(sem(f"{n}_g"), 1)
                        dve.wait_ge(sem(f"{n}_g"), 2 * i + half + 1)
                        ch.did(nc.vector.tensor_tensor(th, th, xa, ALU.mult))
                        ch.did(nc.vector.memset(ab.rearrange("p (a b) -> p a b", a=8)[:, :, 0:1], 0.0))
                        ch.wait()
                        nc.vector.tensor_tensor_scan(hh, ab, th, 0.0, ALU.mult, ALU.add).then_inc(sem(f"{n}_scan"), 1)
                        dve.wait_ge(sem(f"{n}_scan"), 2 * i + half + 1)
                        dve.wait_ge(sem(f"{n}_C"), 2 * i + half + 1)
                        nc.vector.tensor_tensor(hh, hh, PS[:, 4:8, :].rearrange("p a b -> p (a b)"), ALU.mult)\
                          .then_inc(sem(f"{n}_hc"), 1)
                        dve.wait_ge(sem(f"{n}_hc"), 2 * i + half + 1)
                        ch.step(nc.vector.tensor_reduce(s2, hh.rearrange("p (n l) -> p l n", n=8), AX.X, ALU.add))
                        ch.step(nc.vector.tensor_tensor(y, y, s2, ALU.add))
                    nc.vector.scalar_tensor_tensor(y, xT[:, :], w(f"{n}_D"), y, ALU.mult, ALU.add)\
                      .then_inc(sem(f"{n}_ysum"), 1)
                    dve.wait_ge(sem("y"), before(n, "y") + i + 1)
                    ch.step(nc.vector.tensor_tensor(res[:, :, :], both(PS[:, PB[0], 0:S]), xs[:, :, :], ALU.add))
                    layernorm(n, i, ch, None)
                    ch.end()

            def L3a():
                n = "L3a"
                dve.wait_ge(x_done, base[n])
                qkvg = big[:, :].rearrange("p (t j c) -> p t j c", t=B, j=2)
                dve.wait_ge(w_in[n], 16)
                with dve.Fori(0, B) as i:
                    dve.wait_ge(sem(f"{n}_qkvg_psum"), i + 1)
                    nc.vector.tensor_tensor(qkvg[:, bass.ds(i, 1), :, :].rearrange("p t j c -> p (t j) c"), PS[:, 0:2, :],
                                            w(f"{n}_b").unsqueeze(1).broadcast_to([P, 2, 512]), ALU.add)\
                      .then_inc(sem(f"{n}_qkvg"), 1)
                ch = Chain(dve, sem(f"{n}_mid"), "L3m")
                ch.turn(0)
                dve.wait_ge(sem(f"{n}_qkvg"), B)
                allt = big[:, :].rearrange("p (t c) -> p t c", t=NT)
                gin = rt[:, 0:4, :, :].rearrange("p k t e -> p (k t e)")
                ch.did(nc.vector.tensor_reduce(gin.rearrange("p (t g) -> p t g", t=NT),
                                               allt[:, :, 384:512].rearrange("p t (g k) -> p t g k", k=4), AX.X, ALU.add))
                ch.step(nc.vector.tensor_scalar(allt[:, :, 0:128], allt[:, :, 0:128], R8, None, ALU.mult))
                dve.sem_inc(sem(f"{n}_gin"), 1)
                dve.wait_ge(sem(f"{n}_gexp"), 1)
                ch.step(nc.vector.tensor_scalar(gin, gin, 1.0, None, ALU.add))
                ch.step(nc.vector.reciprocal(gin, gin))
                ab = gin.rearrange("p (t h k) -> p t h k", t=NT, k=2)
                g1 = comb[:, :, :].rearrange("p t e -> p (t e)")
                ga = OT[:, 0, 0:256].rearrange("p (t h) -> p t h", t=NT)
                ch.step(nc.vector.tensor_tensor(ga, ab[:, :, :, 1], w(f"{n}_ga").unsqueeze(1).broadcast_to([P, NT, 16]),
                                                ALU.mult))
                ch.step(nc.vector.scalar_tensor_tensor(ga, ga, -1.0, ab[:, :, :, 0], ALU.add, ALU.mult))
                ch.step(nc.vector.tensor_scalar(ga, ga, 2.0, None, ALU.add))
                rel = w(f"{n}_rel").rearrange("p (a h) -> p a h", a=15)
                sc = QT[:, 0:4, :].rearrange("p a b -> p (a b)").rearrange("p (t u h) -> p t u h", t=B, u=B)
                pr = V[:, :, :].rearrange("p a b -> p (a b)")
                Oall = KT[:, :, :].rearrange("p a b -> p (a b)").rearrange("p (t j c) -> p t j c", t=B, j=2)
                for j in range(2):
                    for t in range(B):
                        q = qkvg[:, t, j, 0:128].unsqueeze(1).broadcast_to([P, B, 128])
                        k = qkvg[:, :, j, 128:256]
                        at = 1024 * (t % 2)
                        prod = pr[:, at:at + 1024].rearrange("p (u c) -> p u c", u=B)
                        ch.did(nc.vector.tensor_tensor(prod, q, k, ALU.mult))
                        ch.did(nc.vector.tensor_tensor(On[:, 0, t * P:(t + 1) * P].rearrange("p (u h) -> p u h", u=B),
                                                       rel[:, 7 - t:15 - t, :],
                                                       ga[:, 2 * t + j, :].unsqueeze(1).broadcast_to([P, B, 16]), ALU.mult))
                        ch.wait()
                        ch.did(nc.vector.tensor_reduce(sc[:, t, :, :], pr[:, at:at + 1024].rearrange(
                            "p (u h d) -> p u h d", u=B, h=16), AX.X, ALU.add))
                    ch.wait()
                    scf = QT[:, 0:4, :].rearrange("p a b -> p (a b)")
                    ch.step(nc.vector.tensor_tensor(scf, scf, On[:, 0, :], ALU.add))
                    scu = scf.rearrange("p (t u h) -> p t h u", t=B, u=B)
                    mx = OT[:, 1, 0:128].rearrange("p (t h) -> p t h", t=B)
                    ch.step(nc.vector.tensor_reduce(mx, scu, AX.X, ALU.max))
                    nc.vector.tensor_tensor(sc, sc, mx.unsqueeze(2).broadcast_to([P, B, B, 16]), ALU.subtract)\
                      .then_inc(sem(f"{n}_s"), 1)
                    dve.wait_ge(sem(f"{n}_p"), j + 1)
                    sm = OT[:, 1, 128:256].rearrange("p (t h) -> p t h", t=B)
                    ch.step(nc.vector.tensor_reduce(sm, scu, AX.X, ALU.add))
                    ch.step(nc.vector.reciprocal(sm, sm))
                    for t in range(B):
                        at = 1024 * (t % 2)
                        ch.step(nc.vector.tensor_tensor(
                            pr[:, at:at + 1024].rearrange("p (u h d) -> p u h d", u=B, h=16),
                            sc[:, t, :, :].unsqueeze(3).broadcast_to([P, B, 16, 8]),
                            qkvg[:, :, j, 256:384].rearrange("p u (h d) -> p u h d", h=16), ALU.mult))
                        ch.step(nc.vector.tensor_reduce(Oall[:, t, j, :], pr[:, at:at + 1024].rearrange(
                            "p (u c) -> p c u", u=B), AX.X, ALU.add))
                        ch.did(nc.vector.tensor_tensor(
                            Oall[:, t, j, :].rearrange("p (h d) -> p h d", h=16),
                            Oall[:, t, j, :].rearrange("p (h d) -> p h d", h=16),
                            sm[:, t, :].unsqueeze(2).broadcast_to([P, 16, 8]), ALU.mult))
                ch.wait()
                dve.sem_inc(sem(f"{n}_O"), 1)
                ch.end()
                ch = Chain(dve, sem("dve_step"), n, before(n, "dve_step"))
                with dve.Fori(0, B) as i:
                    ch.turn(i)
                    dve.wait_ge(sem("y"), before(n, "y") + i + 1)
                    ch.step(nc.vector.tensor_tensor(res[:, :, :], both(PS[:, PB[0], 0:S]), xs[:, :, :], ALU.add))
                    layernorm(n, i, ch, w(f"{n}_bo"))
                    ch.end()

            def L3f():
                n = "L3f"
                dve.wait_ge(x_done, base[n])
                nq = On[:, :, 0:64].bitcast(BF16)
                hq = On[:, :, 128:384].bitcast(BF16)
                dve.wait_ge(w_in[n], 16)
                means = mv[:, :, :].rearrange("p a b -> p (a b)")
                ch = Chain(dve, sem(f"{n}_quant"), "L3q")
                ch.turn(0)
                for k, name in enumerate(("wg", "wu", "wd")):
                    ins = nc.vector.tensor_reduce(means[:, k:k + 1], w(f"{n}_{name}"), AX.X, ALU.add,
                                                  apply_absolute_value=True)
                ins.then_inc(sem(f"{n}_wsum"), 1)
                dve.wait_ge(sem(f"{n}_wmean_psum"), 1)
                wm, ws = sums[:, 0:3, 0], sums[:, 0:3, 1]
                ch.step(nc.vector.tensor_scalar(wm, PS[:, 0, 0:3], 1.0 / (512 * 128), 1e-5, ALU.mult, ALU.max))
                ch.step(nc.vector.reciprocal(ws, wm))
                for k, name in enumerate(("wg", "wu", "wd")):
                    tmp = KT[:, 2 * k:2 * k + 2, :].rearrange("p a b -> p (a b)")
                    ch.step(nc.vector.tensor_scalar(tmp, w(f"{n}_{name}"), sums[:, k, 1:2], 1.0, ALU.mult, ALU.min))
                    ch.step(nc.vector.tensor_scalar(tmp, tmp, -1.0, MAGIC, ALU.max, ALU.add))
                    ins = nc.vector.tensor_scalar(tern[:, k, :], tmp, MAGIC, None, ALU.subtract)
                    if k < 2:
                        ch.did(ins)
                    else:
                        ch.wait()
                        ins.then_inc(sem(f"{n}_tern"), 1)
                ch.end()

                def quantise(ch, src, dst, tmp, j, slot, sig):
                    amax, inv = rts[:, 0, j:j + 1], rts[:, 1, j:j + 1]
                    ch.step(nc.vector.tensor_reduce(amax, src, AX.X, ALU.max, apply_absolute_value=True))
                    ch.step(nc.vector.tensor_scalar(amax, amax, 1e-5, None, ALU.max))
                    ch.step(nc.vector.reciprocal(inv, amax))
                    ch.did(nc.vector.tensor_scalar(rsum[:, slot, j:j + 1], amax, 1.0 / 127, None, ALU.mult))
                    ch.step(nc.vector.tensor_scalar(inv, inv, 127.0, None, ALU.mult))
                    ch.step(nc.vector.tensor_scalar(tmp, src, inv, MAGIC, ALU.mult, ALU.add))
                    ch.step(nc.vector.tensor_scalar(tmp, tmp, MAGIC, 127.0, ALU.subtract, ALU.min))
                    nc.vector.tensor_scalar(dst, tmp, -128.0, None, ALU.max).then_inc(sig, 1)

                ch = Chain(dve, sem("dve_step"), n, before(n, "dve_step"))
                with dve.Fori(0, B) as i:
                    ch.turn(i)
                    dve.wait_ge(sem("staged"), before(n, "staged") + i + 1)
                    for j in range(2):
                        quantise(ch, xs[:, j, :], nq[:, j, :], KT[:, 2 * j, 0:P], j, 1, sem(f"{n}_dve2"))
                    ch.did(nc.vector.tensor_scalar(rsum[:, 0, :], rsum[:, 1, :], sums[:, 0, 0:1], None, ALU.mult))
                    ch.step(nc.vector.tensor_scalar(rsum[:, 2, :], rsum[:, 1, :], sums[:, 1, 0:1], None, ALU.mult))
                    dve.wait_ge(sem(f"{n}_dve2"), i * 4 + 2)
                    dve.sem_inc(sem(f"{n}_nq"), 1)
                    dve.wait_ge(sem(f"{n}_h_psum"), i + 1)
                    for j in range(2):
                        dve.wait_ge(sem(f"{n}_silu"), 2 * i + j + 1)
                        g = QT[:, 2 * j:2 * j + 2, :].rearrange("p a b -> p (a b)")
                        ch.step(nc.vector.scalar_tensor_tensor(g, PS[:, 2 * j + 1, :], rsum[:, 2, j:j + 1], g,
                                                               ALU.mult, ALU.mult))
                        quantise(ch, g, hq[:, j, :], KT[:, 2 * j:2 * j + 2, :].rearrange("p a b -> p (a b)"), j, 3,
                                 sem(f"{n}_dve2"))
                    ch.step(nc.vector.tensor_scalar(rsum[:, 4, :], rsum[:, 3, :], sums[:, 2, 0:1], None, ALU.mult))
                    dve.wait_ge(sem(f"{n}_dve2"), i * 4 + 4)
                    dve.sem_inc(sem(f"{n}_hq"), 1)
                    dve.wait_ge(sem("y"), before(n, "y") + i + 1)
                    for j in range(2):
                        ch.did(nc.vector.scalar_tensor_tensor(res[:, j, :], PS[:, PB[1], j * P:(j + 1) * P],
                                                              rsum[:, 4, j:j + 1], xs[:, j, :], ALU.mult, ALU.add))
                    ch.wait()
                    layernorm(n, i, ch, None)
                    ch.end()

            own = {"L0f": L0f, "L1f": L1f, "L2a": L2a, "L2f": L2f, "L3a": L3a, "L3f": L3f}
            for s in STAGES:
                if s in own:
                    own[s]()
                elif ATTNS[s].small:
                    small_stage(ATTNS[s], small_batch)
                else:
                    dve.wait_ge(x_done, base[s])
                    ch = Chain(dve, sem("dve_step"), s, before(s, "dve_step"))
                    with dve.Fori(0, B) as i:
                        ch.turn(i)
                        attention(ATTNS[s], i, ch)
                        ch.end()


def pack(inputs):
    import numpy as np
    f = {k: np.asarray(v) for k, v in inputs.items()}
    out = np.zeros((P, NCOL), np.float32)

    def put(name, a, rows=P):
        at, n, _ = COLS[name]
        out[0:rows, at:at + n] = a.reshape(rows, n)

    def rep(name, a):
        at, n, _ = COLS[name]
        out[:, at:at + n] = a.reshape(1, n)

    def spread(name, m, dim, rows=P):
        at, n, _ = COLS[name]
        view = out[0:rows, at:at + n].reshape(rows, 4, 4, 32)
        for term in range(3):
            view[:, :, :, TERM * term:TERM * term + dim] = m.reshape(rows, 4, 4, dim)
        out[0:rows, at:at + n] = view.reshape(rows, n)

    def spread_bias(name, v, dim):
        at, n, _ = COLS[name]
        t = np.zeros((4, 4, 32), np.float32)
        for term in range(3):
            t[:, :, TERM * term:TERM * term + dim] = v.reshape(4, 4, dim)
        if name.endswith("bk"):
            t[:, :, SHIFT_ROW:SHIFT_ROW + 2] = 1.0
        if name == "L3x_bq":
            t[:, :, MASK_ROW] = 1.0 / ATTNS["L3x"].scale
        out[:, at:at + n] = t.reshape(4, P).T

    put("ident", np.eye(P, dtype=np.float32))
    rep("w8", 8.0 - np.arange(E, dtype=np.float32))
    put("L0a_wq", f["L0_attn_w_q"])
    put("L0a_wk", f["L0_attn_w_k"])
    put("L0a_wv", f["L0_attn_w_v"])
    put("L0a_wo", f["L0_attn_w_o"])

    def xattn(n, wq, bq, wk, bk, wv, bv, wo, bo):
        spread(f"{n}_wq", wq, 8)
        spread(f"{n}_wk", wk, 8)
        spread_bias(f"{n}_bq", bq, 8)
        spread_bias(f"{n}_bk", bk, 8)
        put(f"{n}_wv", wv)
        rep(f"{n}_bv", bv)
        put(f"{n}_wo", wo)
        rep(f"{n}_bo", bo)
        if ATTNS[n].rope:
            def swap(m):
                return m.reshape(m.shape[:-1] + (64, 2))[..., ::-1].reshape(m.shape)
            spread(f"{n}_wqr", swap(wq), 8)
            spread(f"{n}_wkr", swap(wk), 8)
            spread_bias(f"{n}_bqr", swap(bq), 8)
            spread_bias(f"{n}_bkr", swap(bk), 8)

    xattn("L0x", f["L0_xattn_wq"].T, f["L0_xattn_bq"], f["L0_xattn_wk"].T, f["L0_xattn_bk"],
          f["L0_xattn_wv"].T, f["L0_xattn_bv"], f["L0_xattn_wo"].T, f["L0_xattn_bo"])
    xattn("L1x", f["L1_xattn_W_Q"], f["L1_xattn_b_Q"], f["L1_xattn_W_K"], f["L1_xattn_b_K"],
          f["L1_xattn_W_V"], f["L1_xattn_b_V"], f["L1_xattn_W_O"], f["L1_xattn_b_O"])
    xattn("L2x", f["L2_xattn_w_q"], f["L2_xattn_b_q"], f["L2_xattn_w_k"], f["L2_xattn_b_k"],
          f["L2_xattn_w_v"], f["L2_xattn_b_v"], f["L2_xattn_w_o"], f["L2_xattn_b_o"])
    xattn("L3x", f["L3_xattn_Wq"].T, f["L3_xattn_bq"], f["L3_xattn_Wk"].T, f["L3_xattn_bk"],
          f["L3_xattn_Wv"].T, f["L3_xattn_bv"], f["L3_xattn_Wo"].T, f["L3_xattn_bo"])
    d = np.arange(P) % 32
    put("lo_q", (d // TERM == 2).astype(np.float32))
    put("sign_q", np.where(d // TERM == 2, -1.0, 1.0).astype(np.float32))
    put("lo_k", (d // TERM == 1).astype(np.float32))
    put("sign_k", np.where(d // TERM == 1, -1.0, 1.0).astype(np.float32))
    put("row_mask", (d == MASK_ROW).astype(np.float32))
    put("row_one", (d >= SHIFT_ROW).astype(np.float32))
    fr = (10000.0 ** (-(np.arange(4, dtype=np.float32) * 2.0) / 8)).astype(np.float32)
    put("L2x_freq", np.where(d < SHIFT_ROW, fr[(d // 2) % 4], 0).astype(np.float32))
    put("L2x_sign", np.where(d % 2 == 0, -1.0, 1.0).astype(np.float32))

    for what, src in (("q", "L1_attn_w_aq"), ("k", "L1_attn_w_ak")):
        m = f[src]
        put(f"L1a_w{what}", m)
        put(f"L1a_w{what}r", np.concatenate([m[:, :, 64:], m[:, :, :64]], axis=2))
    put("L1a_wv", f["L1_attn_w_av"])
    put("L1a_wo", f["L1_attn_w_ao"].transpose(1, 0, 2))
    ang = (np.arange(S, dtype=np.float32)[None, :] *
           np.power(np.float32(10000.0), -np.arange(64, dtype=np.float32) / 64)[:, None])
    put("L1a_cos", np.concatenate([np.cos(ang)] * 2).astype(np.float32))
    put("L1a_sin", np.concatenate([-np.sin(ang), np.sin(ang)]).astype(np.float32))

    put("L0f_wg", f["L0_ffn_Wg"])
    put("L0f_w1", f["L0_ffn_W1"].transpose(1, 0, 2))
    put("L0f_b1", f["L0_ffn_b1"].reshape(E, 4, P).transpose(2, 0, 1))
    put("L0f_w2", f["L0_ffn_W2"].reshape(E, 4, P, D).transpose(2, 0, 1, 3))
    put("L0f_b2", f["L0_ffn_b2"], rows=E)

    put("L2a_win", f["L2_attn_W_in"])
    put("L2a_bin", f["L2_attn_b_in"], rows=32)
    put("L2a_wdt1", f["L2_attn_W_dt1"])
    put("L2a_bdt1", f["L2_attn_b_dt1"], rows=64)
    put("L2a_wdt2", f["L2_attn_W_dt2"], rows=64)
    put("L2a_bdt2", f["L2_attn_b_dt2"])
    put("L2a_A", f["L2_attn_A"])
    put("L2a_D", f["L2_attn_D"])

    spread("L2f_wq", f["L2_ffn_q_w"].reshape(D, 16, 8)[:, :, :4], 4)
    spread_bias("L2f_bq", f["L2_ffn_q_b"].reshape(16, 8)[:, :4], 4)
    spread("L2f_wk", f["L2_ffn_k_w"], 4)
    spread_bias("L2f_bk", f["L2_ffn_k_b"], 4)
    put("L2f_wv", f["L2_ffn_v_w"])
    rep("L2f_bv", f["L2_ffn_v_b"])
    put("L2f_wo", f["L2_ffn_o_w"])
    put("L2f_ob", f["L2_ffn_o_b"])
    put("L2f_wr", f["L2_ffn_router_w"])
    rep("L2f_br", f["L2_ffn_router_b"])
    put("L2f_w1", f["L2_ffn_w1"].transpose(1, 0, 2))
    put("L2f_b1", f["L2_ffn_b1"].reshape(E, 2, P).transpose(2, 0, 1))
    put("L2f_w2", f["L2_ffn_w2"].reshape(E, 2, P, D).transpose(2, 0, 1, 3))
    put("L2f_b2", f["L2_ffn_b2"], rows=E)

    gates = np.zeros((16, 8, 16, 8), np.float32)
    for h in range(16):
        gates[h, :, h, :] = f["L3_attn_grep_w"].T
    put("L3a_w", np.concatenate([f["L3_attn_q_w"].T, f["L3_attn_k_w"].T, f["L3_attn_v_w"].T,
                                 gates.reshape(P, P)], axis=1))
    rep("L3a_b", np.concatenate([f["L3_attn_q_b"], f["L3_attn_k_b"], f["L3_attn_v_b"]] + [f["L3_attn_grep_b"]] * 16))
    put("L3a_wo", f["L3_attn_out_w"].T)
    rep("L3a_bo", f["L3_attn_out_b"])
    rep("L3a_ga", f["L3_attn_grep_a"])
    delta = np.arange(-7, 8)
    rep("L3a_rel", f["L3_attn_rel_emb"][np.abs(delta) + 16 * (delta > 0)])

    put("L3f_wg", f["L3_ffn_w_gate"].T)
    put("L3f_wu", f["L3_ffn_w_up"].T)
    put("L3f_wd", f["L3_ffn_w_down"].T.reshape(4, P, D).transpose(1, 0, 2))
    return out


def kernel(**inputs):
    import numpy as np
    import concourse.bacc as bacc
    from concourse.bass_utils import run_bass_kernel_spmd

    f = {k: np.asarray(v) for k, v in inputs.items()}
    arrays = {
        "wpack": pack(inputs),
        "x": np.ascontiguousarray(f["x"].reshape(NT, P, D).transpose(1, 0, 2)),
        "ctx": np.ascontiguousarray(f["ctx_1024"].reshape(B * S, D).T),
        "mask": np.ascontiguousarray(f["mask_Bx1xSxS2_ik1"].reshape(NT, P, S).transpose(1, 0, 2)),
        "kmask": np.ascontiguousarray(f["mask_Bx1x1xS2_ff1"].reshape(1, B * S)),
        "pos": np.ascontiguousarray(f["pos_BxS2"].reshape(1, B * S)),
        "hdm": np.ascontiguousarray(f["L0_attn_head_dim_mask"].reshape(P, 1)),
        "wint": np.concatenate([f["L1_ffn_w_gate"].T, f["L1_ffn_w_up"].T,
                                f["L1_ffn_w_down"].T.reshape(3, P, P).transpose(1, 0, 2).reshape(P, 384)], axis=1),
    }
    nc = bacc.Bacc("TRN2", target_bir_lowering=False, num_devices=1)
    aps = [nc.dram_tensor(f"in_{k}", a.shape, mybir.dt.from_np(a.dtype), kind="ExternalInput").ap() for k, a in arrays.items()]
    out = nc.dram_tensor("y", (P, NT, D), F32, kind="ExternalOutput").ap()
    decoder(nc, *aps, out)
    r = run_bass_kernel_spmd(nc, [{f"in_{k}": a for k, a in arrays.items()}], core_ids=[0])
    y = r.results[0]["y"]
    return np.ascontiguousarray(y.transpose(1, 0, 2).reshape(B, S, D))
```

```python
from contextlib import ExitStack

import concourse.bass as bass
from concourse import mybir

F32 = mybir.dt.float32
BF16 = mybir.dt.bfloat16
F32R = mybir.dt.float32r
I32 = mybir.dt.int32
U32 = mybir.dt.uint32
ALU = mybir.AluOpType
ACT = mybir.ActivationFunctionType
AX = mybir.AxisListType

P = 128
B = 8
S = 256
D = 128
NT = B * S // P
BIG = 1.0e30
E = 8
CAPACITY = 256
CONSTS = 13
TERM = 8
SHIFT_ROW = 24
MASK_ROW = 26
MAGIC = 12582912.0


class Attn:

    def __init__(self, name, heads, dim, small, scale, bias=True, rope=None, causal=False, clip=False,
                 keymask=False, vcols=128, self_attn=False, tail=True):
        self.name, self.heads, self.dim, self.small, self.scale = name, heads, dim, small, scale
        self.bias, self.rope, self.causal, self.clip, self.keymask = bias, rope, causal, clip, keymask
        self.vcols, self.self_attn, self.tail = vcols, self_attn, tail
        self.turned_scores = small and not clip
        self.tiles = 4 if small else heads
        self.group = 2 if small else min(4, self.tiles)
        self.small = small

    def items(self):
        out = []
        for t in range(0, self.tiles, self.group):
            for w in "qk":
                out.append((w, t))
                if self.rope:
                    out.append((w + "r", t))
        return out

    def item_step(self, k):
        return 8 + (k if self.rope else 2 * k)


R8 = 1.0 / 8 ** 0.5
ATTNS = {
    "L0a": Attn("L0a", 1, 128, False, 1.0 / 128 ** 0.5, bias=False, self_attn=True),
    "L0x": Attn("L0x", 16, 8, True, R8, clip=True),
    "L1a": Attn("L1a", 8, 128, False, 1.0, bias=False, rope="half", causal=True, self_attn=True, vcols=1024),
    "L1x": Attn("L1x", 16, 8, True, R8),
    "L2x": Attn("L2x", 16, 8, True, R8, rope="pair", causal=True),
    "L2f": Attn("L2f", 16, 4, True, 0.5, self_attn=True, vcols=64, tail=False),
    "L3x": Attn("L3x", 16, 8, True, R8, keymask=True),
}


def weight_columns():
    cols, at = {}, [0]

    def add(group, name, n):
        cols[name] = (at[0], n, group)
        at[0] += n

    def attn(a):
        n = a.name
        for w in "qk":
            add(n, f"{n}_w{w}", a.tiles * 128)
            if a.bias:
                add(n, f"{n}_b{w}", a.tiles)
            if a.rope:
                add(n, f"{n}_w{w}r", a.tiles * 128)
                if a.bias:
                    add(n, f"{n}_b{w}r", a.tiles)
        add(n, f"{n}_wv", a.vcols)
        if a.bias:
            add(n, f"{n}_bv", a.vcols)
            add(n, f"{n}_bo", 128)
        add(n, f"{n}_wo", a.heads * 128 if n == "L1a" else 128)

    add("const", "ident", 128)
    add("const", "w8", E)
    add("const", "lo_q", 1)
    add("const", "sign_q", 1)
    add("const", "lo_k", 1)
    add("const", "sign_k", 1)
    add("const", "row_mask", 1)
    add("const", "row_one", 1)
    attn(ATTNS["L0a"])
    attn(ATTNS["L0x"])
    add("L0f", "L0f_wg", E)
    add("L0f", "L0f_w1", E * 512)
    add("L0f", "L0f_b1", E * 4)
    add("L0f", "L0f_w2", E * 4 * 128)
    add("L0f", "L0f_b2", 128)
    attn(ATTNS["L1a"])
    add("L1a", "L1a_cos", 256)
    add("L1a", "L1a_sin", 256)
    attn(ATTNS["L1x"])
    attn(ATTNS["L2x"])
    add("L2x", "L2x_freq", 1)
    add("L2x", "L2x_sign", 1)
    add("L2a", "L2a_win", 32)
    add("L2a", "L2a_bin", 1)
    add("L2a", "L2a_wdt1", 64)
    add("L2a", "L2a_bdt1", 1)
    add("L2a", "L2a_wdt2", 128)
    add("L2a", "L2a_bdt2", 1)
    add("L2a", "L2a_A", 16)
    add("L2a", "L2a_D", 1)
    attn(ATTNS["L2f"])
    add("L2f", "L2f_ob", 1)
    add("L2f", "L2f_wr", E)
    add("L2f", "L2f_br", E)
    add("L2f", "L2f_w1", E * 256)
    add("L2f", "L2f_b1", E * 2)
    add("L2f", "L2f_w2", E * 2 * 128)
    add("L2f", "L2f_b2", 128)
    add("L3a", "L3a_w", 512)
    add("L3a", "L3a_b", 512)
    add("L3a", "L3a_wo", 128)
    add("L3a", "L3a_bo", 128)
    add("L3a", "L3a_ga", 16)
    add("L3a", "L3a_rel", 15 * 16)
    attn(ATTNS["L3x"])
    add("L3f", "L3f_wg", 512)
    add("L3f", "L3f_wu", 512)
    add("L3f", "L3f_wd", 512)
    return cols, at[0]


COLS, NCOL = weight_columns()
ORDER = ["L0a", "L0x", "L0f", "L1a", "L1x", "L1f", "L2a", "L2x", "L2f", "L3a", "L3x", "L3f"]


def weight_places():
    span = {}
    for at, n, g in COLS.values():
        a, b = span.get(g, (at, at))
        span[g] = (min(a, at), max(b, at + n))
    size = {g: b - a for g, (a, b) in span.items()}
    width = [max(size.get(s, 0) for s in ORDER[k::2]) for k in range(2)]
    place = {"const": 0}
    for k, s in enumerate(ORDER):
        if s in size:
            place[s] = size["const"] + (k % 2) * width[0]
    return span, place, size["const"] + sum(width)


SPAN, PLACE, WIDTH = weight_places()


class Chain:

    def __init__(self, eng, sem, key, first=0):
        self.eng, self.sem, self.key, self.per, self.first, self.n = eng, sem, key, PER[key], first, 0

    def turn(self, i):
        self.base, self.n = self.first + i * self.per, 0

    def end(self):
        assert self.n == self.per, f"{self.key}: {self.n} steps, {self.per} stated"

    def did(self, ins):
        ins.then_inc(self.sem, 1)
        self.n += 1

    def wait(self):
        self.eng.wait_ge(self.sem, self.base + self.n)

    def step(self, ins):
        self.did(ins)
        self.wait()


STEPS = 20
CHUNKS, CHUNK = 4, 4
TURN_X_STEP, V_STEP, OT_STEP, Y_STEP = 6, 7, 2, 3
STAGES = ORDER

PER = {"L0a": 7, "L1a": 14, "L0r": 43, "L0f": 7, "L1f": 6, "L2a": 0, "L2a_main": 8, "L2a_front": 21, "L2a_tail": 5, "L3a": 7, "L3m": 79, "L3f": 24, "L3f_x": 16, "L3q": 10}
PER.update({"L0x_heads": 2, "L0x_front": 0, "L0x_tail": 8, "L1x_heads": 4, "L1x_front": 0, "L1x_tail": 8, "L2x_heads": 4, "L2x_front": 22, "L2x_tail": 8, "L2f_heads": 4, "L2f_front": 0, "L2f_tail": 33, "L3x_heads": 4, "L3x_front": 3, "L3x_tail": 8})


def counts(n):
    each = {"staged": 1}
    if n not in ("L3a", "L3f"):
        each.update(xT_psum=1, xT=1)
    if n[-1] != "r":
        each.update(var=1, rstd=1)
        if n in ATTNS and ATTNS[n].small:
            each.update({f"{part}_step": PER[f"{n}_{part}"] for part in ("heads", "front", "tail")})
        else:
            each.update(dve_step=PER[n])
        if n not in ("L0f", "L2f", "L2a"):
            each.update(y=1)
    if n == "L3a":
        each.update(oT_psum=1, oT=1)
    if n in ATTNS:
        a = ATTNS[n]
        H, NI, NO = a.heads, len(a.items()), max(1, a.vcols // P)
        each.update(V_psum=1, V=1, item_psum=NI, item_a=(NI + 1) // 2, item_b=NI // 2, scores=H, max=H,
                    probs=H, values=H, on=H if a.vcols > 512 else 1, oT_psum=NO, oT=NO)
        if not a.turned_scores:
            each.update(turned=H, pt_a=(H + 1) // 2, pt_v=H // 2)
        if a.rope == "half":
            each.update(rotated=NI // 2)
        if a.clip:
            each.update(clipped=H)
        if a.small:
            each.update(V_held=1, rounded=2, stack=2, outputs=a.tiles, outputs_psum=1)
            if a.tail:
                each.update(y_read=1)
        if a.keymask:
            each.update(masked=1)
        if a.turned_scores:
            each.update(shift=a.tiles, shift_psum=a.tiles, shifted=a.tiles, probs=H // 2, values=H // 2,
                        turned_scores=H // 2)
    return {role: B * c for role, c in each.items()}


def before(n, role):
    total = 0
    for s in STAGES:
        for part in (s + "r", s) if s in ("L0f", "L3a") else (s,):
            if part == n:
                return total
            total += counts(part).get(role, 0)
    raise KeyError(n)



def decoder(nc, wpack, x_in, ctx_in, mask_in, kmask_in, pos_in, hdm_in, wint_in, out):
    ctx = ExitStack()
    with ctx:
        def sb(name, shape, dt=F32):
            return ctx.enter_context(nc.sbuf_tensor(name, shape, dt))

        sems = {}

        def sem(name):
            if name not in sems:
                sems[name] = ctx.enter_context(nc.semaphore(name))
            return sems[name]

        W = sb("W", [P, WIDTH])
        x_tok = sb("x_tok", [P, NT, D])
        ctxT = sb("ctxT", [P, B * S])
        xs = sb("xs", [P, 2, D])
        cs = sb("cs", [P, S])
        xT = sb("xT", [P, S])
        QT = sb("QT", [P, 8, S])
        KT = sb("KT", [P, 8, S])
        QS = sb("QS", [P, 4, S], F32R)
        KS = sb("KS", [P, 4, S], F32R)
        V = sb("V", [P, 2, 1024])
        negmax = sb("negmax", [P, 16, 2])
        sums = sb("sums", [P, 16, 2])
        rsum = sb("rsum", [P, 16, 2])
        On = sb("On", [P, 2, 1024])
        OT = sb("OT", [P, 8, S])
        res = sb("res", [P, 2, D])
        stats = sb("stats", [P, 2, 6])
        mv = sb("mv", [P, 2, 2])
        veps = sb("veps", [P, 2])
        rstd = sb("rstd", [P, 2])
        mhalf = sb("mhalf", [P, 2])
        identb = sb("identb", [P, P], BF16)
        causal = sb("causal", [P, 2, S], BF16)
        onesb = sb("onesb", [P, P], BF16)
        onesf = sb("onesf", [P, P])
        tri = sb("tri", [P, P], BF16)
        SEL = sb("SEL", [96, 32, P], BF16)
        kmask = sb("kmask", [P, S])
        keep = sb("keep", [P, S])
        kbias = sb("kbias", [P, S])
        causalT = sb("causalT", [P, P], BF16)
        big = sb("big", [P, 8192])
        RT = big[:, 0:1024].rearrange("p (a b) -> p a b", a=4)
        PR = big[:, 1024:2560].rearrange("p (r a b) -> p r a b", r=3, a=2)
        SC = big[:, 2560:3584].rearrange("p (r a b) -> p r a b", r=2, a=2)
        PT = big[:, 3584:4608].rearrange("p (r a b) -> p r a b", r=2, a=2)
        PX = big[:, 1024:3072].rearrange("p (r a b) -> p r a b", r=2, a=2)
        RT4 = big[:, 5888:7936].rearrange("p (r a b) -> p r a b", r=2, a=4)
        VT = big[:, 5632:5888].rearrange("p (a b) -> p a b", a=2)
        SH = big[:, 4608:5632].rearrange("p (t j r c) -> p t j r c", t=4, j=2, r=4)
        wint = sb("wint", [P, 1152], I32)
        wdeq = big[:, 4096:5248]
        tern = sb("tern", [P, 3, 512], BF16)
        comb = sb("comb", [P, NT, E])
        combs = sb("combs", [P, 2, E])
        combT = sb("combT", [E, S])
        rt = sb("rt", [P, 6, NT, E])
        rts = sb("rts", [P, 6, NT])
        ohb = sb("ohb", [P, 2, NT, E], BF16)
        hdm_i = sb("hdm_i", [P, 1], I32)
        hdm = sb("hdm", [P, 1])
        mask_i = sb("mask_i", [P, 2, S], I32)
        cap = sb("cap", [P, 2, S])
        pos_i = sb("pos_i", [P, S], I32)
        rot = sb("rot", [P, 6, S])
        PS = ctx.enter_context(nc.psum_tensor("PS", [P, 8, 512], F32))
        SCB, PTB, OB, PB = (0, 1, 2), (3, 4), 5, (6, 7)
        MAXB, SHB, EXPB = (0, 1), 2, (3, 4)
        GA, GB = 0, 3

        x_done = sem("x_done")
        w_in = {g: sem(f"w_in_{g}") for g in SPAN}
        x_loaded, ctx_loaded, small_loaded = sem("x_loaded"), sem("ctx_loaded"), sem("small_loaded")
        consts, dve_consts = sem("consts"), sem("dve_consts")
        out_sent = sem("out_sent")

        def w(name, a=0, b=None, rows=P):
            at, n, g = COLS[name]
            at += PLACE[g] - SPAN[g][0]
            b = n if b is None else b
            return W[0:rows, at + a:at + b]

        ident = w("ident")

        def tile2(i, b=None):
            return x_tok[:, bass.ds(2 * i, 2), :]

        base = {s: 8 * k + 1 for k, s in enumerate(STAGES)}
        last_x = 8 * len(STAGES) + 1

        def chunk(what, c):
            if what in ("exp", "tanh"):
                at = 1024 * (c + (CHUNKS if what == "tanh" else 0))
                return big[:, at:at + 1024]
            return (QT if what == "x" else V)[:, :, :].rearrange("p a b -> p (a b)")[:, 1024 * (c % 2):1024 * (c % 2) + 1024]

        xN, dN = KT[:, 4, :], KT[:, 5, :]
        dt_now, xT_now = OT[:, 3, :], xT
        bc = OT[0:32, 1, :]
        split_next = OT[0:96, 2, 0:P].bitcast(BF16)
        split_now = OT[0:96, 2, P:2 * P].bitcast(BF16)
        diag = KT[:, 6, 0:P]

        EXPERT_BANKS = {"L0f": ((5, 7), 2, 6), "L2f": ((5, 7, 2, 6), 5, 7)}

        def hidden(e, c, chunks):
            return 4 * (e % 2) + c if chunks == 4 else 4 + 2 * (e % 2) + c

        qkvg = big[:, :].rearrange("p (t j c) -> p t j c", t=B, j=2)

        def place(t):
            return V[:, :, :].rearrange("p a b -> p (a b)")[:, 1024 * (t % 2):1024 * (t % 2) + 1024]

        def key_products(eng, j, t):
            return eng.tensor_tensor(place(t).rearrange("p (u c) -> p u c", u=B),
                                     qkvg[:, t, j, 0:128].unsqueeze(1).broadcast_to([P, B, 128]),
                                     qkvg[:, :, j, 128:256], ALU.mult)

        def value_products(eng, j, t):
            sc = QT[:, 0:4, :].rearrange("p a b -> p (a b)").rearrange("p (t u h) -> p t u h", t=B, u=B)
            return eng.tensor_tensor(place(t).rearrange("p (u h d) -> p u h d", u=B, h=16),
                                     sc[:, t, :, :].unsqueeze(3).broadcast_to([P, B, 16, 8]),
                                     qkvg[:, :, j, 256:384].rearrange("p u (h d) -> p u h d", h=16), ALU.mult)

        def flat_pt(h):
            return PT[:, h % 2, :, :].rearrange("p a b -> p (a b)")

        def keys(a, j):
            return P if a.causal and j == 0 else S

        def turned_blocks(a):
            return [(kb, j) for kb in range(2) for j in range(2) if keys(a, j) > kb * P]

        block = ctx.enter_context(nc.Block())

        @block.sync
        def _(sp):
            sp.dma_start(x_tok[:, :, :], x_in).then_inc(x_loaded, 16)
            def load(g):
                if g in SPAN:
                    a, b = SPAN[g]
                    sp.dma_start(W[:, PLACE[g]:PLACE[g] + b - a], wpack[:, a:b]).then_inc(w_in[g], 16)

            load("const")
            load(STAGES[0])
            sp.dma_start(hdm_i[:, :], hdm_in).then_inc(small_loaded, 16)
            sp.dma_start(wint[:, :], wint_in).then_inc(small_loaded, 16)
            sp.dma_start(ctxT[:, :], ctx_in).then_inc(ctx_loaded, 16)
            for k, s in enumerate(STAGES):
                if k + 1 < len(STAGES):
                    sp.wait_ge(x_done, base[s])
                    load(STAGES[k + 1])
                tile = {"L0x": lambda i: (mask_i[:, :, :], mask_in[:, bass.ds(2 * i, 2), :], "mask_in"),
                        "L2x": lambda i: (pos_i[:, :], pos_in[:, bass.ds(i * S, S)].broadcast_to([P, S]), "pos_in"),
                        "L3x": lambda i: (kmask[:, :], kmask_in[:, bass.ds(i * S, S)].broadcast_to([P, S]), "kmask_in")}
                if s in tile:
                    dst, src, signal = tile[s](0)
                    sp.dma_start(dst, src).then_inc(sem(signal), 16)
                    with sp.Fori(1, B) as i:
                        dst, src, signal = tile[s](i)
                        sp.wait_ge(sem(f"{s}_tile_read"), i)
                        sp.dma_start(dst, src).then_inc(sem(signal), 16)
            sp.wait_ge(x_done, last_x)
            sp.dma_start(out, x_tok[:, :, :]).then_inc(out_sent, 16)
            sp.wait_ge(out_sent, 16)

        @block.gpsimd
        def _(pool):
            nc.gpsimd.memset(mhalf[:, :], -0.5).then_inc(consts, 1)
            nc.gpsimd.memset(onesb[:, :], 1.0).then_inc(consts, 1)
            nc.gpsimd.memset(causal[:, :, :], 0.0).then_inc(consts, 1)
            nc.gpsimd.memset(onesf[:, :], 1.0).then_inc(consts, 1)
            nc.gpsimd.memset(tri[:, :], 1.0).then_inc(consts, 1)
            nc.gpsimd.memset(SEL[:, :, :], 0.0).then_inc(consts, 1)
            pool.wait_ge(consts, 6)
            nc.gpsimd.affine_select(out=tri[:, :], in_=tri[:, :], compare_op=ALU.is_ge, fill=0.0,
                                    base=0, pattern=[[1, P]], channel_multiplier=-1).then_inc(consts, 1)
            for q in range(3):
                pool.wait_ge(consts, 7 + q)
                rows = SEL[32 * q:32 * q + 32, :, :]
                nc.gpsimd.affine_select(out=rows, in_=rows, compare_op=ALU.not_equal, fill=1.0,
                                        base=0, pattern=[[-1, 32], [0, P]], channel_multiplier=1).then_inc(consts, 1)
            pool.wait_ge(consts, 10)
            nc.gpsimd.affine_select(out=causal[:, :, :], in_=causal[:, :, :], compare_op=ALU.is_ge, fill=-BIG,
                                    base=0, pattern=[[128, 2], [-1, S]], channel_multiplier=1).then_inc(consts, 1)
            pool.wait_ge(consts, 11)
            nc.gpsimd.memset(causalT[:, :], 0.0).then_inc(consts, 1)
            pool.wait_ge(consts, 12)
            nc.gpsimd.affine_select(out=causalT[:, :], in_=causalT[:, :], compare_op=ALU.is_ge, fill=-BIG,
                                    base=0, pattern=[[1, P]], channel_multiplier=-1).then_inc(consts, 1)
            pool.wait_ge(consts, CONSTS)

            def inverse_root(s, i):
                pool.wait_ge(sem("var"), before(s, "var") + i + 1)
                nc.gpsimd.tensor_tensor(rstd[:, :], veps[:, :], mhalf[:, :], ALU.pow).then_inc(sem("rstd"), 1)

            def add_mask(s, i):
                nb = len(ATTNS[s].items()) // 2
                pool.wait_ge(sem("item_b"), before(s, "item_b") + (i + 1) * nb)
                nc.gpsimd.tensor_tensor(KT[:, 0:4, :], KT[:, 0:4, :], kbias[:, :].unsqueeze(1).broadcast_to([P, 4, S]),
                                        ALU.add).then_inc(sem("masked"), 1)

            for s in STAGES:
                if s == "L2a":
                    def products(i, first):
                        for c in range(CHUNKS):
                            pool.wait_ge(sem(f"{s}_g"), CHUNKS * i + c + 1)
                            nc.gpsimd.tensor_tensor(chunk("tanh", c), chunk("tanh", c), chunk("x", c), ALU.mult)\
                              .then_inc(sem(f"{s}_prod"), 1)
                            if c == 1 and not first:
                                inverse_root(s, i - 1)

                    products(0, True)
                    with pool.Fori(1, B) as i:
                        products(i, False)
                    inverse_root(s, B - 1)
                elif s == "L3x":
                    add_mask(s, 0)
                    add_mask(s, 1)
                    with pool.Fori(1, B - 1) as i:
                        inverse_root(s, i - 1)
                        add_mask(s, i + 1)
                    inverse_root(s, B - 2)
                    inverse_root(s, B - 1)
                elif s == "L3a":
                    pool.wait_ge(sem(f"{s}_gin"), 1)
                    for j in range(2):
                        for phase, part in enumerate((key_products, value_products)):
                            for t in range(1, B, 2):
                                used = 8 * j + 4 * phase + t // 2
                                if used:
                                    pool.wait_ge(sem(f"{s}_used"), used)
                                if phase and t == 1:
                                    pool.wait_ge(sem(f"{s}_p"), j + 1)
                                part(nc.gpsimd, j, t).then_inc(sem(f"{s}_pool"), 1)
                    with pool.Fori(0, B) as i:
                        inverse_root(s, i)
                elif s == "L1a":
                    items = ATTNS[s].items()
                    with pool.Fori(0, B) as i:
                        for j in range(len(items) // 2):
                            what, t0 = items[2 * j]
                            pool.wait_ge(sem("item_b"), before(s, "item_b") + i * (len(items) // 2) + j + 1)
                            pool.wait_ge(sem("item_a"), before(s, "item_a") + i * (len(items) // 2) + j + 1)
                            dst = (QT if what == "q" else KT)[:, t0:t0 + 4, :]
                            nc.gpsimd.tensor_tensor(dst, dst, RT4[:, j % 2, :, :], ALU.add).then_inc(sem("rotated"), 1)
                        inverse_root(s, i)
                else:
                    with pool.Fori(0, B) as i:
                        inverse_root(s, i)

        @block.tensor
        def _(pe):
            pe.wait_ge(w_in["const"], 16)
            pe.wait_ge(consts, CONSTS)
            pe.wait_ge(dve_consts, 1)

            def attention(a, i):
                n, H = a.name, a.heads
                items = a.items()
                NI = len(items)
                LAG = 2
                pe.wait_ge(w_in[n], 16)
                pe.wait_ge(sem("staged"), before(n, "staged") + i + 1)
                for j in range(2):
                    mm = nc.tensor.transpose(PS[:, PB[0], j * P:(j + 1) * P], xs[:, j, :], ident)
                mm.then_inc(sem("xT_psum"), 1)
                pe.wait_ge(sem("xT"), before(n, "xT") + i + 1)
                src = xT if a.self_attn else cs
                for j in range(2):
                    for c in range(0, a.vcols, 512):
                        c1 = min(c + 512, a.vcols)
                        bank, at = (PB[1], j * a.vcols) if a.vcols <= 256 else ((5, 6, 7, 2)[2 * j + c // 512], 0)
                        mm = nc.tensor.matmul(PS[:, bank, at:at + c1 - c], src[:, j * P:(j + 1) * P],
                                              w(f"{n}_wv", c, c1), start=True, stop=True)
                mm.then_inc(sem("V_psum"), 1)
                for k, (what, t0) in enumerate(items):
                    if k == 1:
                        pe.wait_ge(x_done, base[n] + i)
                    if k >= 2:
                        role = "item_a" if k % 2 == 0 else "item_b"
                        pe.wait_ge(sem(role), before(n, role) + i * ((NI + 1 - k % 2) // 2) + k // 2)
                    rhs = src if what[0] == "k" else xT
                    for t in range(a.group):
                        g = (GA, GB)[k % 2]
                        mm = nc.tensor.matmul(PS[:, g + t // 2, (t % 2) * S:(t % 2 + 1) * S],
                                              w(f"{n}_w{what}", (t0 + t) * P, (t0 + t + 1) * P), rhs[:, :],
                                              start=True, stop=True)
                    mm.then_inc(sem("item_psum"), 1)

                def pt(h):
                    return "pt_v" if h % 2 else "pt_a"

                def half(h):
                    return H // 2 if h % 2 else (H + 1) // 2

                def scores(h):
                    if h >= len(SCB):
                        pe.wait_ge(sem("probs"), before(n, "probs") + i * H + h - len(SCB) + 1)
                    bank = SCB[h % len(SCB)]
                    for j in range(2):
                        nk = keys(a, j)
                        o = PS[:, bank, j * S:j * S + nk]
                        mm = nc.tensor.matmul(o, QT[:, h, j * P:(j + 1) * P], KT[:, h, 0:nk],
                                              start=True, stop=not a.causal)
                        if a.causal:
                            mm = nc.tensor.matmul(o, identb[:, :], causal[:, j, 0:nk], start=False, stop=True)
                    mm.then_inc(sem("scores"), 1)

                def turn(h):
                    pe.wait_ge(sem("probs"), before(n, "probs") + i * H + h + 1)
                    if h >= 2:
                        pe.wait_ge(sem(pt(h)), before(n, pt(h)) + i * half(h) + h // 2)
                    for k, (kb, j) in enumerate(turned_blocks(a)):
                        mm = nc.tensor.transpose(PS[:, PTB[h % 2], k * P:(k + 1) * P],
                                                 PR[:, h % 3, j, kb * P:(kb + 1) * P], ident)
                    mm.then_inc(sem("turned"), 1)

                def values(h):
                    pe.wait_ge(sem(pt(h)), before(n, pt(h)) + i * half(h) + h // 2 + 1)
                    dv = a.vcols // H
                    for j in range(2):
                        if a.vcols > 512:
                            o = PS[:, (5, 6, 7, 5, 6, 7, 5, 6)[h], j * dv:(j + 1) * dv]
                            if h >= 3 and j == 0:
                                pe.wait_ge(sem("on"), before(n, "on") + i * H + h - 2)
                        else:
                            o = PS[:, OB, j * a.vcols + h * dv:j * a.vcols + (h + 1) * dv]
                        places = [(k, kb) for k, (kb, q) in enumerate(turned_blocks(a)) if q == j]
                        for k, kb in places:
                            mm = nc.tensor.matmul(o, flat_pt(h)[:, k * P:(k + 1) * P], V[:, kb, h * dv:(h + 1) * dv],
                                                  start=kb == 0, stop=k == places[-1][0])
                    mm.then_inc(sem("values"), 1)

                pe.wait_ge(sem("item_a"), before(n, "item_a") + (i + 1) * ((NI + 1) // 2))
                pe.wait_ge(sem("item_b"), before(n, "item_b") + (i + 1) * (NI // 2))
                if a.rope:
                    pe.wait_ge(sem("rotated"), before(n, "rotated") + (i + 1) * (NI // 2))
                pe.wait_ge(sem("V"), before(n, "V") + i + 1)
                for h in range(H + LAG + 1):
                    if h < H:
                        scores(h)
                    if LAG <= h < H + LAG:
                        turn(h - LAG)
                    if h > LAG:
                        values(h - LAG - 1)
                NO = max(1, a.vcols // P)
                if a.vcols > 512:
                    for k in range(NO):
                        pe.wait_ge(sem("on"), before(n, "on") + i * H + k + 1)
                        if k >= 2:
                            pe.wait_ge(sem("oT"), before(n, "oT") + i * NO + k - 1)
                        for j in range(2):
                            mm = nc.tensor.transpose(PS[:, PTB[k % 2], j * P:(j + 1) * P],
                                                     On[:, j, k * P:(k + 1) * P], ident)
                        mm.then_inc(sem("oT_psum"), 1)
                else:
                    pe.wait_ge(sem("on"), before(n, "on") + i + 1)
                    for j in range(2):
                        mm = nc.tensor.transpose(PS[:, PTB[0], j * P:(j + 1) * P], On[:, j, 0:P], ident)
                    mm.then_inc(sem("oT_psum"), 1)
                pe.wait_ge(sem("oT"), before(n, "oT") + (i + 1) * NO)
                for j in range(2):
                    for k in range(NO):
                        mm = nc.tensor.matmul(PS[:, GB, j * P:(j + 1) * P], OT[:, k, j * P:(j + 1) * P],
                                              w(f"{n}_wo", k * P, (k + 1) * P), start=k == 0, stop=k == NO - 1)
                mm.then_inc(sem("y"), 1)

            def small_front(a, b, s, tails):
                n, items = a.name, a.items()
                NI = len(items)
                src = xT if a.self_attn else cs
                if s == TURN_X_STEP:
                    if not tails:
                        pe.wait_ge(w_in[n], 16)
                    if tails and not a.tail:
                        pe.wait_ge(x_done, base[n] + b - 1)
                    pe.wait_ge(sem("staged"), before(n, "staged") + b + 1)
                    for j in range(2):
                        mm = nc.tensor.transpose(PS[:, PB[0], j * P:(j + 1) * P], xs[:, j, :], ident)
                    mm.then_inc(sem("xT_psum"), 1)
                if s == V_STEP:
                    pe.wait_ge(sem("xT"), before(n, "xT") + b + 1)
                    if tails and a.tail:
                        pe.wait_ge(sem("y_read"), before(n, "y_read") + b - 1)
                    for j in range(2):
                        mm = nc.tensor.matmul(PS[:, PB[1], j * a.vcols:(j + 1) * a.vcols], src[:, j * P:(j + 1) * P],
                                              w(f"{n}_wv"), start=True, stop=True)
                    mm.then_inc(sem("V_psum"), 1)
                for k, (what, t0) in enumerate(items):
                    if s != a.item_step(k):
                        continue
                    if k == 1:
                        pe.wait_ge(sem("V_held"), before(n, "V_held") + b + 1)
                    if k >= 2:
                        role = "item_b" if k % 2 else "item_a"
                        pe.wait_ge(sem(role), before(n, role) + b * (NI // 2) + k // 2)
                    rhs = src if what[0] == "k" else xT
                    for t in range(2):
                        mm = nc.tensor.matmul(PS[:, PB[k % 2], t * S:(t + 1) * S],
                                              w(f"{n}_w{what}", (t0 + t) * P, (t0 + t + 1) * P), rhs[:, :],
                                              start=True, stop=True)
                    mm.then_inc(sem("item_psum"), 1)

            def small_tail(a, i, s):
                n, rows = a.name, min(P, a.vcols)
                if s == OT_STEP:
                    pe.wait_ge(sem("on"), before(n, "on") + i + 1)
                    if rows < P:
                        pe.sem_inc(sem("on_passed"), 1)
                    for j in range(2):
                        mm = nc.tensor.transpose(PS[0:rows, PB[0], j * P:(j + 1) * P], On[:, j, 0:rows], ident)
                    mm.then_inc(sem("oT_psum"), 1)
                if s == Y_STEP:
                    pe.wait_ge(sem("oT"), before(n, "oT") + i + 1)
                    for j in range(2):
                        mm = nc.tensor.matmul(PS[:, PB[1], j * P:(j + 1) * P], OT[:, 0, j * P:(j + 1) * P],
                                              w(f"{n}_wo"), start=True, stop=True)
                    mm.then_inc(sem("y"), 1)

            def small_batch(a, i, first, last):
                n, H, T = a.name, a.heads, a.tiles
                NV = H // 2 if a.turned_scores else H

                def scores(h):
                    r, t = slice(32 * (h % 4), 32 * (h % 4) + 32), h // 4
                    ring = SCB if a.clip else MAXB
                    if h >= len(ring):
                        role = "clipped" if a.clip else "max"
                        pe.wait_ge(sem(role), before(n, role) + i * H + h - len(ring) + 1)
                    for j in range(2):
                        o = PS[:, ring[h % len(ring)], j * S:(j + 1) * S]
                        mm = nc.tensor.matmul(o, QS[r, t, j * P:(j + 1) * P], KS[r, t, :],
                                              start=True, stop=not a.causal)
                        if a.causal:
                            mm = nc.tensor.matmul(o, identb[:, :], causal[:, j, :], start=False, stop=True)
                    mm.then_inc(sem("scores"), 1)

                def turn(h):
                    pt = "pt_v" if h % 2 else "pt_a"
                    pe.wait_ge(sem("probs"), before(n, "probs") + i * H + h + 1)
                    if h >= 2:
                        pe.wait_ge(sem(pt), before(n, pt) + i * (H // 2) + h // 2)
                    for kb in range(2):
                        for j in range(2):
                            mm = nc.tensor.transpose(PS[:, PTB[h % 2], kb * S + j * P:kb * S + (j + 1) * P],
                                                     PR[:, h % 3, j, kb * P:(kb + 1) * P], ident)
                    mm.then_inc(sem("turned"), 1)

                def shift(t):
                    pe.wait_ge(sem("shift"), before(n, "shift") + i * T + t + 1)
                    if t >= 1:
                        pe.wait_ge(sem("shifted"), before(n, "shifted") + i * T + t)
                    for j in range(2):
                        mm = nc.tensor.transpose(PS[:, SHB, j * P:(j + 1) * P],
                                                 SH[:, t, j, :, :].rearrange("p r c -> p (r c)"), ident)
                    mm.then_inc(sem("shift_psum"), 1)

                def turned_scores(p):
                    t = p // 2
                    if p % 2 == 0:
                        pe.wait_ge(sem("shifted"), before(n, "shifted") + i * T + t + 1)
                    if p >= 1:
                        pe.wait_ge(sem("probs"), before(n, "probs") + i * (H // 2) + p)
                    for half in range(2):
                        h = 2 * p + half
                        r, bank = slice(32 * (h % 4), 32 * (h % 4) + 32), EXPB[half]
                        if a.causal:
                            nc.tensor.matmul(PS[:, bank, P:S], KS[r, t, 0:P], QS[r, t, P:S], start=True, stop=True)
                            for kb in range(2):
                                o = PS[:, bank, 2 * kb * P:(2 * kb + 1) * P]
                                nc.tensor.matmul(o, KS[r, t, kb * P:(kb + 1) * P], QS[r, t, kb * P:(kb + 1) * P],
                                                 start=True, stop=False)
                                mm = nc.tensor.matmul(o, identb[:, :], causalT[:, :], start=False, stop=True)
                        else:
                            for kb in range(2):
                                mm = nc.tensor.matmul(PS[:, bank, kb * S:(kb + 1) * S], KS[r, t, kb * P:(kb + 1) * P],
                                                      QS[r, t, :], start=True, stop=True)
                    mm.then_inc(sem("turned_scores"), 1)

                def head_values(h, px):
                    r, v = slice(32 * (h % 4), 32 * (h % 4) + 32), slice(32 * h, 32 * h + 32)
                    if h == 0:
                        pe.wait_ge(sem("V"), before(n, "V") + i + 1)
                        if not a.tail and not first:
                            pe.wait_ge(x_done, base[n] + i)
                    if h % 4 == 0 and h >= 4:
                        pe.wait_ge(sem("outputs"), before(n, "outputs") + i * T + h // 4)
                    if a.causal:
                        nc.tensor.matmul(PS[r, OB, 0:P], V[:, 0, v], px[:, 0:P], start=True, stop=True)
                        nc.tensor.matmul(PS[r, OB, P:S], V[:, 0, v], px[:, P:S], start=True, stop=False)
                        return nc.tensor.matmul(PS[r, OB, P:S], V[:, 1, v], px[:, S:S + P], start=False, stop=True)
                    nc.tensor.matmul(PS[r, OB, 0:S], V[:, 0, v], px[:, 0:S], start=True, stop=False)
                    return nc.tensor.matmul(PS[r, OB, 0:S], V[:, 1, v], px[:, S:2 * S], start=False, stop=True)

                def values(p):
                    if a.turned_scores:
                        pe.wait_ge(sem("probs"), before(n, "probs") + i * NV + p + 1)
                        head_values(2 * p, PX[:, p % 2, 0, :])
                        mm = head_values(2 * p + 1, PX[:, p % 2, 1, :])
                    else:
                        pt = "pt_v" if p % 2 else "pt_a"
                        pe.wait_ge(sem(pt), before(n, pt) + i * (H // 2) + p // 2 + 1)
                        mm = head_values(p, PT[:, p % 2, :, :].rearrange("p a b -> p (a b)"))
                    mm.then_inc(sem("values"), 1)

                pe.wait_ge(sem("stack"), before(n, "stack") + 2 * i + 2)
                for s in range(STEPS):
                    if s < H:
                        scores(s)
                    if a.turned_scores:
                        t, r = s // 4 - 1, s % 4
                        if t >= 0 and r == 0:
                            shift(t)
                        if t >= 0 and r % 2:
                            p = 2 * t + r // 2
                            turned_scores(p)
                            if p >= 1:
                                values(p - 1)
                    else:
                        if 2 <= s < H + 2:
                            turn(s - 2)
                        if 3 <= s < H + 3:
                            values(s - 3)
                    if not first and a.tail:
                        small_tail(a, i - 1, s)
                    if not last:
                        small_front(a, i + 1, s, not first)
                if a.turned_scores:
                    values(H // 2 - 1)
                for t in range(T):
                    pe.wait_ge(sem("outputs"), before(n, "outputs") + i * T + t + 1)
                    for j in range(2):
                        mm = nc.tensor.transpose(PS[:, EXPB[0] + j, t * P:(t + 1) * P],
                                                 OT[:, 4 + t, j * P:(j + 1) * P], ident)
                mm.then_inc(sem("outputs_psum"), 1)

            def small_stage(a):
                for s in range(STEPS):
                    small_front(a, 0, s, False)
                small_batch(a, 0, True, False)
                with pe.Fori(1, B - 1) as i:
                    small_batch(a, i, False, False)
                small_batch(a, B - 1, False, True)
                for s in (OT_STEP, Y_STEP):
                    small_tail(a, B - 1, s)

            def turn_x(n, i):
                pe.wait_ge(sem("staged"), before(n, "staged") + i + 1)
                for j in range(2):
                    mm = nc.tensor.transpose(PS[:, PB[0], j * P:(j + 1) * P], xs[:, j, :], ident)
                mm.then_inc(sem("xT_psum"), 1)
                pe.wait_ge(sem("xT"), before(n, "xT") + i + 1)

            def transpose_x(n, i, bank):
                pe.wait_ge(sem("staged"), before(n, "staged") + i + 1)
                for j in range(2):
                    mm = nc.tensor.transpose(PS[:, bank, j * P:(j + 1) * P], xs[:, j, :], ident)
                mm.then_inc(sem("xT_psum"), 1)

            def experts(n, i, src, chunks, first, turn_next):
                HB = (GA, GB)
                YB, combT_bank, b2_bank = EXPERT_BANKS[n]
                for e in range(E + 1):
                    if e < E:
                        if e >= 2 or not first:
                            pe.wait_ge(sem(f"{n}_h"), i * E + e - 1)
                        for c in range(chunks):
                            mm = nc.tensor.matmul(PS[:, HB[e % 2] + c // 2, (c % 2) * S:(c % 2 + 1) * S],
                                                  w(f"{n}_w1", (e * chunks + c) * P, (e * chunks + c + 1) * P),
                                                  src[:, :], start=True, stop=True)
                        mm.then_inc(sem(f"{n}_h_psum"), 1)
                    if e >= 1:
                        g = e - 1
                        pe.wait_ge(sem(f"{n}_h"), i * E + g + 1)
                        if g >= len(YB) or not first:
                            pe.wait_ge(sem(f"{n}_acc"), i * E + g - len(YB) + 1)
                        for j in range(2):
                            for c in range(chunks):
                                mm = nc.tensor.matmul(PS[:, YB[g % len(YB)], j * P:(j + 1) * P],
                                                      QT[:, hidden(g, c, chunks), j * P:(j + 1) * P],
                                                      w(f"{n}_w2", (g * chunks + c) * P, (g * chunks + c + 1) * P),
                                                      start=c == 0, stop=c == chunks - 1)
                        mm.then_inc(sem(f"{n}_ye"), 1)
                    if e == (E - 3 if turn_next is not None else E):
                        pe.wait_ge(sem(f"{n}_combs"), i + 1)
                        if combT_bank in YB:
                            pe.wait_ge(sem(f"{n}_acc"), i * E + E - 3)
                        for j in range(2):
                            mm = nc.tensor.transpose(PS[0:E, combT_bank, j * P:(j + 1) * P], combs[:, j, :], ident)
                        mm.then_inc(sem(f"{n}_combT_psum"), 1)
                    if e == (E - 1 if turn_next is not None else E):
                        pe.wait_ge(sem(f"{n}_combT"), i + 1)
                        if b2_bank in YB:
                            pe.wait_ge(sem(f"{n}_acc"), i * E + E - 2)
                        for j in range(2):
                            mm = nc.tensor.matmul(PS[:, b2_bank, j * P:(j + 1) * P], combT[:, j * P:(j + 1) * P],
                                                  w(f"{n}_b2", rows=E), start=True, stop=True)
                        mm.then_inc(sem(f"{n}_yb"), 1)
                        if turn_next:
                            transpose_x(n, i + 1, 2)

            def L0f():
                n = "L0f"
                pe.wait_ge(w_in[n], 16)
                for i0, i1, first in ((0, 1, True), (1, B, False)):
                    with pe.Fori(i0, i1) as i:
                        turn_x(n + "r", i)
                        if not first:
                            pe.wait_ge(sem(f"{n}_lg"), i)
                        for j in range(2):
                            mm = nc.tensor.matmul(PS[:, PB[1], j * E:(j + 1) * E], xT[:, j * P:(j + 1) * P],
                                                  w(f"{n}_wg"), start=True, stop=True)
                        mm.then_inc(sem(f"{n}_lg_psum"), 1)
                pe.wait_ge(sem(f"{n}_onehots"), 1)
                for k in range(2):
                    nc.tensor.matmul(PS[:, 0, k * P:(k + 1) * P], tri[:, :],
                                     ohb[:, k, :, :].rearrange("p t e -> p (t e)"), start=True, stop=True)
                    mm = nc.tensor.matmul(PS[:, 1, k * P:(k + 1) * P], onesb[:, :],
                                          ohb[:, k, :, :].rearrange("p t e -> p (t e)"), start=True, stop=True)
                mm.then_inc(sem(f"{n}_counts"), 1)
                pe.wait_ge(sem(f"{n}_routed"), 1)
                transpose_x(n, 0, 2)
                for i0, i1, first, last in ((0, 1, True, False), (1, B - 1, False, False), (B - 1, B, False, True)):
                    with pe.Fori(i0, i1) as i:
                        pe.wait_ge(sem("xT"), before(n, "xT") + i + 1)
                        experts(n, i, xT, 4, first, not last)

            def L2f():
                n = "L2f"
                a = ATTNS[n]

                def batch(i, first, last):
                    small_batch(a, i, first, last)
                    if not last:
                        for role in ("item_a", "item_b"):
                            pe.wait_ge(sem(role), before(n, role) + (i + 2) * (len(a.items()) // 2))
                    small_tail(a, i, OT_STEP)
                    pe.wait_ge(sem("oT"), before(n, "oT") + i + 1)
                    nc.tensor.matmul(PS[:, PB[1], 0:S], w(f"{n}_wo", rows=64), OT[0:64, 0, :],
                                     start=True, stop=True).then_inc(sem(f"{n}_mla_psum"), 1)
                    pe.wait_ge(sem(f"{n}_mla"), i + 1)
                    for j in range(2):
                        mm = nc.tensor.matmul(PS[:, PB[1], j * E:(j + 1) * E], OT[:, 1, j * P:(j + 1) * P],
                                              w(f"{n}_wr"), start=True, stop=True)
                    mm.then_inc(sem(f"{n}_lg_psum"), 1)
                    pe.wait_ge(sem(f"{n}_lg"), i + 1)
                    experts(n, i, OT[:, 1, :], 2, True, None)

                for s in range(STEPS):
                    small_front(a, 0, s, False)
                batch(0, True, False)
                with pe.Fori(1, B - 1) as i:
                    batch(i, False, False)
                batch(B - 1, False, True)

            def L1f():
                n = "L1f"
                pe.wait_ge(sem("wdeq_ready"), 1)
                with pe.Fori(0, B) as i:
                    turn_x(n, i)
                    for k, bank in enumerate((GA, GB)):
                        for c in range(3):
                            at = k * 384 + c * P
                            mm = nc.tensor.matmul(PS[:, bank + c // 2, (c % 2) * S:(c % 2 + 1) * S],
                                                  wdeq[:, at:at + P], xT[:, :], start=True, stop=True)
                        mm.then_inc(sem(f"{n}_h_psum"), 1)
                    pe.wait_ge(sem(f"{n}_h"), i + 1)
                    for j in range(2):
                        for c in range(3):
                            mm = nc.tensor.matmul(PS[:, PB[1], j * P:(j + 1) * P], QT[:, 3 + c, j * P:(j + 1) * P],
                                                  wdeq[:, 768 + c * P:896 + c * P], start=c == 0, stop=c == 2)
                    mm.then_inc(sem("y"), 1)

            def L2a():
                n = "L2a"
                BB, CB, YB, FB = (0, 2), 4, 6, 7

                def front(b, c):
                    if c == 0:
                        pe.wait_ge(sem("staged"), before(n, "staged") + b + 1)
                        for j in range(2):
                            mm = nc.tensor.transpose(PS[:, FB, j * P:(j + 1) * P], xs[:, j, :], ident)
                        mm.then_inc(sem("xT_psum"), 1)
                    if c == 1:
                        pe.wait_ge(sem("xT"), before(n, "xT") + b + 1)
                        nc.tensor.matmul(PS[0:32, FB, 0:S], w(f"{n}_win"), xN, start=True, stop=True)
                        nc.tensor.matmul(PS[0:64, FB, S:2 * S], w(f"{n}_wdt1"), xN, start=True, stop=True)\
                          .then_inc(sem(f"{n}_bc_psum"), 1)
                    if c == 2:
                        pe.wait_ge(sem(f"{n}_bc"), b + 1)
                        nc.tensor.matmul(PS[:, FB, 0:S], w(f"{n}_wdt2", rows=64), OT[0:64, 0, :], start=True, stop=True)\
                          .then_inc(sem(f"{n}_dt_psum"), 1)

                def batch(i, first, last):
                    def spread(c, bank, row):
                        for k in range(CHUNK):
                            mm = nc.tensor.matmul(PS[:, bank + k // 2, (k % 2) * S:(k % 2 + 1) * S],
                                                  SEL[:, row + CHUNK * c + k, :], split_now, start=True, stop=True)
                        return mm

                    pe.wait_ge(sem(f"{n}_stack"), i + 1)
                    spread(0, BB[0], 0).then_inc(sem(f"{n}_B"), 1)
                    for c in range(CHUNKS + 1):
                        if c + 1 < CHUNKS:
                            if c >= 1:
                                pe.wait_ge(sem(f"{n}_g"), CHUNKS * i + c)
                            spread(c + 1, BB[(c + 1) % 2], 0).then_inc(sem(f"{n}_B"), 1)
                        if c == 0:
                            pe.wait_ge(sem(f"{n}_xnow"), i + 1)
                            if not first:
                                pe.wait_ge(sem(f"{n}_y_read"), i)
                            for j in range(2):
                                mm = nc.tensor.matmul(PS[:, YB, j * P:(j + 1) * P], xT_now[:, j * P:(j + 1) * P], diag,
                                                      start=j == 0, stop=False)
                            mm.then_inc(sem(f"{n}_dx"), 1)
                        else:
                            pe.wait_ge(sem(f"{n}_hc"), CHUNKS * i + c)
                        if c < CHUNKS:
                            spread(c, CB, 16).then_inc(sem(f"{n}_C"), 1)
                        if c >= 1:
                            h = chunk("h", c - 1)
                            for j in range(2):
                                for k in range(CHUNK):
                                    at = k * S + j * P
                                    mm = nc.tensor.matmul(PS[:, YB, j * P:(j + 1) * P], h[:, at:at + P], ident,
                                                          start=False, stop=c == CHUNKS and j == 1 and k == CHUNK - 1)
                            mm.then_inc(sem(f"{n}_summed"), 1)
                        if not last:
                            front(i + 1, c)

                pe.wait_ge(w_in[n], 16)
                for c in range(CHUNKS):
                    front(0, c)
                batch(0, True, False)
                with pe.Fori(1, B - 1) as i:
                    batch(i, False, False)
                batch(B - 1, False, True)

            def L3a():
                n = "L3a"
                pe.wait_ge(w_in[n], 16)
                for i0, i1, first in ((0, 1, True), (1, B, False)):
                    with pe.Fori(i0, i1) as i:
                        turn_x(n + "r", i)
                        if not first:
                            pe.wait_ge(sem(f"{n}_qkvg"), i)
                        for j in range(2):
                            mm = nc.tensor.matmul(PS[:, j, :], xT[:, j * P:(j + 1) * P], w(f"{n}_w"),
                                                  start=True, stop=True)
                        mm.then_inc(sem(f"{n}_qkvg_psum"), 1)
                with pe.Fori(0, B) as i:
                    pe.wait_ge(sem("staged"), before(n, "staged") + i + 1)
                    for j in range(2):
                        mm = nc.tensor.transpose(PS[:, PTB[0], j * P:(j + 1) * P], On[:, j, 0:P], ident)
                    mm.then_inc(sem("oT_psum"), 1)
                    pe.wait_ge(sem("oT"), before(n, "oT") + i + 1)
                    pe.wait_ge(x_done, base[n] + i)
                    for j in range(2):
                        mm = nc.tensor.matmul(PS[:, PB[0], j * P:(j + 1) * P], OT[:, 0, j * P:(j + 1) * P],
                                              w(f"{n}_wo"), start=True, stop=True)
                    mm.then_inc(sem("y"), 1)

            def L3f():
                n = "L3f"
                pe.wait_ge(sem(f"{n}_wsum"), 1)
                nc.tensor.matmul(PS[:, 0, 0:3], onesf[:, :], mv[:, :, :].rearrange("p a b -> p (a b)")[:, 0:3],
                                 start=True, stop=True).then_inc(sem(f"{n}_wmean_psum"), 1)
                pe.wait_ge(sem(f"{n}_tern"), 1)
                nT = OT[:, 0, :].bitcast(BF16)
                mT = OT[:, 4:8, :].rearrange("p a b -> p (a b)").bitcast(BF16)
                nq = On[:, :, 0:64].bitcast(BF16)
                hq = On[:, :, 128:384].bitcast(BF16)
                idb = identb[:, :]
                with pe.Fori(0, B) as i:
                    pe.wait_ge(sem(f"{n}_nq"), i + 1)
                    for j in range(2):
                        mm = nc.tensor.transpose(PS[:, PB[0], :].bitcast(BF16)[:, j * P:(j + 1) * P], nq[:, j, :], idb)
                    mm.then_inc(sem(f"{n}_nT_psum"), 1)
                    pe.wait_ge(sem(f"{n}_nT"), i + 1)
                    for j in range(2):
                        for k in range(2):
                            mm = nc.tensor.matmul(PS[:, 2 * j + k, :], nT[:, j * P:(j + 1) * P], tern[:, k, :],
                                                  start=True, stop=True)
                    mm.then_inc(sem(f"{n}_h_psum"), 1)
                    pe.wait_ge(sem(f"{n}_hq"), i + 1)
                    for j in range(2):
                        for c in range(4):
                            mm = nc.tensor.transpose(PS[:, 4 + j, :].bitcast(BF16)[:, c * P:(c + 1) * P],
                                                     hq[:, j, c * P:(c + 1) * P], idb)
                    mm.then_inc(sem(f"{n}_mT_psum"), 1)
                    pe.wait_ge(sem(f"{n}_mT"), i + 1)
                    for j in range(2):
                        for c in range(4):
                            mm = nc.tensor.matmul(PS[:, PB[1], j * P:(j + 1) * P],
                                                  mT[:, (4 * j + c) * P:(4 * j + c + 1) * P],
                                                  tern[:, 2, c * P:(c + 1) * P], start=c == 0, stop=c == 3)
                    mm.then_inc(sem("y"), 1)

            own = {"L0f": L0f, "L1f": L1f, "L2a": L2a, "L2f": L2f, "L3a": L3a, "L3f": L3f}
            for s in STAGES:
                if s in own:
                    own[s]()
                elif ATTNS[s].small:
                    small_stage(ATTNS[s])
                else:
                    with pe.Fori(0, B) as i:
                        attention(ATTNS[s], i)

        @block.scalar
        def _(act):
            def attention(a, i):
                n, H = a.name, a.heads
                items = a.items()
                NI = len(items)
                act.wait_ge(w_in[n], 16)
                if n == "L0a":
                    act.wait_ge(sem("hdm_ready"), 1)
                act.wait_ge(x_done, base[n])
                nc.scalar.copy(xs[:, :, :], tile2(i)).then_inc(sem("staged"), 1)
                act.wait_ge(sem("xT_psum"), before(n, "xT_psum") + i + 1)
                nc.scalar.copy(xT[:, :], PS[:, PB[0], 0:S]).then_inc(sem("xT"), 1)
                if a.vcols > 512:
                    act.wait_ge(sem("V_psum"), before(n, "V_psum") + i + 1)
                    for k in range(4):
                        ins = nc.scalar.copy(V[:, k // 2, (k % 2) * 512:(k % 2 + 1) * 512], PS[:, (5, 6, 7, 2)[k], :])
                    ins.then_inc(sem("V"), 1)
                for k, (what, t0) in enumerate(items):
                    if k % 2 and not a.rope:
                        act.wait_ge(sem("item_psum"), before(n, "item_psum") + i * NI + k + 1)
                        for t in range(a.group):
                            src = PS[:, GB + t // 2, (t % 2) * S:(t % 2 + 1) * S]
                            ins = nc.scalar.copy(KT[:, t0 + t, :], src)
                        ins.then_inc(sem("item_b"), 1)
                for h in range(H + 3):
                    if h < H:
                        act.wait_ge(sem("max"), before(n, "max") + i * H + h + 1)
                        if h >= 3:
                            act.wait_ge(sem("turned"), before(n, "turned") + i * H + h - 2)
                        for j in range(2):
                            nk = keys(a, j)
                            ins = nc.scalar.activation(PR[:, h % 3, j, 0:nk], PS[:, SCB[h % 3], j * S:j * S + nk], ACT.Exp,
                                                       bias=negmax[:, h, j:j + 1], accum_out=sums[:, h, j:j + 1])
                        ins.then_inc(sem("probs"), 1)
                    g = h - 2
                    if g >= 0 and g < H and g % 2 == 0:
                        act.wait_ge(sem("turned"), before(n, "turned") + i * H + g + 1)
                        if g >= 2:
                            act.wait_ge(sem("values"), before(n, "values") + i * H + g - 1)
                        cols = P * len(turned_blocks(a))
                        nc.scalar.copy(flat_pt(0)[:, 0:cols], PS[:, PTB[0], 0:cols]).then_inc(sem("pt_a"), 1)
                NO = max(1, a.vcols // P)
                for k in range(NO):
                    act.wait_ge(sem("oT_psum"), before(n, "oT_psum") + i * NO + k + 1)
                    src = PS[:, PTB[k % 2], 0:S]
                    if n == "L0a":
                        ins = nc.scalar.activation(OT[:, 0, :], src, ACT.Copy, scale=hdm[:, 0:1])
                    else:
                        ins = nc.scalar.copy(OT[:, k, :], src)
                    ins.then_inc(sem("oT"), 1)

            def small_front(a, b, s, first=False):
                n, NI = a.name, len(a.items())
                if s == 1:
                    if first:
                        act.wait_ge(w_in[n], 16)
                        act.wait_ge(x_done, base[n])
                        act.wait_ge(ctx_loaded, 16)
                    else:
                        act.wait_ge(sem("item_psum"), before(n, "item_psum") + b * NI)
                    st = nc.scalar.copy(xs[:, :, :], tile2(b))
                    if not a.self_attn:
                        st = nc.scalar.copy(cs[:, :], ctxT[:, bass.ds(b * S, S)])
                    st.then_inc(sem("staged"), 1)
                if s == TURN_X_STEP:
                    act.wait_ge(sem("xT_psum"), before(n, "xT_psum") + b + 1)
                    nc.scalar.copy(xT[:, :], PS[:, PB[0], 0:S]).then_inc(sem("xT"), 1)
                if n == "L2x" and s == TURN_X_STEP + 1:
                    act.wait_ge(sem("angles"), b + 1)
                    nc.scalar.activation(rot[:, 4, :], rot[:, 4, :], ACT.Sin).then_inc(sem("sines"), 1)
                    nc.scalar.activation(rot[:, 0, :], rot[:, 5, :], ACT.Sin).then_inc(sem("sines"), 1)
                for k, (what, t0) in enumerate(a.items()):
                    if s == a.item_step(k) + 1 and k % 2 and not a.rope and not a.keymask:
                        act.wait_ge(sem("item_psum"), before(n, "item_psum") + b * NI + k + 1)
                        for t in range(2):
                            ins = nc.scalar.activation(KT[:, t0 + t, :], PS[:, PB[1], t * S:(t + 1) * S], ACT.Identity,
                                                       bias=w(f"{n}_bk", t0 + t, t0 + t + 1))
                        ins.then_inc(sem("item_b"), 1)

            def round_k(a, b, first):
                n, NI = a.name, len(a.items())
                if not first:
                    if a.turned_scores:
                        act.wait_ge(sem("turned_scores"), before(n, "turned_scores") + b * (a.heads // 2))
                    else:
                        act.wait_ge(sem("scores"), before(n, "scores") + b * a.heads)
                act.wait_ge(sem("item_b"), before(n, "item_b") + (b + 1) * (NI // 2))
                if a.keymask:
                    act.wait_ge(sem("masked"), before(n, "masked") + b + 1)
                nc.scalar.activation(KS[:, :, :], KT[:, 0:4, :], ACT.Copy, scale=w("sign_k")).then_inc(sem("rounded"), 1)

            def round_q(a, b):
                n, NI = a.name, len(a.items())
                act.wait_ge(sem("item_a"), before(n, "item_a") + (b + 1) * (NI // 2))
                nc.scalar.activation(QS[:, :, :], QT[:, 0:4, :], ACT.Copy, scale=w("sign_q")).then_inc(sem("rounded"), 1)

            def small_tail(a, i, s):
                n, rows = a.name, min(P, a.vcols)
                if s == OT_STEP:
                    act.wait_ge(sem("oT_psum"), before(n, "oT_psum") + i + 1)
                    nc.scalar.copy(OT[0:rows, 0, :], PS[0:rows, PB[0], 0:S]).then_inc(sem("oT"), 1)

            def small_batch(a, i, first, last):
                n, H, T = a.name, a.heads, a.tiles
                NV = H // 2 if a.turned_scores else H

                def exponentials(p):
                    act.wait_ge(sem("turned_scores"), before(n, "turned_scores") + i * NV + p + 1)
                    if p >= 2:
                        act.wait_ge(sem("values"), before(n, "values") + i * NV + p - 1)
                    cols = 3 * P if a.causal else 4 * P
                    nc.scalar.activation(PX[:, p % 2, :, 0:cols], PS[:, EXPB[0]:EXPB[0] + 2, 0:cols], ACT.Exp)\
                      .then_inc(sem("probs"), 1)

                def clipped_exponentials(h):
                    act.wait_ge(sem("max"), before(n, "max") + i * H + h + 1)
                    if h >= 3:
                        act.wait_ge(sem("turned"), before(n, "turned") + i * H + h - 2)
                    for j in range(2):
                        ins = nc.scalar.activation(PR[:, h % 3, j, :], SC[:, h % 2, j, :], ACT.Exp,
                                                   bias=negmax[:, h, j:j + 1])
                    ins.then_inc(sem("probs"), 1)

                def turned(h):
                    act.wait_ge(sem("turned"), before(n, "turned") + i * H + h + 1)
                    if h >= 2:
                        act.wait_ge(sem("values"), before(n, "values") + i * H + h - 1)
                    nc.scalar.copy(PT[:, 0, :, :], PS[:, PTB[0], :].rearrange("p (a b) -> p a b", a=2))\
                      .then_inc(sem("pt_a"), 1)

                def outputs(t):
                    act.wait_ge(sem("values"), before(n, "values") + i * NV + (t + 1) * (NV // T))
                    nc.scalar.copy(OT[:, 4 + t, :], PS[:, OB, 0:S]).then_inc(sem("outputs"), 1)

                for s in range(STEPS):
                    if a.turned_scores:
                        if s >= 5 and s % 2:
                            exponentials((s - 5) // 2)
                        if s in (9, 13, 17):
                            outputs((s - 9) // 4)
                    else:
                        if s < H:
                            clipped_exponentials(s)
                        if 2 <= s < H + 2 and s % 2 == 0:
                            turned(s - 2)
                        if s >= 7 and s % 4 == 3:
                            outputs((s - 7) // 4)
                    if not first and a.tail:
                        small_tail(a, i - 1, s)
                    if not last:
                        small_front(a, i + 1, s)
                if not last:
                    round_k(a, i + 1, False)
                if a.turned_scores:
                    outputs(T - 1)
                if not last:
                    round_q(a, i + 1)

            def small_stage(a):
                for s in range(STEPS):
                    small_front(a, 0, s, True)
                round_k(a, 0, True)
                round_q(a, 0)
                small_batch(a, 0, True, False)
                with act.Fori(1, B - 1) as i:
                    small_batch(a, i, False, False)
                small_batch(a, B - 1, False, True)
                small_tail(a, B - 1, OT_STEP)

            def stage_x(n, i):
                act.wait_ge(x_done, base[n])
                nc.scalar.copy(xs[:, :, :], tile2(i)).then_inc(sem("staged"), 1)

            def copy_xT(n, i):
                act.wait_ge(sem("xT_psum"), before(n, "xT_psum") + i + 1)
                nc.scalar.copy(xT[:, :], PS[:, PB[0], 0:S]).then_inc(sem("xT"), 1)

            def experts(n, i, chunks, func, first):
                for e in range(E):
                    act.wait_ge(sem(f"{n}_h_psum"), i * E + e + 1)
                    if e >= 2 or not first:
                        act.wait_ge(sem(f"{n}_ye"), i * E + e - 1)
                    for c in range(chunks):
                        ins = nc.scalar.activation(QT[:, hidden(e, c, chunks), :],
                                                   PS[:, (GA, GB)[e % 2] + c // 2, (c % 2) * S:(c % 2 + 1) * S],
                                                   func, bias=w(f"{n}_b1", e * chunks + c, e * chunks + c + 1))
                    ins.then_inc(sem(f"{n}_h"), 1)
                    if e == (E - 2 if chunks == 4 else E - 1):
                        act.wait_ge(sem(f"{n}_combT_psum"), i + 1)
                        nc.scalar.copy(combT[:, :], PS[0:E, EXPERT_BANKS[n][1], 0:S])\
                          .then_inc(sem(f"{n}_combT"), 1)

            def L0f():
                n = "L0f"
                act.wait_ge(w_in[n], 16)
                with act.Fori(0, B) as i:
                    act.wait_ge(x_done, base[n])
                    nc.scalar.copy(xs[:, :, :], tile2(i)).then_inc(sem("staged"), 1)
                    copy_xT(n + "r", i)
                act.wait_ge(sem(f"{n}_shifted"), 1)
                nc.scalar.activation(rt[:, 1, :, :], rt[:, 0, :, :], ACT.Exp).then_inc(sem(f"{n}_exp"), 1)
                def next_x(i):
                    act.wait_ge(sem("xT_psum"), before(n, "xT_psum") + i + 1)
                    nc.scalar.copy(xT[:, :], PS[:, 2, 0:S]).then_inc(sem("xT"), 1)

                nc.scalar.copy(xs[:, :, :], tile2(0)).then_inc(sem("staged"), 1)
                next_x(0)
                for i0, i1, first, last in ((0, 1, True, False), (1, B - 1, False, False), (B - 1, B, False, True)):
                    with act.Fori(i0, i1) as i:
                        if not last:
                            nc.scalar.copy(xs[:, :, :], tile2(i + 1)).then_inc(sem("staged"), 1)
                        experts(n, i, 4, ACT.Gelu_apprx_tanh, first)
                        if not last:
                            next_x(i + 1)

            def L2f():
                n = "L2f"
                a = ATTNS[n]

                def batch(i, first, last):
                    small_batch(a, i, first, last)
                    small_tail(a, i, OT_STEP)
                    act.wait_ge(sem(f"{n}_mla_psum"), i + 1)
                    nc.scalar.activation(OT[:, 1, :], PS[:, PB[1], 0:S], ACT.Identity, bias=w(f"{n}_ob"))\
                      .then_inc(sem(f"{n}_mla"), 1)
                    act.wait_ge(sem(f"{n}_shifted"), i + 1)
                    nc.scalar.activation(rt[:, 1, 0:2, :], rt[:, 0, 0:2, :], ACT.Exp).then_inc(sem(f"{n}_exp"), 1)
                    experts(n, i, 2, ACT.Gelu, True)

                for s in range(STEPS):
                    small_front(a, 0, s, True)
                round_k(a, 0, True)
                round_q(a, 0)
                batch(0, True, False)
                with act.Fori(1, B - 1) as i:
                    batch(i, False, False)
                batch(B - 1, False, True)

            def L1f():
                n = "L1f"
                with act.Fori(0, B) as i:
                    stage_x(n, i)
                    copy_xT(n, i)
                    act.wait_ge(sem(f"{n}_h_psum"), i * 2 + 1)
                    nc.scalar.activation(QT[:, 0:3, :], PS[:, GA:GA + 2, :].rearrange("p a b -> p (a b)")[:, 0:768]
                                         .rearrange("p (a b) -> p a b", a=3), ACT.Silu).then_inc(sem(f"{n}_silu"), 1)

            def L2a():
                n = "L2a"
                u = OT[:, 4, :]

                def front(b, c, first=False):
                    if c == 0:
                        if not first:
                            act.wait_ge(sem("xT_psum"), before(n, "xT_psum") + b)
                        nc.scalar.copy(xs[:, :, :], tile2(b)).then_inc(sem("staged"), 1)
                    if c == 3:
                        act.wait_ge(sem(f"{n}_zdt"), b + 1)
                        nc.scalar.activation(u, OT[:, 6, :], ACT.Abs).then_inc(sem(f"{n}_absz"), 1)
                        act.wait_ge(sem(f"{n}_absz"), b + 1)
                        nc.scalar.activation(u, u, ACT.Exp, scale=-1.0).then_inc(sem(f"{n}_u"), 1)

                def batch(i, first, last):
                    act.wait_ge(sem(f"{n}_dt"), i + 1)
                    if not first:
                        act.wait_ge(sem(f"{n}_dx"), i)
                        act.wait_ge(sem(f"{n}_abar"), CHUNKS * i)
                    nc.scalar.copy(xT_now[:, :], xN)
                    nc.scalar.copy(dt_now, dN).then_inc(sem(f"{n}_xnow"), 1)
                    act.wait_ge(sem(f"{n}_xnow"), i + 1)
                    for c in range(CHUNKS):
                        if not first:
                            act.wait_ge(sem(f"{n}_scan"), CHUNKS * (i - 1) + c + 1)
                        for k in range(CHUNK):
                            s, at = CHUNK * c + k, slice(k * S, (k + 1) * S)
                            nc.scalar.activation(chunk("exp", c)[:, at], dt_now, ACT.Exp, scale=w(f"{n}_A", s, s + 1))
                            nc.scalar.activation(chunk("tanh", c)[:, at], dt_now, ACT.Tanh, scale=negmax[:, s, 0:1])
                        if not (first and c < 2):
                            act.wait_ge(sem(f"{n}_prod"), CHUNKS * i + c - 1)
                        for k in range(CHUNK):
                            s, at = CHUNK * c + k, slice(k * S, (k + 1) * S)
                            ins = nc.scalar.activation(chunk("x", c)[:, at], xT_now[:, :], ACT.Copy,
                                                       scale=negmax[:, s, 1:2])
                        ins.then_inc(sem(f"{n}_abar"), 1)
                        if not last:
                            front(i + 1, c)

                act.wait_ge(w_in[n], 16)
                act.wait_ge(sem(f"{n}_Aready"), 1)
                act.wait_ge(x_done, base[n])
                for c in range(CHUNKS):
                    front(0, c, True)
                batch(0, True, False)
                with act.Fori(1, B - 1) as i:
                    batch(i, False, False)
                batch(B - 1, False, True)

            def L3a():
                n = "L3a"
                act.wait_ge(w_in[n], 16)
                with act.Fori(0, B) as i:
                    act.wait_ge(x_done, base[n])
                    nc.scalar.copy(xs[:, :, :], tile2(i)).then_inc(sem("staged"), 1)
                    copy_xT(n + "r", i)
                act.wait_ge(sem(f"{n}_gin"), 1)
                nc.scalar.activation(rt[:, 0:4, :, :], rt[:, 0:4, :, :], ACT.Exp, scale=-1.0).then_inc(sem(f"{n}_gexp"), 1)
                for j in range(2):
                    act.wait_ge(sem(f"{n}_s"), j + 1)
                    nc.scalar.activation(QT[:, 0:4, :], QT[:, 0:4, :], ACT.Exp).then_inc(sem(f"{n}_p"), 1)
                act.wait_ge(sem(f"{n}_O"), 1)
                for i0, i1, first in ((0, 1, True), (1, B, False)):
                    with act.Fori(i0, i1) as i:
                        nc.scalar.copy(On[:, :, 0:P], KT[:, :, :].rearrange("p a b -> p (a b)")
                                       .rearrange("p (t d) -> p t d", t=NT)[:, bass.ds(2 * i, 2), :])\
                          .then_inc(sem("staged"), 1)
                        act.wait_ge(sem("oT_psum"), before(n, "oT_psum") + i + 1)
                        if not first:
                            act.wait_ge(sem("y"), before(n, "y") + i)
                        nc.scalar.copy(OT[:, 0, :], PS[:, PTB[0], 0:S]).then_inc(sem("oT"), 1)

            def L3f():
                n = "L3f"
                nT = OT[:, 0, :].bitcast(BF16)
                mT = OT[:, 4:8, :].rearrange("p a b -> p (a b)").bitcast(BF16)
                stage_x(n, 0)

                def batch(i, last):
                    act.wait_ge(sem(f"{n}_nT_psum"), i + 1)
                    nc.scalar.copy(nT[:, 0:S], PS[:, PB[0], :].bitcast(BF16)[:, 0:S]).then_inc(sem(f"{n}_nT"), 1)
                    if not last:
                        stage_x(n, i + 1)
                    act.wait_ge(sem(f"{n}_h_psum"), i + 1)
                    for j in range(2):
                        nc.scalar.activation(QT[:, 2 * j:2 * j + 2, :].rearrange("p a b -> p (a b)"), PS[:, 2 * j, :],
                                             ACT.Silu, scale=rsum[:, 0, j:j + 1]).then_inc(sem(f"{n}_silu"), 1)
                    act.wait_ge(sem(f"{n}_mT_psum"), i + 1)
                    for j in range(2):
                        ins = nc.scalar.copy(mT[:, 512 * j:512 * (j + 1)], PS[:, 4 + j, :].bitcast(BF16)[:, 0:512])
                    ins.then_inc(sem(f"{n}_mT"), 1)

                with act.Fori(0, B - 1) as i:
                    batch(i, False)
                batch(B - 1, True)

            own = {"L0f": L0f, "L1f": L1f, "L2a": L2a, "L2f": L2f, "L3a": L3a, "L3f": L3f}
            for s in STAGES:
                if s in own:
                    own[s]()
                elif ATTNS[s].small:
                    small_stage(ATTNS[s])
                else:
                    with act.Fori(0, B) as i:
                        attention(ATTNS[s], i)

        @block.vector
        def _(dve):
            dve.wait_ge(small_loaded, 32)
            dve.wait_ge(w_in["const"], 16)
            nc.vector.tensor_copy(identb[:, :], ident).then_inc(dve_consts, 1)
            nc.vector.tensor_copy(hdm[:, :], hdm_i[:, :]).then_inc(sem("hdm_ready"), 1)
            dve.wait_ge(x_loaded, 16)
            nc.vector.memset(veps[:, :], 0.0).then_inc(x_done, 1)

            def prepare(s):
                a = ATTNS[s]
                dve.wait_ge(x_done, base[s])
                H, dv = a.heads, a.vcols // a.heads
                nc.vector.memset(SH[:, :, :, :, :], 0.0).then_inc(sem(f"{s}_cleared"), 1)
                nc.vector.memset(V[:, :, 0:32 * H], 0.0).then_inc(sem(f"{s}_cleared"), 1)
                dve.wait_ge(sem(f"{s}_cleared"), 2)
                for j in range(2):
                    ones = V[:, j, 0:32 * H].rearrange("p (h d) -> p h d", h=H)[:, :, dv]
                    nc.vector.memset(ones, 1.0).then_inc(sem(f"{s}_cleared"), 1)
                dve.wait_ge(sem(f"{s}_cleared"), 4)

            def layernorm(s, i, ch, bo):
                moments(ch, bo)
                normalise(s, i, ch)

            def moments(ch, bo):
                if bo is not None:
                    ch.step(nc.vector.tensor_tensor(res[:, :, :], res[:, :, :],
                                                    bo.unsqueeze(1).broadcast_to([P, 2, D]), ALU.add))
                for j in range(2):
                    ch.did(nc.vector.bn_stats(stats[:, j, :], res[:, j, :]))
                ch.wait()
                dve.sem_inc(sem("stats_passed"), 1)
                for j in range(2):
                    ch.did(nc.vector.bn_aggr(mv[:, j, :], stats[:, j, :]))
                ch.wait()
                nc.vector.tensor_scalar(veps[:, :], mv[:, :, 1], 1e-5, None, ALU.add).then_inc(sem("var"), 1)

            def normalise(s, i, ch):
                dve.wait_ge(sem("rstd"), before(s, "rstd") + i + 1)
                for j in range(2):
                    ins = nc.vector.tensor_scalar(x_tok[:, bass.ds(2 * i + j, 1), :].rearrange("p a d -> p (a d)"),
                                                  res[:, j, :], mv[:, j, 0:1], rstd[:, j:j + 1],
                                                  ALU.subtract, ALU.mult)
                    if j == 0:
                        ch.did(ins)
                    else:
                        ch.wait()
                        ins.then_inc(x_done, 1)

            def attention(a, i, ch):
                n, H = a.name, a.heads
                items = a.items()
                NI = len(items)
                dve.wait_ge(w_in[n], 16)
                dve.wait_ge(sem("V_psum"), before(n, "V_psum") + i + 1)
                if a.vcols <= 512:
                    nc.vector.tensor_copy(V[:, :, 0:a.vcols],
                                          PS[:, PB[1], 0:2 * a.vcols].rearrange("p (a b) -> p a b", a=2))\
                      .then_inc(sem("V"), 1)
                for k, (what, t0) in enumerate(items):
                    if k % 2 and not a.rope:
                        continue
                    dve.wait_ge(sem("item_psum"), before(n, "item_psum") + i * NI + k + 1)
                    g = (GA, GB)[k % 2]
                    dst = QT if what[0] == "q" else KT
                    if a.rope:
                        j = k // 2
                        if what[1:] and j >= 2:
                            dve.wait_ge(sem("rotated"), before(n, "rotated") + i * (NI // 2) + j - 1)
                        to = RT4[:, j % 2, :, :] if what[1:] else dst[:, t0:t0 + 4, :]
                        src = PS[:, g:g + 2, :].rearrange("p a (b s) -> p (a b) s", b=2)
                        t = (w("L1a_sin") if what[1:] else w("L1a_cos")).unsqueeze(1).broadcast_to([P, 4, S])
                        if what[0] == "q":
                            ins = nc.vector.scalar_tensor_tensor(to, src, 1.0 / 128, t, ALU.mult, ALU.mult)
                        else:
                            ins = nc.vector.tensor_tensor(to, src, t, ALU.mult)
                        ins.then_inc(sem("item_b" if k % 2 else "item_a"), 1)
                    else:
                        for t in range(a.group):
                            ins = nc.vector.tensor_scalar(QT[:, t0 + t, :], PS[:, g + t // 2, (t % 2) * S:(t % 2 + 1) * S],
                                                          a.scale, None, ALU.mult)
                        ins.then_inc(sem("item_a"), 1)
                for h in range(H + 3):
                    if h < H:
                        dve.wait_ge(sem("scores"), before(n, "scores") + i * H + h + 1)
                        if a.causal:
                            for j in range(2):
                                ins = nc.vector.tensor_reduce(negmax[:, h, j:j + 1],
                                                              PS[:, SCB[h % 3], j * S:j * S + keys(a, j)],
                                                              AX.X, ALU.max, negate=True)
                        else:
                            ins = nc.vector.tensor_reduce(negmax[:, h, :], both(PS[:, SCB[h % 3], :]),
                                                          AX.X, ALU.max, negate=True)
                        ins.then_inc(sem("max"), 1)
                    g = h - 2
                    if g >= 0 and g < H and g % 2 == 1:
                        dve.wait_ge(sem("turned"), before(n, "turned") + i * H + g + 1)
                        if g >= 2:
                            dve.wait_ge(sem("values"), before(n, "values") + i * H + g - 1)
                        cols = P * len(turned_blocks(a))
                        nc.vector.tensor_copy(flat_pt(1)[:, 0:cols], PS[:, PTB[1], 0:cols]).then_inc(sem("pt_v"), 1)
                    if a.vcols > 512 and h >= 3:
                        g = h - 3
                        dve.wait_ge(sem("values"), before(n, "values") + i * H + g + 1)
                        ch.step(nc.vector.reciprocal(rsum[:, g, :], sums[:, g, :]))
                        ins = nc.vector.tensor_tensor(
                            On[:, :, g * P:(g + 1) * P],
                            PS[:, (5, 6, 7, 5, 6, 7, 5, 6)[g], 0:2 * P].rearrange("p (a b) -> p a b", a=2),
                            rsum[:, g, :].unsqueeze(2).broadcast_to([P, 2, P]), ALU.mult)
                        ins.then_inc(sem("on"), 1)
                if a.vcols <= 512:
                    dv = a.vcols // H
                    dve.wait_ge(sem("values"), before(n, "values") + i * H + H)
                    ch.step(nc.vector.reciprocal(rsum[:, 0:H, :], sums[:, 0:H, :]))
                    for j in range(2):
                        ins = nc.vector.tensor_tensor(
                            On[:, j, 0:a.vcols].rearrange("p (h d) -> p h d", h=H),
                            PS[:, OB, j * a.vcols:(j + 1) * a.vcols].rearrange("p (h d) -> p h d", h=H),
                            rsum[:, 0:H, j].unsqueeze(2).broadcast_to([P, H, dv]), ALU.mult)
                    ins.then_inc(sem("on"), 1)
                dve.wait_ge(sem("y"), before(n, "y") + i + 1)
                ch.step(nc.vector.tensor_tensor(res[:, :, :], PS[:, GB, 0:S].rearrange("p (a b) -> p a b", a=2),
                                                tile2(i), ALU.add))
                layernorm(n, i, ch, None)

            def small_chains(a):
                return [Chain(dve, sem(f"{part}_step"), f"{a.name}_{part}", before(a.name, f"{part}_step"))
                        for part in ("heads", "front", "tail")]

            def small_front(a, b, ch, s):
                n, items = a.name, a.items()
                NI = len(items)
                if s == 0:
                    ch.turn(b)
                    dve.wait_ge(w_in[n], 16)
                if a.keymask and s == 5:
                    dve.wait_ge(sem("kmask_in"), b * 16 + 16)
                    ch.did(nc.vector.tensor_scalar(kbias[:, :], kmask[:, :], 0.0, -1.0e9,
                                                   ALU.is_equal, ALU.mult))
                    ch.step(nc.vector.tensor_scalar(keep[:, :], kmask[:, :], 0.0, w("row_one"),
                                                    ALU.not_equal, ALU.max))
                    dve.sem_inc(sem(f"{n}_tile_read"), 1)
                    ch.step(nc.vector.tensor_scalar(kbias[:, :], kbias[:, :], w("row_mask"), None, ALU.mult))
                if n == "L2x" and s == 5:
                    angles(b, ch)
                if n == "L2x" and s == 8:
                    rotations(b, ch)
                if s == V_STEP + 1:
                    dve.wait_ge(sem("V_psum"), before(n, "V_psum") + b + 1)
                    nc.vector.tensor_tensor(VT[:, :, 0:a.vcols],
                                            PS[:, PB[1], 0:2 * a.vcols].rearrange("p (a b) -> p a b", a=2),
                                            w(f"{n}_bv").unsqueeze(1).broadcast_to([P, 2, a.vcols]), ALU.add)\
                      .then_inc(sem("V_held"), 1)
                for k, (what, t0) in enumerate(items):
                    if s != a.item_step(k) + 1 or (what == "k" and not a.rope and not a.keymask):
                        continue
                    dve.wait_ge(sem("item_psum"), before(n, "item_psum") + b * NI + k + 1)
                    dst = (QT if what[0] == "q" else KT)[:, t0:t0 + 2, :]
                    for t in range(2):
                        src, bias = PS[:, PB[k % 2], t * S:(t + 1) * S], w(f"{n}_b{what}", t0 + t, t0 + t + 1)
                        if a.rope:
                            tab = (1 if what[1:] else 0) + (2 if what[0] == "q" else 0)
                            ins = nc.vector.scalar_tensor_tensor((RT if what[1:] else dst)[:, t, :], src, bias,
                                                                 rot[:, tab, :], ALU.add, ALU.mult)
                        elif what == "k":
                            ins = nc.vector.scalar_tensor_tensor(dst[:, t, :], src, bias, keep[:, :],
                                                                 ALU.add, ALU.mult)
                        else:
                            ins = nc.vector.tensor_scalar(dst[:, t, :], src, bias, a.scale, ALU.add, ALU.mult)
                    if what[1:]:
                        ch.step(ins)
                        dve.wait_ge(sem("item_a"), before(n, "item_a") + b * (NI // 2) + k // 2 + 1)
                        ins = nc.vector.tensor_tensor(dst, dst, RT[:, 0:2, :], ALU.add)
                    ins.then_inc(sem("item_b" if k % 2 else "item_a"), 1)
                    if what[1:]:
                        dve.wait_ge(sem("item_b"), before(n, "item_b") + b * (NI // 2) + k // 2 + 1)
                if s == STEPS - 1:
                    ch.end()

            def small_rounding(a, b):
                n = a.name
                for k, (dst, src, x) in enumerate(((KS, KT, "k"), (QS, QT, "q"))):
                    dve.wait_ge(sem("rounded"), before(n, "rounded") + 2 * b + k + 1)
                    nc.vector.scalar_tensor_tensor(dst[:, :, :], src[:, 0:4, :], w(f"lo_{x}"),
                                                   dst[:, :, :].bitcast(F32), ALU.mult, ALU.add)\
                      .then_inc(sem("stack"), 1)

            def small_outputs(a, i, ch):
                n, H, dv = a.name, a.heads, a.vcols // a.heads
                ch.turn(i)
                dve.wait_ge(sem("outputs_psum"), before(n, "outputs_psum") + i + 1)
                o = [PS[:, EXPB[0] + j, :].rearrange("p (h d) -> p h d", h=H) for j in range(2)]
                for j in range(2):
                    ch.did(nc.vector.reciprocal(rsum[:, 0:H, j], o[j][:, :, dv]))
                ch.wait()
                for j in range(2):
                    ins = nc.vector.tensor_tensor(
                        On[:, j, 0:a.vcols].rearrange("p (h d) -> p h d", h=H), o[j][:, :, 0:dv],
                        rsum[:, 0:H, j].unsqueeze(2).broadcast_to([P, H, dv]), ALU.mult)
                ins.then_inc(sem("on"), 1)

            def small_tail(a, i, ch, s):
                n = a.name
                if s == Y_STEP + 1:
                    dve.wait_ge(sem("y"), before(n, "y") + i + 1)
                    nc.vector.tensor_tensor(res[:, :, :], PS[:, PB[1], 0:S].rearrange("p (a b) -> p a b", a=2),
                                            tile2(i), ALU.add).then_inc(sem("y_read"), 1)
                    dve.wait_ge(sem("y_read"), before(n, "y_read") + i + 1)
                if s == Y_STEP + 2:
                    moments(ch, w(f"{n}_bo"))
                if s == Y_STEP + 3:
                    normalise(n, i, ch)
                    ch.end()

            def small_batch(a, i, chains, first, last):
                n, H, T, dv = a.name, a.heads, a.tiles, a.vcols // a.heads
                ch, front, tail = chains

                def maximum(h):
                    dve.wait_ge(sem("scores"), before(n, "scores") + i * H + h + 1)
                    if a.clip:
                        if h >= 2:
                            dve.wait_ge(sem("probs"), before(n, "probs") + i * H + h - 1)
                        nc.vector.scalar_tensor_tensor(
                            SC[:, h % 2, :, :], PS[:, SCB[h % 3], :].rearrange("p (a b) -> p a b", a=2), -100.0,
                            cap[:, :, :], ALU.max, ALU.min).then_inc(sem("clipped"), 1)
                        dve.wait_ge(sem("clipped"), before(n, "clipped") + i * H + h + 1)
                        src = SC[:, h % 2, :, :]
                    else:
                        src = PS[:, MAXB[h % 2], :].rearrange("p (a b) -> p a b", a=2)
                    nc.vector.tensor_reduce(negmax[:, h, :], src, AX.X, ALU.max, negate=True)\
                      .then_inc(sem("max"), 1)

                def shift(t):
                    dve.wait_ge(sem("max"), before(n, "max") + i * H + 4 * t + 4)
                    m = negmax[:, 4 * t:4 * t + 4, :].rearrange("p r j -> p j r")
                    hi, lo = SH[:, t, :, :, SHIFT_ROW], SH[:, t, :, :, SHIFT_ROW + 1]
                    ch.step(nc.vector.tensor_copy(hi.bitcast(F32R), m))
                    nc.vector.tensor_tensor(lo, m, hi, ALU.subtract).then_inc(sem("shift"), 1)

                def shifted(t):
                    dve.wait_ge(sem("shift_psum"), before(n, "shift_psum") + i * T + t + 1)
                    dve.wait_ge(sem("stack"), before(n, "stack") + 2 * i + 2)
                    nc.vector.tensor_tensor(QS[:, t, :], QS[:, t, :].bitcast(F32), PS[:, SHB, 0:S], ALU.add)\
                      .then_inc(sem("shifted"), 1)

                def turned(h):
                    dve.wait_ge(sem("turned"), before(n, "turned") + i * H + h + 1)
                    if h >= 2:
                        dve.wait_ge(sem("values"), before(n, "values") + i * H + h - 1)
                    nc.vector.tensor_copy(PT[:, 1, :, :], PS[:, PTB[1], :].rearrange("p (a b) -> p a b", a=2))\
                      .then_inc(sem("pt_v"), 1)

                ch.turn(i)
                if not first and a.tail:
                    small_outputs(a, i - 1, tail)
                dve.wait_ge(sem("V_held"), before(n, "V_held") + i + 1)
                for j in range(2):
                    ins = nc.vector.tensor_copy(V[:, j, 0:32 * H].rearrange("p (h d) -> p h d", h=H)[:, :, 0:dv],
                                                VT[:, j, 0:a.vcols].rearrange("p (h d) -> p h d", h=H))
                ins.then_inc(sem("V"), 1)
                if a.clip:
                    dve.wait_ge(sem("mask_in"), i * 16 + 16)
                    ch.step(nc.vector.tensor_scalar(cap[:, :, :], mask_i[:, :, :], 0.0, -BIG,
                                                    ALU.is_equal, ALU.mult))
                    dve.sem_inc(sem(f"{n}_tile_read"), 1)
                    ch.step(nc.vector.tensor_scalar(cap[:, :, :], cap[:, :, :], 100.0, None, ALU.add))
                for s in range(STEPS):
                    if s < H:
                        maximum(s)
                    if a.turned_scores:
                        if s < H and s % 4 == 3:
                            shift(s // 4)
                        if s % 4 == 0 and 4 <= s <= H:
                            shifted(s // 4 - 1)
                    elif 2 <= s < H + 2 and s % 2:
                        turned(s - 2)
                    if not first and a.tail:
                        small_tail(a, i - 1, tail, s)
                    if not last:
                        small_front(a, i + 1, front, s)
                ch.end()
                if not last:
                    small_rounding(a, i + 1)

            def small_stage(a, batch):
                prepare(a.name)
                chains = small_chains(a)
                for s in range(STEPS):
                    small_front(a, 0, chains[1], s)
                small_rounding(a, 0)
                batch(a, 0, chains, True, False)
                with dve.Fori(1, B - 1) as i:
                    batch(a, i, chains, False, False)
                batch(a, B - 1, chains, False, True)
                if a.tail:
                    small_outputs(a, B - 1, chains[2])
                    for s in range(STEPS):
                        small_tail(a, B - 1, chains[2], s)

            def angles(i, ch):
                dve.wait_ge(sem("pos_in"), i * 16 + 16)
                two_pi = 6.283185307179586
                hi = 6.28125
                mid = 0.0019350051879882812
                lo = two_pi - hi - mid
                ch.step(nc.vector.tensor_copy(rot[:, 1, :], pos_i[:, :]))
                dve.sem_inc(sem("L2x_tile_read"), 1)
                ch.step(nc.vector.tensor_scalar(rot[:, 1, :], rot[:, 1, :], w("L2x_freq"), None, ALU.mult))
                for c, shift in ((4, 0.0), (5, two_pi / 4)):
                    ch.step(nc.vector.tensor_scalar(rot[:, 2, :], rot[:, 1, :], 1.0 / two_pi, shift / two_pi, ALU.mult, ALU.add))
                    ch.step(nc.vector.tensor_scalar(rot[:, 2, :], rot[:, 2, :], MAGIC, MAGIC, ALU.add, ALU.subtract))
                    ch.step(nc.vector.scalar_tensor_tensor(rot[:, 3, :], rot[:, 2, :], -hi, rot[:, 1, :], ALU.mult, ALU.add))
                    ch.step(nc.vector.scalar_tensor_tensor(rot[:, 3, :], rot[:, 2, :], -mid, rot[:, 3, :], ALU.mult, ALU.add))
                    ch.step(nc.vector.scalar_tensor_tensor(rot[:, 3, :], rot[:, 2, :], -lo, rot[:, 3, :], ALU.mult, ALU.add))
                    ch.step(nc.vector.tensor_scalar(rot[:, 3, :], rot[:, 3, :], shift, 3.1415925, ALU.add, ALU.min))
                    ins = nc.vector.tensor_scalar(rot[:, c, :], rot[:, 3, :], -3.1415925, None, ALU.max)
                    if c == 4:
                        ch.step(ins)
                    else:
                        ins.then_inc(sem("angles"), 1)

            def rotations(i, ch):
                dve.wait_ge(sem("sines"), i * 2 + 2)
                ch.did(nc.vector.tensor_scalar(rot[:, 1, :], rot[:, 4, :], w("L2x_sign"), None, ALU.mult))
                ch.did(nc.vector.tensor_scalar(rot[:, 2, :], rot[:, 0, :], ATTNS["L2x"].scale, None, ALU.mult))
                ch.did(nc.vector.tensor_scalar(rot[:, 3, :], rot[:, 4, :], w("L2x_sign"), ATTNS["L2x"].scale,
                                               ALU.mult, ALU.mult))
                ch.wait()

            def flat(t):
                return t.rearrange("p a b -> p (a b)")

            def both(t):
                return t.rearrange("p (a b) -> p a b", a=2)

            def top2(T, ch, count=None):
                def r(k):
                    return rt[:, k, 0:T, :]

                def c(k):
                    return rts[:, k, 0:T]

                def wide(k):
                    return c(k).unsqueeze(2).broadcast_to([P, T, E])

                ch.step(nc.vector.tensor_reduce(c(0), r(1), AX.X, ALU.add))
                ch.step(nc.vector.reciprocal(c(1), c(0)))
                ch.step(nc.vector.tensor_tensor(r(1), r(1), wide(1), ALU.mult))
                for k in range(2):
                    ch.step(nc.vector.tensor_reduce(c(2 + k), r(1), AX.X, ALU.max))
                    ch.step(nc.vector.tensor_tensor(r(4), r(1), wide(2 + k), ALU.is_equal))
                    ch.step(nc.vector.tensor_tensor(r(4), r(4), w("w8").unsqueeze(1).broadcast_to([P, T, E]), ALU.mult))
                    ch.step(nc.vector.tensor_reduce(c(4), r(4), AX.X, ALU.max))
                    ch.step(nc.vector.tensor_tensor(r(2 + k), r(4), wide(4), ALU.is_equal))
                    if k == 0:
                        ch.step(nc.vector.scalar_tensor_tensor(r(1), r(2), -2.0, r(1), ALU.mult, ALU.add))

            def weigh(T, ch, eps, dst, sig):
                def c(k):
                    return rts[:, k, 0:T]

                ch.step(nc.vector.tensor_tensor(c(4), c(2), c(3), ALU.add))
                ch.step(nc.vector.tensor_scalar(c(4), c(4), eps, None, ALU.add))
                ch.step(nc.vector.reciprocal(c(5), c(4)))
                for k in (2, 3):
                    ch.did(nc.vector.tensor_tensor(c(k), c(k), c(5), ALU.mult))
                ch.wait()
                for k in (2, 3):
                    ch.did(nc.vector.tensor_tensor(rt[:, k, 0:T, :], rt[:, k, 0:T, :],
                                                   c(k).unsqueeze(2).broadcast_to([P, T, E]), ALU.mult))
                ch.wait()
                nc.vector.tensor_tensor(dst, rt[:, 2, 0:T, :], rt[:, 3, 0:T, :], ALU.add).then_inc(sig, 1)

            def experts(n, i, ch, factor, start):
                ring, _, b2_bank = EXPERT_BANKS[n]
                for e in range(E):
                    dve.wait_ge(sem(f"{n}_ye"), i * E + e + 1)
                    if e == 0:
                        dve.wait_ge(sem(f"{n}_combs"), i + 1)
                    else:
                        dve.wait_ge(sem(f"{n}_acc"), i * E + e)
                    for j in range(2):
                        ins = nc.vector.scalar_tensor_tensor(res[:, j, :], PS[:, ring[e % len(ring)], j * P:(j + 1) * P],
                                                             combs[:, j, e:e + 1], (start if e == 0 else res)[:, j, :],
                                                             ALU.mult, ALU.add)
                    ins.then_inc(sem(f"{n}_acc"), 1)
                dve.wait_ge(sem(f"{n}_yb"), i + 1)
                dve.wait_ge(sem(f"{n}_acc"), i * E + E)
                ch.step(nc.vector.tensor_tensor(res[:, :, :], res[:, :, :], both(PS[:, b2_bank, 0:S]), ALU.add))

            def L0f():
                n = "L0f"
                dve.wait_ge(x_done, base[n])
                dve.wait_ge(w_in[n], 16)
                with dve.Fori(0, B) as i:
                    dve.wait_ge(sem(f"{n}_lg_psum"), i + 1)
                    nc.vector.tensor_copy(rt[:, 0, bass.ds(2 * i, 2), :], PS[:, PB[1], 0:2 * E].rearrange(
                        "p (a b) -> p a b", a=2)).then_inc(sem(f"{n}_lg"), 1)
                ch = Chain(dve, sem(f"{n}_route"), "L0r")
                ch.turn(0)
                dve.wait_ge(sem(f"{n}_lg"), B)
                ch.step(nc.vector.tensor_reduce(rts[:, 0, :], rt[:, 0, :, :], AX.X, ALU.max))
                nc.vector.tensor_tensor(rt[:, 0, :, :], rt[:, 0, :, :], rts[:, 0, :].unsqueeze(2).broadcast_to([P, NT, E]),
                                        ALU.subtract).then_inc(sem(f"{n}_shifted"), 1)
                dve.wait_ge(sem(f"{n}_exp"), 1)
                top2(NT, ch)
                nc.vector.tensor_copy(ohb[:, :, :, :], rt[:, 2:4, :, :]).then_inc(sem(f"{n}_onehots"), 1)
                dve.wait_ge(sem(f"{n}_counts"), 1)
                cnt = big[:, 0:256].rearrange("p (k t e) -> p k t e", k=2, t=NT)
                pre = big[:, 256:512].rearrange("p (k t e) -> p k t e", k=2, t=NT)
                ch.step(nc.vector.tensor_copy(big[:, 0:256], PS[:, 1, 0:256]))
                a, b = cnt, pre
                for d in (1, 2, 4, 8):
                    ch.did(nc.vector.tensor_copy(b[:, :, 0:d, :], a[:, :, 0:d, :]))
                    for k in range(2):
                        ch.did(nc.vector.tensor_tensor(b[:, k, d:NT, :], a[:, k, d:NT, :], a[:, k, 0:NT - d, :], ALU.add))
                    ch.wait()
                    a, b = b, a
                ch.step(nc.vector.tensor_scalar(big[:, 512:520], a[:, 0, NT - 1, :], float(CAPACITY), None, ALU.min))
                pos = big[:, 768:1024].rearrange("p (k t e) -> p k t e", k=2, t=NT)
                ch.did(nc.vector.tensor_copy(big[:, 768:1024], PS[:, 0, 0:256]))
                ch.wait()
                for k in range(2):
                    ch.did(nc.vector.tensor_tensor(pos[:, k, 1:NT, :], pos[:, k, 1:NT, :], a[:, k, 0:NT - 1, :], ALU.add))
                ch.wait()
                ch.step(nc.vector.tensor_tensor(pos[:, 1, :, :], pos[:, 1, :, :],
                                                big[:, 512:520].unsqueeze(1).broadcast_to([P, NT, E]), ALU.add))
                ch.step(nc.vector.tensor_scalar(big[:, 768:1024], big[:, 768:1024], float(CAPACITY), None, ALU.is_le))
                for k in range(2):
                    ch.did(nc.vector.tensor_tensor(rt[:, 2 + k, :, :], rt[:, 2 + k, :, :], pos[:, k, :, :], ALU.mult))
                ch.wait()
                weigh(NT, ch, 1e-9, comb[:, :, :], sem(f"{n}_routed"))
                ch.end()
                dve.wait_ge(sem(f"{n}_routed"), 1)
                ch = Chain(dve, sem("dve_step"), n, before(n, "dve_step"))
                with dve.Fori(0, B) as i:
                    ch.turn(i)
                    nc.vector.tensor_copy(combs[:, :, :], comb[:, bass.ds(2 * i, 2), :]).then_inc(sem(f"{n}_combs"), 1)
                    dve.wait_ge(x_done, base[n] + i)
                    ch.step(nc.vector.tensor_copy(res[:, :, :], tile2(i)))
                    experts(n, i, ch, 1.0, res)
                    layernorm(n, i, ch, None)
                    ch.end()

            def L2f():
                n = "L2f"

                def batch(a, i, chains, first, last):
                    small_batch(a, i, chains, first, last)
                    ch = chains[2]
                    small_outputs(a, i, ch)
                    dve.wait_ge(sem(f"{n}_lg_psum"), i + 1)
                    nc.vector.tensor_tensor(rt[:, 0, 0:2, :], PS[:, PB[1], 0:2 * E].rearrange("p (a b) -> p a b", a=2),
                                            w(f"{n}_br").unsqueeze(1).broadcast_to([P, 2, E]), ALU.add)\
                      .then_inc(sem(f"{n}_lg"), 1)
                    dve.wait_ge(sem(f"{n}_lg"), i + 1)
                    ch.step(nc.vector.tensor_reduce(rts[:, 0, 0:2], rt[:, 0, 0:2, :], AX.X, ALU.max))
                    nc.vector.tensor_tensor(rt[:, 0, 0:2, :], rt[:, 0, 0:2, :],
                                            rts[:, 0, 0:2].unsqueeze(2).broadcast_to([P, 2, E]),
                                            ALU.subtract).then_inc(sem(f"{n}_shifted"), 1)
                    dve.wait_ge(sem(f"{n}_exp"), i + 1)
                    top2(2, ch)
                    weigh(2, ch, 1e-8, combs[:, :, :], sem(f"{n}_combs"))
                    ch.step(nc.vector.memset(OT[:, 7, :], 0.0))
                    experts(n, i, ch, 1.0, OT[:, 7, :].rearrange("p (a b) -> p a b", a=2))
                    ch.step(nc.vector.tensor_scalar(res[:, :, :], res[:, :, :], 0.3, None, ALU.mult))
                    ch.step(nc.vector.scalar_tensor_tensor(flat(res[:, :, :]), flat(tile2(i)), 2.0, flat(res[:, :, :]),
                                                           ALU.mult, ALU.add))
                    layernorm(n, i, ch, None)
                    ch.end()

                small_stage(ATTNS[n], batch)

            def L1f():
                n = "L1f"
                dve.wait_ge(x_done, base[n])
                nc.vector.tensor_scalar(wdeq[:, :], wint[:, :], 1.0 / 127.0, None, ALU.mult).then_inc(sem("wdeq_ready"), 1)
                ch = Chain(dve, sem("dve_step"), n, before(n, "dve_step"))
                with dve.Fori(0, B) as i:
                    ch.turn(i)
                    dve.wait_ge(sem(f"{n}_h_psum"), i * 2 + 2)
                    dve.wait_ge(sem(f"{n}_silu"), i + 1)
                    nc.vector.tensor_tensor(QT[:, 3:6, :], QT[:, 0:3, :],
                                            PS[:, GB:GB + 2, :].rearrange("p a b -> p (a b)")[:, 0:768]
                                            .rearrange("p (a b) -> p a b", a=3), ALU.mult).then_inc(sem(f"{n}_h"), 1)
                    dve.wait_ge(sem("y"), before(n, "y") + i + 1)
                    ch.step(nc.vector.tensor_tensor(res[:, :, :], both(PS[:, PB[1], 0:S]), tile2(i), ALU.add))
                    layernorm(n, i, ch, None)
                    ch.end()

            def L2a():
                n = "L2a"
                dve.wait_ge(x_done, base[n])
                z, u = OT[:, 6, :], OT[:, 4, :]
                s1, s2, s3 = KT[:, 0, :], KT[:, 1, :], KT[:, 2, :]
                dve.wait_ge(w_in[n], 16)
                nc.vector.tensor_scalar(negmax[:, :, 0], w(f"{n}_A"), 0.5, None, ALU.mult)
                nc.vector.tensor_scalar(diag, ident, w(f"{n}_D"), None, ALU.mult)
                nc.vector.reciprocal(negmax[:, :, 1], w(f"{n}_A")).then_inc(sem(f"{n}_Aready"), 1)
                main, fch, tch = (Chain(dve, sem(f"{n}_{part}_step"), f"{n}_{part}") for part in ("main", "front", "tail"))

                def front(b, c):
                    ch = fch
                    if c == 1:
                        ch.turn(b)
                        dve.wait_ge(sem("xT_psum"), before(n, "xT_psum") + b + 1)
                        nc.vector.tensor_copy(xN, PS[:, 7, 0:S]).then_inc(sem("xT"), 1)
                    if c == 2:
                        dve.wait_ge(sem(f"{n}_bc_psum"), b + 1)
                        ch.did(nc.vector.tensor_scalar(bc, PS[0:32, 7, 0:S], w(f"{n}_bin", rows=32), None, ALU.add))
                        nc.vector.tensor_scalar(OT[0:64, 0, :], PS[0:64, 7, S:2 * S], w(f"{n}_bdt1", rows=64), None,
                                                ALU.add).then_inc(sem(f"{n}_bc"), 1)
                        ch.wait()
                        st = split_next
                        ch.step(nc.vector.tensor_copy(st[0:32, :], bc))
                        ch.step(nc.vector.tensor_tensor(bc, bc, st[0:32, :], ALU.subtract))
                        ch.step(nc.vector.tensor_copy(st[32:64, :], bc))
                        ch.step(nc.vector.tensor_copy(KT[0:32, 3, :], st[32:64, :]))
                        ch.step(nc.vector.tensor_tensor(bc, bc, KT[0:32, 3, :], ALU.subtract))
                        ch.step(nc.vector.tensor_copy(st[64:96, :], bc))
                    if c == 3:
                        dve.wait_ge(sem(f"{n}_dt_psum"), b + 1)
                        nc.vector.tensor_scalar(z, PS[:, 7, 0:S], w(f"{n}_bdt2"), None, ALU.add)\
                          .then_inc(sem(f"{n}_zdt"), 1)
                    if c == 4:
                        dve.wait_ge(sem(f"{n}_u"), b + 1)
                        ch.step(nc.vector.tensor_scalar(s1, u, 2.0, None, ALU.add))
                        ch.step(nc.vector.reciprocal(s2, s1))
                        ch.step(nc.vector.tensor_tensor(s1, u, s2, ALU.mult))
                        ch.step(nc.vector.tensor_tensor(s2, s1, s1, ALU.mult))
                        ch.step(nc.vector.tensor_scalar(s3, s2, 2.0 / 17, None, ALU.mult))
                        for k in (15, 13, 11, 9, 7, 5, 3):
                            ch.step(nc.vector.scalar_tensor_tensor(s3, s3, 2.0 / k, s2, ALU.add, ALU.mult))
                        ch.step(nc.vector.scalar_tensor_tensor(s3, s3, 2.0, s1, ALU.add, ALU.mult))
                        ch.step(nc.vector.scalar_tensor_tensor(z, z, 0.0, s3, ALU.max, ALU.add))
                        nc.vector.tensor_scalar(dN, z, 1e-7, 1e6, ALU.max, ALU.min).then_inc(sem(f"{n}_dt"), 1)
                        ch.end()

                def tail(i, c):
                    ch = tch
                    if c == 0:
                        ch.turn(i)
                        dve.wait_ge(sem(f"{n}_summed"), CHUNKS * (i + 1))
                        nc.vector.tensor_tensor(res[:, :, :], both(PS[:, 6, 0:S]), tile2(i), ALU.add)\
                          .then_inc(sem(f"{n}_y_read"), 1)
                        dve.wait_ge(sem(f"{n}_y_read"), i + 1)
                    if c == 1:
                        moments(ch, None)
                    if c == 2:
                        normalise(n, i, ch)
                        ch.end()

                def batch(i, first, last):
                    ch = main
                    ch.turn(i)
                    if not first:
                        dve.wait_ge(sem(f"{n}_C"), CHUNKS * i)
                    nc.vector.tensor_copy(split_now, split_next).then_inc(sem(f"{n}_stack"), 1)
                    for c in range(CHUNKS + 1):
                        if c < CHUNKS:
                            now = CHUNKS * i + c + 1
                            e, t, x = chunk("exp", c), chunk("tanh", c), chunk("x", c)
                            dve.wait_ge(sem(f"{n}_abar"), now)
                            ch.did(nc.vector.scalar_tensor_tensor(t, e, 1.0, t, ALU.add, ALU.mult))
                            dve.wait_ge(sem(f"{n}_B"), now)
                            bank = (0, 2)[c % 2]
                            ch.step(nc.vector.tensor_tensor(x, x, flat(PS[:, bank:bank + 2, :]), ALU.mult))
                            nc.vector.memset(e.rearrange("p (a b) -> p a b", a=CHUNK)[:, :, 0:1], 0.0)\
                              .then_inc(sem(f"{n}_g"), 1)
                        if not first:
                            tail(i - 1, c)
                        if not last and c == CHUNKS:
                            front(i + 1, c)
                        if c >= 1:
                            now = CHUNKS * i + c
                            e, t, h = chunk("exp", c - 1), chunk("tanh", c - 1), chunk("h", c - 1)
                            dve.wait_ge(sem(f"{n}_prod"), now)
                            if not (first and c < 3):
                                dve.wait_ge(sem(f"{n}_summed"), now - 2)
                            nc.vector.tensor_tensor_scan(h, e, t, 0.0, ALU.mult, ALU.add).then_inc(sem(f"{n}_scan"), 1)
                            dve.wait_ge(sem(f"{n}_scan"), now)
                            dve.wait_ge(sem(f"{n}_C"), now)
                            nc.vector.tensor_tensor(h, h, flat(PS[:, 4:6, :]), ALU.mult).then_inc(sem(f"{n}_hc"), 1)
                        if not last and c < CHUNKS:
                            front(i + 1, c)
                    ch.end()

                for c in range(CHUNKS + 1):
                    front(0, c)
                batch(0, True, False)
                with dve.Fori(1, B - 1) as i:
                    batch(i, False, False)
                batch(B - 1, False, True)
                for c in range(3):
                    tail(B - 1, c)

            def L3a():
                n = "L3a"
                dve.wait_ge(x_done, base[n])
                qkvg = big[:, :].rearrange("p (t j c) -> p t j c", t=B, j=2)
                dve.wait_ge(w_in[n], 16)
                with dve.Fori(0, B) as i:
                    dve.wait_ge(sem(f"{n}_qkvg_psum"), i + 1)
                    nc.vector.tensor_tensor(qkvg[:, bass.ds(i, 1), :, :].rearrange("p t j c -> p (t j) c"), PS[:, 0:2, :],
                                            w(f"{n}_b").unsqueeze(1).broadcast_to([P, 2, 512]), ALU.add)\
                      .then_inc(sem(f"{n}_qkvg"), 1)
                ch = Chain(dve, sem(f"{n}_mid"), "L3m")
                ch.turn(0)
                dve.wait_ge(sem(f"{n}_qkvg"), B)
                allt = big[:, :].rearrange("p (t c) -> p t c", t=NT)
                gin = rt[:, 0:4, :, :].rearrange("p k t e -> p (k t e)")
                ch.did(nc.vector.tensor_reduce(gin.rearrange("p (t g) -> p t g", t=NT),
                                               allt[:, :, 384:512].rearrange("p t (g k) -> p t g k", k=4), AX.X, ALU.add))
                ch.step(nc.vector.tensor_scalar(allt[:, :, 0:128], allt[:, :, 0:128], R8, None, ALU.mult))
                dve.sem_inc(sem(f"{n}_gin"), 1)
                dve.wait_ge(sem(f"{n}_gexp"), 1)
                ch.step(nc.vector.tensor_scalar(gin, gin, 1.0, None, ALU.add))
                ch.step(nc.vector.reciprocal(gin, gin))
                ab = gin.rearrange("p (t h k) -> p t h k", t=NT, k=2)
                g1 = comb[:, :, :].rearrange("p t e -> p (t e)")
                ga = OT[:, 0, 0:256].rearrange("p (t h) -> p t h", t=NT)
                ch.step(nc.vector.tensor_tensor(ga, ab[:, :, :, 1], w(f"{n}_ga").unsqueeze(1).broadcast_to([P, NT, 16]),
                                                ALU.mult))
                ch.step(nc.vector.scalar_tensor_tensor(ga, ga, -1.0, ab[:, :, :, 0], ALU.add, ALU.mult))
                ch.step(nc.vector.tensor_scalar(ga, ga, 2.0, None, ALU.add))
                rel = w(f"{n}_rel").rearrange("p (a h) -> p a h", a=15)
                sc = QT[:, 0:4, :].rearrange("p a b -> p (a b)").rearrange("p (t u h) -> p t u h", t=B, u=B)
                pr = V[:, :, :].rearrange("p a b -> p (a b)")
                Oall = KT[:, :, :].rearrange("p a b -> p (a b)").rearrange("p (t j c) -> p t j c", t=B, j=2)
                for j in range(2):
                    for t in range(B):
                        at = 1024 * (t % 2)
                        if t % 2 == 0:
                            ch.did(key_products(nc.vector, j, t))
                        ch.did(nc.vector.tensor_tensor(On[:, 0, t * P:(t + 1) * P].rearrange("p (u h) -> p u h", u=B),
                                                       rel[:, 7 - t:15 - t, :],
                                                       ga[:, 2 * t + j, :].unsqueeze(1).broadcast_to([P, B, 16]), ALU.mult))
                        ch.wait()
                        if t % 2:
                            dve.wait_ge(sem(f"{n}_pool"), 8 * j + t // 2 + 1)
                        ins = nc.vector.tensor_reduce(sc[:, t, :, :], pr[:, at:at + 1024].rearrange(
                            "p (u h d) -> p u h d", u=B, h=16), AX.X, ALU.add)
                        if t % 2:
                            ins.then_inc(sem(f"{n}_used"), 1)
                        else:
                            ch.did(ins)
                    ch.wait()
                    dve.wait_ge(sem(f"{n}_used"), 8 * j + 4)
                    scf = QT[:, 0:4, :].rearrange("p a b -> p (a b)")
                    ch.step(nc.vector.tensor_tensor(scf, scf, On[:, 0, :], ALU.add))
                    scu = scf.rearrange("p (t u h) -> p t h u", t=B, u=B)
                    mx = OT[:, 1, 0:128].rearrange("p (t h) -> p t h", t=B)
                    ch.step(nc.vector.tensor_reduce(mx, scu, AX.X, ALU.max))
                    nc.vector.tensor_tensor(sc, sc, mx.unsqueeze(2).broadcast_to([P, B, B, 16]), ALU.subtract)\
                      .then_inc(sem(f"{n}_s"), 1)
                    dve.wait_ge(sem(f"{n}_p"), j + 1)
                    sm = OT[:, 1, 128:256].rearrange("p (t h) -> p t h", t=B)
                    ch.step(nc.vector.tensor_reduce(sm, scu, AX.X, ALU.add))
                    ch.step(nc.vector.reciprocal(sm, sm))
                    for t in range(B):
                        at = 1024 * (t % 2)
                        if t % 2:
                            dve.wait_ge(sem(f"{n}_pool"), 8 * j + 4 + t // 2 + 1)
                        else:
                            ch.step(value_products(nc.vector, j, t))
                        ins = nc.vector.tensor_reduce(Oall[:, t, j, :], pr[:, at:at + 1024].rearrange(
                            "p (u c) -> p c u", u=B), AX.X, ALU.add)
                        if t % 2:
                            ins.then_inc(sem(f"{n}_used"), 1)
                            dve.wait_ge(sem(f"{n}_used"), 8 * j + 4 + t // 2 + 1)
                        else:
                            ch.step(ins)
                        ch.did(nc.vector.tensor_tensor(
                            Oall[:, t, j, :].rearrange("p (h d) -> p h d", h=16),
                            Oall[:, t, j, :].rearrange("p (h d) -> p h d", h=16),
                            sm[:, t, :].unsqueeze(2).broadcast_to([P, 16, 8]), ALU.mult))
                ch.wait()
                dve.sem_inc(sem(f"{n}_O"), 1)
                ch.end()
                ch = Chain(dve, sem("dve_step"), n, before(n, "dve_step"))
                with dve.Fori(0, B) as i:
                    ch.turn(i)
                    dve.wait_ge(sem("y"), before(n, "y") + i + 1)
                    ch.step(nc.vector.tensor_tensor(res[:, :, :], both(PS[:, PB[0], 0:S]), tile2(i), ALU.add))
                    layernorm(n, i, ch, w(f"{n}_bo"))
                    ch.end()

            def L3f():
                n = "L3f"
                dve.wait_ge(x_done, base[n])
                nq = On[:, :, 0:64].bitcast(BF16)
                hq = On[:, :, 128:384].bitcast(BF16)
                dve.wait_ge(w_in[n], 16)
                means = mv[:, :, :].rearrange("p a b -> p (a b)")
                ch = Chain(dve, sem(f"{n}_quant"), "L3q")
                ch.turn(0)
                for k, name in enumerate(("wg", "wu", "wd")):
                    ins = nc.vector.tensor_reduce(means[:, k:k + 1], w(f"{n}_{name}"), AX.X, ALU.add,
                                                  apply_absolute_value=True)
                ins.then_inc(sem(f"{n}_wsum"), 1)
                dve.wait_ge(sem(f"{n}_wmean_psum"), 1)
                wm, ws = sums[:, 0:3, 0], sums[:, 0:3, 1]
                ch.step(nc.vector.tensor_scalar(wm, PS[:, 0, 0:3], 1.0 / (512 * 128), 1e-5, ALU.mult, ALU.max))
                ch.step(nc.vector.reciprocal(ws, wm))
                for k, name in enumerate(("wg", "wu", "wd")):
                    tmp = KT[:, 2 * k:2 * k + 2, :].rearrange("p a b -> p (a b)")
                    ch.step(nc.vector.tensor_scalar(tmp, w(f"{n}_{name}"), sums[:, k, 1:2], 1.0, ALU.mult, ALU.min))
                    ch.step(nc.vector.tensor_scalar(tmp, tmp, -1.0, MAGIC, ALU.max, ALU.add))
                    ins = nc.vector.tensor_scalar(tern[:, k, :], tmp, MAGIC, None, ALU.subtract)
                    if k < 2:
                        ch.did(ins)
                    else:
                        ch.wait()
                        ins.then_inc(sem(f"{n}_tern"), 1)
                ch.end()

                def quantise(ch, src, dst, tmp, j, slot, sig):
                    amax, inv = rts[:, 0, j:j + 1], rts[:, 1, j:j + 1]
                    ch.step(nc.vector.tensor_reduce(amax, src, AX.X, ALU.max, apply_absolute_value=True))
                    ch.step(nc.vector.tensor_scalar(amax, amax, 1e-5, None, ALU.max))
                    ch.step(nc.vector.reciprocal(inv, amax))
                    ch.did(nc.vector.tensor_scalar(rsum[:, slot, j:j + 1], amax, 1.0 / 127, None, ALU.mult))
                    ch.step(nc.vector.tensor_scalar(inv, inv, 127.0, None, ALU.mult))
                    ch.step(nc.vector.tensor_scalar(tmp, src, inv, MAGIC, ALU.mult, ALU.add))
                    ch.step(nc.vector.tensor_scalar(tmp, tmp, MAGIC, 127.0, ALU.subtract, ALU.min))
                    nc.vector.tensor_scalar(dst, tmp, -128.0, None, ALU.max).then_inc(sig, 1)

                xch = Chain(dve, sem(f"{n}_x_step"), "L3f_x")
                ch = Chain(dve, sem("dve_step"), n, before(n, "dve_step"))

                def quantise_x(i):
                    xch.turn(i)
                    dve.wait_ge(sem("staged"), before(n, "staged") + i + 1)
                    for j in range(2):
                        quantise(xch, xs[:, j, :], nq[:, j, :], KT[:, 2 * j, 0:P], j, 1, sem(f"{n}_xq"))
                    xch.did(nc.vector.tensor_scalar(rsum[:, 0, :], rsum[:, 1, :], sums[:, 0, 0:1], None, ALU.mult))
                    xch.step(nc.vector.tensor_scalar(rsum[:, 2, :], rsum[:, 1, :], sums[:, 1, 0:1], None, ALU.mult))
                    xch.end()
                    dve.wait_ge(sem(f"{n}_xq"), i * 2 + 2)
                    dve.sem_inc(sem(f"{n}_nq"), 1)

                def batch(i, last):
                    ch.turn(i)
                    dve.wait_ge(sem(f"{n}_h_psum"), i + 1)
                    for j in range(2):
                        dve.wait_ge(sem(f"{n}_silu"), 2 * i + j + 1)
                        g = QT[:, 2 * j:2 * j + 2, :].rearrange("p a b -> p (a b)")
                        ch.step(nc.vector.scalar_tensor_tensor(g, PS[:, 2 * j + 1, :], rsum[:, 2, j:j + 1], g,
                                                               ALU.mult, ALU.mult))
                        quantise(ch, g, hq[:, j, :], KT[:, 2 * j:2 * j + 2, :].rearrange("p a b -> p (a b)"), j, 3,
                                 sem(f"{n}_gq"))
                    ch.step(nc.vector.tensor_scalar(rsum[:, 4, :], rsum[:, 3, :], sums[:, 2, 0:1], None, ALU.mult))
                    dve.wait_ge(sem(f"{n}_gq"), i * 2 + 2)
                    dve.sem_inc(sem(f"{n}_hq"), 1)
                    if not last:
                        quantise_x(i + 1)
                    dve.wait_ge(sem("y"), before(n, "y") + i + 1)
                    for j in range(2):
                        ch.did(nc.vector.scalar_tensor_tensor(
                            res[:, j, :], PS[:, PB[1], j * P:(j + 1) * P], rsum[:, 4, j:j + 1],
                            x_tok[:, bass.ds(2 * i + j, 1), :].rearrange("p a d -> p (a d)"), ALU.mult, ALU.add))
                    ch.wait()
                    layernorm(n, i, ch, None)
                    ch.end()

                quantise_x(0)
                with dve.Fori(0, B - 1) as i:
                    batch(i, False)
                batch(B - 1, True)

            own = {"L0f": L0f, "L1f": L1f, "L2a": L2a, "L2f": L2f, "L3a": L3a, "L3f": L3f}
            for s in STAGES:
                if s in own:
                    own[s]()
                elif ATTNS[s].small:
                    small_stage(ATTNS[s], small_batch)
                else:
                    dve.wait_ge(x_done, base[s])
                    ch = Chain(dve, sem("dve_step"), s, before(s, "dve_step"))
                    with dve.Fori(0, B) as i:
                        ch.turn(i)
                        attention(ATTNS[s], i, ch)
                        ch.end()


def pack(inputs):
    import numpy as np
    f = {k: np.asarray(v) for k, v in inputs.items()}
    out = np.zeros((P, NCOL), np.float32)

    def put(name, a, rows=P):
        at, n, _ = COLS[name]
        out[0:rows, at:at + n] = a.reshape(rows, n)

    def rep(name, a):
        at, n, _ = COLS[name]
        out[:, at:at + n] = a.reshape(1, n)

    def spread(name, m, dim, rows=P):
        at, n, _ = COLS[name]
        view = out[0:rows, at:at + n].reshape(rows, 4, 4, 32)
        for term in range(3):
            view[:, :, :, TERM * term:TERM * term + dim] = m.reshape(rows, 4, 4, dim)
        out[0:rows, at:at + n] = view.reshape(rows, n)

    def spread_bias(name, v, dim):
        at, n, _ = COLS[name]
        t = np.zeros((4, 4, 32), np.float32)
        for term in range(3):
            t[:, :, TERM * term:TERM * term + dim] = v.reshape(4, 4, dim)
        if name.endswith("bk"):
            t[:, :, SHIFT_ROW:SHIFT_ROW + 2] = 1.0
        if name == "L3x_bq":
            t[:, :, MASK_ROW] = 1.0 / ATTNS["L3x"].scale
        out[:, at:at + n] = t.reshape(4, P).T

    put("ident", np.eye(P, dtype=np.float32))
    rep("w8", 8.0 - np.arange(E, dtype=np.float32))
    put("L0a_wq", f["L0_attn_w_q"])
    put("L0a_wk", f["L0_attn_w_k"])
    put("L0a_wv", f["L0_attn_w_v"])
    put("L0a_wo", f["L0_attn_w_o"])

    def xattn(n, wq, bq, wk, bk, wv, bv, wo, bo):
        spread(f"{n}_wq", wq, 8)
        spread(f"{n}_wk", wk, 8)
        spread_bias(f"{n}_bq", bq, 8)
        spread_bias(f"{n}_bk", bk, 8)
        put(f"{n}_wv", wv)
        rep(f"{n}_bv", bv)
        put(f"{n}_wo", wo)
        rep(f"{n}_bo", bo)
        if ATTNS[n].rope:
            def swap(m):
                return m.reshape(m.shape[:-1] + (64, 2))[..., ::-1].reshape(m.shape)
            spread(f"{n}_wqr", swap(wq), 8)
            spread(f"{n}_wkr", swap(wk), 8)
            spread_bias(f"{n}_bqr", swap(bq), 8)
            spread_bias(f"{n}_bkr", swap(bk), 8)

    xattn("L0x", f["L0_xattn_wq"].T, f["L0_xattn_bq"], f["L0_xattn_wk"].T, f["L0_xattn_bk"],
          f["L0_xattn_wv"].T, f["L0_xattn_bv"], f["L0_xattn_wo"].T, f["L0_xattn_bo"])
    xattn("L1x", f["L1_xattn_W_Q"], f["L1_xattn_b_Q"], f["L1_xattn_W_K"], f["L1_xattn_b_K"],
          f["L1_xattn_W_V"], f["L1_xattn_b_V"], f["L1_xattn_W_O"], f["L1_xattn_b_O"])
    xattn("L2x", f["L2_xattn_w_q"], f["L2_xattn_b_q"], f["L2_xattn_w_k"], f["L2_xattn_b_k"],
          f["L2_xattn_w_v"], f["L2_xattn_b_v"], f["L2_xattn_w_o"], f["L2_xattn_b_o"])
    xattn("L3x", f["L3_xattn_Wq"].T, f["L3_xattn_bq"], f["L3_xattn_Wk"].T, f["L3_xattn_bk"],
          f["L3_xattn_Wv"].T, f["L3_xattn_bv"], f["L3_xattn_Wo"].T, f["L3_xattn_bo"])
    d = np.arange(P) % 32
    put("lo_q", (d // TERM == 2).astype(np.float32))
    put("sign_q", np.where(d // TERM == 2, -1.0, 1.0).astype(np.float32))
    put("lo_k", (d // TERM == 1).astype(np.float32))
    put("sign_k", np.where(d // TERM == 1, -1.0, 1.0).astype(np.float32))
    put("row_mask", (d == MASK_ROW).astype(np.float32))
    put("row_one", (d >= SHIFT_ROW).astype(np.float32))
    fr = (10000.0 ** (-(np.arange(4, dtype=np.float32) * 2.0) / 8)).astype(np.float32)
    put("L2x_freq", np.where(d < SHIFT_ROW, fr[(d // 2) % 4], 0).astype(np.float32))
    put("L2x_sign", np.where(d % 2 == 0, -1.0, 1.0).astype(np.float32))

    for what, src in (("q", "L1_attn_w_aq"), ("k", "L1_attn_w_ak")):
        m = f[src]
        put(f"L1a_w{what}", m)
        put(f"L1a_w{what}r", np.concatenate([m[:, :, 64:], m[:, :, :64]], axis=2))
    put("L1a_wv", f["L1_attn_w_av"])
    put("L1a_wo", f["L1_attn_w_ao"].transpose(1, 0, 2))
    ang = (np.arange(S, dtype=np.float32)[None, :] *
           np.power(np.float32(10000.0), -np.arange(64, dtype=np.float32) / 64)[:, None])
    put("L1a_cos", np.concatenate([np.cos(ang)] * 2).astype(np.float32))
    put("L1a_sin", np.concatenate([-np.sin(ang), np.sin(ang)]).astype(np.float32))

    put("L0f_wg", f["L0_ffn_Wg"])
    put("L0f_w1", f["L0_ffn_W1"].transpose(1, 0, 2))
    put("L0f_b1", f["L0_ffn_b1"].reshape(E, 4, P).transpose(2, 0, 1))
    put("L0f_w2", f["L0_ffn_W2"].reshape(E, 4, P, D).transpose(2, 0, 1, 3))
    put("L0f_b2", f["L0_ffn_b2"], rows=E)

    put("L2a_win", f["L2_attn_W_in"])
    put("L2a_bin", f["L2_attn_b_in"], rows=32)
    put("L2a_wdt1", f["L2_attn_W_dt1"])
    put("L2a_bdt1", f["L2_attn_b_dt1"], rows=64)
    put("L2a_wdt2", f["L2_attn_W_dt2"], rows=64)
    put("L2a_bdt2", f["L2_attn_b_dt2"])
    put("L2a_A", f["L2_attn_A"])
    put("L2a_D", f["L2_attn_D"])

    spread("L2f_wq", f["L2_ffn_q_w"].reshape(D, 16, 8)[:, :, :4], 4)
    spread_bias("L2f_bq", f["L2_ffn_q_b"].reshape(16, 8)[:, :4], 4)
    spread("L2f_wk", f["L2_ffn_k_w"], 4)
    spread_bias("L2f_bk", f["L2_ffn_k_b"], 4)
    put("L2f_wv", f["L2_ffn_v_w"])
    rep("L2f_bv", f["L2_ffn_v_b"])
    put("L2f_wo", f["L2_ffn_o_w"])
    put("L2f_ob", f["L2_ffn_o_b"])
    put("L2f_wr", f["L2_ffn_router_w"])
    rep("L2f_br", f["L2_ffn_router_b"])
    put("L2f_w1", f["L2_ffn_w1"].transpose(1, 0, 2))
    put("L2f_b1", f["L2_ffn_b1"].reshape(E, 2, P).transpose(2, 0, 1))
    put("L2f_w2", f["L2_ffn_w2"].reshape(E, 2, P, D).transpose(2, 0, 1, 3))
    put("L2f_b2", f["L2_ffn_b2"], rows=E)

    gates = np.zeros((16, 8, 16, 8), np.float32)
    for h in range(16):
        gates[h, :, h, :] = f["L3_attn_grep_w"].T
    put("L3a_w", np.concatenate([f["L3_attn_q_w"].T, f["L3_attn_k_w"].T, f["L3_attn_v_w"].T,
                                 gates.reshape(P, P)], axis=1))
    rep("L3a_b", np.concatenate([f["L3_attn_q_b"], f["L3_attn_k_b"], f["L3_attn_v_b"]] + [f["L3_attn_grep_b"]] * 16))
    put("L3a_wo", f["L3_attn_out_w"].T)
    rep("L3a_bo", f["L3_attn_out_b"])
    rep("L3a_ga", f["L3_attn_grep_a"])
    delta = np.arange(-7, 8)
    rep("L3a_rel", f["L3_attn_rel_emb"][np.abs(delta) + 16 * (delta > 0)])

    put("L3f_wg", f["L3_ffn_w_gate"].T)
    put("L3f_wu", f["L3_ffn_w_up"].T)
    put("L3f_wd", f["L3_ffn_w_down"].T.reshape(4, P, D).transpose(1, 0, 2))
    return out


def kernel(**inputs):
    import numpy as np
    import concourse.bacc as bacc
    from concourse.bass_utils import run_bass_kernel_spmd

    f = {k: np.asarray(v) for k, v in inputs.items()}
    arrays = {
        "wpack": pack(inputs),
        "x": np.ascontiguousarray(f["x"].reshape(NT, P, D).transpose(1, 0, 2)),
        "ctx": np.ascontiguousarray(f["ctx_1024"].reshape(B * S, D).T),
        "mask": np.ascontiguousarray(f["mask_Bx1xSxS2_ik1"].reshape(NT, P, S).transpose(1, 0, 2)),
        "kmask": np.ascontiguousarray(f["mask_Bx1x1xS2_ff1"].reshape(1, B * S)),
        "pos": np.ascontiguousarray(f["pos_BxS2"].reshape(1, B * S)),
        "hdm": np.ascontiguousarray(f["L0_attn_head_dim_mask"].reshape(P, 1)),
        "wint": np.concatenate([f["L1_ffn_w_gate"].T, f["L1_ffn_w_up"].T,
                                f["L1_ffn_w_down"].T.reshape(3, P, P).transpose(1, 0, 2).reshape(P, 384)], axis=1),
    }
    nc = bacc.Bacc("TRN2", target_bir_lowering=False, num_devices=1)
    aps = [nc.dram_tensor(f"in_{k}", a.shape, mybir.dt.from_np(a.dtype), kind="ExternalInput").ap() for k, a in arrays.items()]
    out = nc.dram_tensor("y", (P, NT, D), F32, kind="ExternalOutput").ap()
    decoder(nc, *aps, out)
    r = run_bass_kernel_spmd(nc, [{f"in_{k}": a for k, a in arrays.items()}], core_ids=[0])
    y = r.results[0]["y"]
    return np.ascontiguousarray(y.transpose(1, 0, 2).reshape(B, S, D))
```
